# Optimizing a Trainium2 kernel written in Bass

```python
import numpy as np
import jax
import jax.numpy as jnp

def _softmax(x, axis=-1):
    return jax.nn.softmax(x, axis=axis)

def _gelu(x):
    return jax.nn.gelu(x, approximate=True)

def _silu(x):
    return jax.nn.silu(x)

def _sigmoid(x):
    return jax.nn.sigmoid(x)

def _layernorm(x, axis=-1, eps=1e-05):
    m = jnp.mean(x, axis=axis, keepdims=True)
    v = jnp.var(x, axis=axis, keepdims=True)
    return (x - m) / jnp.sqrt(v + eps)

def _scatter_add(tgt, idx, src, axis=0):
    return tgt.at[idx].add(src)

def _segment_sum(src, seg, n):
    return jax.ops.segment_sum(src, seg, n)
kernel_name = 'mk_decoder_preln_d4_seqx_r8_caeb89'

def setup_inputs(seed: int=0):
    np.random.seed(seed)
    _w = jnp.asarray

    def _rec_inputs():
        import jax
        import jax.numpy as jnp
        _rk = jax.random.key(seed)
        x = -0.0002928 + 1 * jax.random.normal(jax.random.fold_in(_rk, 1), (128, 64, 128), jnp.float32)
        _lenS = 64 - jax.random.randint(jax.random.fold_in(_rk, 7), (128,), 0, max(1, 64 // 4) + 1, jnp.int32)
        _lenS2 = 64 - jax.random.randint(jax.random.fold_in(_rk, 8), (128,), 0, max(1, 64 // 4) + 1, jnp.int32)
        _ctx_1024P = jax.random.normal(jax.random.fold_in(_rk, 11), (128, 16, 128), jnp.float32)
        _ctx_1024c = jax.random.dirichlet(jax.random.fold_in(_rk, 511), 0.3 * jnp.ones((16,), jnp.float32), (128, 64))
        _ctx_1024t = jnp.einsum('bsk,bkd->bsd', _ctx_1024c, _ctx_1024P)
        _ctx_1024t = _ctx_1024t * jax.lax.rsqrt(jnp.mean(jnp.square(_ctx_1024t)) + 1e-12) * 0.953939
        ctx_1024 = -1.39393e-06 + 0.999914 * (_ctx_1024t + 0.3 * jax.random.normal(jax.random.fold_in(_rk, 611), (128, 64, 128), jnp.float32))
        _validS = jnp.arange(64)[None, :] < _lenS[:, None]
        _validS2 = jnp.arange(64)[None, :] < _lenS2[:, None]
        _causal = jnp.tril(jnp.ones((64, 64), dtype=bool))
        mask_1x1xSxS2_ik0 = jnp.where(jnp.broadcast_to(_validS2[0:1, None, None, :], (1, 1, 64, 64)), 0, 1).astype(jnp.int32)
        return (x, ctx_1024, mask_1x1xSxS2_ik0)
    x, ctx_1024, mask_1x1xSxS2_ik0 = _rec_inputs()

    def _L0_attn_setup():
        import jax, jax.numpy as jnp
        import numpy as np
        N_HEADS = 16

        def _rope(t, sin, cos):
            t_rot = jnp.stack([-t[..., 1::2], t[..., ::2]], axis=-1).reshape(t.shape)
            return t * cos + t_rot * sin
        key = jax.random.key(seed)
        ks = jax.random.split(key, 5)
        B, S, D = (2, 256, 128)
        scale = 1.0 / np.sqrt(D)
        return {'x': jax.random.normal(ks[0], (B, S, D), dtype=jnp.float32), 'Wq': jax.random.normal(ks[1], (D, D), dtype=jnp.float32) * scale, 'Wk': jax.random.normal(ks[2], (D, D), dtype=jnp.float32) * scale, 'Wv': jax.random.normal(ks[3], (D, D), dtype=jnp.float32) * scale, 'Wo': jax.random.normal(ks[4], (D, D), dtype=jnp.float32) * scale}
    _L0_attn_all = _L0_attn_setup()
    _L0_attn_in = {k: v for k, v in _L0_attn_all.items() if k in ('Wq', 'Wk', 'Wv', 'Wo')}
    del _L0_attn_all

    def _L0_xattn_setup():
        import jax, jax.numpy as jnp
        import numpy as np
        import math
        H = 16
        D = 128
        DH = D // H
        A = 1000.0

        def _alibi_bias(L, dtype):
            hh = jnp.arange(1, H + 1, dtype=jnp.float32)
            m = jnp.exp(-jnp.power(5000.0, (hh - 1.0) / (H - 1.0) * 0.8))
            seq = jnp.arange(L, dtype=jnp.float32)
            dist = jnp.abs(seq[:, None] - seq[None, :])
            bias = m[:, None, None] * jax.nn.softplus(A + dist)
            return bias.astype(dtype)
        key = jax.random.key(seed)
        ks = jax.random.split(key, 11)
        B, L = (2, 256)
        s = 1.0 / math.sqrt(D)
        inp = {'q': jax.random.normal(ks[0], (B, L, D), jnp.float32), 'k': jax.random.normal(ks[1], (B, L, D), jnp.float32), 'v': jax.random.normal(ks[2], (B, L, D), jnp.float32), 'Wq': jax.random.normal(ks[3], (D, D), jnp.float32) * s, 'bq': jnp.zeros((D,), jnp.float32), 'Wk': jax.random.normal(ks[4], (D, D), jnp.float32) * s, 'bk': jnp.zeros((D,), jnp.float32), 'Wv': jax.random.normal(ks[5], (D, D), jnp.float32) * s, 'bv': jnp.zeros((D,), jnp.float32), 'Wo': jax.random.normal(ks[6], (D, D), jnp.float32) * s, 'bo': jnp.zeros((D,), jnp.float32)}
        return inp
    _L0_xattn_all = _L0_xattn_setup()
    _L0_xattn_in = {k: v for k, v in _L0_xattn_all.items() if k in ('Wq', 'bq', 'Wk', 'bk', 'Wv', 'bv', 'Wo', 'bo')}
    del _L0_xattn_all

    def _L0_ffn_setup():
        import jax, jax.numpy as jnp
        import numpy as np
        B, S, D, F, E, R = (4, 256, 128, 512, 8, 4)
        key = jax.random.key(seed)
        ks = jax.random.split(key, 8)
        s_in = 1.0 / np.sqrt(D)
        s_ff = 1.0 / np.sqrt(F)
        return {'hidden_states': jax.random.normal(ks[0], (B, S, D), jnp.float32), 'gate_W': jax.random.normal(ks[1], (E, D), jnp.float32) * s_in, 'gate_b': jnp.zeros((E,), jnp.float32), 'wi_W': jax.random.normal(ks[2], (F, D), jnp.float32) * s_in, 'wi_b': jnp.zeros((F,), jnp.float32), 'wo_W': jax.random.normal(ks[3], (D, F), jnp.float32) * s_ff, 'wo_b': jnp.zeros((D,), jnp.float32), 'lora_A': jax.random.normal(ks[4], (E, R, D), jnp.float32) * s_in, 'lora_B': jax.random.normal(ks[5], (E, F, R), jnp.float32) * 0.02}
    _L0_ffn_all = _L0_ffn_setup()
    _L0_ffn_in = {k: v for k, v in _L0_ffn_all.items() if k in ('gate_W', 'gate_b', 'wi_W', 'wi_b', 'wo_W', 'wo_b', 'lora_A', 'lora_B')}
    del _L0_ffn_all

    def _L1_attn_setup():
        import jax, jax.numpy as jnp
        import numpy as np
        D = 128
        H = 16
        HKV = 4
        HD = D // H
        L = 64
        EPS = 1e-06
        LN_EPS = 1e-05
        B, S = (2, 128)

        def _feat(x):
            return jax.nn.elu(x) + 1.0
        key = jax.random.key(seed)
        ks = jax.random.split(key, 8)
        w = lambda k, shape: jax.random.normal(k, shape, jnp.float32) * 0.02
        return {'x': jax.random.normal(ks[0], (B, S, D), jnp.float32), 'Wq': w(ks[1], (D, D)), 'bq': jnp.zeros((D,), jnp.float32), 'Wk': w(ks[2], (D, HKV * HD)), 'bk': jnp.zeros((HKV * HD,), jnp.float32), 'Wv': w(ks[3], (D, HKV * HD)), 'bv': jnp.zeros((HKV * HD,), jnp.float32), 'Wc': w(ks[4], (HKV * HD, L)), 'We': w(ks[5], (L, HKV * HD)), 'Wo': w(ks[6], (D, D)), 'bo': jnp.zeros((D,), jnp.float32), 'gamma': jnp.ones((D,), jnp.float32), 'beta': jnp.zeros((D,), jnp.float32)}
    _L1_attn_all = _L1_attn_setup()
    _L1_attn_in = {k: v for k, v in _L1_attn_all.items() if k in ('Wq', 'bq', 'Wk', 'bk', 'Wv', 'bv', 'Wc', 'We', 'Wo', 'bo', 'gamma', 'beta')}
    del _L1_attn_all

    def _L1_xattn_setup():
        import jax, jax.numpy as jnp
        import numpy as np
        HEAD = 16
        MAX_ITER = 3
        EPS = 1e-05
        B, CTX, DIMS = (8, 256, 128)

        def _freqs_base(hd):
            mel_max = 2595.0 * np.log10(1.0 + 4000.0 / 200.0)
            lin = np.linspace(0.0, mel_max, hd // 2)
            return jnp.asarray(200.0 * (10.0 ** (lin / 2595.0) - 1.0) / 1000.0, dtype=jnp.float32)

        def _ln(x, g, b):
            m = jnp.mean(x, -1, keepdims=True)
            v = jnp.mean((x - m) ** 2, -1, keepdims=True)
            return (x - m) * jax.lax.rsqrt(v + EPS) * g + b

        def _rope(x, theta, fb):
            c = x.shape[-2]
            ang = jnp.arange(c, dtype=x.dtype)[:, None] * (theta / 220.0 * fb)
            cs, sn = (jnp.cos(ang), jnp.sin(ang))
            xr, xi = (x[..., 0::2], x[..., 1::2])
            return jnp.stack([xr * cs - xi * sn, xr * sn + xi * cs], -1).reshape(x.shape)

        def _sdpa(q, k, v, temp):
            s = jnp.where((temp != 1.0) & (temp > 0.0), (1.0 / temp) ** 0.5, 1.0)
            q = q * s
            d = q.shape[-1]
            logits = jnp.einsum('...qd,...kd->...qk', q, k) * d ** (-0.5)
            return jnp.einsum('...qk,...kd->...qd', jax.nn.softmax(logits, -1), v)

        def _focus(xq, xkv, p):
            b, cq, dims = xq.shape
            ckv = xkv.shape[1]
            hd = dims // HEAD
            fb = _freqs_base(hd)
            q = _ln(xq, p['lna_g'], p['lna_b']) @ p['Wq'].T
            kv = _ln(xkv, p['lna_g'], p['lna_b']) @ p['Wkv'].T
            k, v = jnp.split(kv, 2, axis=-1)
            sh = lambda t: t.reshape(b, -1, HEAD, hd).transpose(0, 2, 1, 3)
            q, k, v = (sh(q), sh(k), sh(v))
            q = _rope(q, p['theta'], fb)
            k = _rope(k, p['theta'], fb)
            es = min(HEAD, ckv)
            curq = q
            prev = jnp.zeros_like(q)
            attn_out = jnp.zeros_like(q)
            done = jnp.asarray(False)
            for it in range(MAX_ITER):
                qp = curq[:, :, :es] @ p['Wqh'].T + p['bqh']
                kp = k[:, :, :es] @ p['Wkh'].T + p['bkh']
                vp = v[:, :, :es] @ p['Wvh'].T + p['bvh']
                ai = _sdpa(_ln(qp, p['lnb_g'], p['lnb_b']), _ln(kp, p['lnb_g'], p['lnb_b']), vp, p['temp'])
                iter_out = jnp.zeros_like(curq).at[:, :, :es].set(ai)
                diff = jnp.mean(jnp.abs(iter_out - prev))
                if it == 0:
                    attn_out, prev, curq, k, v = (iter_out, iter_out, curq + iter_out, kp, vp)
                else:
                    stop = diff < p['threshold'] + p['factor'] * diff
                    attn_out = jnp.where(done, attn_out, iter_out)
                    new_done = done | stop
                    cont = ~new_done
                    prev = jnp.where(cont, iter_out, prev)
                    curq = jnp.where(cont, curq + iter_out, curq)
                    k = jnp.where(cont, kp, k)
                    v = jnp.where(cont, vp, v)
                    done = new_done
            return attn_out.transpose(0, 2, 1, 3).reshape(b, cq, dims)

        def _slide(x, p):
            b, ctx, dims = x.shape
            win = dims // HEAD
            span = win + win // HEAD
            nwin = ctx // win
            out0 = _focus(x[:, :win], x[:, :win], p)
            qw = x[:, win:].reshape(b, nwin - 1, win, dims)
            starts = (jnp.arange(1, nwin) + 1) * win - span
            idx = starts[:, None] + jnp.arange(span)[None, :]
            kw = x[:, idx]
            outs = jax.vmap(lambda a, c: _focus(a, c, p), in_axes=(1, 1), out_axes=1)(qw, kw)
            return jnp.concatenate([out0[:, None], outs], axis=1).reshape(b, ctx, dims)

        def _forward(x, xa, Wq, Wkv, Wout, lna_g, lna_b, lnb_g, lnb_b, Wqh, bqh, Wkh, bkh, Wvh, bvh, theta, threshold, factor, temp):
            p = dict(Wq=Wq, Wkv=Wkv, lna_g=lna_g, lna_b=lna_b, lnb_g=lnb_g, lnb_b=lnb_b, Wqh=Wqh, bqh=bqh, Wkh=Wkh, bkh=bkh, Wvh=Wvh, bvh=bvh, theta=theta, threshold=threshold, factor=factor, temp=temp)
            y = _slide(x, p)
            ya = _slide(xa, p)
            return _focus(y, ya, p) @ Wout.T
        key = jax.random.key(seed)
        ks = jax.random.split(key, 16)
        hd = DIMS // HEAD
        r = lambda k, shp, s: jax.random.normal(k, shp, jnp.float32) * s
        f = lambda v: jnp.asarray(v, jnp.float32)
        return {'x': jax.random.normal(ks[0], (B, CTX, DIMS), jnp.float32), 'xa': jax.random.normal(ks[1], (B, CTX, DIMS), jnp.float32), 'Wq': r(ks[2], (DIMS, DIMS), DIMS ** (-0.5)), 'Wkv': r(ks[3], (2 * DIMS, DIMS), DIMS ** (-0.5)), 'Wout': r(ks[4], (DIMS, DIMS), DIMS ** (-0.5)), 'lna_g': jnp.ones((DIMS,), jnp.float32), 'lna_b': jnp.zeros((DIMS,), jnp.float32), 'lnb_g': jnp.ones((hd,), jnp.float32), 'lnb_b': jnp.zeros((hd,), jnp.float32), 'Wqh': r(ks[5], (hd, hd), hd ** (-0.5)), 'bqh': r(ks[6], (hd,), 0.01), 'Wkh': r(ks[7], (hd, hd), hd ** (-0.5)), 'bkh': r(ks[8], (hd,), 0.01), 'Wvh': r(ks[9], (hd, hd), hd ** (-0.5)), 'bvh': r(ks[10], (hd,), 0.01), 'theta': f(10000.0), 'threshold': f(0.01), 'factor': f(0.1), 'temp': f(1.0)}
    _L1_xattn_all = _L1_xattn_setup()
    _L1_xattn_in = {k: v for k, v in _L1_xattn_all.items() if k in ('Wq', 'Wkv', 'Wout', 'lna_g', 'lna_b', 'lnb_g', 'lnb_b', 'Wqh', 'bqh', 'Wkh', 'bkh', 'Wvh', 'bvh', 'theta', 'threshold', 'factor', 'temp')}
    del _L1_xattn_all

    def _L1_ffn_setup():
        import jax, jax.numpy as jnp
        import numpy as np
        B, S, DIM = (4, 512, 128)
        BASE_COUPLING = 0.1
        NUM_CYCLES = 3

        def _gelu(x):
            return jax.nn.gelu(x, approximate=False)

        def _coupling_net(h, w1, b1, w2, b2, w3, b3, w4, b4):
            h = _gelu(h @ w1 + b1)
            h = _gelu(h @ w2 + b2)
            h = _gelu(h @ w3 + b3)
            return jax.nn.sigmoid(h @ w4 + b4)

        def _global_net(h, w1, b1, w2, b2, w3, b3):
            h = _gelu(h @ w1 + b1)
            h = _gelu(h @ w2 + b2)
            return jax.nn.sigmoid(h @ w3 + b3)

        def _twist(x):
            o_r, o_i, p_r, p_i = jnp.split(x, 4, axis=-1)
            return jnp.concatenate([p_r, -p_i, -o_r, o_i], axis=-1)
        key = jax.random.key(seed)
        ks = jax.random.split(key, 9)
        d = DIM

        def w(k, fan_in, fan_out):
            return jax.random.normal(k, (fan_in, fan_out), dtype=jnp.float32) / np.sqrt(fan_in).astype(np.float32)
        inp = {'x': jax.random.normal(ks[0], (B, S, d), dtype=jnp.float32)}
        cn_dims = [(d, d), (d, d // 2), (d // 2, d // 4), (d // 4, 1)]
        for i, (a, b) in enumerate(cn_dims):
            inp[f'cn_w{i + 1}'] = w(ks[1 + i], a, b)
            inp[f'cn_b{i + 1}'] = jnp.zeros((b,), dtype=jnp.float32)
        gc_dims = [(d, d // 2), (d // 2, d // 4), (d // 4, 1)]
        for i, (a, b) in enumerate(gc_dims):
            inp[f'gc_w{i + 1}'] = w(ks[5 + i], a, b)
            inp[f'gc_b{i + 1}'] = jnp.zeros((b,), dtype=jnp.float32)
        inp['adaptive_range'] = jnp.full((1,), 0.2, dtype=jnp.float32)
        return inp
    _L1_ffn_all = _L1_ffn_setup()
    _L1_ffn_in = {k: v for k, v in _L1_ffn_all.items() if k in ('cn_w1', 'cn_b1', 'cn_w2', 'cn_b2', 'cn_w3', 'cn_b3', 'cn_w4', 'cn_b4', 'gc_w1', 'gc_b1', 'gc_w2', 'gc_b2', 'gc_w3', 'gc_b3', 'adaptive_range')}
    del _L1_ffn_all

    def _L2_attn_setup():
        import jax, jax.numpy as jnp
        import numpy as np
        D_STATE = 16
        D_CONV = 4

        def layer_norm(x, g, b, eps=1e-05):
            mu = jnp.mean(x, axis=-1, keepdims=True)
            var = jnp.mean(jnp.square(x - mu), axis=-1, keepdims=True)
            return (x - mu) * jax.lax.rsqrt(var + eps) * g + b

        def silu(x):
            return x * jax.nn.sigmoid(x)

        def mamba(x, in_w, conv_w, conv_b, xproj_w, dt_w, dt_b, Alog, Dp, out_w):
            Bsz, L, _ = x.shape
            di = Dp.shape[0]
            xz = jnp.einsum('bld,ed->ble', x, in_w)
            xs, z = jnp.split(xz, 2, axis=-1)
            xt = xs.transpose(0, 2, 1)
            xt = jax.lax.conv_general_dilated(xt, conv_w[:, None, :], (1,), [(D_CONV - 1, 0)], feature_group_count=di, dimension_numbers=('NCH', 'OIH', 'NCH'))
            xs = silu((xt + conv_b[None, :, None]).transpose(0, 2, 1))
            dbl = jnp.einsum('bld,ed->ble', xs, xproj_w)
            dt_rank = dt_w.shape[1]
            dt, Bc, Cc = jnp.split(dbl, [dt_rank, dt_rank + D_STATE], axis=-1)
            dt = jax.nn.softplus(jnp.einsum('blr,dr->bld', dt, dt_w) + dt_b)
            A = -jnp.exp(Alog)
            dA = jnp.exp(dt[..., None] * A)
            dBx = dt[..., None] * Bc[:, :, None, :] * xs[..., None]

            def step(h, inp):
                dA_t, dBx_t, C_t = inp
                h = dA_t * h + dBx_t
                y = jnp.einsum('bds,bs->bd', h, C_t)
                return (h, y)
            h0 = jnp.zeros((Bsz, di, D_STATE), x.dtype)
            _, ys = jax.lax.scan(step, h0, (dA.transpose(1, 0, 2, 3), dBx.transpose(1, 0, 2, 3), Cc.transpose(1, 0, 2)))
            y = ys.transpose(1, 0, 2) + Dp * xs
            y = y * silu(z)
            return jnp.einsum('bld,od->blo', y, out_w)

        def _make_mamba_params(key, d_model, scale=0.02):
            di = 2 * d_model
            dt_rank = (d_model + 15) // 16
            ks = jax.random.split(key, 7)
            in_w = jax.random.normal(ks[0], (2 * di, d_model), jnp.float32) * scale
            conv_w = jax.random.normal(ks[1], (di, D_CONV), jnp.float32) * scale
            conv_b = jnp.zeros((di,), jnp.float32)
            xproj_w = jax.random.normal(ks[2], (dt_rank + 2 * D_STATE, di), jnp.float32) * scale
            dt_w = jax.random.normal(ks[3], (di, dt_rank), jnp.float32) * scale
            dt_b = jax.random.uniform(ks[4], (di,), jnp.float32, -5.0, -2.0)
            Alog = jnp.log(jnp.tile(jnp.arange(1, D_STATE + 1, dtype=jnp.float32), (di, 1)))
            Dp = jnp.ones((di,), jnp.float32)
            out_w = jax.random.normal(ks[5], (d_model, di), jnp.float32) * scale
            return (in_w, conv_w, conv_b, xproj_w, dt_w, dt_b, Alog, Dp, out_w)
        key = jax.random.key(seed)
        B, L, D = (4, 256, 128)
        DFF = 4 * D
        ks = jax.random.split(key, 8)
        x = jax.random.normal(ks[0], (B, L, D), jnp.float32)
        m1 = _make_mamba_params(ks[1], D)
        m2 = _make_mamba_params(ks[2], D)
        names1 = ['m1_in_w', 'm1_conv_w', 'm1_conv_b', 'm1_xproj_w', 'm1_dt_w', 'm1_dt_b', 'm1_Alog', 'm1_D', 'm1_out_w']
        names2 = ['m2_in_w', 'm2_conv_w', 'm2_conv_b', 'm2_xproj_w', 'm2_dt_w', 'm2_dt_b', 'm2_Alog', 'm2_D', 'm2_out_w']
        inp = {'x': x}
        inp.update(dict(zip(names1, m1)))
        inp.update(dict(zip(names2, m2)))
        inp['norm_g'] = jnp.ones((D,), jnp.float32)
        inp['norm_b'] = jnp.zeros((D,), jnp.float32)
        inp['ffn_g'] = jnp.ones((D,), jnp.float32)
        inp['ffn_b'] = jnp.zeros((D,), jnp.float32)
        inp['ff1_w'] = jax.random.normal(ks[3], (DFF, D), jnp.float32) * 0.02
        inp['ff1_b'] = jnp.zeros((DFF,), jnp.float32)
        inp['ff2_w'] = jax.random.normal(ks[4], (D, DFF), jnp.float32) * 0.02
        inp['ff2_b'] = jnp.zeros((D,), jnp.float32)
        return inp
    _L2_attn_all = _L2_attn_setup()
    _L2_attn_in = {k: v for k, v in _L2_attn_all.items() if k in ('m1_in_w', 'm1_conv_w', 'm1_conv_b', 'm1_xproj_w', 'm1_dt_w', 'm1_dt_b', 'm1_Alog', 'm1_D', 'm1_out_w', 'm2_in_w', 'm2_conv_w', 'm2_conv_b', 'm2_xproj_w', 'm2_dt_w', 'm2_dt_b', 'm2_Alog', 'm2_D', 'm2_out_w', 'norm_g', 'norm_b', 'ffn_g', 'ffn_b', 'ff1_w', 'ff1_b', 'ff2_w', 'ff2_b')}
    del _L2_attn_all

    def _L2_xattn_setup():
        import jax, jax.numpy as jnp
        import numpy as np
        DIM = 128
        NUM_HEADS = 8
        HEAD_DIM = 64
        INNER = NUM_HEADS * HEAD_DIM
        key = jax.random.key(seed)
        ks = jax.random.split(key, 7)
        B, N, M = (8, 64, 512)
        x = jax.random.normal(ks[0], (B, N, DIM), dtype=jnp.float32)
        context = jax.random.normal(ks[1], (B, M, DIM), dtype=jnp.float32)
        s_in = 1.0 / np.sqrt(DIM)
        s_inner = 1.0 / np.sqrt(INNER)
        Wq = jax.random.normal(ks[2], (DIM, INNER), dtype=jnp.float32) * s_in
        Wk = jax.random.normal(ks[3], (DIM, INNER), dtype=jnp.float32) * s_in
        Wv = jax.random.normal(ks[4], (DIM, INNER), dtype=jnp.float32) * s_in
        Wo = jax.random.normal(ks[5], (INNER, DIM), dtype=jnp.float32) * s_inner
        bo = jax.random.normal(ks[6], (DIM,), dtype=jnp.float32) * 0.01
        return {'x': x, 'context': context, 'Wq': Wq, 'Wk': Wk, 'Wv': Wv, 'Wo': Wo, 'bo': bo}
    _L2_xattn_all = _L2_xattn_setup()
    _L2_xattn_in = {k: v for k, v in _L2_xattn_all.items() if k in ('Wq', 'Wk', 'Wv', 'Wo', 'bo')}
    del _L2_xattn_all

    def _L2_ffn_setup():
        import math
        import jax, jax.numpy as jnp
        import numpy as np
        B, T, D = (4, 512, 128)
        H = 16
        HD = D // H
        CAP = int(512 * 0.125)
        DFF = int(D * 4 * 2 / 3)
        EPS = 1e-06

        def rmsnorm(x, g):
            return x * jax.lax.rsqrt(jnp.mean(x * x, axis=-1, keepdims=True) + EPS) * g
        key = jax.random.key(seed)
        ks = jax.random.split(key, 9)
        s = lambda k, shape: jax.random.normal(k, shape, jnp.float32) * 0.02
        return {'x': jax.random.normal(ks[0], (B, T, D), jnp.float32), 'w_router': s(ks[1], (D,)), 'W_qkv': s(ks[2], (3 * D, D)), 'W_out': s(ks[3], (D, D)), 'g1': jnp.ones((D,), jnp.float32), 'g2': jnp.ones((D,), jnp.float32), 'W1': s(ks[4], (DFF, D)), 'W2': s(ks[5], (DFF, D)), 'W3': s(ks[6], (D, DFF))}
    _L2_ffn_all = _L2_ffn_setup()
    _L2_ffn_in = {k: v for k, v in _L2_ffn_all.items() if k in ('w_router', 'W_qkv', 'W_out', 'g1', 'g2', 'W1', 'W2', 'W3')}
    del _L2_ffn_all

    def _L3_attn_setup():
        import math
        import jax, jax.numpy as jnp
        import numpy as np
        HIDDEN = 128
        NUM_HEADS = 16
        NUM_QUERIES = 2
        NUM_Q_HEADS = NUM_HEADS * NUM_QUERIES
        HEAD_DIM = 64
        Q_DIM = NUM_Q_HEADS * HEAD_DIM
        KV_DIM = NUM_HEADS * HEAD_DIM
        BATCH, SEQ = (4, 128)

        def _alibi_slopes(num_heads: int) -> np.ndarray:
            closest_pow2 = 2 ** int(math.floor(math.log2(num_heads)))
            base = 2.0 ** (-2.0 ** (-(math.log2(closest_pow2) - 3)))
            powers = np.arange(1, closest_pow2 + 1, dtype=np.float32)
            slopes = base ** powers
            if closest_pow2 != num_heads:
                extra_base = 2.0 ** (-2.0 ** (-(math.log2(2 * closest_pow2) - 3)))
                extra_powers = np.arange(1, 2 * (num_heads - closest_pow2) + 1, 2, dtype=np.float32)
                slopes = np.concatenate([slopes, extra_base ** extra_powers])
            return slopes[:num_heads].astype(np.float32)
        ALIBI_SLOPES = jnp.asarray(_alibi_slopes(NUM_Q_HEADS))
        key = jax.random.key(seed)
        k1, k2, k3 = jax.random.split(key, 3)
        inputs = jax.random.normal(k1, (BATCH, SEQ, HIDDEN), dtype=jnp.float32)
        W_qkv = jax.random.normal(k2, (HIDDEN, Q_DIM + 2 * KV_DIM), dtype=jnp.float32) * (1.0 / math.sqrt(HIDDEN))
        W_out = jax.random.normal(k3, (Q_DIM, HIDDEN), dtype=jnp.float32) * (1.0 / math.sqrt(Q_DIM))
        return {'inputs': inputs, 'W_qkv': W_qkv, 'W_out': W_out}
    _L3_attn_all = _L3_attn_setup()
    _L3_attn_in = {k: v for k, v in _L3_attn_all.items() if k in ('W_qkv', 'W_out')}
    del _L3_attn_all

    def _L3_xattn_setup():
        import math
        import jax, jax.numpy as jnp
        import numpy as np
        N_HEAD = 16

        def _slopes(n_head):
            cp2 = 2 ** int(math.floor(math.log2(n_head)))
            slopes = 0.5 ** np.arange(1, cp2 + 1)
            if cp2 < n_head:
                intra = 1.0 / math.sqrt(2.0)
                pair = intra ** np.arange(1, 1 + 2 * (n_head - cp2), 2)
                slopes = np.sort(np.concatenate([slopes, pair]))[::-1]
            return jnp.asarray(slopes, dtype=jnp.float32)

        def _alibi_bias(S):
            d = jnp.arange(S)[:, None] - jnp.arange(S)[None, :]
            return -jnp.maximum(d, 0).astype(jnp.float32)
        key = jax.random.key(seed)
        B, S, D = (2, 256, 128)
        ks = jax.random.split(key, 12)
        f = lambda k, sh: jax.random.normal(k, sh, dtype=jnp.float32)
        inp = {'q': f(ks[0], (B, S, D)), 'k': f(ks[1], (B, S, D)), 'v': f(ks[2], (B, S, D)), 'mask': jnp.tril(jnp.ones((S, S), dtype=jnp.int32))[None, None], 'wq_w': f(ks[3], (D, D)) * 0.02, 'wq_b': f(ks[4], (D,)) * 0.02, 'wk_w': f(ks[5], (D, D)) * 0.02, 'wk_b': f(ks[6], (D,)) * 0.02, 'wv_w': f(ks[7], (D, D)) * 0.02, 'wv_b': f(ks[8], (D,)) * 0.02, 'out_w': f(ks[9], (D, D)) * 0.02, 'out_b': f(ks[10], (D,)) * 0.02}
        return inp
    _L3_xattn_all = _L3_xattn_setup()
    _L3_xattn_in = {k: v for k, v in _L3_xattn_all.items() if k in ('wq_w', 'wq_b', 'wk_w', 'wk_b', 'wv_w', 'wv_b', 'out_w', 'out_b')}
    del _L3_xattn_all

    def _L3_ffn_setup():
        import jax, jax.numpy as jnp
        import numpy as np
        EPS = 1e-09
        key = jax.random.key(seed)
        k0, k1, k2, k3 = jax.random.split(key, 4)
        B, S, H, F, E = (4, 256, 128, 256, 8)
        return {'hidden_states': jax.random.normal(k0, (B, S, H), dtype=jnp.float32), 'router_w': jax.random.normal(k1, (H, E), dtype=jnp.float32) * 0.02, 'w1': jax.random.normal(k2, (E, H, F), dtype=jnp.float32) * 0.02, 'w2': jax.random.normal(k3, (E, F, H), dtype=jnp.float32) * 0.02}
    _L3_ffn_all = _L3_ffn_setup()
    _L3_ffn_in = {k: v for k, v in _L3_ffn_all.items() if k in ('router_w', 'w1', 'w2')}
    del _L3_ffn_all
    return {'x': x, 'ctx_1024': ctx_1024, 'mask_1x1xSxS2_ik0': mask_1x1xSxS2_ik0, 'L0_attn_Wq': _L0_attn_in['Wq'], 'L0_attn_Wk': _L0_attn_in['Wk'], 'L0_attn_Wv': _L0_attn_in['Wv'], 'L0_attn_Wo': _L0_attn_in['Wo'], 'L0_xattn_Wq': _L0_xattn_in['Wq'], 'L0_xattn_bq': _L0_xattn_in['bq'], 'L0_xattn_Wk': _L0_xattn_in['Wk'], 'L0_xattn_bk': _L0_xattn_in['bk'], 'L0_xattn_Wv': _L0_xattn_in['Wv'], 'L0_xattn_bv': _L0_xattn_in['bv'], 'L0_xattn_Wo': _L0_xattn_in['Wo'], 'L0_xattn_bo': _L0_xattn_in['bo'], 'L0_ffn_gate_W': _L0_ffn_in['gate_W'], 'L0_ffn_gate_b': _L0_ffn_in['gate_b'], 'L0_ffn_wi_W': _L0_ffn_in['wi_W'], 'L0_ffn_wi_b': _L0_ffn_in['wi_b'], 'L0_ffn_wo_W': _L0_ffn_in['wo_W'], 'L0_ffn_wo_b': _L0_ffn_in['wo_b'], 'L0_ffn_lora_A': _L0_ffn_in['lora_A'], 'L0_ffn_lora_B': _L0_ffn_in['lora_B'], 'L1_attn_Wq': _L1_attn_in['Wq'], 'L1_attn_bq': _L1_attn_in['bq'], 'L1_attn_Wk': _L1_attn_in['Wk'], 'L1_attn_bk': _L1_attn_in['bk'], 'L1_attn_Wv': _L1_attn_in['Wv'], 'L1_attn_bv': _L1_attn_in['bv'], 'L1_attn_Wc': _L1_attn_in['Wc'], 'L1_attn_We': _L1_attn_in['We'], 'L1_attn_Wo': _L1_attn_in['Wo'], 'L1_attn_bo': _L1_attn_in['bo'], 'L1_attn_gamma': _L1_attn_in['gamma'], 'L1_attn_beta': _L1_attn_in['beta'], 'L1_xattn_Wq': _L1_xattn_in['Wq'], 'L1_xattn_Wkv': _L1_xattn_in['Wkv'], 'L1_xattn_Wout': _L1_xattn_in['Wout'], 'L1_xattn_lna_g': _L1_xattn_in['lna_g'], 'L1_xattn_lna_b': _L1_xattn_in['lna_b'], 'L1_xattn_lnb_g': _L1_xattn_in['lnb_g'], 'L1_xattn_lnb_b': _L1_xattn_in['lnb_b'], 'L1_xattn_Wqh': _L1_xattn_in['Wqh'], 'L1_xattn_bqh': _L1_xattn_in['bqh'], 'L1_xattn_Wkh': _L1_xattn_in['Wkh'], 'L1_xattn_bkh': _L1_xattn_in['bkh'], 'L1_xattn_Wvh': _L1_xattn_in['Wvh'], 'L1_xattn_bvh': _L1_xattn_in['bvh'], 'L1_xattn_theta': _L1_xattn_in['theta'], 'L1_xattn_threshold': _L1_xattn_in['threshold'], 'L1_xattn_factor': _L1_xattn_in['factor'], 'L1_xattn_temp': _L1_xattn_in['temp'], 'L1_ffn_cn_w1': _L1_ffn_in['cn_w1'], 'L1_ffn_cn_b1': _L1_ffn_in['cn_b1'], 'L1_ffn_cn_w2': _L1_ffn_in['cn_w2'], 'L1_ffn_cn_b2': _L1_ffn_in['cn_b2'], 'L1_ffn_cn_w3': _L1_ffn_in['cn_w3'], 'L1_ffn_cn_b3': _L1_ffn_in['cn_b3'], 'L1_ffn_cn_w4': _L1_ffn_in['cn_w4'], 'L1_ffn_cn_b4': _L1_ffn_in['cn_b4'], 'L1_ffn_gc_w1': _L1_ffn_in['gc_w1'], 'L1_ffn_gc_b1': _L1_ffn_in['gc_b1'], 'L1_ffn_gc_w2': _L1_ffn_in['gc_w2'], 'L1_ffn_gc_b2': _L1_ffn_in['gc_b2'], 'L1_ffn_gc_w3': _L1_ffn_in['gc_w3'], 'L1_ffn_gc_b3': _L1_ffn_in['gc_b3'], 'L1_ffn_adaptive_range': _L1_ffn_in['adaptive_range'], 'L2_attn_m1_in_w': _L2_attn_in['m1_in_w'], 'L2_attn_m1_conv_w': _L2_attn_in['m1_conv_w'], 'L2_attn_m1_conv_b': _L2_attn_in['m1_conv_b'], 'L2_attn_m1_xproj_w': _L2_attn_in['m1_xproj_w'], 'L2_attn_m1_dt_w': _L2_attn_in['m1_dt_w'], 'L2_attn_m1_dt_b': _L2_attn_in['m1_dt_b'], 'L2_attn_m1_Alog': _L2_attn_in['m1_Alog'], 'L2_attn_m1_D': _L2_attn_in['m1_D'], 'L2_attn_m1_out_w': _L2_attn_in['m1_out_w'], 'L2_attn_m2_in_w': _L2_attn_in['m2_in_w'], 'L2_attn_m2_conv_w': _L2_attn_in['m2_conv_w'], 'L2_attn_m2_conv_b': _L2_attn_in['m2_conv_b'], 'L2_attn_m2_xproj_w': _L2_attn_in['m2_xproj_w'], 'L2_attn_m2_dt_w': _L2_attn_in['m2_dt_w'], 'L2_attn_m2_dt_b': _L2_attn_in['m2_dt_b'], 'L2_attn_m2_Alog': _L2_attn_in['m2_Alog'], 'L2_attn_m2_D': _L2_attn_in['m2_D'], 'L2_attn_m2_out_w': _L2_attn_in['m2_out_w'], 'L2_attn_norm_g': _L2_attn_in['norm_g'], 'L2_attn_norm_b': _L2_attn_in['norm_b'], 'L2_attn_ffn_g': _L2_attn_in['ffn_g'], 'L2_attn_ffn_b': _L2_attn_in['ffn_b'], 'L2_attn_ff1_w': _L2_attn_in['ff1_w'], 'L2_attn_ff1_b': _L2_attn_in['ff1_b'], 'L2_attn_ff2_w': _L2_attn_in['ff2_w'], 'L2_attn_ff2_b': _L2_attn_in['ff2_b'], 'L2_xattn_Wq': _L2_xattn_in['Wq'], 'L2_xattn_Wk': _L2_xattn_in['Wk'], 'L2_xattn_Wv': _L2_xattn_in['Wv'], 'L2_xattn_Wo': _L2_xattn_in['Wo'], 'L2_xattn_bo': _L2_xattn_in['bo'], 'L2_ffn_w_router': _L2_ffn_in['w_router'], 'L2_ffn_W_qkv': _L2_ffn_in['W_qkv'], 'L2_ffn_W_out': _L2_ffn_in['W_out'], 'L2_ffn_g1': _L2_ffn_in['g1'], 'L2_ffn_g2': _L2_ffn_in['g2'], 'L2_ffn_W1': _L2_ffn_in['W1'], 'L2_ffn_W2': _L2_ffn_in['W2'], 'L2_ffn_W3': _L2_ffn_in['W3'], 'L3_attn_W_qkv': _L3_attn_in['W_qkv'], 'L3_attn_W_out': _L3_attn_in['W_out'], 'L3_xattn_wq_w': _L3_xattn_in['wq_w'], 'L3_xattn_wq_b': _L3_xattn_in['wq_b'], 'L3_xattn_wk_w': _L3_xattn_in['wk_w'], 'L3_xattn_wk_b': _L3_xattn_in['wk_b'], 'L3_xattn_wv_w': _L3_xattn_in['wv_w'], 'L3_xattn_wv_b': _L3_xattn_in['wv_b'], 'L3_xattn_out_w': _L3_xattn_in['out_w'], 'L3_xattn_out_b': _L3_xattn_in['out_b'], 'L3_ffn_router_w': _L3_ffn_in['router_w'], 'L3_ffn_w1': _L3_ffn_in['w1'], 'L3_ffn_w2': _L3_ffn_in['w2']}

def reference(x, ctx_1024, mask_1x1xSxS2_ik0, L0_attn_Wq, L0_attn_Wk, L0_attn_Wv, L0_attn_Wo, L0_xattn_Wq, L0_xattn_bq, L0_xattn_Wk, L0_xattn_bk, L0_xattn_Wv, L0_xattn_bv, L0_xattn_Wo, L0_xattn_bo, L0_ffn_gate_W, L0_ffn_gate_b, L0_ffn_wi_W, L0_ffn_wi_b, L0_ffn_wo_W, L0_ffn_wo_b, L0_ffn_lora_A, L0_ffn_lora_B, L1_attn_Wq, L1_attn_bq, L1_attn_Wk, L1_attn_bk, L1_attn_Wv, L1_attn_bv, L1_attn_Wc, L1_attn_We, L1_attn_Wo, L1_attn_bo, L1_attn_gamma, L1_attn_beta, L1_xattn_Wq, L1_xattn_Wkv, L1_xattn_Wout, L1_xattn_lna_g, L1_xattn_lna_b, L1_xattn_lnb_g, L1_xattn_lnb_b, L1_xattn_Wqh, L1_xattn_bqh, L1_xattn_Wkh, L1_xattn_bkh, L1_xattn_Wvh, L1_xattn_bvh, L1_xattn_theta, L1_xattn_threshold, L1_xattn_factor, L1_xattn_temp, L1_ffn_cn_w1, L1_ffn_cn_b1, L1_ffn_cn_w2, L1_ffn_cn_b2, L1_ffn_cn_w3, L1_ffn_cn_b3, L1_ffn_cn_w4, L1_ffn_cn_b4, L1_ffn_gc_w1, L1_ffn_gc_b1, L1_ffn_gc_w2, L1_ffn_gc_b2, L1_ffn_gc_w3, L1_ffn_gc_b3, L1_ffn_adaptive_range, L2_attn_m1_in_w, L2_attn_m1_conv_w, L2_attn_m1_conv_b, L2_attn_m1_xproj_w, L2_attn_m1_dt_w, L2_attn_m1_dt_b, L2_attn_m1_Alog, L2_attn_m1_D, L2_attn_m1_out_w, L2_attn_m2_in_w, L2_attn_m2_conv_w, L2_attn_m2_conv_b, L2_attn_m2_xproj_w, L2_attn_m2_dt_w, L2_attn_m2_dt_b, L2_attn_m2_Alog, L2_attn_m2_D, L2_attn_m2_out_w, L2_attn_norm_g, L2_attn_norm_b, L2_attn_ffn_g, L2_attn_ffn_b, L2_attn_ff1_w, L2_attn_ff1_b, L2_attn_ff2_w, L2_attn_ff2_b, L2_xattn_Wq, L2_xattn_Wk, L2_xattn_Wv, L2_xattn_Wo, L2_xattn_bo, L2_ffn_w_router, L2_ffn_W_qkv, L2_ffn_W_out, L2_ffn_g1, L2_ffn_g2, L2_ffn_W1, L2_ffn_W2, L2_ffn_W3, L3_attn_W_qkv, L3_attn_W_out, L3_xattn_wq_w, L3_xattn_wq_b, L3_xattn_wk_w, L3_xattn_wk_b, L3_xattn_wv_w, L3_xattn_wv_b, L3_xattn_out_w, L3_xattn_out_b, L3_ffn_router_w, L3_ffn_w1, L3_ffn_w2):
    import jax
    import jax.numpy as jnp

    def _L0_attn_ref(x, Wq, Wk, Wv, Wo):
        import jax, jax.numpy as jnp
        import numpy as np
        N_HEADS = 16

        def _rope(t, sin, cos):
            t_rot = jnp.stack([-t[..., 1::2], t[..., ::2]], axis=-1).reshape(t.shape)
            return t * cos + t_rot * sin
        B, S, D = x.shape
        H = N_HEADS
        dk = D // H
        q = (x @ Wq.T).reshape(B, S, H, dk).transpose(0, 2, 1, 3)
        k = (x @ Wk.T).reshape(B, S, H, dk).transpose(0, 2, 1, 3)
        v = (x @ Wv.T).reshape(B, S, H, dk).transpose(0, 2, 1, 3)
        inv_freq = 1.0 / 10000.0 ** (jnp.arange(0, dk, 2, dtype=jnp.float32) / dk)
        pos = jnp.arange(S, dtype=jnp.float32)
        freqs = pos[:, None] * inv_freq[None, :]
        sin = jnp.repeat(jnp.sin(freqs), 2, axis=-1)
        cos = jnp.repeat(jnp.cos(freqs), 2, axis=-1)
        q = _rope(q, sin, cos)
        k = _rope(k, sin, cos)
        scores = jnp.einsum('bhqd,bhkd->bhqk', q, k) / jnp.sqrt(jnp.float32(dk))
        slopes = 2.0 ** (-8.0 * jnp.arange(H, dtype=jnp.float32) / H)
        rel = -jnp.abs(pos[:, None] - pos[None, :])
        scores = scores + slopes[None, :, None, None] * rel[None, None]
        attn = jax.nn.softmax(scores, axis=-1)
        out = jnp.einsum('bhqk,bhkd->bhqd', attn, v)
        out = out.transpose(0, 2, 1, 3).reshape(B, S, D)
        return out @ Wo.T

    def _L0_xattn_ref(q, k, v, Wq, bq, Wk, bk, Wv, bv, Wo, bo):
        import jax, jax.numpy as jnp
        import numpy as np
        import math
        H = 16
        D = 128
        DH = D // H
        A = 1000.0

        def _alibi_bias(L, dtype):
            hh = jnp.arange(1, H + 1, dtype=jnp.float32)
            m = jnp.exp(-jnp.power(5000.0, (hh - 1.0) / (H - 1.0) * 0.8))
            seq = jnp.arange(L, dtype=jnp.float32)
            dist = jnp.abs(seq[:, None] - seq[None, :])
            bias = m[:, None, None] * jax.nn.softplus(A + dist)
            return bias.astype(dtype)
        B, L, _ = q.shape

        def proj(x, W, b):
            return (x @ W.T + b).reshape(B, L, H, DH).transpose(0, 2, 1, 3)
        Q = proj(q, Wq, bq)
        K = proj(k, Wk, bk)
        V = proj(v, Wv, bv)
        scores = jnp.einsum('bhid,bhjd->bhij', Q, K) / math.sqrt(DH)
        scores = scores + _alibi_bias(L, scores.dtype)[None]
        attn = jax.nn.softmax(scores, axis=-1)
        x = jnp.einsum('bhij,bhjd->bhid', attn, V)
        x = x.transpose(0, 2, 1, 3).reshape(B, L, D)
        return x @ Wo.T + bo

    def _L0_ffn_ref(hidden_states, gate_W, gate_b, wi_W, wi_b, wo_W, wo_b, lora_A, lora_B):
        import jax, jax.numpy as jnp
        import numpy as np
        B, S, D, F, E, R = (4, 256, 128, 512, 8, 4)
        x = hidden_states
        logits = jnp.einsum('bsd,ed->bse', x, gate_W) + gate_b
        top1 = jnp.argmax(jax.nn.softmax(logits, axis=-1), axis=-1)
        base = jnp.einsum('bsd,fd->bsf', x, wi_W) + wi_b
        out = jnp.zeros_like(x)
        for i in range(lora_A.shape[0]):
            lora = jnp.einsum('bsr,fr->bsf', jnp.einsum('bsd,rd->bsr', x, lora_A[i]), lora_B[i])
            inter = jax.nn.relu(base + lora)
            expert_out = jnp.einsum('bsf,df->bsd', inter, wo_W) + wo_b
            mask = (top1 == i).astype(x.dtype)[..., None]
            out = out + mask * expert_out
        return out

    def _L1_attn_ref(x, Wq, bq, Wk, bk, Wv, bv, Wc, We, Wo, bo, gamma, beta):
        import jax, jax.numpy as jnp
        import numpy as np
        D = 128
        H = 16
        HKV = 4
        HD = D // H
        L = 64
        EPS = 1e-06
        LN_EPS = 1e-05
        B, S = (2, 128)

        def _feat(x):
            return jax.nn.elu(x) + 1.0
        b, s, _ = x.shape
        residual = x
        q = x @ Wq + bq
        k = x @ Wk + bk
        v = x @ Wv + bv
        k = k @ Wc @ We
        v = v @ Wc @ We
        q = q.reshape(b, s, H, HD).transpose(0, 2, 1, 3)
        k = k.reshape(b, s, HKV, HD).transpose(0, 2, 1, 3)
        v = v.reshape(b, s, HKV, HD).transpose(0, 2, 1, 3)
        rep = H // HKV
        k = jnp.repeat(k, rep, axis=1)
        v = jnp.repeat(v, rep, axis=1)
        qf = _feat(q)
        kf = _feat(k)
        kv = jnp.einsum('bhsf,bhsd->bhsfd', kf, v)
        kv_cum = jnp.cumsum(kv, axis=2)
        num = jnp.einsum('bhsf,bhsfd->bhsd', qf, kv_cum)
        den = jnp.einsum('bhsf,bhsf->bhs', qf, jnp.cumsum(kf, axis=2))[..., None] + EPS
        o = num / den
        o = o.transpose(0, 2, 1, 3).reshape(b, s, D)
        o = o @ Wo + bo
        y = residual + o
        mu = jnp.mean(y, axis=-1, keepdims=True)
        var = jnp.var(y, axis=-1, keepdims=True)
        return (y - mu) / jnp.sqrt(var + LN_EPS) * gamma + beta

    def _L1_xattn_ref(x, xa, Wq, Wkv, Wout, lna_g, lna_b, lnb_g, lnb_b, Wqh, bqh, Wkh, bkh, Wvh, bvh, theta, threshold, factor, temp):
        import jax, jax.numpy as jnp
        import numpy as np
        HEAD = 16
        MAX_ITER = 3
        EPS = 1e-05
        B, CTX, DIMS = (8, 256, 128)

        def _freqs_base(hd):
            mel_max = 2595.0 * np.log10(1.0 + 4000.0 / 200.0)
            lin = np.linspace(0.0, mel_max, hd // 2)
            return jnp.asarray(200.0 * (10.0 ** (lin / 2595.0) - 1.0) / 1000.0, dtype=jnp.float32)

        def _ln(x, g, b):
            m = jnp.mean(x, -1, keepdims=True)
            v = jnp.mean((x - m) ** 2, -1, keepdims=True)
            return (x - m) * jax.lax.rsqrt(v + EPS) * g + b

        def _rope(x, theta, fb):
            c = x.shape[-2]
            ang = jnp.arange(c, dtype=x.dtype)[:, None] * (theta / 220.0 * fb)
            cs, sn = (jnp.cos(ang), jnp.sin(ang))
            xr, xi = (x[..., 0::2], x[..., 1::2])
            return jnp.stack([xr * cs - xi * sn, xr * sn + xi * cs], -1).reshape(x.shape)

        def _sdpa(q, k, v, temp):
            s = jnp.where((temp != 1.0) & (temp > 0.0), (1.0 / temp) ** 0.5, 1.0)
            q = q * s
            d = q.shape[-1]
            logits = jnp.einsum('...qd,...kd->...qk', q, k) * d ** (-0.5)
            return jnp.einsum('...qk,...kd->...qd', jax.nn.softmax(logits, -1), v)

        def _focus(xq, xkv, p):
            b, cq, dims = xq.shape
            ckv = xkv.shape[1]
            hd = dims // HEAD
            fb = _freqs_base(hd)
            q = _ln(xq, p['lna_g'], p['lna_b']) @ p['Wq'].T
            kv = _ln(xkv, p['lna_g'], p['lna_b']) @ p['Wkv'].T
            k, v = jnp.split(kv, 2, axis=-1)
            sh = lambda t: t.reshape(b, -1, HEAD, hd).transpose(0, 2, 1, 3)
            q, k, v = (sh(q), sh(k), sh(v))
            q = _rope(q, p['theta'], fb)
            k = _rope(k, p['theta'], fb)
            es = min(HEAD, ckv)
            curq = q
            prev = jnp.zeros_like(q)
            attn_out = jnp.zeros_like(q)
            done = jnp.asarray(False)
            for it in range(MAX_ITER):
                qp = curq[:, :, :es] @ p['Wqh'].T + p['bqh']
                kp = k[:, :, :es] @ p['Wkh'].T + p['bkh']
                vp = v[:, :, :es] @ p['Wvh'].T + p['bvh']
                ai = _sdpa(_ln(qp, p['lnb_g'], p['lnb_b']), _ln(kp, p['lnb_g'], p['lnb_b']), vp, p['temp'])
                iter_out = jnp.zeros_like(curq).at[:, :, :es].set(ai)
                diff = jnp.mean(jnp.abs(iter_out - prev))
                if it == 0:
                    attn_out, prev, curq, k, v = (iter_out, iter_out, curq + iter_out, kp, vp)
                else:
                    stop = diff < p['threshold'] + p['factor'] * diff
                    attn_out = jnp.where(done, attn_out, iter_out)
                    new_done = done | stop
                    cont = ~new_done
                    prev = jnp.where(cont, iter_out, prev)
                    curq = jnp.where(cont, curq + iter_out, curq)
                    k = jnp.where(cont, kp, k)
                    v = jnp.where(cont, vp, v)
                    done = new_done
            return attn_out.transpose(0, 2, 1, 3).reshape(b, cq, dims)

        def _slide(x, p):
            b, ctx, dims = x.shape
            win = dims // HEAD
            span = win + win // HEAD
            nwin = ctx // win
            out0 = _focus(x[:, :win], x[:, :win], p)
            qw = x[:, win:].reshape(b, nwin - 1, win, dims)
            starts = (jnp.arange(1, nwin) + 1) * win - span
            idx = starts[:, None] + jnp.arange(span)[None, :]
            kw = x[:, idx]
            outs = jax.vmap(lambda a, c: _focus(a, c, p), in_axes=(1, 1), out_axes=1)(qw, kw)
            return jnp.concatenate([out0[:, None], outs], axis=1).reshape(b, ctx, dims)

        def _forward(x, xa, Wq, Wkv, Wout, lna_g, lna_b, lnb_g, lnb_b, Wqh, bqh, Wkh, bkh, Wvh, bvh, theta, threshold, factor, temp):
            p = dict(Wq=Wq, Wkv=Wkv, lna_g=lna_g, lna_b=lna_b, lnb_g=lnb_g, lnb_b=lnb_b, Wqh=Wqh, bqh=bqh, Wkh=Wkh, bkh=bkh, Wvh=Wvh, bvh=bvh, theta=theta, threshold=threshold, factor=factor, temp=temp)
            y = _slide(x, p)
            ya = _slide(xa, p)
            return _focus(y, ya, p) @ Wout.T
        return _forward(x, xa, Wq, Wkv, Wout, lna_g, lna_b, lnb_g, lnb_b, Wqh, bqh, Wkh, bkh, Wvh, bvh, theta, threshold, factor, temp)

    def _L1_ffn_ref(x, cn_w1, cn_b1, cn_w2, cn_b2, cn_w3, cn_b3, cn_w4, cn_b4, gc_w1, gc_b1, gc_w2, gc_b2, gc_w3, gc_b3, adaptive_range):
        import jax, jax.numpy as jnp
        import numpy as np
        B, S, DIM = (4, 512, 128)
        BASE_COUPLING = 0.1
        NUM_CYCLES = 3

        def _gelu(x):
            return jax.nn.gelu(x, approximate=False)

        def _coupling_net(h, w1, b1, w2, b2, w3, b3, w4, b4):
            h = _gelu(h @ w1 + b1)
            h = _gelu(h @ w2 + b2)
            h = _gelu(h @ w3 + b3)
            return jax.nn.sigmoid(h @ w4 + b4)

        def _global_net(h, w1, b1, w2, b2, w3, b3):
            h = _gelu(h @ w1 + b1)
            h = _gelu(h @ w2 + b2)
            return jax.nn.sigmoid(h @ w3 + b3)

        def _twist(x):
            o_r, o_i, p_r, p_i = jnp.split(x, 4, axis=-1)
            return jnp.concatenate([p_r, -p_i, -o_r, o_i], axis=-1)
        global_context = x.mean(axis=1, keepdims=True)
        gf = _global_net(global_context, gc_w1, gc_b1, gc_w2, gc_b2, gc_w3, gc_b3)
        out = x
        for _ in range(NUM_CYCLES):
            tf = _coupling_net(out, cn_w1, cn_b1, cn_w2, cn_b2, cn_w3, cn_b3, cn_w4, cn_b4)
            combined = 0.7 * gf + 0.3 * tf
            coupling = BASE_COUPLING + adaptive_range * (combined - 0.5) * 2.0
            out = out + coupling * _twist(out)
        return out

    def _L2_attn_ref(x, m1_in_w, m1_conv_w, m1_conv_b, m1_xproj_w, m1_dt_w, m1_dt_b, m1_Alog, m1_D, m1_out_w, m2_in_w, m2_conv_w, m2_conv_b, m2_xproj_w, m2_dt_w, m2_dt_b, m2_Alog, m2_D, m2_out_w, norm_g, norm_b, ffn_g, ffn_b, ff1_w, ff1_b, ff2_w, ff2_b):
        import jax, jax.numpy as jnp
        import numpy as np
        D_STATE = 16
        D_CONV = 4

        def layer_norm(x, g, b, eps=1e-05):
            mu = jnp.mean(x, axis=-1, keepdims=True)
            var = jnp.mean(jnp.square(x - mu), axis=-1, keepdims=True)
            return (x - mu) * jax.lax.rsqrt(var + eps) * g + b

        def silu(x):
            return x * jax.nn.sigmoid(x)

        def mamba(x, in_w, conv_w, conv_b, xproj_w, dt_w, dt_b, Alog, Dp, out_w):
            Bsz, L, _ = x.shape
            di = Dp.shape[0]
            xz = jnp.einsum('bld,ed->ble', x, in_w)
            xs, z = jnp.split(xz, 2, axis=-1)
            xt = xs.transpose(0, 2, 1)
            xt = jax.lax.conv_general_dilated(xt, conv_w[:, None, :], (1,), [(D_CONV - 1, 0)], feature_group_count=di, dimension_numbers=('NCH', 'OIH', 'NCH'))
            xs = silu((xt + conv_b[None, :, None]).transpose(0, 2, 1))
            dbl = jnp.einsum('bld,ed->ble', xs, xproj_w)
            dt_rank = dt_w.shape[1]
            dt, Bc, Cc = jnp.split(dbl, [dt_rank, dt_rank + D_STATE], axis=-1)
            dt = jax.nn.softplus(jnp.einsum('blr,dr->bld', dt, dt_w) + dt_b)
            A = -jnp.exp(Alog)
            dA = jnp.exp(dt[..., None] * A)
            dBx = dt[..., None] * Bc[:, :, None, :] * xs[..., None]

            def step(h, inp):
                dA_t, dBx_t, C_t = inp
                h = dA_t * h + dBx_t
                y = jnp.einsum('bds,bs->bd', h, C_t)
                return (h, y)
            h0 = jnp.zeros((Bsz, di, D_STATE), x.dtype)
            _, ys = jax.lax.scan(step, h0, (dA.transpose(1, 0, 2, 3), dBx.transpose(1, 0, 2, 3), Cc.transpose(1, 0, 2)))
            y = ys.transpose(1, 0, 2) + Dp * xs
            y = y * silu(z)
            return jnp.einsum('bld,od->blo', y, out_w)

        def _make_mamba_params(key, d_model, scale=0.02):
            di = 2 * d_model
            dt_rank = (d_model + 15) // 16
            ks = jax.random.split(key, 7)
            in_w = jax.random.normal(ks[0], (2 * di, d_model), jnp.float32) * scale
            conv_w = jax.random.normal(ks[1], (di, D_CONV), jnp.float32) * scale
            conv_b = jnp.zeros((di,), jnp.float32)
            xproj_w = jax.random.normal(ks[2], (dt_rank + 2 * D_STATE, di), jnp.float32) * scale
            dt_w = jax.random.normal(ks[3], (di, dt_rank), jnp.float32) * scale
            dt_b = jax.random.uniform(ks[4], (di,), jnp.float32, -5.0, -2.0)
            Alog = jnp.log(jnp.tile(jnp.arange(1, D_STATE + 1, dtype=jnp.float32), (di, 1)))
            Dp = jnp.ones((di,), jnp.float32)
            out_w = jax.random.normal(ks[5], (d_model, di), jnp.float32) * scale
            return (in_w, conv_w, conv_b, xproj_w, dt_w, dt_b, Alog, Dp, out_w)
        h = layer_norm(x, norm_g, norm_b)
        fwd = mamba(h, m1_in_w, m1_conv_w, m1_conv_b, m1_xproj_w, m1_dt_w, m1_dt_b, m1_Alog, m1_D, m1_out_w)
        bwd = mamba(h[:, ::-1], m2_in_w, m2_conv_w, m2_conv_b, m2_xproj_w, m2_dt_w, m2_dt_b, m2_Alog, m2_D, m2_out_w)
        block_out = jax.nn.gelu(fwd + bwd + x, approximate=False)
        x = x + block_out
        hf = layer_norm(x, ffn_g, ffn_b)
        hf = jax.nn.gelu(jnp.einsum('bld,hd->blh', hf, ff1_w) + ff1_b, approximate=False)
        x = x + jnp.einsum('blh,dh->bld', hf, ff2_w) + ff2_b
        return x

    def _L2_xattn_ref(x, context, Wq, Wk, Wv, Wo, bo):
        import jax, jax.numpy as jnp
        import numpy as np
        DIM = 128
        NUM_HEADS = 8
        HEAD_DIM = 64
        INNER = NUM_HEADS * HEAD_DIM
        B, N, _ = x.shape
        M = context.shape[1]
        scale = HEAD_DIM ** (-0.5)
        q = (x @ Wq).reshape(B, N, NUM_HEADS, HEAD_DIM).transpose(0, 2, 1, 3)
        k = (context @ Wk).reshape(B, M, NUM_HEADS, HEAD_DIM).transpose(0, 2, 1, 3)
        v = (context @ Wv).reshape(B, M, NUM_HEADS, HEAD_DIM).transpose(0, 2, 1, 3)
        attn = jax.nn.softmax(jnp.einsum('bhnd,bhmd->bhnm', q, k) * scale, axis=-1)
        out = jnp.einsum('bhnm,bhmd->bhnd', attn, v)
        out = out.transpose(0, 2, 1, 3).reshape(B, N, INNER)
        return out @ Wo + bo

    def _L2_ffn_ref(x, w_router, W_qkv, W_out, g1, g2, W1, W2, W3):
        import math
        import jax, jax.numpy as jnp
        import numpy as np
        B, T, D = (4, 512, 128)
        H = 16
        HD = D // H
        CAP = int(512 * 0.125)
        DFF = int(D * 4 * 2 / 3)
        EPS = 1e-06

        def rmsnorm(x, g):
            return x * jax.lax.rsqrt(jnp.mean(x * x, axis=-1, keepdims=True) + EPS) * g
        Bq, Tq, Dq = x.shape
        scores = x @ w_router
        _, idx = jax.lax.top_k(scores, CAP)
        x_sel = jnp.take_along_axis(x, idx[:, :, None], axis=1)
        h = rmsnorm(x_sel, g1)
        qkv = (h @ W_qkv.T).reshape(Bq, CAP, 3, H, HD)
        q, k, v = jnp.moveaxis(qkv, 2, 0)
        att = jnp.einsum('bqhd,bkhd->bhqk', q, k) / math.sqrt(HD)
        mask = jnp.triu(jnp.ones((CAP, CAP), bool), 1)
        att = jnp.where(mask, -jnp.inf, att)
        att = jax.nn.softmax(att, axis=-1)
        o = jnp.einsum('bhqk,bkhd->bqhd', att, v).reshape(Bq, CAP, Dq)
        x_attn = o @ W_out.T
        h2 = rmsnorm(x_sel + x_attn, g2)
        x_ff = jax.nn.silu(h2 @ W1.T) * (h2 @ W2.T) @ W3.T
        x_proc = x_sel + x_attn + x_ff
        out = x.at[jnp.arange(Bq)[:, None], idx].set(x_proc)
        return out

    def _L3_attn_ref(inputs, W_qkv, W_out):
        import math
        import jax, jax.numpy as jnp
        import numpy as np
        HIDDEN = 128
        NUM_HEADS = 16
        NUM_QUERIES = 2
        NUM_Q_HEADS = NUM_HEADS * NUM_QUERIES
        HEAD_DIM = 64
        Q_DIM = NUM_Q_HEADS * HEAD_DIM
        KV_DIM = NUM_HEADS * HEAD_DIM
        BATCH, SEQ = (4, 128)

        def _alibi_slopes(num_heads: int) -> np.ndarray:
            closest_pow2 = 2 ** int(math.floor(math.log2(num_heads)))
            base = 2.0 ** (-2.0 ** (-(math.log2(closest_pow2) - 3)))
            powers = np.arange(1, closest_pow2 + 1, dtype=np.float32)
            slopes = base ** powers
            if closest_pow2 != num_heads:
                extra_base = 2.0 ** (-2.0 ** (-(math.log2(2 * closest_pow2) - 3)))
                extra_powers = np.arange(1, 2 * (num_heads - closest_pow2) + 1, 2, dtype=np.float32)
                slopes = np.concatenate([slopes, extra_base ** extra_powers])
            return slopes[:num_heads].astype(np.float32)
        ALIBI_SLOPES = jnp.asarray(_alibi_slopes(NUM_Q_HEADS))
        B, S, _ = inputs.shape
        qkv = inputs @ W_qkv
        q = qkv[..., :Q_DIM].reshape(B, S, NUM_Q_HEADS, HEAD_DIM).transpose(0, 2, 1, 3)
        k = qkv[..., Q_DIM:Q_DIM + KV_DIM].reshape(B, S, NUM_HEADS, HEAD_DIM).transpose(0, 2, 1, 3)
        v = qkv[..., Q_DIM + KV_DIM:].reshape(B, S, NUM_HEADS, HEAD_DIM).transpose(0, 2, 1, 3)
        k = jnp.repeat(k, NUM_QUERIES, axis=1)
        v = jnp.repeat(v, NUM_QUERIES, axis=1)
        pos = jnp.arange(S)
        rel = (pos[None, :] - pos[:, None]).astype(jnp.float32)
        bias = ALIBI_SLOPES[:, None, None] * rel[None, :, :]
        scores = jnp.einsum('bhqd,bhkd->bhqk', q, k) / math.sqrt(HEAD_DIM)
        scores = scores + bias[None]
        causal = pos[:, None] >= pos[None, :]
        scores = jnp.where(causal[None, None], scores, -jnp.inf)
        attn = jax.nn.softmax(scores, axis=-1)
        out = jnp.einsum('bhqk,bhkd->bhqd', attn, v)
        out = out.transpose(0, 2, 1, 3).reshape(B, S, Q_DIM)
        return out @ W_out

    def _L3_xattn_ref(q, k, v, mask, wq_w, wq_b, wk_w, wk_b, wv_w, wv_b, out_w, out_b):
        import math
        import jax, jax.numpy as jnp
        import numpy as np
        N_HEAD = 16

        def _slopes(n_head):
            cp2 = 2 ** int(math.floor(math.log2(n_head)))
            slopes = 0.5 ** np.arange(1, cp2 + 1)
            if cp2 < n_head:
                intra = 1.0 / math.sqrt(2.0)
                pair = intra ** np.arange(1, 1 + 2 * (n_head - cp2), 2)
                slopes = np.sort(np.concatenate([slopes, pair]))[::-1]
            return jnp.asarray(slopes, dtype=jnp.float32)

        def _alibi_bias(S):
            d = jnp.arange(S)[:, None] - jnp.arange(S)[None, :]
            return -jnp.maximum(d, 0).astype(jnp.float32)
        B, S, D = q.shape
        H = N_HEAD
        hd = D // H
        lin = lambda x, w, b: x @ w.T + b
        split = lambda x: x.reshape(B, S, H, hd).transpose(0, 2, 1, 3)
        wq = split(lin(q, wq_w, wq_b))
        wk = split(lin(k, wk_w, wk_b))
        wv = split(lin(v, wv_w, wv_b))
        qk = jnp.einsum('bhsd,bhtd->bhst', wq, wk)
        alibi = _alibi_bias(S)[None, :, :] * _slopes(H)[:, None, None]
        attn = qk + alibi[None]
        attn = jnp.where(mask == 0, jnp.float32(-1000000000.0), attn)
        attn = jax.nn.softmax(attn, axis=-1)
        out = jnp.einsum('bhst,bhtd->bhsd', attn, wv)
        out = out.transpose(0, 2, 1, 3).reshape(B, S, D)
        return lin(out, out_w, out_b)

    def _L3_ffn_ref(hidden_states, router_w, w1, w2):
        import jax, jax.numpy as jnp
        import numpy as np
        EPS = 1e-09
        TOP_K = 2
        orig_shape = hidden_states.shape
        H = orig_shape[-1]
        E = router_w.shape[-1]
        flat = hidden_states.reshape(-1, H)
        T = flat.shape[0]
        gate_logits = flat @ router_w
        gate_probs = jax.nn.softmax(gate_logits, axis=-1)
        topk_w, topk_idx = jax.lax.top_k(gate_probs, TOP_K)
        topk_w = topk_w / jnp.clip(topk_w.sum(-1, keepdims=True), EPS)
        cw = jnp.zeros((T, E), dtype=flat.dtype).at[jnp.arange(T)[:, None], topk_idx].add(topk_w)
        h = jax.nn.silu(jnp.einsum('td,edf->etf', flat, w1))
        y = jnp.einsum('etf,efd->etd', h, w2)
        out = jnp.einsum('etd,te->td', y, cw)
        return out.reshape(orig_shape)
    x = x + _L0_attn_ref(_layernorm(x, axis=-1), L0_attn_Wq, L0_attn_Wk, L0_attn_Wv, L0_attn_Wo)
    x = x + _L0_xattn_ref(_layernorm(x, axis=-1), ctx_1024, ctx_1024, L0_xattn_Wq, L0_xattn_bq, L0_xattn_Wk, L0_xattn_bk, L0_xattn_Wv, L0_xattn_bv, L0_xattn_Wo, L0_xattn_bo)
    x = x + _L0_ffn_ref(_layernorm(x, axis=-1), L0_ffn_gate_W, L0_ffn_gate_b, L0_ffn_wi_W, L0_ffn_wi_b, L0_ffn_wo_W, L0_ffn_wo_b, L0_ffn_lora_A, L0_ffn_lora_B)
    x = x + _L1_attn_ref(_layernorm(x, axis=-1), L1_attn_Wq, L1_attn_bq, L1_attn_Wk, L1_attn_bk, L1_attn_Wv, L1_attn_bv, L1_attn_Wc, L1_attn_We, L1_attn_Wo, L1_attn_bo, L1_attn_gamma, L1_attn_beta)
    x = x + _L1_xattn_ref(_layernorm(x, axis=-1), ctx_1024, L1_xattn_Wq, L1_xattn_Wkv, L1_xattn_Wout, L1_xattn_lna_g, L1_xattn_lna_b, L1_xattn_lnb_g, L1_xattn_lnb_b, L1_xattn_Wqh, L1_xattn_bqh, L1_xattn_Wkh, L1_xattn_bkh, L1_xattn_Wvh, L1_xattn_bvh, L1_xattn_theta, L1_xattn_threshold, L1_xattn_factor, L1_xattn_temp)
    x = x + _L1_ffn_ref(_layernorm(x, axis=-1), L1_ffn_cn_w1, L1_ffn_cn_b1, L1_ffn_cn_w2, L1_ffn_cn_b2, L1_ffn_cn_w3, L1_ffn_cn_b3, L1_ffn_cn_w4, L1_ffn_cn_b4, L1_ffn_gc_w1, L1_ffn_gc_b1, L1_ffn_gc_w2, L1_ffn_gc_b2, L1_ffn_gc_w3, L1_ffn_gc_b3, L1_ffn_adaptive_range)
    x = x + _L2_attn_ref(_layernorm(x, axis=-1), L2_attn_m1_in_w, L2_attn_m1_conv_w, L2_attn_m1_conv_b, L2_attn_m1_xproj_w, L2_attn_m1_dt_w, L2_attn_m1_dt_b, L2_attn_m1_Alog, L2_attn_m1_D, L2_attn_m1_out_w, L2_attn_m2_in_w, L2_attn_m2_conv_w, L2_attn_m2_conv_b, L2_attn_m2_xproj_w, L2_attn_m2_dt_w, L2_attn_m2_dt_b, L2_attn_m2_Alog, L2_attn_m2_D, L2_attn_m2_out_w, L2_attn_norm_g, L2_attn_norm_b, L2_attn_ffn_g, L2_attn_ffn_b, L2_attn_ff1_w, L2_attn_ff1_b, L2_attn_ff2_w, L2_attn_ff2_b)
    x = x + _L2_xattn_ref(_layernorm(x, axis=-1), ctx_1024, L2_xattn_Wq, L2_xattn_Wk, L2_xattn_Wv, L2_xattn_Wo, L2_xattn_bo)
    x = x + _L2_ffn_ref(_layernorm(x, axis=-1), L2_ffn_w_router, L2_ffn_W_qkv, L2_ffn_W_out, L2_ffn_g1, L2_ffn_g2, L2_ffn_W1, L2_ffn_W2, L2_ffn_W3)
    x = x + _L3_attn_ref(_layernorm(x, axis=-1), L3_attn_W_qkv, L3_attn_W_out)
    x = x + _L3_xattn_ref(_layernorm(x, axis=-1), ctx_1024, ctx_1024, mask_1x1xSxS2_ik0, L3_xattn_wq_w, L3_xattn_wq_b, L3_xattn_wk_w, L3_xattn_wk_b, L3_xattn_wv_w, L3_xattn_wv_b, L3_xattn_out_w, L3_xattn_out_b)
    x = x + _L3_ffn_ref(_layernorm(x, axis=-1), L3_ffn_router_w, L3_ffn_w1, L3_ffn_w2)
    return x

_drawn_inputs = setup_inputs


def setup_inputs(seed=0):
    import zlib

    import numpy as np

    out = dict(_drawn_inputs(seed))
    spreads = {'L0_xattn_bq': (0.0, 0.357),
     'L0_xattn_bk': (0.0, 0.8),
     'L0_xattn_bv': (0.0, 0.1),
     'L0_xattn_bo': (0.0, 0.1),
     'L0_ffn_gate_b': (0.0, 0.8),
     'L0_ffn_wi_b': (0.0, 0.1),
     'L0_ffn_wo_b': (0.0, 0.1),
     'L1_attn_bq': (0.0, 0.8),
     'L1_attn_bk': (0.0, 0.8),
     'L1_attn_bv': (0.0, 0.8),
     'L1_attn_bo': (0.0, 0.1),
     'L1_attn_gamma': (1.0, 0.2),
     'L1_attn_beta': (0.0, 0.1),
     'L1_xattn_lna_g': (1.0, 0.2),
     'L1_xattn_lna_b': (0.0, 0.1),
     'L1_xattn_lnb_g': (1.0, 0.6),
     'L1_xattn_lnb_b': (0.0, 0.8),
     'L1_ffn_cn_b1': (0.0, 0.8),
     'L1_ffn_cn_b2': (0.0, 0.8),
     'L1_ffn_cn_b3': (0.0, 0.8),
     'L1_ffn_gc_b1': (0.0, 0.8),
     'L1_ffn_gc_b2': (0.0, 0.8),
     'L2_attn_m1_conv_b': (0.0, 0.8),
     'L2_attn_m1_D': (1.0, 0.6),
     'L2_attn_m2_conv_b': (0.0, 0.8),
     'L2_attn_m2_D': (1.0, 0.6),
     'L2_attn_norm_g': (1.0, 0.6),
     'L2_attn_norm_b': (0.0, 0.8),
     'L2_attn_ffn_g': (1.0, 0.6),
     'L2_attn_ffn_b': (0.0, 0.8),
     'L2_attn_ff1_b': (0.0, 0.8),
     'L2_attn_ff2_b': (0.0, 0.445),
     'L2_ffn_g1': (1.0, 0.6),
     'L2_ffn_g2': (1.0, 0.6)}
    factors = {'L0_ffn_gate_W': 3.186,
     'L0_ffn_lora_A': 2.973,
     'L0_ffn_lora_B': 2.977,
     'L1_attn_Wq': 8.0,
     'L1_attn_Wk': 8.0,
     'L1_attn_Wv': 8.0,
     'L1_attn_Wc': 8.0,
     'L1_attn_We': 8.0,
     'L1_attn_Wo': 8.0,
     'L1_xattn_bqh': 8.0,
     'L1_xattn_bkh': 8.0,
     'L1_xattn_bvh': 8.0,
     'L1_ffn_cn_w1': 8.0,
     'L1_ffn_cn_w2': 8.0,
     'L1_ffn_cn_w3': 8.0,
     'L1_ffn_cn_w4': 8.0,
     'L1_ffn_gc_w1': 8.0,
     'L1_ffn_gc_w2': 4.408,
     'L1_ffn_gc_w3': 6.763,
     'L2_attn_m1_in_w': 8.0,
     'L2_attn_m1_conv_w': 8.0,
     'L2_attn_m1_xproj_w': 8.0,
     'L2_attn_m1_dt_w': 8.0,
     'L2_attn_m1_dt_b': 8.0,
     'L2_attn_m1_Alog': 8.0,
     'L2_attn_m1_out_w': 8.0,
     'L2_attn_m2_in_w': 8.0,
     'L2_attn_m2_conv_w': 8.0,
     'L2_attn_m2_xproj_w': 8.0,
     'L2_attn_m2_dt_w': 8.0,
     'L2_attn_m2_dt_b': 8.0,
     'L2_attn_m2_Alog': 8.0,
     'L2_attn_m2_out_w': 8.0,
     'L2_attn_ff1_w': 5.028,
     'L2_attn_ff2_w': 4.627,
     'L2_xattn_bo': 8.0,
     'L2_ffn_w_router': 8.0,
     'L2_ffn_W_qkv': 8.0,
     'L2_ffn_W_out': 8.0,
     'L2_ffn_W1': 8.0,
     'L2_ffn_W2': 8.0,
     'L2_ffn_W3': 8.0,
     'L3_xattn_wq_w': 8.0,
     'L3_xattn_wq_b': 8.0,
     'L3_xattn_wk_w': 8.0,
     'L3_xattn_wk_b': 8.0,
     'L3_xattn_wv_w': 8.0,
     'L3_xattn_wv_b': 8.0,
     'L3_xattn_out_w': 8.0,
     'L3_xattn_out_b': 8.0,
     'L3_ffn_router_w': 8.0,
     'L3_ffn_w1': 8.0,
     'L3_ffn_w2': 8.0}
    for name, (base, spread) in spreads.items():
        noise = np.random.default_rng([zlib.crc32(name.encode()), seed]).standard_normal(out[name].shape)
        drawn = base * np.exp(spread * noise) if base else spread * noise
        out[name] = jnp.asarray(drawn.astype(out[name].dtype))
    for name, factor in factors.items():
        out[name] = (out[name] * factor).astype(out[name].dtype)
    return out
```

```python
import math
from contextlib import ExitStack

import numpy as np

import concourse.bass as bass
from concourse import mybir
from concourse.alu_op_type import AluOpType as ALU

F32 = mybir.dt.float32
I32 = mybir.dt.int32
ACT = mybir.ActivationFunctionType
AX = mybir.AxisListType.X

P = 128
D = 128
S = 64
TPG = 4
GT = TPG * P
SPG = GT // S
BIG = 1e30


class Core:

    def __init__(self, nc, ctx, groups):
        def sb(name, shape, dt=F32):
            return ctx.enter_context(nc.sbuf_tensor(name, shape, dt))
        self.nc, self.NG, self.NT = nc, groups, groups * TPG
        pad = self.NT + TPG
        self.X = sb("X", [P, pad, D])
        self.Y = sb("Y", [P, pad, D])
        self.MV = sb("MV", [P, pad, 2])
        self.RS = sb("RS", [P, pad])
        self.NM = sb("NM", [P, pad])
        self.RS2 = sb("RS2", [P, pad])
        self.NM2 = sb("NM2", [P, pad])
        self.tmp = sb("stat_tmp", [P, pad])
        self.ident = sb("ident", [P, P])
        self.ones = sb("ones", [P, P])


class Scope:

    def __init__(self, nc, ctx, name):
        self.nc, self.ctx, self.name = nc, ctx, name
        self.sems = []
        ctx.callback(self.clear)

    def clear(self):
        self.nc.clear_and_free_semaphores(self.sems)
        self.nc.all_engine_barrier()

    def sb(self, name, shape, dt=F32):
        return self.ctx.enter_context(self.nc.sbuf_tensor(f"{self.name}_{name}", shape, dt))

    def ps(self, name, shape):
        return self.ctx.enter_context(self.nc.psum_tensor(f"{self.name}_{name}", shape, F32))

    def sem(self, name):
        self.sems.append(self.nc.alloc_semaphore(name=f"{self.name}_{name}"))
        return self.sems[-1]


def bc(ap, shape):
    return ap.to_broadcast(shape)


def load_x(C, x, constants):
    nc = C.nc
    with ExitStack() as ctx:
        sc = Scope(nc, ctx, "load")
        loaded, zeroed = sc.sem("loaded"), sc.sem("zeroed")
        st = sc.sb("st", [P, TPG, 6])
        mv = sc.sb("mv", [P, TPG, 2])
        block = ctx.enter_context(nc.Block())

        @block.sync
        def _(sp):
            sp.dma_start(C.X[:, 0:C.NT, :], x.rearrange("(n p) d -> p n d", p=P)).then_inc(loaded, 16)
            sp.dma_start(C.ident[:], constants["ident"]).then_inc(loaded, 16)

        @block.gpsimd
        def _(pool):
            nc.gpsimd.memset(C.Y[:], 0.0).then_inc(zeroed, 1)
            nc.gpsimd.memset(C.ones[:], 1.0).then_inc(zeroed, 1)
            nc.gpsimd.memset(C.X[:, C.NT:, :], 0.0).then_inc(zeroed, 1)
            nc.gpsimd.memset(C.MV[:, C.NT:, :], 0.0).then_inc(zeroed, 1)

        @block.vector
        def _(dve):
            dve.wait_ge(loaded, 32)
            with dve.Fori(0, C.NG) as i:
                row_stats(nc, dve, C, C.X, st, mv, i)


def row_stats(nc, dve, C, src, st, mv, i):
    for p in range(TPG):
        nc.vector.bn_stats(st[:, p, :], src[:, i * TPG + p, :])
    dve.drain()
    for p in range(TPG):
        nc.vector.bn_aggr(mv[:, p, :], st[:, p, :])
    dve.drain()
    nc.vector.tensor_copy(C.MV[:, bass.ds(i * TPG, TPG), :], mv[:])


def norm_scales(C, name, eps, second=None):
    nc = C.nc
    with ExitStack() as ctx:
        sc = Scope(nc, ctx, name)
        shifted, rooted = sc.sem("shifted"), sc.sem("rooted")
        block = ctx.enter_context(nc.Block())
        mean, var = C.MV[:, :, 0], C.MV[:, :, 1]

        @block.vector
        def _(dve):
            nc.vector.tensor_scalar(C.tmp[:], var, eps, None, ALU.add).then_inc(shifted, 1)
            dve.wait_ge(rooted, 1)
            nc.vector.reciprocal(C.RS[:], C.tmp[:])
            dve.drain()
            nc.vector.scalar_tensor_tensor(C.NM[:], mean, -1.0, C.RS[:], ALU.mult, ALU.mult)
            if second is not None:
                nc.vector.tensor_tensor(C.tmp[:], C.RS[:], C.RS[:], ALU.mult)
                dve.drain()
                nc.vector.tensor_tensor(C.tmp[:], C.tmp[:], var, ALU.mult)
                dve.drain()
                nc.vector.tensor_scalar(C.tmp[:], C.tmp[:], second, None, ALU.add).then_inc(shifted, 1)
                dve.wait_ge(rooted, 2)
                nc.vector.reciprocal(C.tmp[:], C.tmp[:])
                dve.drain()
                nc.vector.tensor_tensor(C.RS2[:], C.tmp[:], C.RS[:], ALU.mult)
                dve.drain()
                nc.vector.scalar_tensor_tensor(C.NM2[:], mean, -1.0, C.RS2[:], ALU.mult, ALU.mult)

        @block.scalar
        def _(act):
            for n in range(1 if second is None else 2):
                act.wait_ge(shifted, n + 1)
                nc.scalar.activation(C.tmp[:], C.tmp[:], ACT.Sqrt).then_inc(rooted, 1)


def inner_scales(C, name, eps, mean_square):
    nc = C.nc
    with ExitStack() as ctx:
        sc = Scope(nc, ctx, name)
        shifted, rooted = sc.sem("shifted"), sc.sem("rooted")
        block = ctx.enter_context(nc.Block())
        mean, var = C.MV[:, :, 0], C.MV[:, :, 1]

        @block.vector
        def _(dve):
            if mean_square:
                nc.vector.tensor_tensor(C.tmp[:], mean, mean, ALU.mult)
                dve.drain()
                nc.vector.tensor_tensor(C.tmp[:], C.tmp[:], var, ALU.add)
                dve.drain()
                nc.vector.tensor_scalar(C.tmp[:], C.tmp[:], eps, None, ALU.add).then_inc(shifted, 1)
            else:
                nc.vector.tensor_scalar(C.tmp[:], var, eps, None, ALU.add).then_inc(shifted, 1)
            dve.wait_ge(rooted, 1)
            nc.vector.reciprocal(C.RS2[:], C.tmp[:])
            dve.drain()
            if not mean_square:
                nc.vector.scalar_tensor_tensor(C.NM2[:], mean, -1.0, C.RS2[:], ALU.mult, ALU.mult)

        @block.scalar
        def _(act):
            act.wait_ge(shifted, 1)
            nc.scalar.activation(C.tmp[:], C.tmp[:], ACT.Sqrt).then_inc(rooted, 1)



NH, HD = 16, 8
NB = NH // 2
RG, HR = 4, 4
UT = 2
UPG = TPG // UT
VW = HD + 1


def attn16(C, name, mode, W, kT_dram=None):
    nc = C.nc
    cross, linear, rank = mode in ("ctx", "mask"), mode == "linear", mode == "rank"
    to_y = linear or rank
    with ExitStack() as ctx:
        sc = Scope(nc, ctx, name)
        sb, ps, sem = sc.sb, sc.ps, sc.sem
        wq, wo = sb("wq", [P, D]), sb("wo", [P, D])
        bq, bv = sb("bq", [P, 1]), sb("bv", [P, 1])
        bo = sb("bo", [1, D])
        hmask = sb("hmask", [P, HR])
        bkm = sb("bkm", [P, HR])
        if linear:
            wk, wv = sb("wk", [P, 32]), sb("wv", [P, 32])
            wc, we = sb("wc", [32, S]), sb("we", [S, D])
            bk32, bv32 = sb("bk32", [32, 1]), sb("bv32", [32, 1])
            k32, c64 = sb("k32", [32, 2, GT]), sb("c64", [S, 2, GT])
        else:
            wk, wv = sb("wk", [P, D]), sb("wv", [P, D])
            bk = sb("bk", [P, 1])
        if mode == "rope":
            wqr, wkr = sb("wqr", [P, D]), sb("wkr", [P, D])
            cosT, sinT = sb("cosT", [P, S]), sb("sinT", [P, S])
        if mode in ("rope", "linear"):
            t1, t2 = sb("t1", [P, GT]), sb("t2", [P, GT])
            kf = sb("kf", [P, GT])
        if mode in ("rope", "ctx", "mask"):
            table = sb("table", [P, NH, S])
        if mode == "mask":
            keepi, keep = sb("keepi", [P, S], I32), sb("keep", [P, S])
            off = sb("off", [P, S])
        if linear or rank:
            tril = sb("tril", [P, S])
        if rank:
            g1, wr = sb("g1", [P, 1]), sb("wr", [P, D])
            s_own, s_rep = sb("s_own", [P, TPG]), sb("s_rep", [P, TPG, P])
            hidden, r1, r2 = sb("hidden", [P, TPG, S]), sb("r1", [P, TPG, S]), sb("r2", [P, TPG, S])
            prod = sb("prod", [P, D])
        xn, xnT = sb("xn", [P, TPG, D]), sb("xnT", [P, GT])
        xt = sb("xt", [P, UT, D])
        kvb = sb("kvb", [P, GT]) if cross else xnT
        qT = sb("qT", [P, GT])
        kbd = sb("kbd", [P, SPG, HR, S])
        vbd = sb("vbd", [P, SPG, NB, 2, VW])
        s1 = sb("s1", [P, UPG, UT, NH, S])
        mx = sb("mx", [P, UT, NH])
        pT = sb("pT", [P, 2, 4, P])
        rden = sb("rden", [P, UT, NH])
        on, oT = sb("on", [P, UT, D]), sb("oT", [P, UT, P])
        st, mv = sb("st", [P, UT, 6]), sb("mv", [P, TPG, 2])

        ps_s = ps("ps_s", [P, RG, UT * HR * S])
        ps_t = ps("ps_t", [P, 2, 4 * P])
        ps_j = ps("ps_j", [P, GT])
        ps_o = ps("ps_o", [P, 512])
        o_acc = ps_o[:, 0:UT * NH * VW].rearrange("p (t h e) -> p t h e", t=UT, e=VW)
        j_tr = ps_j[:, 0:UT * P].rearrange("p (t q) -> p t q", t=UT)
        j_out = ps_j[:, UT * P:2 * UT * P].rearrange("p (t q) -> p t q", t=UT)

        loaded, prepared = sem("loaded"), sem("prepared")
        kv_loaded = sem("kv_loaded")
        xn_ready, xT_done, xT_ready = sem("xn_ready"), sem("xT_done"), sem("xT_ready")
        q_done, q_ready = sem("q_done"), sem("q_ready")
        k_done, k_ready, v_done, v_ready = sem("k_done"), sem("k_ready"), sem("v_done"), sem("v_ready")
        kf_ready, e_in, e_out = sem("kf_ready"), sem("e_in"), sem("e_out")
        low_done, low_ready = sem("low_done"), sem("low_ready")
        rank_done, rank_in = sem("rank_done"), sem("rank_in")
        scores_done, scores_read = sem("scores_done"), sem("scores_read")
        shifted, probs = sem("shifted"), sem("probs")
        pT_done, pT_ready = sem("pT_done"), sem("pT_ready")
        pv_done, on_ready = sem("pv_done"), sem("on_ready")
        oT_done, oT_ready = sem("oT_done"), sem("oT_ready")
        out_done, out_read = sem("out_done"), sem("out_read")
        block = ctx.enter_context(nc.Block())
        loads = [(wq, W["wq"]), (wo, W["wo"]), (wk, W["wk"]), (wv, W["wv"]), (hmask, W["hmask"])]
        if "bo" in W:
            loads.append((bo, W["bo"]))
        if "bq" in W:
            loads.append((bq, W["bq"]))
        if cross:
            loads += [(bk, W["bk"]), (bv, W["bv"])]
        if mode == "rope":
            loads += [(cosT, W["cosT"]), (sinT, W["sinT"])]
        if mode in ("rope", "ctx", "mask"):
            loads.append((table, W["table"]))
        if mode == "mask":
            loads.append((keepi, W["mask"]))
        if linear:
            loads += [(wc, W["wc"]), (we, W["we"]), (bk32, W["bk"]), (bv32, W["bv"])]
        if linear or rank:
            loads.append((tril, W["tril"]))
        if rank:
            loads += [(g1, W["g1"]), (wr, W["wr"])]
        n_loaded = 16 * len(loads)

        @block.sync
        def _(sp):
            for to, of in loads:
                sp.dma_start(to[:], of).then_inc(loaded, 16)
            if cross:
                sp.dma_start(kvb[:], kT_dram[:, 0:GT]).then_inc(kv_loaded, 16)
                with sp.Fori(1, C.NG) as i:
                    sp.wait_ge(v_done, i)
                    sp.dma_start(kvb[:], kT_dram[:, bass.ds(i * GT, GT)]).then_inc(kv_loaded, 16)

        def front_dve(dve, j):
            rs, nm = (C.RS2, C.NM2) if rank else (C.RS, C.NM)
            for p in range(TPG):
                n = j * TPG + p
                last = nc.vector.tensor_scalar(xn[:, p, :], C.X[:, n, :], rs[:, bass.ds(n, 1)],
                                               nm[:, bass.ds(n, 1)], ALU.mult, ALU.add)
            last.then_inc(xn_ready, 1)

        def front_pe(pe, j):
            pe.wait_ge(xn_ready, j + 1)
            for p in range(TPG):
                last = nc.tensor.transpose(ps_j[:, p * P:(p + 1) * P], xn[:, p, :], C.ident[:])
            last.then_inc(xT_done, 1)

        def front_act(act, j):
            act.wait_ge(xT_done, j + 1)
            nc.scalar.activation(xnT[:], ps_j[:], ACT.Copy).then_inc(xT_ready, 1)

        @block.tensor
        def _(pe):
            pe.wait_ge(loaded, n_loaded)
            pe.wait_ge(prepared, 2)

            def queries_keys(u):
                for t in range(UT):
                    for b in range(2):
                        q = 2 * (UT * u + t) + b
                        for g in range(RG):
                            r = slice(32 * g, 32 * g + 32)
                            last = nc.tensor.matmul(ps_s[S * b:S * b + S, g, t * HR * S:(t + 1) * HR * S],
                                                    qT[r, q * S:(q + 1) * S], kbd[r, q, :, :], start=True, stop=True)
                last.then_inc(scores_done, 1)

            def turn_probs(u, m):
                for t in range(4):
                    h = (m % 2) * HR * 2 + 2 * t
                    last = nc.tensor.transpose(ps_t[:, m % 2, t * P:(t + 1) * P],
                                               s1[:, u, m // 2, h:h + 2, :].rearrange("p h k -> p (h k)"), C.ident[:])
                last.then_inc(pT_done, 1)

            def weigh_values(u, m):
                for t in range(4):
                    n = (m % 2) * 4 + t
                    for b in range(2):
                        last = nc.tensor.matmul(o_acc[S * b:S * b + S, m // 2, 2 * n:2 * n + 2, :].rearrange("p h v -> p (h v)"),
                                                pT[:, m % 2, t, S * b:S * b + S],
                                                vbd[:, 2 * (UT * u + m // 2) + b, n, :, :].rearrange("p e v -> p (e v)"),
                                                start=True, stop=True)
                return last

            def turn_output(w):
                pe.wait_ge(on_ready, w + 1)
                for t in range(UT):
                    last = nc.tensor.transpose(j_tr[:, t, :], on[:, t, :], C.ident[:])
                last.then_inc(oT_done, 1)

            def project_output(w):
                pe.wait_ge(oT_ready, w + 1)
                for t in range(UT):
                    last = nc.tensor.matmul(j_out[:, t, :], oT[:, t, :], wo[:], start=True, stop="bo" not in W)
                    if "bo" in W:
                        last = nc.tensor.matmul(j_out[:, t, :], C.ones[0:1, :], bo[0:1, :], start=False, stop=True)
                last.then_inc(out_done, 1)

            front_pe(pe, 0)
            with pe.Fori(0, C.NG) as i:
                pe.wait_ge(xT_ready, i + 1)
                if not linear:
                    pe.wait_ge(scores_read, i * UPG + 1)
                pe.wait_ge(out_read, i * UPG + 1)
                nc.tensor.matmul(ps_j[:], wq[:], xnT[:], start=True, stop=True).then_inc(q_done, 1)
                if mode == "rope":
                    nc.tensor.matmul(ps_s[:, 0, :], wqr[:], xnT[:], start=True, stop=True).then_inc(q_done, 1)
                    nc.tensor.matmul(ps_s[:, 1, :], wk[:], xnT[:], start=True, stop=True).then_inc(k_done, 1)
                    nc.tensor.matmul(ps_s[:, 2, :], wkr[:], xnT[:], start=True, stop=True).then_inc(k_done, 1)
                elif linear:
                    nc.tensor.matmul(ps_s[0:32, 0, :], wk[:], xnT[:], start=True, stop=True)
                    nc.tensor.matmul(ps_s[0:32, 1, :], wv[:], xnT[:], start=True, stop=True).then_inc(low_done, 1)
                    pe.wait_ge(low_ready, i * 2 + 1)
                    for kv in range(2):
                        last = nc.tensor.matmul(ps_s[0:S, 2 + kv, :], wc[:], k32[:, kv, :],
                                                start=True, stop=True)
                    last.then_inc(low_done, 1)
                    pe.wait_ge(low_ready, i * 2 + 2)
                    nc.tensor.matmul(ps_s[:, 0, :], we[:], c64[:, 0, :], start=True, stop=True).then_inc(k_done, 1)
                else:
                    if cross:
                        pe.wait_ge(kv_loaded, i * 16 + 16)
                    nc.tensor.matmul(ps_s[:, 0, :], wk[:], kvb[:], start=True, stop=True).then_inc(k_done, 1)
                for s in range(SPG):
                    src = c64[:, 1, s * S:(s + 1) * S] if linear else kvb[:, s * S:(s + 1) * S]
                    for b in range(2):
                        last = nc.tensor.matmul(ps_t[S * b:S * b + S, s // 4, (s % 4) * D:(s % 4 + 1) * D], src,
                                                we[:] if linear else wv[:], start=True, stop=True)
                last.then_inc(v_done, 1)
                if rank:
                    pe.wait_ge(q_ready, i + 1)
                    pe.wait_ge(rank_in, i + 1)
                    for p in range(TPG):
                        last = nc.tensor.transpose(ps_j[:, p * P:(p + 1) * P], s_rep[:, p, :], C.ident[:])
                    last.then_inc(rank_done, 1)
                pe.wait_ge(q_ready, i + 1)
                pe.wait_ge(k_ready, i + 1)
                queries_keys(0)
                if linear:
                    pe.wait_ge(probs, i * UPG + 1)
                else:
                    pe.wait_ge(scores_read, i * UPG + 2)
                queries_keys(1)
                pe.wait_ge(v_ready, i + 1)
                for u in range(UPG):
                    w = i * UPG + u
                    pe.wait_ge(probs, w + 1)
                    turn_probs(u, 0)
                    turn_probs(u, 1)
                    if u == 1:
                        turn_output(w - 1)
                    for m in range(2 * UT):
                        pe.wait_ge(pT_ready, w * 2 * UT + m + 1)
                        last = weigh_values(u, m)
                        if m + 2 < 2 * UT:
                            turn_probs(u, m + 2)
                    last.then_inc(pv_done, 1)
                    if u == 1:
                        project_output(w - 1)
                pe.wait_ge(out_read, i * UPG + 2)
                front_pe(pe, i + 1)
                pe.wait_ge(xT_ready, i + 2)
                turn_output(i * UPG + 1)
                project_output(i * UPG + 1)

        @block.scalar
        def _(act):
            act.wait_ge(loaded, n_loaded)
            act.wait_ge(prepared, 2)

            def output_copy(w):
                act.wait_ge(oT_done, w + 1)
                if cross:
                    last = nc.scalar.activation(oT[:], j_tr, ACT.Identity, bias=bv[:, 0:1])
                else:
                    last = nc.scalar.activation(oT[:], j_tr, ACT.Copy)
                last.then_inc(oT_ready, 1)

            front_act(act, 0)
            with act.Fori(0, C.NG) as i:
                if linear:
                    act.wait_ge(low_done, i * 2 + 1)
                    nc.scalar.activation(k32[:, 0, :], ps_s[0:32, 0, :], ACT.Identity, bias=bk32[:, 0:1])
                    nc.scalar.activation(k32[:, 1, :], ps_s[0:32, 1, :], ACT.Identity,
                                         bias=bv32[:, 0:1]).then_inc(low_ready, 1)
                    act.wait_ge(e_in, i * 2 + 1)
                    nc.scalar.activation(t2[:], t2[:], ACT.Exp).then_inc(e_out, 1)
                    act.wait_ge(low_done, i * 2 + 2)
                    nc.scalar.activation(c64[:], ps_s[0:S, 2:4, :],
                                         ACT.Copy).then_inc(low_ready, 1)
                    act.wait_ge(e_in, i * 2 + 2)
                    nc.scalar.activation(t2[:], t2[:], ACT.Exp).then_inc(e_out, 1)
                if mode in ("rope", "linear"):
                    act.wait_ge(kf_ready, i + 1)
                else:
                    act.wait_ge(k_done, i + 1)
                for h in range(HR):
                    to = kbd[:, :, h, :]
                    if mode in ("rope", "linear"):
                        last = nc.scalar.activation(to, kf[:].rearrange("p (s k) -> p s k", k=S), ACT.Copy,
                                                    scale=hmask[:, h:h + 1])
                    else:
                        last = nc.scalar.activation(to, ps_s[:, 0, :].rearrange("p (s k) -> p s k", k=S),
                                                    ACT.Identity, scale=hmask[:, h:h + 1], bias=bkm[:, h:h + 1])
                last.then_inc(k_ready, 1)
                for u in range(UPG):
                    w = i * UPG + u
                    if not linear:
                        act.wait_ge(shifted, w + 1)
                        nc.scalar.activation(s1[:, u, :, :, :], s1[:, u, :, :, :], ACT.Exp).then_inc(probs, 1)
                    for m in range(2 * UT):
                        if u == 1 and m == 2:
                            output_copy(w - 1)
                        act.wait_ge(pT_done, w * 2 * UT + m + 1)
                        nc.scalar.activation(pT[:, m % 2, :, :], ps_t[:, m % 2, :].rearrange("p (t q) -> p t q", q=P),
                                             ACT.Copy).then_inc(pT_ready, 1)
                front_act(act, i + 1)
                output_copy(i * UPG + 1)

        @block.gpsimd
        def _(pool):
            nc.gpsimd.memset(vbd[:], 0.0)
            pool.drain()
            for e in range(2):
                nc.gpsimd.memset(vbd[S * e:S * e + S, :, :, e, HD:VW], 1.0)
            pool.drain()
            nc.gpsimd.memset(xt[:], 0.0).then_inc(prepared, 1)
            if rank:
                pool.wait_ge(loaded, n_loaded)

        @block.vector
        def _(dve):
            dve.wait_ge(loaded, n_loaded)
            if cross:
                nc.vector.tensor_scalar(bkm[:], hmask[:], bk[:, 0:1], None, ALU.mult)
            else:
                nc.vector.memset(bkm[:], 0.0)
            if mode == "rope":
                for w, r in ((wq, wqr), (wk, wkr)):
                    pairs, turned = w[:].rearrange("p (n e) -> p n e", e=2), r[:].rearrange("p (n e) -> p n e", e=2)
                    nc.vector.tensor_scalar(turned[:, :, 0], pairs[:, :, 1], -1.0, None, ALU.mult)
                    nc.vector.tensor_copy(turned[:, :, 1], pairs[:, :, 0])
            if mode == "mask":
                nc.vector.tensor_copy(keep[:], keepi[:])
                dve.drain()
                nc.vector.tensor_scalar(keep[:], keep[:], 0.0, None, ALU.not_equal)
                dve.drain()
                nc.vector.tensor_scalar(off[:], keep[:], 1e9, -1e9, ALU.mult, ALU.add)
                nc.vector.tensor_tensor(table[:], table[:], bc(keep[:].unsqueeze(1), [P, NH, S]), ALU.mult)
                dve.drain()
                nc.vector.tensor_tensor(table[:], table[:], bc(off[:].unsqueeze(1), [P, NH, S]), ALU.add)
            if rank:
                for w in (wq, wk, wv):
                    nc.vector.tensor_scalar(w[:], w[:], g1[:, 0:1], None, ALU.mult)
            dve.drain()
            nc.vector.memset(mv[:], 0.0)
            nc.vector.memset(mx[:], 0.0).then_inc(scores_read, 1)
            nc.vector.memset(rden[:], 0.0).then_inc(out_read, 1)
            dve.wait_ge(prepared, 1)
            dve.drain()
            nc.vector.memset(st[:], 0.0).then_inc(prepared, 1)

            def rotate(to, plain, turned, at):
                cs, sn = (bc(w[:].unsqueeze(1), [P, SPG, S]) for w in (cosT, sinT))
                v = lambda a: a.rearrange("p (s k) -> p s k", k=S)
                nc.vector.tensor_tensor(v(t1[:]), v(plain), cs, ALU.mult)
                nc.vector.tensor_tensor(v(t2[:]), v(turned), sn, ALU.mult)
                dve.drain()
                return nc.vector.tensor_tensor(to, t1[:], t2[:], ALU.add)

            def feature(to, src, bias, count):
                nc.vector.tensor_scalar(t1[:], src, bias, 0.0, ALU.add, ALU.max)
                nc.vector.tensor_scalar(t2[:], src, bias, 0.0, ALU.add, ALU.min).then_inc(e_in, 1)
                dve.drain()
                dve.wait_ge(e_out, count)
                return nc.vector.tensor_tensor(to, t1[:], t2[:], ALU.add)

            def scores(u, w):
                dve.wait_ge(scores_done, w + 1)
                out = s1[:, u, :, :, :]
                if mode in ("rope", "ctx"):
                    nc.vector.tensor_tensor(out.rearrange("p t (g h) k -> p t g (h k)", g=RG),
                                            ps_s[:].rearrange("p g (t x) -> p t g x", t=UT),
                                            bc(table[:].rearrange("p (g h) k -> p g (h k)", g=RG).unsqueeze(1),
                                               [P, UT, RG, HR * S]), ALU.add).then_inc(scores_read, 1)
                else:
                    for t in range(UT):
                        with_ = tril[:] if linear else hidden[:, UT * u + t, :] if rank else keep[:]
                        last = nc.vector.tensor_tensor(
                            out[:, t, :, :].rearrange("p (g h) k -> p g h k", g=RG),
                            ps_s[:, :, t * HR * S:(t + 1) * HR * S].rearrange("p g (h k) -> p g h k", k=S),
                            bc(with_.unsqueeze(1).unsqueeze(1), [P, RG, HR, S]), ALU.add if rank else ALU.mult)
                    last.then_inc(probs if linear else scores_read, 1)
                    if linear:
                        return
                dve.drain()
                if mode == "mask":
                    nc.vector.tensor_tensor(out, out, bc(table[:].unsqueeze(1), [P, UT, NH, S]), ALU.add)
                    dve.drain()
                nc.vector.tensor_reduce(mx[:], out, AX, ALU.max)
                dve.drain()
                nc.vector.tensor_tensor(out, out, bc(mx[:].unsqueeze(3), [P, UT, NH, S]),
                                        ALU.subtract).then_inc(shifted, 1)

            def normalise(w):
                dve.wait_ge(pv_done, w + 1)
                if linear:
                    nc.vector.tensor_scalar(rden[:], o_acc[:, :, :, HD], 1e-6, None, ALU.add)
                    dve.drain()
                    nc.vector.reciprocal(rden[:], rden[:])
                else:
                    nc.vector.reciprocal(rden[:], o_acc[:, :, :, HD])
                dve.drain()
                nc.vector.tensor_tensor(on[:].rearrange("p t (h e) -> p t h e", e=HD), o_acc[:, :, :, 0:HD],
                                        bc(rden[:].unsqueeze(3), [P, UT, NH, HD]), ALU.mult).then_inc(on_ready, 1)

            def residual(u, i, w):
                rows = bass.ds(i * TPG + u * UT, UT)
                if to_y:
                    for t in range(UT):
                        n = i * TPG + u * UT + t
                        nc.vector.tensor_scalar(xt[:, t, :], C.X[:, n, :], C.RS[:, bass.ds(n, 1)],
                                                C.NM[:, bass.ds(n, 1)], ALU.mult, ALU.add)
                    dve.drain()
                dve.wait_ge(out_done, w + 1)
                to = (C.Y if to_y else C.X)[:, rows, :]
                nc.vector.tensor_tensor(to, j_out, xt[:] if to_y else to, ALU.add).then_inc(out_read, 1)
                dve.drain()
                for t in range(UT):
                    nc.vector.bn_stats(st[:, t, :], (C.Y if to_y else C.X)[:, i * TPG + u * UT + t, :])
                dve.drain()
                for t in range(UT):
                    nc.vector.bn_aggr(mv[:, u * UT + t, :], st[:, t, :])

            front_dve(dve, 0)
            with dve.Fori(0, C.NG) as i:
                if rank:
                    for p in range(TPG):
                        n = i * TPG + p
                        nc.vector.tensor_scalar(xt[:, 0, :], C.X[:, n, :], C.RS[:, bass.ds(n, 1)],
                                                C.NM[:, bass.ds(n, 1)], ALU.mult, ALU.add)
                        dve.drain()
                        nc.vector.tensor_tensor(prod[:], xt[:, 0, :], wr[:], ALU.mult)
                        dve.drain()
                        nc.vector.tensor_reduce(s_own[:, p:p + 1], prod[:], AX, ALU.add)
                    dve.drain()
                    nc.vector.tensor_copy(s_rep[:], bc(s_own[:].unsqueeze(2), [P, TPG, P])).then_inc(rank_in, 1)
                if mode == "rope":
                    dve.wait_ge(q_done, i * 2 + 2)
                    rotate(qT[:], ps_j[:], ps_s[:, 0, :], 0)
                    dve.drain()
                    nc.vector.tensor_scalar(qT[:], qT[:], HD ** -0.5, None, ALU.mult).then_inc(q_ready, 1)
                    dve.wait_ge(k_done, i * 2 + 2)
                    rotate(kf[:], ps_s[:, 1, :], ps_s[:, 2, :], 1).then_inc(kf_ready, 1)
                elif linear:
                    dve.wait_ge(q_done, i + 1)
                    feature(qT[:], ps_j[:], bq[:, 0:1], i * 2 + 1).then_inc(q_ready, 1)
                    dve.drain()
                    dve.wait_ge(k_done, i + 1)
                    feature(kf[:], ps_s[:, 0, :], 0.0, i * 2 + 2).then_inc(kf_ready, 1)
                else:
                    dve.wait_ge(q_done, i + 1)
                    scale = 1.0 if mode == "mask" else HD ** -0.5
                    if cross:
                        nc.vector.tensor_scalar(qT[:], ps_j[:], bq[:, 0:1], scale, ALU.add,
                                                ALU.mult).then_inc(q_ready, 1)
                    else:
                        nc.vector.tensor_scalar(qT[:], ps_j[:], scale, None, ALU.mult).then_inc(q_ready, 1)
                dve.wait_ge(v_done, i + 1)
                for t in range(2):
                    for e in range(2):
                        r = slice(S * e, S * e + S)
                        src = ps_t[r, t, :].rearrange("p (s n e d) -> p s n e d", s=4, n=NB, e=2)[:, :, :, e, :]
                        last = nc.vector.tensor_copy(vbd[r, 4 * t:4 * t + 4, :, e, 0:HD], src)
                last.then_inc(v_ready, 1)
                if rank:
                    dve.wait_ge(rank_done, i + 1)
                    row = ps_j[:].rearrange("p (t b k) -> p t b k", t=TPG, b=2)
                    for b in range(2):
                        r = slice(S * b, S * b + S)
                        own = bc(s_own[r, :].unsqueeze(2), [S, TPG, S])
                        nc.vector.tensor_tensor(r1[r, :, :], row[r, :, b, :], own, ALU.is_gt)
                        nc.vector.tensor_tensor(r2[r, :, :], row[r, :, b, :], own, ALU.is_equal)
                    dve.drain()
                    nc.vector.tensor_tensor(r2[:], r2[:], bc(tril[:].unsqueeze(1), [P, TPG, S]), ALU.mult)
                    dve.drain()
                    nc.vector.tensor_tensor(r1[:], r1[:], r2[:], ALU.add)
                    dve.drain()
                    nc.vector.tensor_scalar(hidden[:], r1[:], BIG, -BIG, ALU.mult, ALU.add)
                    dve.drain()
                w = i * UPG
                scores(0, w)
                scores(1, w + 1)
                normalise(w)
                front_dve(dve, i + 1)
                residual(0, i, w)
                normalise(w + 1)
                residual(1, i, w + 1)
                dve.drain()
                nc.vector.tensor_copy(C.MV[:, bass.ds(i * TPG, TPG), :], mv[:])


class Front:

    def __init__(self, C, sc, bank, src, scale, shift):
        self.C, self.nc, self.bank, self.src, self.scale, self.shift = C, C.nc, bank, src, scale, shift
        self.xn, self.xnT = sc.sb("xn", [P, TPG, D]), sc.sb("xnT", [P, GT])
        self.xn_ready, self.xT_done, self.xT_ready = sc.sem("xn_ready"), sc.sem("xT_done"), sc.sem("xT_ready")

    def dve(self, j):
        nc = self.nc
        for p in range(TPG):
            n = j * TPG + p
            if self.shift is None:
                last = nc.vector.tensor_scalar(self.xn[:, p, :], self.src[:, n, :], self.scale[:, bass.ds(n, 1)], None,
                                               ALU.mult)
            else:
                last = nc.vector.tensor_scalar(self.xn[:, p, :], self.src[:, n, :], self.scale[:, bass.ds(n, 1)],
                                               self.shift[:, bass.ds(n, 1)], ALU.mult, ALU.add)
        last.then_inc(self.xn_ready, 1)

    def pe(self, pe, j):
        pe.wait_ge(self.xn_ready, j + 1)
        for p in range(TPG):
            last = self.nc.tensor.transpose(self.bank[:, p * P:(p + 1) * P], self.xn[:, p, :], self.C.ident[:])
        last.then_inc(self.xT_done, 1)

    def act(self, act, j):
        act.wait_ge(self.xT_done, j + 1)
        self.nc.scalar.activation(self.xnT[:], self.bank[:], ACT.Copy).then_inc(self.xT_ready, 1)


def group_stats(nc, dve, C, src, st, mv, i):
    for p in range(TPG):
        nc.vector.bn_stats(st[:, p, :], src[:, i * TPG + p, :])
    dve.drain()
    for p in range(TPG):
        nc.vector.bn_aggr(mv[:, p, :], st[:, p, :])
    dve.drain()
    nc.vector.tensor_copy(C.MV[:, bass.ds(i * TPG, TPG), :], mv[:])


def rows(t, i):
    return t[:, bass.ds(i * TPG, TPG), :]


def affine_norm(C, name, gamma_d, beta_d):
    nc = C.nc
    with ExitStack() as ctx:
        sc = Scope(nc, ctx, name)
        gamma, beta = sc.sb("gamma", [P, D]), sc.sb("beta", [P, D])
        y = sc.sb("y", [P, TPG, D])
        st, mv = sc.sb("st", [P, TPG, 6]), sc.sb("mv", [P, TPG, 2])
        loaded = sc.sem("loaded")
        block = ctx.enter_context(nc.Block())

        @block.sync
        def _(sp):
            sp.dma_start(gamma[:], gamma_d[:]).then_inc(loaded, 16)
            sp.dma_start(beta[:], beta_d[:]).then_inc(loaded, 16)

        @block.vector
        def _(dve):
            dve.wait_ge(loaded, 32)
            with dve.Fori(0, C.NG) as i:
                for p in range(TPG):
                    n = i * TPG + p
                    nc.vector.tensor_scalar(y[:, p, :], C.Y[:, n, :], C.RS2[:, bass.ds(n, 1)], C.NM2[:, bass.ds(n, 1)],
                                            ALU.mult, ALU.add)
                dve.drain()
                nc.vector.tensor_tensor(y[:], y[:], bc(gamma[:].unsqueeze(1), [P, TPG, D]), ALU.mult)
                dve.drain()
                nc.vector.tensor_tensor(y[:], y[:], bc(beta[:].unsqueeze(1), [P, TPG, D]), ALU.add)
                dve.drain()
                nc.vector.tensor_tensor(rows(C.X, i), rows(C.X, i), y[:], ALU.add)
                dve.drain()
                group_stats(nc, dve, C, C.X, st, mv, i)
                dve.drain()


def gated_ffn(C, name, W):
    nc = C.nc
    F = W["w1"].shape[1]
    chunks = [(f, min(P, F - f)) for f in range(0, F, P)]
    NF = len(chunks)
    with ExitStack() as ctx:
        sc = Scope(nc, ctx, name)
        sb, ps, sem = sc.sb, sc.ps, sc.sem
        w1, w2, w3 = sb("w1", [P, F]), sb("w2", [P, F]), sb("w3", [P, NF, D])
        g = sb("g", [P, 1])
        act_b, hid = sb("act", [P, NF, GT]), sb("hid", [P, NF, GT])
        st, mv = sb("st", [P, TPG, 6]), sb("mv", [P, TPG, 2])
        ps_j, ps_o = ps("ps_j", [P, GT]), ps("ps_o", [P, GT])
        ps_u, ps_v = ps("ps_u", [P, NF, GT]), ps("ps_v", [P, NF, GT])
        fr = Front(C, sc, ps_j, C.Y, C.RS2, None)
        loaded, folded = sem("loaded"), sem("folded")
        gate_done, up_done, gated, hidden = sem("gate_done"), sem("up_done"), sem("gated"), sem("hidden")
        out_done, out_read = sem("out_done"), sem("out_read")
        block = ctx.enter_context(nc.Block())

        @block.sync
        def _(sp):
            for to, of in ((w1[:], W["w1"]), (w2[:], W["w2"]), (g[:], W["g"])):
                sp.dma_start(to, of).then_inc(loaded, 16)
            for c, (f, n) in enumerate(chunks):
                sp.dma_start(w3[0:n, c, :], W["w3"][f:f + n, :]).then_inc(loaded, 16)

        n_loaded = 16 * (3 + NF)

        @block.tensor
        def _(pe):
            pe.wait_ge(loaded, n_loaded)
            pe.wait_ge(folded, 1)
            fr.pe(pe, 0)
            with pe.Fori(0, C.NG) as i:
                pe.wait_ge(fr.xT_ready, i + 1)
                for w, to, done in ((w1, ps_u, gate_done), (w2, ps_v, up_done)):
                    for c, (f, n) in enumerate(chunks):
                        nc.tensor.matmul(to[0:n, c, :], w[:, f:f + n], fr.xnT[:], start=True,
                                         stop=True).then_inc(done, 1)
                fr.pe(pe, i + 1)
                pe.wait_ge(out_read, i + 1)
                pe.wait_ge(hidden, i * NF + NF)
                for p in range(TPG):
                    for c, (f, n) in enumerate(chunks):
                        last = nc.tensor.matmul(ps_o[:, p * D:(p + 1) * D], hid[0:n, c, p * P:(p + 1) * P],
                                                w3[0:n, c, :], start=(c == 0), stop=(c == NF - 1))
                last.then_inc(out_done, 1)

        @block.scalar
        def _(act):
            fr.act(act, 0)
            with act.Fori(0, C.NG) as i:
                for c, (f, n) in enumerate(chunks):
                    act.wait_ge(gate_done, i * NF + c + 1)
                    nc.scalar.activation(act_b[0:n, c, :], ps_u[0:n, c, :], ACT.Silu).then_inc(gated, 1)
                fr.act(act, i + 1)

        @block.vector
        def _(dve):
            dve.wait_ge(loaded, n_loaded)
            nc.vector.tensor_scalar(w1[:], w1[:], g[:, 0:1], None, ALU.mult)
            nc.vector.tensor_scalar(w2[:], w2[:], g[:, 0:1], None, ALU.mult).then_inc(folded, 1)
            nc.vector.memset(mv[:], 0.0).then_inc(out_read, 1)
            fr.dve(0)
            with dve.Fori(0, C.NG) as i:
                dve.wait_ge(fr.xT_done, i + 1)
                fr.dve(i + 1)
                nc.vector.tensor_tensor(rows(C.X, i), rows(C.X, i), rows(C.Y, i), ALU.add)
                for c, (f, n) in enumerate(chunks):
                    dve.wait_ge(up_done, i * NF + c + 1)
                    dve.wait_ge(gated, i * NF + c + 1)
                    nc.vector.tensor_tensor(hid[0:n, c, :], act_b[0:n, c, :], ps_v[0:n, c, :],
                                            ALU.mult).then_inc(hidden, 1)
                dve.wait_ge(out_done, i + 1)
                nc.vector.tensor_tensor(rows(C.X, i), ps_o[:].rearrange("p (t d) -> p t d", d=D), rows(C.X, i),
                                        ALU.add).then_inc(out_read, 1)
                dve.drain()
                group_stats(nc, dve, C, C.X, st, mv, i)


NE = 8


def first_max(nc, dve, values, falling, onehot, best, place):
    wide = [P, TPG, NE]
    nc.vector.tensor_reduce(best[:], values, AX, ALU.max)
    dve.drain()
    nc.vector.tensor_tensor(onehot[:], values, bc(best[:].unsqueeze(2), wide), ALU.is_ge)
    dve.drain()
    nc.vector.tensor_tensor(onehot[:], onehot[:], bc(falling[:].unsqueeze(1), wide), ALU.mult)
    dve.drain()
    nc.vector.tensor_reduce(place[:], onehot[:], AX, ALU.max)
    dve.drain()
    nc.vector.tensor_tensor(onehot[:], onehot[:], bc(place[:].unsqueeze(2), wide), ALU.is_equal)
    dve.drain()


def lora_ffn(C, name, W):
    nc = C.nc
    F, R = W["wi"].shape[1], W["B"].shape[0]
    NF, RE = F // P, R // NE
    with ExitStack() as ctx:
        sc = Scope(nc, ctx, name)
        sb, ps, sem = sc.sb, sc.ps, sc.sem
        wi, wo, ga, lb = sb("wi", [P, F]), sb("wo", [P, NF, D]), sb("ga", [P, NE + R]), sb("lb", [R, F])
        gb, wib, wob, falling = sb("gb", [P, NE]), sb("wib", [P, NF]), sb("wob", [1, D]), sb("falling", [P, NE])
        logits, onehot = sb("logits", [P, TPG, NE]), sb("onehot", [P, TPG, NE])
        best, place = sb("best", [P, TPG]), sb("place", [P, TPG])
        low, lowT = sb("low", [P, TPG, R]), sb("lowT", [R, GT])
        hid = sb("hid", [P, NF, GT])
        st, mv = sb("st", [P, TPG, 6]), sb("mv", [P, TPG, 2])
        ps_j, ps_o = ps("ps_j", [P, GT]), ps("ps_o", [P, GT])
        ps_g, ps_l, ps_h = ps("ps_g", [P, TPG, NE + R]), ps("ps_l", [R, GT]), ps("ps_h", [P, NF, GT])
        fr = Front(C, sc, ps_j, C.X, C.RS, C.NM)
        loaded = sem("loaded")
        gate_done, low_ready, lowT_done, lowT_ready = (sem(n) for n in ("gate_done", "low_ready", "lowT_done", "lowT_ready"))
        hid_done, hid_ready, out_done, out_read = (sem(n) for n in ("hid_done", "hid_ready", "out_done", "out_read"))
        block = ctx.enter_context(nc.Block())
        loads = [(wi[:], W["wi"]), (wo[:], W["wo"].rearrange("(c p) d -> p c d", p=P)), (ga[:], W["ga"]), (lb[:], W["B"]),
                 (gb[:], W["gb"]), (wib[:], W["wib"]), (wob[:], W["wob"]), (falling[:], W["falling"])]
        n_loaded = 16 * len(loads)

        @block.sync
        def _(sp):
            for to, of in loads:
                sp.dma_start(to, of).then_inc(loaded, 16)

        @block.tensor
        def _(pe):
            pe.wait_ge(loaded, n_loaded)
            fr.pe(pe, 0)
            with pe.Fori(0, C.NG) as i:
                pe.wait_ge(fr.xT_ready, i + 1)
                for p in range(TPG):
                    last = nc.tensor.matmul(ps_g[:, p, :], fr.xnT[:, p * P:(p + 1) * P], ga[:], start=True, stop=True)
                last.then_inc(gate_done, 1)
                for c in range(NF):
                    nc.tensor.matmul(ps_h[:, c, :], wi[:, c * P:(c + 1) * P], fr.xnT[:], start=True, stop=False)
                pe.wait_ge(low_ready, i + 1)
                for p in range(TPG):
                    last = nc.tensor.transpose(ps_l[:, p * P:(p + 1) * P], low[:, p, :], C.ident[:])
                last.then_inc(lowT_done, 1)
                fr.pe(pe, i + 1)
                pe.wait_ge(lowT_ready, i + 1)
                for c in range(NF):
                    nc.tensor.matmul(ps_h[:, c, :], lb[:, c * P:(c + 1) * P], lowT[:], start=False,
                                     stop=True).then_inc(hid_done, 1)
                pe.wait_ge(out_read, i + 1)
                pe.wait_ge(hid_ready, i * NF + NF)
                for p in range(TPG):
                    o = ps_o[:, p * D:(p + 1) * D]
                    for c in range(NF):
                        nc.tensor.matmul(o, hid[:, c, p * P:(p + 1) * P], wo[:, c, :], start=(c == 0), stop=False)
                    last = nc.tensor.matmul(o, C.ones[0:1, :], wob[0:1, :], start=False, stop=True)
                last.then_inc(out_done, 1)

        @block.scalar
        def _(act):
            act.wait_ge(loaded, n_loaded)
            fr.act(act, 0)
            with act.Fori(0, C.NG) as i:
                act.wait_ge(lowT_done, i + 1)
                nc.scalar.activation(lowT[:], ps_l[:], ACT.Copy).then_inc(lowT_ready, 1)
                fr.act(act, i + 1)
                for c in range(NF):
                    act.wait_ge(hid_done, i * NF + c + 1)
                    nc.scalar.activation(hid[:, c, :], ps_h[:, c, :], ACT.Relu, bias=wib[:, c:c + 1]).then_inc(hid_ready, 1)

        @block.vector
        def _(dve):
            dve.wait_ge(loaded, n_loaded)
            nc.vector.memset(mv[:], 0.0).then_inc(out_read, 1)
            fr.dve(0)
            with dve.Fori(0, C.NG) as i:
                dve.wait_ge(gate_done, i + 1)
                nc.vector.tensor_tensor(logits[:], ps_g[:, :, 0:NE], bc(gb[:].unsqueeze(1), [P, TPG, NE]), ALU.add)
                dve.drain()
                first_max(nc, dve, logits[:], falling, onehot, best, place)
                for p in range(TPG):
                    last = nc.vector.tensor_tensor(low[:, p, :].rearrange("p (e r) -> p e r", r=RE),
                                                   ps_g[:, p, NE:].rearrange("p (e r) -> p e r", r=RE),
                                                   bc(onehot[:, p, :].unsqueeze(2), [P, NE, RE]), ALU.mult)
                last.then_inc(low_ready, 1)
                fr.dve(i + 1)
                dve.wait_ge(out_done, i + 1)
                nc.vector.tensor_tensor(rows(C.X, i), ps_o[:].rearrange("p (t d) -> p t d", d=D), rows(C.X, i),
                                        ALU.add).then_inc(out_read, 1)
                dve.drain()
                group_stats(nc, dve, C, C.X, st, mv, i)


def topk_ffn(C, name, W):
    nc = C.nc
    F = W["w1"].shape[2]
    NF = F // P
    with ExitStack() as ctx:
        sc = Scope(nc, ctx, name)
        sb, ps, sem = sc.sb, sc.ps, sc.sem
        w1, w2, wr = sb("w1", [P, NE, F]), sb("w2", [P, NE, NF, D]), sb("wr", [P, NE])
        falling = sb("falling", [P, NE])
        prob, rest = sb("prob", [P, TPG, NE]), sb("rest", [P, TPG, NE])
        one1, one2 = sb("one1", [P, TPG, NE]), sb("one2", [P, TPG, NE])
        best1, best2, place, total = (sb(n, [P, TPG]) for n in ("best1", "best2", "place", "total"))
        cw = sb("cw", [P, TPG, NE])
        hid = sb("hid", [P, 2, NF, GT])
        acc = sb("acc", [P, TPG, D])
        st, mv = sb("st", [P, TPG, 6]), sb("mv", [P, TPG, 2])
        ps_j = ps("ps_j", [P, GT])
        ps_g = ps("ps_g", [P, TPG, NE])
        ps_h, ps_o = ps("ps_h", [P, 2, NF, GT]), ps("ps_o", [P, 2, GT])
        fr = Front(C, sc, ps_j, C.X, C.RS, C.NM)
        loaded = sem("loaded")
        gate_done, shifted, exped = sem("gate_done"), sem("shifted"), sem("exped")
        hid_done, hid_ready, out_done, out_read = (sem(n) for n in ("hid_done", "hid_ready", "out_done", "out_read"))
        block = ctx.enter_context(nc.Block())
        loads = [(w1[:], W["w1"].rearrange("e d f -> d e f")),
                 (wr[:], W["wr"]), (falling[:], W["falling"])]
        loads += [(w2[:, e, :, :], W["w2"][e].rearrange("(c p) d -> p c d", p=P)) for e in range(NE)]
        n_loaded = 16 * len(loads)

        @block.sync
        def _(sp):
            for to, of in loads:
                sp.dma_start(to, of).then_inc(loaded, 16)

        @block.tensor
        def _(pe):
            pe.wait_ge(loaded, n_loaded)

            def expert_in(i, e):
                if e >= 2:
                    pe.wait_ge(hid_ready, i * NE + e - 1)
                for c in range(NF):
                    last = nc.tensor.matmul(ps_h[:, e % 2, c, :], w1[:, e, c * P:(c + 1) * P], fr.xnT[:],
                                            start=True, stop=True)
                last.then_inc(hid_done, 1)

            def expert_out(i, e):
                pe.wait_ge(hid_ready, i * NE + e + 1)
                pe.wait_ge(out_read, i * NE + e + 1)
                for p in range(TPG):
                    for c in range(NF):
                        last = nc.tensor.matmul(ps_o[:, e % 2, p * D:(p + 1) * D], hid[:, e % 2, c, p * P:(p + 1) * P],
                                                w2[:, e, c, :], start=(c == 0), stop=(c == NF - 1))
                last.then_inc(out_done, 1)

            fr.pe(pe, 0)
            with pe.Fori(0, C.NG) as i:
                pe.wait_ge(fr.xT_ready, i + 1)
                for p in range(TPG):
                    last = nc.tensor.matmul(ps_g[:, p, :], fr.xnT[:, p * P:(p + 1) * P], wr[:], start=True, stop=True)
                last.then_inc(gate_done, 1)
                expert_in(i, 0)
                for e in range(NE):
                    if e + 1 < NE:
                        expert_in(i, e + 1)
                    else:
                        fr.pe(pe, i + 1)
                    expert_out(i, e)

        @block.scalar
        def _(act):
            fr.act(act, 0)
            with act.Fori(0, C.NG) as i:
                act.wait_ge(shifted, i + 1)
                nc.scalar.activation(prob[:], prob[:], ACT.Exp).then_inc(exped, 1)
                for e in range(NE):
                    act.wait_ge(hid_done, i * NE + e + 1)
                    if e >= 2:
                        act.wait_ge(out_done, i * NE + e - 1)
                    nc.scalar.activation(hid[:, e % 2, :, :], ps_h[:, e % 2, :, :], ACT.Silu).then_inc(hid_ready, 1)
                fr.act(act, i + 1)

        @block.vector
        def _(dve):
            dve.wait_ge(loaded, n_loaded)
            nc.vector.memset(mv[:], 0.0).then_inc(out_read, 1)
            nc.vector.memset(st[:], 0.0).then_inc(out_read, 1)
            fr.dve(0)
            wide = [P, TPG, NE]
            over = lambda t: bc(t[:].unsqueeze(2), wide)
            with dve.Fori(0, C.NG) as i:
                dve.wait_ge(gate_done, i + 1)
                nc.vector.tensor_reduce(best1[:], ps_g[:], AX, ALU.max)
                dve.drain()
                nc.vector.tensor_tensor(prob[:], ps_g[:], over(best1), ALU.subtract).then_inc(shifted, 1)
                dve.wait_ge(fr.xT_done, i + 1)
                fr.dve(i + 1)
                dve.wait_ge(exped, i + 1)
                nc.vector.tensor_reduce(total[:], prob[:], AX, ALU.add)
                dve.drain()
                nc.vector.reciprocal(total[:], total[:])
                dve.drain()
                nc.vector.tensor_tensor(prob[:], prob[:], over(total), ALU.mult)
                dve.drain()
                first_max(nc, dve, prob[:], falling, one1, best1, place)
                nc.vector.scalar_tensor_tensor(rest[:], one1[:], -2.0, prob[:], ALU.mult, ALU.add)
                dve.drain()
                first_max(nc, dve, rest[:], falling, one2, best2, place)
                nc.vector.tensor_tensor(total[:], best1[:], best2[:], ALU.add)
                dve.drain()
                nc.vector.tensor_scalar(total[:], total[:], 1e-9, None, ALU.max)
                dve.drain()
                nc.vector.reciprocal(total[:], total[:])
                nc.vector.tensor_tensor(one1[:], one1[:], one2[:], ALU.add)
                dve.drain()
                nc.vector.tensor_tensor(cw[:], prob[:], over(total), ALU.mult)
                dve.drain()
                nc.vector.tensor_tensor(cw[:], cw[:], one1[:], ALU.mult)
                dve.drain()
                for e in range(NE):
                    dve.wait_ge(out_done, i * NE + e + 1)
                    for p in range(TPG):
                        o = ps_o[:, e % 2, p * D:(p + 1) * D]
                        before = C.X[:, i * TPG + p, :] if e == 0 else acc[:, p, :]
                        to = C.X[:, i * TPG + p, :] if e == NE - 1 else acc[:, p, :]
                        last = nc.vector.scalar_tensor_tensor(to, o, cw[:, p, e:e + 1], before, ALU.mult, ALU.add)
                    last.then_inc(out_read, 1)
                    dve.drain()



HW = 64
UH = 8
NJ = UH // 2


def attn64(C, name, W, groups_of_heads, q_per_kv, kT_dram=None):
    nc = C.nc
    HG, NK = groups_of_heads, NJ // q_per_kv
    KH = HG * NK
    chunks = [("q", c) for c in range(HG * NJ)] + [("k", c) for c in range(KH)] + [("v", s) for s in range(SPG)]
    NC_ = len(chunks)
    UPI = UPG * HG
    cross = kT_dram is not None
    with ExitStack() as ctx:
        sc = Scope(nc, ctx, name)
        sb, ps, sem = sc.sb, sc.ps, sc.sem
        wq, wk, wv = sb("wq", [P, HG * NJ, P]), sb("wk", [P, KH, P]), sb("wv", [P, 2, KH * HW])
        wo = sb("wo", [P, HG * NJ, D])
        bo = sb("bo", [1, D])
        if not cross:
            table = sb("table", [P, HG, UH, S])
        kvb = sb("kvb", [P, GT]) if cross else None
        qT, kT = sb("qT", [P, HG * NJ, GT]), sb("kT", [P, KH, GT])
        val = sb("val", [P, SPG, KH, HW])
        s1 = sb("s1", [P, 2, UT, UH, S])
        mx, den = sb("mx", [P, UT, UH]), sb("den", [P, UT, UH])
        pT, oT = sb("pT", [P, UT, NJ, P]), sb("oT", [P, UT, NJ, P])
        st, mv = sb("st", [P, TPG, 6]), sb("mv", [P, TPG, 2])
        ps_s, ps_t, ps_o = ps("ps_s", [P, 2, GT]), ps("ps_t", [P, UT, GT]), ps("ps_o", [P, UT, GT])
        ps_out, ps_j = ps("ps_out", [P, UT, D]), ps("ps_j", [P, GT])
        fr = Front(C, sc, ps_j, C.X, C.RS, C.NM)
        if not cross:
            kvb = fr.xnT
        loaded, kv_loaded = sem("loaded"), sem("kv_loaded")
        proj_done, act_taken, dve_taken = sem("proj_done"), sem("act_taken"), sem("dve_taken")
        scores_done, scores_read, shifted, exped, probs = (
            sem(n) for n in ("scores_done", "scores_read", "shifted", "exped", "probs"))
        pT_done, pT_ready, oT_done, oT_ready = (sem(n) for n in ("pT_done", "pT_ready", "oT_done", "oT_ready"))
        out_done, out_read = sem("out_done"), sem("out_read")
        begun = sem("begun")
        block = ctx.enter_context(nc.Block())
        loads = [(wq[:], W["wq"]), (wk[:], W["wk"]), (wv[:], W["wv"]), (wo[:], W["wo"])]
        loads += [(bo[:], W["bo"])] if cross else [(table[:], W["table"])]
        n_loaded = 16 * len(loads)

        def bank(c):
            return (ps_s, ps_t)[c % 4 // 2][:, c % 2, :]

        @block.sync
        def _(sp):
            for to, of in loads:
                sp.dma_start(to, of).then_inc(loaded, 16)
            if cross:
                sp.dma_start(kvb[:], kT_dram[:, 0:GT]).then_inc(kv_loaded, 16)
                with sp.Fori(1, C.NG) as i:
                    sp.wait_ge(proj_done, i * NC_)
                    sp.dma_start(kvb[:], kT_dram[:, bass.ds(i * GT, GT)]).then_inc(kv_loaded, 16)

        @block.tensor
        def _(pe):
            pe.wait_ge(loaded, n_loaded)

            def hold(pe):
                pe.sem_inc(begun, 1)

            def project(i, c):
                kind, n = chunks[c]
                if c >= 4:
                    pe.wait_ge(dve_taken if c % 2 else act_taken, i * (NC_ // 2) + (c - 4) // 2 + 1)
                if kind == "q":
                    last = nc.tensor.matmul(bank(c), wq[:, n, :], fr.xnT[:], start=True, stop=True)
                elif kind == "k":
                    last = nc.tensor.matmul(bank(c), wk[:, n, :], kvb[:], start=True, stop=True)
                else:
                    for half in range(2):
                        last = nc.tensor.matmul(bank(c)[HW * half:HW * half + HW, 0:KH * HW],
                                                kvb[:, n * S:(n + 1) * S], wv[:, half, :], start=True, stop=True)
                last.then_inc(proj_done, 1)

            def queries_keys(i, x):
                u, hg = x // HG, x % HG
                if not cross:
                    pe.wait_ge(scores_read, i * UPI + x + 1)
                elif x > 0:
                    pe.wait_ge(shifted, i * UPI + x)
                hold(pe)
                for t in range(UT):
                    for b in range(2):
                        q = 2 * (UT * u + t) + b
                        cols = slice(q * S, q * S + S)
                        for j in range(NJ):
                            for half in range(2):
                                r = slice(HW * half, HW * half + HW)
                                last = nc.tensor.matmul(
                                    ps_s[S * b:S * b + S, half, (t * NJ + j) * S:(t * NJ + j + 1) * S],
                                    qT[r, hg * NJ + j, cols], kT[r, hg * NK + j // q_per_kv, cols], start=True, stop=True)
                last.then_inc(scores_done, 1)

            def turn_probs(i, x):
                pe.wait_ge(probs, i * UPI + x + 1)
                for t in range(UT):
                    for j in range(NJ):
                        last = nc.tensor.transpose(ps_t[:, t, j * P:(j + 1) * P], 
                                               s1[:, x % 2, t, 2 * j:2 * j + 2, :].rearrange("p a k -> p (a k)"), C.ident[:])
                last.then_inc(pT_done, 1)

            def weigh_values(i, x):
                u, hg = x // HG, x % HG
                pe.wait_ge(pT_ready, i * UPI + x + 1)
                hold(pe)
                for t in range(UT):
                    for b in range(2):
                        q = 2 * (UT * u + t) + b
                        for k in range(NK):
                            for half in range(2):
                                r = slice(HW * half, HW * half + HW)
                                js = slice(k * q_per_kv, (k + 1) * q_per_kv)
                                last = nc.tensor.matmul(
                                    ps_o[r, t, :].rearrange("p (j q) -> p j q", q=P)[:, js, S * b:S * b + S],
                                    val[r, q, hg * NK + k, :], pT[r, t, js, S * b:S * b + S], start=True, stop=True)
                last.then_inc(oT_done, 1)

            def project_output(i, x):
                u, hg = x // HG, x % HG
                pe.wait_ge(oT_ready, i * UPI + x + 1)
                if hg == 0:
                    pe.wait_ge(out_read, i * UPG + u + 1)
                for t in range(UT):
                    for j in range(NJ):
                        end = hg == HG - 1 and j == NJ - 1
                        last = nc.tensor.matmul(ps_out[:, t, :], oT[:, t, j, :], wo[:, hg * NJ + j, :],
                                                start=hg == 0 and t == 0 and j == 0,
                                                stop=end and not cross, skip_group_check=True)
                    if cross and hg == HG - 1:
                        last = nc.tensor.matmul(ps_out[:, t, :], C.ones[0:1, :], bo[0:1, :], start=False, stop=True,
                                                skip_group_check=True)
                if hg == HG - 1:
                    last.then_inc(out_done, 1)

            fr.pe(pe, 0)
            with pe.Fori(0, C.NG) as i:
                pe.wait_ge(fr.xT_ready, i + 1)
                if cross:
                    pe.wait_ge(kv_loaded, i * 16 + 16)
                for c in range(NC_):
                    project(i, c)
                for taken in (act_taken, dve_taken):
                    pe.wait_ge(taken, i * (NC_ // 2) + NC_ // 2)
                queries_keys(i, 0)
                for x in range(UPI):
                    if x + 1 < UPI:
                        queries_keys(i, x + 1)
                    else:
                        fr.pe(pe, i + 1)
                    turn_probs(i, x)
                    if x > 0:
                        project_output(i, x - 1)
                    weigh_values(i, x)
                project_output(i, UPI - 1)

        def take(eng, copy, scaled, i, odd):
            for c in range(odd, NC_, 2):
                kind, n = chunks[c]
                eng.wait_ge(proj_done, i * NC_ + c + 1)
                if kind == "q":
                    last = scaled(qT[:, n, :], bank(c))
                elif kind == "k":
                    last = copy(kT[:, n, :], bank(c))
                else:
                    last = copy(val[:, n, :, :].rearrange("p k d -> p (k d)"), bank(c)[:, 0:KH * HW])
                last.then_inc(dve_taken if odd else act_taken, 1)

        @block.scalar
        def _(act):
            act_copy = lambda to, of: nc.scalar.activation(to, of, ACT.Copy)
            act_scaled = lambda to, of: nc.scalar.activation(to, of, ACT.Copy, scale=HW ** -0.5)

            def output_copy(i, x):
                act.wait_ge(oT_done, i * UPI + x + 1)
                nc.scalar.activation(oT[:].rearrange("p t j q -> p t (j q)"), ps_o[:], ACT.Copy).then_inc(oT_ready, 1)

            fr.act(act, 0)
            with act.Fori(0, C.NG) as i:
                take(act, act_copy, act_scaled, i, 0)
                for x in range(UPI):
                    act.wait_ge(shifted, i * UPI + x + 1)
                    nc.scalar.activation(s1[:, x % 2, :, :, :], s1[:, x % 2, :, :, :], ACT.Exp).then_inc(exped, 1)
                    if x > 0:
                        output_copy(i, x - 1)
                    if x == UPI - 1:
                        fr.act(act, i + 1)
                    act.wait_ge(pT_done, i * UPI + x + 1)
                    nc.scalar.activation(pT[:].rearrange("p t j q -> p t (j q)"), ps_t[:], ACT.Copy).then_inc(pT_ready, 1)
                output_copy(i, UPI - 1)

        @block.vector
        def _(dve):
            dve_copy = nc.vector.tensor_copy
            dve_scaled = lambda to, of: nc.vector.tensor_scalar(to, of, HW ** -0.5, None, ALU.mult)
            dve.wait_ge(loaded, n_loaded)
            nc.vector.memset(mx[:], 0.0).then_inc(scores_read, 1)
            nc.vector.memset(mv[:], 0.0).then_inc(out_read, 1)

            def shift(i, x):
                w, out = i * UPI + x, s1[:, x % 2, :, :, :]
                raw = ps_s[:].rearrange("p a (t j k) -> p t a j k", t=UT, k=S)
                halves = out.rearrange("p t (j a) k -> p t a j k", a=2)
                most = mx[:].rearrange("p t (j a) -> p t a j", a=2)
                dve.wait_ge(scores_done, w + 1)
                if not cross:
                    for t in range(UT):
                        last = nc.vector.tensor_tensor(halves[:, t, :, :, :], raw[:, t, :, :, :],
                                                       table[:, x % HG, :, :].rearrange("p (a j) k -> p a j k", a=2), ALU.add)
                    last.then_inc(scores_read, 1)
                    dve.drain()
                    nc.vector.tensor_reduce(mx[:], out, AX, ALU.max)
                    dve.drain()
                    nc.vector.tensor_tensor(out, out, bc(mx[:].unsqueeze(3), [P, UT, UH, S]),
                                            ALU.subtract).then_inc(shifted, 1)
                else:
                    for t in range(UT):
                        nc.vector.tensor_reduce(most[:, t, :, :], raw[:, t, :, :, :], AX, ALU.max)
                    dve.drain()
                    for t in range(UT):
                        last = nc.vector.tensor_tensor(
                            halves[:, t, :, :, :], raw[:, t, :, :, :],
                            bc(most[:, t, :, :].unsqueeze(3), [P, 2, NJ, S]), ALU.subtract)
                    last.then_inc(shifted, 1)

            def normalise(i, x):
                out = s1[:, x % 2, :, :, :]
                dve.wait_ge(exped, i * UPI + x + 1)
                nc.vector.tensor_reduce(den[:], out, AX, ALU.add)
                dve.drain()
                nc.vector.reciprocal(den[:], den[:])
                dve.drain()
                nc.vector.tensor_tensor(out, out, bc(den[:].unsqueeze(3), [P, UT, UH, S]), ALU.mult).then_inc(probs, 1)

            def residual(i, u):
                dve.wait_ge(out_done, i * UPG + u + 1)
                to = C.X[:, bass.ds(i * TPG + u * UT, UT), :]
                nc.vector.tensor_tensor(to, ps_out[:], to, ALU.add).then_inc(out_read, 1)

            fr.dve(0)
            with dve.Fori(0, C.NG) as i:
                take(dve, dve_copy, dve_scaled, i, 1)
                shift(i, 0)
                for x in range(UPI):
                    if x + 1 < UPI:
                        shift(i, x + 1)
                    else:
                        fr.dve(i + 1)
                    normalise(i, x)
                    if x % HG == 0 and x > 0:
                        residual(i, x // HG - 1)
                residual(i, UPG - 1)
                dve.drain()
                group_stats(nc, dve, C, C.X, st, mv, i)



NST = 2
CYCLES, LAYERS = 3, 4


def coupled_ffn(C, name, W):
    nc = C.nc
    widths = [D, D, D // 2, D // 4, D]
    gwidths = [D, D // 2, D // 4, D]
    with ExitStack() as ctx:
        sc = Scope(nc, ctx, name)
        sb, ps, sem = sc.sb, sc.ps, sc.sem
        w = [sb(f"w{n}", [widths[n], widths[n + 1]]) for n in range(LAYERS)]
        b = [sb(f"b{n}", [widths[n + 1], 1]) for n in range(LAYERS)]
        gw = [sb(f"gw{n}", [gwidths[n], gwidths[n + 1]]) for n in range(3)]
        gb = [sb(f"gb{n}", [gwidths[n + 1], 1]) for n in range(3)]
        perm, reach = sb("perm", [P, P]), sb("reach", [P, 1])
        reach2, offset = sb("reach2", [P, 1]), sb("offset", [P, 1])
        xn = sb("xn", [P, NST * TPG, D])
        cur, h, tf = sb("cur", [P, NST, GT]), sb("h", [P, NST, GT]), sb("tf", [P, NST, GT])
        mean, gh, gf = sb("mean", [P, NST, SPG]), sb("gh", [P, NST * SPG]), sb("gf", [P, NST, SPG])
        st, mv = sb("st", [P, TPG, 6]), sb("mv", [P, TPG, 2])
        ps_j, ps_g = ps("ps_j", [P, GT]), ps("ps_g", [P, 512])
        ps_c, ps_w, ps_b = ps("ps_c", [P, NST, GT]), ps("ps_w", [P, NST, GT]), ps("ps_b", [P, NST, GT])
        loaded, prepared = sem("loaded"), sem("prepared")
        xn_ready, xT_done, cur_ready, mean_ready = (sem(n) for n in ("xn_ready", "xT_done", "cur_ready", "mean_ready"))
        g_done, g_act = sem("g_done"), sem("g_act")
        l_done, l_act, tw_done, updated = sem("l_done"), sem("l_act"), sem("tw_done"), sem("updated")
        back_done = sem("back_done")
        begun = sem("begun")
        block = ctx.enter_context(nc.Block())
        loads = [(t[:], W[k]) for k, t in
                 [(f"w{n}", w[n]) for n in range(4)] + [(f"b{n}", b[n]) for n in range(4)]
                 + [(f"gw{n}", gw[n]) for n in range(3)] + [(f"gb{n}", gb[n]) for n in range(3)]
                 + [("perm", perm), ("reach", reach)]]
        n_loaded = 16 * len(loads)
        NL = CYCLES * LAYERS * NST

        @block.sync
        def _(sp):
            for to, of in loads:
                sp.dma_start(to, of).then_inc(loaded, 16)

        def step(c, l, k):
            return (c * LAYERS + l) * NST + k + 1

        @block.tensor
        def _(pe):
            pe.wait_ge(loaded, n_loaded)

            def hold(rows_in):
                if rows_in == S:
                    pe.sem_inc(begun, 1)

            with pe.Fori(0, C.NG // NST) as i:
                pe.wait_ge(xn_ready, i + 1)
                for k in range(NST):
                    if k:
                        pe.wait_ge(cur_ready, i * NST + k)
                    for p in range(TPG):
                        last = nc.tensor.transpose(ps_j[:, p * P:(p + 1) * P], xn[:, k * TPG + p, :], C.ident[:])
                    last.then_inc(xT_done, 1)
                for c in range(CYCLES):
                    for l in range(LAYERS):
                        for k in range(NST):
                            if l:
                                pe.wait_ge(l_act, i * NL + step(c, l - 1, k))
                            elif c:
                                pe.wait_ge(updated, i * CYCLES * NST + (c - 1) * NST + k + 1)
                            else:
                                pe.wait_ge(cur_ready, i * NST + k + 1)
                            hold(widths[l])
                            rhs = h[0:widths[l], k, :] if l else cur[:, k, :]
                            nc.tensor.matmul(ps_c[0:widths[l + 1], k, :], w[l][:], rhs, start=True,
                                             stop=True).then_inc(l_done, 1)
                            if l == 0:
                                nc.tensor.matmul(ps_w[:, k, :], perm[:], cur[:, k, :], start=True,
                                                 stop=True).then_inc(tw_done, 1)
                        if c == 0 and l < 3:
                            if l == 0:
                                pe.wait_ge(mean_ready, i + 1)
                            else:
                                pe.wait_ge(g_act, i * 3 + l)
                            hold(gwidths[l])
                            rhs = gh[0:gwidths[l], :] if l else mean[:].rearrange("p k s -> p (k s)")
                            nc.tensor.matmul(ps_g[0:gwidths[l + 1], 0:NST * SPG], gw[l][:], rhs, start=True,
                                             stop=True).then_inc(g_done, 1)
                for k in range(NST):
                    pe.wait_ge(updated, i * CYCLES * NST + (CYCLES - 1) * NST + k + 1)
                    for p in range(TPG):
                        last = nc.tensor.transpose(ps_b[:, k, p * P:(p + 1) * P], cur[:, k, p * P:(p + 1) * P], C.ident[:])
                    last.then_inc(back_done, 1)

        @block.scalar
        def _(act):
            act.wait_ge(loaded, n_loaded)
            with act.Fori(0, C.NG // NST) as i:
                for k in range(NST):
                    act.wait_ge(xT_done, i * NST + k + 1)
                    nc.scalar.activation(cur[:, k, :], ps_j[:], ACT.Copy).then_inc(cur_ready, 1)
                for c in range(CYCLES):
                    for l in range(LAYERS):
                        n = widths[l + 1]
                        if c == 0 and l:
                            act.wait_ge(g_done, i * 3 + l)
                            m = gwidths[l]
                            to = gf[:].rearrange("p k s -> p (k s)") if l == 3 else gh[0:m, :]
                            nc.scalar.activation(to, ps_g[0:m, 0:NST * SPG], ACT.Sigmoid if l == 3 else ACT.Gelu,
                                                 bias=gb[l - 1][:, 0:1]).then_inc(g_act, 1)
                        for k in range(NST):
                            act.wait_ge(l_done, i * NL + step(c, l, k))
                            to, fn = (tf[:, k, :], ACT.Sigmoid) if l == 3 else (h[0:n, k, :], ACT.Gelu)
                            nc.scalar.activation(to, ps_c[0:n, k, :], fn, bias=b[l][:, 0:1]).then_inc(l_act, 1)

        @block.vector
        def _(dve):
            dve.wait_ge(loaded, n_loaded)
            nc.vector.tensor_scalar(reach2[:], reach[:], 2.0, None, ALU.mult)
            nc.vector.tensor_scalar(offset[:], reach[:], -1.0, 0.1, ALU.mult, ALU.add)
            nc.vector.memset(mv[:], 0.0)
            dve.drain()
            seqs = lambda t: t.rearrange("p (s n) -> p s n", n=S)
            with dve.Fori(0, C.NG // NST) as i:
                for p in range(NST * TPG):
                    n = i * NST * TPG + p
                    last = nc.vector.tensor_scalar(xn[:, p, :], C.X[:, n, :], C.RS[:, bass.ds(n, 1)],
                                                   C.NM[:, bass.ds(n, 1)], ALU.mult, ALU.add)
                last.then_inc(xn_ready, 1)
                for k in range(NST):
                    dve.wait_ge(cur_ready, i * NST + k + 1)
                    nc.vector.tensor_reduce(mean[:, k, :], seqs(cur[:, k, :]), AX, ALU.add)
                dve.drain()
                nc.vector.tensor_scalar(mean[:], mean[:], 1.0 / S, None, ALU.mult).then_inc(mean_ready, 1)
                dve.wait_ge(g_act, i * 3 + 3)
                nc.vector.tensor_scalar(gf[:], gf[:], 0.7, None, ALU.mult)
                dve.drain()
                for c in range(CYCLES):
                    for k in range(NST):
                        t = tf[:, k, :]
                        dve.wait_ge(l_act, i * NL + step(c, 3, k))
                        nc.vector.scalar_tensor_tensor(seqs(t), seqs(t), 0.3, bc(gf[:, k, :].unsqueeze(2), [P, SPG, S]),
                                                       ALU.mult, ALU.add)
                        dve.drain()
                        nc.vector.tensor_scalar(t, t, reach2[:, 0:1], offset[:, 0:1], ALU.mult, ALU.add)
                        dve.drain()
                        dve.wait_ge(tw_done, i * CYCLES * NST + c * NST + k + 1)
                        nc.vector.tensor_tensor(t, t, ps_w[:, k, :], ALU.mult)
                        dve.drain()
                        nc.vector.tensor_tensor(cur[:, k, :], cur[:, k, :], t, ALU.add).then_inc(updated, 1)
                for k in range(NST):
                    g = i * NST + k
                    dve.wait_ge(back_done, i * NST + k + 1)
                    nc.vector.tensor_tensor(rows(C.X, g), ps_b[:, k, :].rearrange("p (t d) -> p t d", d=D), rows(C.X, g),
                                            ALU.add)
                    dve.drain()
                    group_stats(nc, dve, C, C.X, st, mv, g)
                    dve.drain()



DI, NS, NTAP, DTR = 256, 16, 4, 8
NHF = DI // P
PADW = S + NTAP - 1


def mamba(C, name, W, first):
    nc = C.nc
    with ExitStack() as ctx:
        sc = Scope(nc, ctx, name)
        sb, ps, sem = sc.sb, sc.ps, sc.sem
        g, be = sb("g", [P, 1]), sb("be", [P, 1])
        in_w, taps = sb("in_w", [P, 2 * DI]), sb("taps", [P, NTAP, DI])
        conv_b, xp = sb("conv_b", [P, NHF]), sb("xp", [P, NHF, DTR + 2 * NS])
        dt_w, dt_b = sb("dt_w", [DTR, DI]), sb("dt_b", [P, NHF])
        A, Dp = sb("A", [P, NHF, NS]), sb("Dp", [P, NHF])
        diagD, out_w = sb("diagD", [P, NHF, P]), sb("out_w", [P, NHF, D])
        sel = sb("sel", [DTR + 2 * NS, 2 * NS, P])
        flip = sb("flip", [P, P])
        xn = sb("xn", [P, TPG, D])
        hT = sb("hT", [P, SPG, PADW])
        xs, sz = sb("xs", [P, NHF, GT]), sb("sz", [P, NHF, GT])
        dbl = sb("dbl", [DTR + 2 * NS, GT])
        pos, e, ln, q = (sb(n, [P, NHF, GT]) for n in ("pos", "e", "ln", "q"))
        dt, dtx = sb("dt", [P, NHF, GT]), sb("dtx", [P, NHF, GT])
        dA, dBx, hs = sb("dA", [P, 2, NHF, GT]), sb("dBx", [P, NHF, GT]), sb("hs", [P, NHF, GT])
        yc = sb("yc", [P, 2, NHF, GT])
        ps_B, ps_C, ps_y = ps("ps_B", [P, 2, GT]), ps("ps_C", [P, 2, GT]), ps("ps_y", [P, NHF, GT])
        ps_j, ps_k = ps("ps_j", [P, GT]), ps("ps_k", [P, GT])
        loaded, prepared = sem("loaded"), sem("prepared")
        xn_ready, xT_done, hT_ready = sem("xn_ready"), sem("xT_done"), sem("hT_ready")
        xs_done, z_done, xs_ready, z_ready = sem("xs_done"), sem("z_done"), sem("xs_ready"), sem("z_ready")
        dbl_done, dbl_ready, dt_done = sem("dbl_done"), sem("dbl_ready"), sem("dt_done")
        neg_ready, e_ready, ln_ready, dt_ready = sem("neg_ready"), sem("e_ready"), sem("ln_ready"), sem("dt_ready")
        B_done, C_done, B_read, decay = sem("B_done"), sem("C_done"), sem("B_read"), sem("decay")
        scanned, yc_ready, y_added = sem("scanned"), sem("yc_ready"), sem("y_added")
        y_ready, out_done, out_read, a_ready = sem("y_ready"), sem("out_done"), sem("out_read"), sem("a_ready")
        block = ctx.enter_context(nc.Block())
        loads = [(g, "g"), (be, "be"), (in_w, "in_w"), (taps, "taps"), (conv_b, "conv_b"), (xp, "xp"), (dt_w, "dt_w"),
                 (dt_b, "dt_b"), (A, "A"), (Dp, "D"), (out_w, "out_w"), (sel, "sel")]
        if not first:
            loads.append((flip, "flip"))
        n_loaded = 16 * len(loads)

        @block.sync
        def _(sp):
            for to, k in loads:
                sp.dma_start(to[:], W[k]).then_inc(loaded, 16)

        @block.gpsimd
        def _(pool):
            nc.gpsimd.memset(hT[:], 0.0).then_inc(prepared, 1)
            nc.gpsimd.memset(dA[:], 0.0).then_inc(prepared, 1)

        n_prepared = 3

        @block.tensor
        def _(pe):
            pe.wait_ge(loaded, n_loaded)
            pe.wait_ge(prepared, n_prepared)

            def turn(j):
                pe.wait_ge(xn_ready, j + 1)
                for p in range(TPG):
                    to = ps_k[:, p * P:(p + 1) * P]
                    if first:
                        last = nc.tensor.transpose(to, xn[:, p, :], C.ident[:])
                    else:
                        last = nc.tensor.matmul(to, xn[:, p, :], flip[:], start=True, stop=True)
                last.then_inc(xT_done, 1)

            def spread(s, i):
                if s >= 2:
                    pe.wait_ge(B_read, i * NS + s - 1)
                nc.tensor.matmul(ps_B[:, s % 2, :], sel[:, s, :], dbl[:], start=True, stop=True).then_inc(B_done, 1)
                if s >= 2:
                    pe.wait_ge(yc_ready, i * NS + s - 1)
                nc.tensor.matmul(ps_C[:, s % 2, :], sel[:, NS + s, :], dbl[:], start=True, stop=True).then_inc(C_done, 1)

            turn(0)
            with pe.Fori(0, C.NG) as i:
                pe.wait_ge(hT_ready, i + 1)
                for m in range(NHF):
                    for k in range(NTAP):
                        last = nc.tensor.matmul(ps_B[:, m, :], taps[:, k, m * P:(m + 1) * P], hT[:, :, k:k + S],
                                                start=k == 0, stop=k == NTAP - 1)
                    last.then_inc(xs_done, 1)
                for m in range(NHF):
                    nc.tensor.matmul(ps_C[:, m, :], in_w[:, DI + m * P:DI + (m + 1) * P], hT[:, :, NTAP - 1:], start=True,
                                     stop=True).then_inc(z_done, 1)
                pe.wait_ge(xs_ready, i * NHF + NHF)
                pe.wait_ge(out_read, i + 1)
                for m in range(NHF):
                    last = nc.tensor.matmul(ps_j[0:DTR + 2 * NS, :], xp[:, m, :], xs[:, m, :], start=m == 0, stop=m == NHF - 1)
                last.then_inc(dbl_done, 1)
                pe.wait_ge(dbl_ready, i + 1)
                for m in range(NHF):
                    last = nc.tensor.matmul(ps_y[:, m, :], dt_w[:, m * P:(m + 1) * P], dbl[0:DTR, :], start=True, stop=True)
                last.then_inc(dt_done, 1)
                pe.wait_ge(z_ready, i * NHF + NHF)
                spread(0, i)
                spread(1, i)
                turn(i + 1)
                for s in range(NS):
                    pe.wait_ge(yc_ready, i * NS + s + 1)
                    for m in range(NHF):
                        last = nc.tensor.matmul(ps_y[:, m, :], C.ident[:], yc[:, s % 2, m, :], start=s == 0, stop=False)
                    last.then_inc(y_added, 1)
                    if s + 2 < NS:
                        spread(s + 2, i)
                for m in range(NHF):
                    last = nc.tensor.matmul(ps_y[:, m, :], diagD[:, m, :], xs[:, m, :], start=False, stop=True)
                last.then_inc(y_added, 1)
                pe.wait_ge(y_ready, i + 1)
                for p in range(TPG):
                    for m in range(NHF):
                        last = nc.tensor.matmul(ps_j[:, p * D:(p + 1) * D], q[:, m, p * P:(p + 1) * P], out_w[:, m, :],
                                                start=m == 0, stop=m == NHF - 1)
                last.then_inc(out_done, 1)

        @block.scalar
        def _(act):
            act.wait_ge(loaded, n_loaded)
            nc.scalar.activation(A[:], A[:], ACT.Exp).then_inc(a_ready, 1)
            act.wait_ge(prepared, n_prepared)

            def copy_rows(j):
                act.wait_ge(xT_done, j + 1)
                nc.scalar.activation(hT[:, :, NTAP - 1:], ps_k[:].rearrange("p (s n) -> p s n", n=S), ACT.Identity,
                                     scale=g[:, 0:1], bias=be[:, 0:1]).then_inc(hT_ready, 1)

            copy_rows(0)
            with act.Fori(0, C.NG) as i:
                for m in range(NHF):
                    act.wait_ge(xs_done, i * NHF + m + 1)
                    nc.scalar.activation(xs[:, m, :], ps_B[:, m, :], ACT.Silu, bias=conv_b[:, m:m + 1]).then_inc(xs_ready, 1)
                for m in range(NHF):
                    act.wait_ge(z_done, i * NHF + m + 1)
                    nc.scalar.activation(sz[:, m, :], ps_C[:, m, :], ACT.Silu).then_inc(z_ready, 1)
                act.wait_ge(neg_ready, i + 1)
                nc.scalar.activation(e[:], e[:], ACT.Exp).then_inc(e_ready, 1)
                act.drain()
                nc.scalar.activation(ln[:], e[:], ACT.Ln, bias=1.0).then_inc(ln_ready, 1)
                act.wait_ge(dt_ready, i + 1)
                for s in range(NS):
                    if s >= 2:
                        act.wait_ge(scanned, i * NS + s - 1)
                    for m in range(NHF):
                        seqs = lambda t: t.rearrange("p (s n) -> p s n", n=S)[:, :, 1:]
                        last = nc.scalar.activation(seqs(dA[:, s % 2, m, :]), seqs(dt[:, m, :]), ACT.Exp,
                                                    scale=A[:, m, s:s + 1])
                    last.then_inc(decay, 1)
                    if s == 1:
                        copy_rows(i + 1)

        @block.vector
        def _(dve):
            dve.wait_ge(loaded, n_loaded)
            for k in range(NTAP):
                nc.vector.tensor_tensor(taps[:, k, :], taps[:, k, :], in_w[:, 0:DI], ALU.mult)
            for m in range(NHF):
                nc.vector.tensor_scalar(diagD[:, m, :], C.ident[:], Dp[:, m:m + 1], None, ALU.mult)
            nc.vector.memset(q[:], 0.0).then_inc(out_read, 1)
            dve.wait_ge(a_ready, 1)
            nc.vector.tensor_scalar(A[:], A[:], -1.0, None, ALU.mult).then_inc(prepared, 1)

            def normalise(j):
                for p in range(TPG):
                    n = j * TPG + p
                    last = nc.vector.tensor_scalar(xn[:, p, :], C.X[:, n, :], C.RS2[:, bass.ds(n, 1)],
                                                   C.NM2[:, bass.ds(n, 1)], ALU.mult, ALU.add)
                last.then_inc(xn_ready, 1)

            normalise(0)
            with dve.Fori(0, C.NG) as i:
                dve.wait_ge(dbl_done, i + 1)
                nc.vector.tensor_copy(dbl[:], ps_j[0:DTR + 2 * NS, :]).then_inc(dbl_ready, 1)
                normalise(i + 1)
                dve.wait_ge(dt_done, i + 1)
                for m in range(NHF):
                    nc.vector.tensor_scalar(pos[:, m, :], ps_y[:, m, :], dt_b[:, m:m + 1], 0.0, ALU.add, ALU.max)
                    nc.vector.tensor_scalar(e[:, m, :], ps_y[:, m, :], dt_b[:, m:m + 1], 0.0, ALU.add, ALU.min)
                dve.drain()
                nc.vector.tensor_tensor(e[:], e[:], pos[:], ALU.subtract).then_inc(neg_ready, 1)
                dve.wait_ge(e_ready, i + 1)
                nc.vector.tensor_scalar(q[:], e[:], 1.0, -1.0, ALU.add, ALU.add)
                dve.drain()
                dve.wait_ge(ln_ready, i + 1)
                nc.vector.scalar_tensor_tensor(ln[:], q[:], 0.0, ln[:], ALU.is_equal, ALU.add)
                nc.vector.scalar_tensor_tensor(dtx[:], q[:], 0.0, q[:], ALU.is_equal, ALU.add)
                dve.drain()
                nc.vector.reciprocal(dtx[:], dtx[:])
                nc.vector.tensor_tensor(ln[:], ln[:], e[:], ALU.mult)
                dve.drain()
                nc.vector.tensor_tensor(ln[:], ln[:], dtx[:], ALU.mult)
                dve.drain()
                nc.vector.tensor_tensor(dt[:], ln[:], pos[:], ALU.add).then_inc(dt_ready, 1)
                dve.drain()
                nc.vector.tensor_tensor(dtx[:], dt[:], xs[:], ALU.mult)
                dve.drain()
                for s in range(NS):
                    both = [P, NHF, GT]
                    dve.wait_ge(B_done, i * NS + s + 1)
                    nc.vector.tensor_tensor(dBx[:], dtx[:], bc(ps_B[:, s % 2, :].unsqueeze(1), both),
                                            ALU.mult).then_inc(B_read, 1)
                    dve.drain()
                    dve.wait_ge(decay, i * NS + s + 1)
                    flat = lambda t: t.rearrange("p m n -> p (m n)")
                    nc.vector.tensor_tensor_scan(flat(hs[:]), flat(dA[:, s % 2, :, :]), flat(dBx[:]), 0.0, ALU.mult,
                                                 ALU.add).then_inc(scanned, 1)
                    dve.drain()
                    if s >= 2:
                        dve.wait_ge(y_added, i * (NS + 1) + s - 1)
                    dve.wait_ge(C_done, i * NS + s + 1)
                    nc.vector.tensor_tensor(yc[:, s % 2, :, :], hs[:], bc(ps_C[:, s % 2, :].unsqueeze(1), both),
                                            ALU.mult).then_inc(yc_ready, 1)
                if first:
                    for p in range(TPG):
                        n = i * TPG + p
                        nc.vector.tensor_scalar(C.Y[:, n, :], C.X[:, n, :], C.RS[:, bass.ds(n, 1)],
                                                C.NM[:, bass.ds(n, 1)], ALU.mult, ALU.add)
                dve.wait_ge(y_added, (i + 1) * (NS + 1))
                nc.vector.tensor_tensor(q[:], sz[:], ps_y[:], ALU.mult).then_inc(y_ready, 1)
                dve.drain()
                dve.wait_ge(out_done, i + 1)
                nc.vector.tensor_tensor(rows(C.Y, i), ps_j[:].rearrange("p (t d) -> p t d", d=D), rows(C.Y, i),
                                        ALU.add).then_inc(out_read, 1)
                dve.drain()


def mamba_join(C, name):
    nc = C.nc
    with ExitStack() as ctx:
        sc = Scope(nc, ctx, name)
        xn, t = sc.sb("xn", [P, 2, TPG, D]), sc.sb("t", [P, TPG, D])
        st, mv = sc.sb("st", [P, TPG, 6]), sc.sb("mv", [P, TPG, 2])
        activated, joined = sc.sem("activated"), sc.sem("joined")
        block = ctx.enter_context(nc.Block())

        @block.scalar
        def _(act):
            with act.Fori(0, C.NG) as i:
                act.wait_ge(joined, i + 1)
                nc.scalar.activation(t[:], rows(C.Y, i), ACT.Gelu).then_inc(activated, 1)

        @block.vector
        def _(dve):
            nc.vector.memset(mv[:], 0.0).then_inc(joined, 1)
            with dve.Fori(0, C.NG) as i:
                for p in range(TPG):
                    n = i * TPG + p
                    nc.vector.tensor_scalar(xn[:, 0, p, :], C.X[:, n, :], C.RS[:, bass.ds(n, 1)],
                                            C.NM[:, bass.ds(n, 1)], ALU.mult, ALU.add)
                dve.drain()
                dve.wait_ge(activated, i + 1)
                nc.vector.tensor_tensor(rows(C.Y, i), xn[:, 0, :, :], t[:], ALU.add).then_inc(joined, 1)
                dve.drain()
                group_stats(nc, dve, C, C.Y, st, mv, i)
                dve.drain()


def gelu_ffn(C, name, W):
    nc = C.nc
    F = W["w1"].shape[1]
    NF = F // P
    with ExitStack() as ctx:
        sc = Scope(nc, ctx, name)
        sb, ps, sem = sc.sb, sc.ps, sc.sem
        w1, w2, b1, b2 = sb("w1", [P, F]), sb("w2", [P, NF, D]), sb("b1", [P, NF]), sb("b2", [1, D])
        g, be = sb("g", [P, 1]), sb("be", [P, 1])
        hid = sb("hid", [P, NF, GT])
        st, mv = sb("st", [P, TPG, 6]), sb("mv", [P, TPG, 2])
        ps_j, ps_o, ps_h = ps("ps_j", [P, GT]), ps("ps_o", [P, GT]), ps("ps_h", [P, NF, GT])
        fr = Front(C, sc, ps_j, C.Y, C.RS2, C.NM2)
        loaded, hid_done, hid_ready = sem("loaded"), sem("hid_done"), sem("hid_ready")
        out_done, out_read = sem("out_done"), sem("out_read")
        block = ctx.enter_context(nc.Block())
        loads = [(w1[:], W["w1"]), (w2[:], W["w2"].rearrange("(c p) d -> p c d", p=P)), (b1[:], W["b1"]), (b2[:], W["b2"]),
                 (g[:], W["g"]), (be[:], W["be"])]
        n_loaded = 16 * len(loads)

        @block.sync
        def _(sp):
            for to, of in loads:
                sp.dma_start(to, of).then_inc(loaded, 16)

        @block.tensor
        def _(pe):
            pe.wait_ge(loaded, n_loaded)
            fr.pe(pe, 0)
            with pe.Fori(0, C.NG) as i:
                pe.wait_ge(fr.xT_ready, i + 1)
                for c in range(NF):
                    nc.tensor.matmul(ps_h[:, c, :], w1[:, c * P:(c + 1) * P], fr.xnT[:], start=True,
                                     stop=True).then_inc(hid_done, 1)
                fr.pe(pe, i + 1)
                pe.wait_ge(out_read, i + 1)
                pe.wait_ge(hid_ready, i * NF + NF)
                for p in range(TPG):
                    o = ps_o[:, p * D:(p + 1) * D]
                    for c in range(NF):
                        nc.tensor.matmul(o, hid[:, c, p * P:(p + 1) * P], w2[:, c, :], start=c == 0, stop=False)
                    last = nc.tensor.matmul(o, C.ones[0:1, :], b2[0:1, :], start=False, stop=True)
                last.then_inc(out_done, 1)

        @block.scalar
        def _(act):
            act.wait_ge(loaded, n_loaded)

            def copy_rows(j):
                act.wait_ge(fr.xT_done, j + 1)
                nc.scalar.activation(fr.xnT[:], ps_j[:], ACT.Identity, scale=g[:, 0:1],
                                     bias=be[:, 0:1]).then_inc(fr.xT_ready, 1)

            copy_rows(0)
            with act.Fori(0, C.NG) as i:
                for c in range(NF):
                    act.wait_ge(hid_done, i * NF + c + 1)
                    nc.scalar.activation(hid[:, c, :], ps_h[:, c, :], ACT.Gelu, bias=b1[:, c:c + 1]).then_inc(hid_ready, 1)
                copy_rows(i + 1)

        @block.vector
        def _(dve):
            nc.vector.memset(mv[:], 0.0).then_inc(out_read, 1)
            fr.dve(0)
            with dve.Fori(0, C.NG) as i:
                dve.wait_ge(fr.xT_done, i + 1)
                fr.dve(i + 1)
                nc.vector.tensor_tensor(rows(C.X, i), rows(C.X, i), rows(C.Y, i), ALU.add)
                dve.drain()
                dve.wait_ge(out_done, i + 1)
                nc.vector.tensor_tensor(rows(C.X, i), ps_o[:].rearrange("p (t d) -> p t d", d=D), rows(C.X, i),
                                        ALU.add).then_inc(out_read, 1)
                dve.drain()
                group_stats(nc, dve, C, C.X, st, mv, i)



FT = 16
FW = 8
ITERS = 3
PAIRS = HD // 2
STEPS = FT // 4
TWO_PI = (6.28125, 0.0019350051879882812, 3.0199159819567553e-07)
ROUND = 1.5 * 2.0 ** 23


def focus_block(C, name, ctx_rows, scratch_in, scratch_out, W):
    nc = C.nc
    with ExitStack() as ctx:
        sc = Scope(nc, ctx, name)
        sb, ps, sem = sc.sb, sc.ps, sc.sem
        row = [P, FT, D]
        weights = {k: sb("w_" + k, [P, D]) for k in ("q", "k", "v", "qh", "kh", "vh", "out")}
        bias = {k: sb("b_" + k, [P, D]) for k in ("qh", "kh", "vh")}
        lna_g, lna_b = sb("lna_g", [P, 1]), sb("lna_b", [P, 1])
        lnb_g, lnb_b = sb("lnb_g", [P, 2, HD]), sb("lnb_b", [P, 2, HD])
        theta, temp, thr, factor = (sb(n, [P, 1]) for n in ("theta", "temp", "thr", "factor"))
        base, place = sb("base", [P, PAIRS]), sb("place", [P, 2, FT])
        xa, xb = sb("xa", row), sb("xb", row)
        hat_a, hat_b = sb("hat_a", row), sb("hat_b", row)
        cur, prev, ai = sb("cur", row), sb("prev", row), sb("ai", row)
        k0, v0 = sb("k0", row), sb("v0", row)
        qk = sb("qk", [P, 2, FT, D])
        prod = C.Y[:, 0:4 * FT, :].rearrange("p t d -> p (t d)")
        score = sb("score", [P, FT * FT * NH])
        most, den = sb("most", [P, FT, NH]), sb("den", [P, FT, NH])
        hm, hv = sb("hm", [P, 2 * FT * NH]), sb("hv", [P, 2 * FT * NH])
        st, mv, rs = sb("st", [P, FT, 6]), sb("mv", [P, FT, 2]), sb("rs", [P, FT])
        ang, turns = sb("ang", [P, 2, 2, FT, PAIRS]), sb("turns", [P, 2, 2, FT, PAIRS])
        trig = sb("trig", [P, 2, 2, FT, PAIRS])
        cond, scale = sb("cond", [P, 1]), sb("scale", [P, 1])
        diff, done, kept = sb("diff", [P, 2]), sb("done", [P, 2]), sb("kept", [P, 2])
        gst, gmv = sb("gst", [P, TPG, 6]), sb("gmv", [P, TPG, 2])
        rT = sb("rT", [P, 2, 4 * P])
        ps_t = ps("ps_t", [P, 2, 4 * P])
        ps_p = ps("ps_p", [P, 2, 3, 4 * D])
        loaded, sent, fetched, returned = sem("loaded"), sem("sent"), sem("fetched"), sem("returned")
        src_ready, turned, rT_ready, multiplied, taken = (
            sem(n) for n in ("src_ready", "turned", "rT_ready", "multiplied", "taken"))
        asked, answered = sem("asked"), sem("answered")
        sums_in, summed, out_ready = sem("sums_in"), sem("summed"), sem("out_ready")
        block = ctx.enter_context(nc.Block())
        loads = [(t, "w_" + k) for k, t in weights.items()] + [(t, "b_" + k) for k, t in bias.items()]
        loads += [(lna_g, "lna_g"), (lna_b, "lna_b"), (lnb_g, "lnb_g"), (lnb_b, "lnb_b"), (theta, "theta"), (temp, "temp"),
                  (thr, "thr"), (factor, "factor"), (base, "base"), (place, "place")]
        n_loaded = 16 * len(loads)

        FOCI = (((("a", "qkv"),), 0, 2, FT // FW), ((("a", "qkv"),), 10, 1, FT // FW), ((("a", "q"), ("b", "kv")), 20, 2, 1))
        OUT_JOB = 31
        ASKED0 = 2

        def asked_before(f):
            return ASKED0 + sum(n + 2 * ITERS for _, _, n, _ in FOCI[:f])

        @block.sync
        def _(sp):
            for to, k in loads:
                sp.dma_start(to[:], W[k]).then_inc(loaded, 16)
            by_tile = scratch_in.rearrange("(n b) t d -> b t n d", b=2)
            for b in range(2):
                sp.dma_start(by_tile[b], C.X[S * b:S * b + FT, 0:C.NT, :]).then_inc(sent, 16)
            sp.dma_start(xb[:], ctx_rows[:, 0:FT, :]).then_inc(fetched, 16)
            sp.wait_ge(sent, 32)
            sp.dma_start(xa[:], scratch_in).then_inc(fetched, 16)
            sp.wait_ge(out_ready, 1)
            sp.dma_start(scratch_out, hat_a[:]).then_inc(sent, 16)
            sp.wait_ge(sent, 48)
            by_tile = scratch_out.rearrange("(n b) t d -> b t n d", b=2)
            for b in range(2):
                sp.dma_start(C.Y[S * b:S * b + FT, 0:C.NT, :], by_tile[b]).then_inc(returned, 16)

        @block.tensor
        def _(pe):
            pe.wait_ge(loaded, n_loaded)

            def turn(src, job, t):
                n = job * STEPS + t
                for r in range(4):
                    last = nc.tensor.transpose(ps_t[:, t % 2, r * P:(r + 1) * P], src[:, 4 * t + r, :], C.ident[:])
                last.then_inc(turned, 1)

            def multiply(ws, job, t):
                n = job * STEPS + t
                pe.wait_ge(rT_ready, n + 1)
                if t >= 2:
                    pe.wait_ge(taken, n - 1)
                for o, w in enumerate(ws):
                    for r in range(4):
                        last = nc.tensor.matmul(ps_p[:, t % 2, o, r * D:(r + 1) * D], rT[:, t % 2, r * P:(r + 1) * P],
                                                weights[w][:], start=True, stop=True)
                last.then_inc(multiplied, 1)

            def run(src, ws, job):
                pe.wait_ge(src_ready, job + 1)
                pe.wait_ge(taken, job * STEPS) if not (isinstance(job, int) and job == 0) else None
                turn(src, job, 0)
                for t in range(1, STEPS):
                    turn(src, job, t)
                    multiply(ws, job, t - 1)
                multiply(ws, job, STEPS - 1)

            def iteration(job):
                for n, (src, w) in enumerate(((cur, "qh"), (k0, "kh"), (v0, "vh"))):
                    run(src, (w,), job + n)

            for f, (inputs, first, _, nw) in enumerate(FOCI):
                for n, (src, ws) in enumerate(inputs):
                    run(hat_a if src == "a" else hat_b, tuple(ws), first + n)
                with pe.Fori(0, ITERS - 1) as it:
                    iteration(it * 3 + first + len(inputs))
                iteration(first + len(inputs) + 3 * (ITERS - 1))
                pe.wait_ge(sums_in, f + 1)
                nc.tensor.matmul(ps_p[:, 0, 2, 0:nw], C.ones[:], diff[:, 0:nw], start=True, stop=True).then_inc(summed, 1)
            run(xa, ("out",), OUT_JOB)

        @block.scalar
        def _(act):
            act.wait_ge(loaded, n_loaded)

            def copies(job, affine):
                for t in range(STEPS):
                    act.wait_ge(turned, job * STEPS + t + 1)
                    if affine:
                        last = nc.scalar.activation(rT[:, t % 2, :], ps_t[:, t % 2, :], ACT.Identity, scale=lna_g[:, 0:1],
                                                    bias=lna_b[:, 0:1])
                    else:
                        last = nc.scalar.activation(rT[:, t % 2, :], ps_t[:, t % 2, :], ACT.Copy)
                    last.then_inc(rT_ready, 1)

            def answer(n, buf, fn):
                act.wait_ge(asked, n)
                nc.scalar.activation(buf, buf, fn).then_inc(answered, 1)

            def iteration(job, n, width):
                for m in range(3):
                    copies(job + m, False)
                answer(n + 1, hv[:], ACT.Sqrt)
                answer(n + 2, score[:, 0:width], ACT.Exp)

            answer(1, trig[:].rearrange("p a b t f -> p (a b t f)"), ACT.Sin)
            answer(2, scale[:], ACT.Sqrt)
            for f, (inputs, first, norms, nw) in enumerate(FOCI):
                for n in range(norms):
                    answer(asked_before(f) + n + 1, rs[:], ACT.Sqrt)
                for n in range(len(inputs)):
                    copies(first + n, True)
                width = FT * FT // nw * NH
                with act.Fori(0, ITERS - 1) as it:
                    iteration(it * 3 + first + len(inputs), it * 2 + asked_before(f) + norms, width)
                iteration(first + len(inputs) + 3 * (ITERS - 1), asked_before(f) + norms + 2 * (ITERS - 1), width)
            copies(OUT_JOB, False)

        @block.vector
        def _(dve):
            dve.wait_ge(loaded, n_loaded)
            tt, ts, stt = nc.vector.tensor_tensor, nc.vector.tensor_scalar, nc.vector.scalar_tensor_tensor

            ts(cond[:], theta[:], 1.0 / 220.0, None, ALU.mult)
            dve.drain()
            ts(base[:], base[:], cond[:, 0:1], None, ALU.mult)
            dve.drain()
            for a in range(2):
                for b in range(2):
                    tt(ang[:, a, b, :, :], bc(place[:, a, :].unsqueeze(2), [P, FT, PAIRS]),
                       bc(base[:].unsqueeze(1), [P, FT, PAIRS]), ALU.mult)
            dve.drain()
            for b in range(2):
                ts(turns[:, :, b, :, :], ang[:, :, b, :, :], 1.0 / (2.0 * math.pi), 0.25 * b, ALU.mult, ALU.add)
            dve.drain()
            ts(turns[:], turns[:], ROUND, None, ALU.add)
            dve.drain()
            ts(turns[:], turns[:], -ROUND, None, ALU.add)
            dve.drain()
            for part in TWO_PI:
                stt(ang[:].rearrange("p a b t f -> p (a b t f)"), turns[:].rearrange("p a b t f -> p (a b t f)"), -part,
                    ang[:].rearrange("p a b t f -> p (a b t f)"), ALU.mult, ALU.add)
                dve.drain()
            ts(ang[:, :, 1, :, :], ang[:, :, 1, :, :], math.pi / 2, None, ALU.add)
            dve.drain()
            edge = 3.1415925
            ts(trig[:], ang[:], edge, -edge, ALU.min, ALU.max).then_inc(asked, 1)
            dve.wait_ge(answered, 1)
            ts(cond[:], temp[:], 0.0, None, ALU.is_gt)
            ts(scale[:], temp[:], 1.0, None, ALU.not_equal)
            dve.drain()
            tt(cond[:], cond[:], scale[:], ALU.mult)
            dve.drain()
            ts(diff[:, 0:1], temp[:], 1e-38, -1.0, ALU.max, ALU.add)
            dve.drain()
            tt(diff[:, 0:1], diff[:, 0:1], cond[:], ALU.mult)
            dve.drain()
            ts(diff[:, 0:1], diff[:, 0:1], 1.0, None, ALU.add)
            dve.drain()
            nc.vector.reciprocal(scale[:], diff[:, 0:1]).then_inc(asked, 1)
            dve.wait_ge(answered, 2)
            ts(scale[:], scale[:], HD ** -0.5, None, ALU.mult)
            dve.drain()
            ts(lnb_g[:, 0, :], lnb_g[:, 0, :], scale[:, 0:1], None, ALU.mult)
            ts(lnb_b[:, 0, :], lnb_b[:, 0, :], scale[:, 0:1], None, ALU.mult)
            dve.drain()

            def norm_rows(to, src, n):
                for t in range(FT):
                    nc.vector.bn_stats(st[:, t, :], src[:, t, :])
                dve.drain()
                for t in range(FT):
                    nc.vector.bn_aggr(mv[:, t, :], st[:, t, :])
                dve.drain()
                ts(rs[:], mv[:, :, 1], 1e-5, None, ALU.add).then_inc(asked, 1)
                tt(to[:], src[:], bc(mv[:, :, 0].unsqueeze(2), row), ALU.subtract)
                dve.wait_ge(answered, n)
                nc.vector.reciprocal(rs[:], rs[:])
                dve.drain()
                last = tt(to[:], to[:], bc(rs[:].unsqueeze(2), row), ALU.mult)
                dve.drain()
                return last

            def take(job, outs):
                for t in range(STEPS):
                    dve.wait_ge(multiplied, job * STEPS + t + 1)
                    for o, (to, b) in enumerate(outs):
                        got = ps_p[:, t % 2, o, :].rearrange("p (r d) -> p r d", d=D)
                        if b is None:
                            last = nc.vector.tensor_copy(to[:, 4 * t:4 * t + 4, :], got)
                        else:
                            last = tt(to[:, 4 * t:4 * t + 4, :], got, bc(b[:].unsqueeze(1), [P, 4, D]), ALU.add)
                    last.then_inc(taken, 1)

            def rotate(buf, a):
                v = buf[:].rearrange("p t (h f e) -> p t h f e", h=NH, e=2)
                part = [prod[:, n * 1024:(n + 1) * 1024].rearrange("p (t h f) -> p t h f", t=FT, h=NH) for n in range(4)]
                sn, cs = (bc(trig[:, a, n, :, :].unsqueeze(2), [P, FT, NH, PAIRS]) for n in range(2))
                tt(part[0], v[:, :, :, :, 0], cs, ALU.mult)
                tt(part[1], v[:, :, :, :, 1], sn, ALU.mult)
                tt(part[2], v[:, :, :, :, 0], sn, ALU.mult)
                tt(part[3], v[:, :, :, :, 1], cs, ALU.mult)
                dve.drain()
                tt(v[:, :, :, :, 0], part[0], part[1], ALU.subtract)
                last = tt(v[:, :, :, :, 1], part[2], part[3], ALU.add)
                dve.drain()
                return last

            heads = lambda t: t.rearrange("p t (h e) -> p (t h) e", e=HD)
            HT = FT * NH
            wide = [P, HT, HD]

            def iteration(job, n, nw, last_one):
                ck = FT // nw
                take(job, [(qk[:, 0, :, :], bias["qh"])])
                take(job + 1, [(k0, bias["kh"])])
                take(job + 2, [(v0, bias["vh"])])
                dve.drain()
                pair = ((qk[:, 0, :, :], qk[:, 0, :, :], 0), (k0[:], qk[:, 1, :, :], 1))
                for src, to, m in pair:
                    nc.vector.tensor_reduce(hm[:, m * HT:(m + 1) * HT], heads(src), AX, ALU.add)
                dve.drain()
                ts(hm[:], hm[:], 1.0 / HD, None, ALU.mult)
                dve.drain()
                for src, to, m in pair:
                    tt(heads(to), heads(src), bc(hm[:, m * HT:(m + 1) * HT].unsqueeze(2), wide), ALU.subtract)
                dve.drain()
                both = qk[:].rearrange("p m t (h e) -> p (m t h) e", e=HD)
                square = prod[:, 0:2 * FT * D].rearrange("p (x e) -> p x e", e=HD)
                tt(square, both, both, ALU.mult)
                dve.drain()
                nc.vector.tensor_reduce(hv[:], square, AX, ALU.add)
                dve.drain()
                ts(hv[:], hv[:], 1.0 / HD, 1e-5, ALU.mult, ALU.add).then_inc(asked, 1)
                dve.wait_ge(answered, n + 1)
                nc.vector.reciprocal(hv[:], hv[:])
                dve.drain()
                tt(both, both, bc(hv[:].unsqueeze(2), [P, 2 * HT, HD]), ALU.mult)
                dve.drain()
                for m in range(2):
                    x = heads(qk[:, m, :, :])
                    tt(x, x, bc(lnb_g[:, m, :].unsqueeze(1), wide), ALU.mult)
                dve.drain()
                for m in range(2):
                    x = heads(qk[:, m, :, :])
                    tt(x, x, bc(lnb_b[:, m, :].unsqueeze(1), wide), ALU.add)
                dve.drain()
                QC = 8192 // (ck * D)
                for q in range(0, FT, QC):
                    w = q // ck * ck
                    tt(prod.rearrange("p (q k d) -> p q k d", q=QC, k=ck), bc(qk[:, 0, q:q + QC, :].unsqueeze(2), [P, QC, ck, D]),
                       bc(qk[:, 1, w:w + ck, :].unsqueeze(1), [P, QC, ck, D]), ALU.mult)
                    dve.drain()
                    nc.vector.tensor_reduce(score[:, q * ck * NH:(q + QC) * ck * NH],
                                            prod.rearrange("p (x e) -> p x e", e=HD), AX, ALU.add)
                    dve.drain()
                s = score[:, 0:FT * ck * NH].rearrange("p (q k h) -> p q k h", q=FT, k=ck)
                turned_s = s.rearrange("p q k h -> p q h k")
                nc.vector.tensor_reduce(most[:], turned_s, AX, ALU.max)
                dve.drain()
                tt(s, s, bc(most[:].unsqueeze(2), [P, FT, ck, NH]), ALU.subtract).then_inc(asked, 1)
                dve.wait_ge(answered, n + 2)
                nc.vector.tensor_reduce(den[:], turned_s, AX, ALU.add)
                dve.drain()
                nc.vector.reciprocal(den[:], den[:])
                for q in range(0, FT, QC):
                    w = q // ck * ck
                    vals = v0[:, w:w + ck, :].rearrange("p k (h e) -> p h e k", e=HD)
                    for r in range(QC):
                        to = prod[:, r * ck * D:(r + 1) * ck * D].rearrange("p (h e k) -> p h e k", h=NH, e=HD)
                        tt(to, bc(turned_s[:, q + r, :, :].unsqueeze(2), [P, NH, HD, ck]), vals, ALU.mult)
                    dve.drain()
                    nc.vector.tensor_reduce(ai[:, q:q + QC, :].rearrange("p q d -> p (q d)"),
                                            prod.rearrange("p (x k) -> p x k", k=ck), AX, ALU.add)
                    dve.drain()
                tt(heads(ai[:]), heads(ai[:]), bc(den[:].rearrange("p t h -> p (t h)").unsqueeze(2), wide), ALU.mult)
                dve.drain()
                if last_one:
                    return
                change = prod[:, 0:FT * D]
                tt(change.rearrange("p (t d) -> p t d", d=D), ai[:], prev[:], ALU.subtract)
                dve.drain()
                nc.vector.tensor_reduce(diff[:, 0:nw], change.rearrange("p (w x) -> p w x", w=nw), AX, ALU.add,
                                        apply_absolute_value=True)
                nc.vector.tensor_copy(prev[:], ai[:])
                tt(cur[:], cur[:], ai[:], ALU.add).then_inc(src_ready, 3)
                dve.drain()

            dve.wait_ge(fetched, 32)
            for f, (inputs, first, norms, nw) in enumerate(FOCI):
                n = asked_before(f)
                if f == 0:
                    norm_rows(xa, xa, n + 1)
                    norm_rows(hat_a, xa, n + 2)
                elif f == 1:
                    norm_rows(hat_a, xb, n + 1)
                else:
                    norm_rows(hat_a, xa, n + 1)
                    norm_rows(hat_b, xb, n + 2)
                nc.vector.memset(prev[:], 0.0).then_inc(src_ready, len(inputs))
                outs = [(cur, None), (k0, None), (v0, None)]
                if len(inputs) == 1:
                    take(first, outs)
                else:
                    take(first, outs[0:1])
                    take(first + 1, outs[1:3])
                dve.drain()
                rotate(cur, f // 2)
                rotate(k0, f // 2)
                nc.vector.memset(den[:], 0.0).then_inc(src_ready, 3)
                job0 = first + len(inputs)
                with dve.Fori(0, ITERS - 1) as it:
                    iteration(it * 3 + job0, it * 2 + n + norms, nw, False)
                nc.vector.tensor_copy(done[:, 0:nw], diff[:, 0:nw]).then_inc(sums_in, 1)
                iteration(job0 + 3 * (ITERS - 1), n + norms + 2 * (ITERS - 1), nw, True)
                dve.wait_ge(summed, f + 1)
                count = P * NH * (FW if nw > 1 else S) * HD
                ts(kept[:, 0:nw], ps_p[:, 0, 2, 0:nw], 1.0 / count, None, ALU.mult)
                dve.drain()
                ts(done[:, 0:nw], kept[:, 0:nw], factor[:, 0:1], thr[:, 0:1], ALU.mult, ALU.add)
                dve.drain()
                tt(done[:, 0:nw], kept[:, 0:nw], done[:, 0:nw], ALU.is_lt)
                dve.drain()
                ts(kept[:, 0:nw], done[:, 0:nw], -1.0, 1.0, ALU.mult, ALU.add)
                dve.drain()
                to = xb if f == 1 else xa
                flat = lambda t, w: t[:, w * FT // nw:(w + 1) * FT // nw, :].rearrange("p t d -> p (t d)")
                for w in range(nw):
                    ts(flat(ai, w), flat(ai, w), kept[:, w:w + 1], None, ALU.mult)
                dve.drain()
                for w in range(nw):
                    last = stt(flat(to, w), flat(prev, w), done[:, w:w + 1], flat(ai, w), ALU.mult, ALU.add)
                if f == 2:
                    last.then_inc(src_ready, 1)
                dve.drain()
            take(OUT_JOB, [(hat_a, None)])
            dve.drain()
            nc.vector.memset(den[:], 0.0).then_inc(out_ready, 1)
            dve.wait_ge(returned, 32)
            for b in range(2):
                r = slice(S * b, S * b + FT)
                tt(C.X[r, 0:C.NT, :], C.X[r, 0:C.NT, :], C.Y[r, 0:C.NT, :], ALU.add)
            dve.drain()
            with dve.Fori(0, C.NG) as i:
                row_stats(nc, dve, C, C.X, gst, gmv, i)
                dve.drain()


def store_x(C, out):
    nc = C.nc
    with ExitStack() as ctx:
        sc = Scope(nc, ctx, "store")
        stored = sc.sem("stored")
        block = ctx.enter_context(nc.Block())

        @block.sync
        def _(sp):
            sp.dma_start(out.rearrange("(n p) d -> p n d", p=P), C.X[:, 0:C.NT, :]).then_inc(stored, 16)
            sp.wait_ge(stored, 16)



def constants():
    c = {"ident": np.eye(P, dtype=np.float32)}
    pos = np.arange(S, dtype=np.float32)
    lower = np.tril(np.ones((S, S), np.float32))
    c["tril"] = np.concatenate([lower, lower])
    row = np.arange(P)
    c["hmask"] = (row[:, None] // HD % HR == np.arange(HR)[None, :]).astype(np.float32)
    inv = (1.0 / 10000.0 ** (np.arange(0, HD, 2, dtype=np.float32) / HD)).astype(np.float32)
    ang = (pos[:, None] * inv[None, :]).astype(np.float32)
    c["cosT"] = np.tile(np.repeat(np.cos(ang), 2, axis=1).T, (NH, 1)).astype(np.float32)
    c["sinT"] = np.tile(np.repeat(np.sin(ang), 2, axis=1).T, (NH, 1)).astype(np.float32)
    c["falling"] = np.tile(np.arange(NE, 0, -1, dtype=np.float32), (P, 1))
    dist = np.abs(pos[:, None] - pos[None, :])

    def twice(t):
        t = t.astype(np.float32).transpose(1, 0, 2)
        return np.concatenate([t, t])
    slopes = 2.0 ** (-8.0 * np.arange(NH) / NH)
    c["table0"] = twice(-slopes[:, None, None].astype(np.float32) * dist)
    m = np.exp(-np.power(5000.0, (np.arange(1, NH + 1) - 1.0) / (NH - 1.0) * 0.8))
    c["table1"] = twice(m[:, None, None].astype(np.float32) * (1000.0 + dist))
    slopes = 0.5 ** np.arange(1, NH + 1)
    c["table3"] = twice(-np.maximum(pos[:, None] - pos[None, :], 0) * slopes[:, None, None].astype(np.float32))
    slopes = (2.0 ** (-2.0 ** -(math.log2(32) - 3))) ** np.arange(1, 33, dtype=np.float32)
    rel = pos[None, :] - pos[:, None]
    bias = np.where(rel <= 0, slopes.astype(np.float32)[:, None, None] * rel, np.float32(-BIG))
    bias = bias.reshape(4, 2, 2, 2, S, S).transpose(0, 2, 1, 3, 4, 5).reshape(32, S, S)
    c["table_a3"] = twice(bias).reshape(P, 4, UH, S)
    perm = np.zeros((P, P), np.float32)
    quarter = np.arange(D // 4)
    for to, of, sign in ((0, 2, 1), (1, 3, -1), (2, 0, -1), (3, 1, 1)):
        perm[of * 32 + quarter, to * 32 + quarter] = sign
    c["perm"] = perm
    sel = np.zeros((DTR + 2 * NS, 2 * NS, P), np.float32)
    sel[DTR + np.arange(2 * NS), np.arange(2 * NS), :] = 1
    c["sel"] = sel
    c["flip"] = np.kron(np.eye(2, dtype=np.float32), np.eye(S, dtype=np.float32)[::-1]).astype(np.float32)
    mel = np.linspace(0.0, 2595.0 * np.log10(1.0 + 4000.0 / 200.0), PAIRS)
    c["base"] = np.tile((200.0 * (10.0 ** (mel / 2595.0) - 1.0) / 1000.0).astype(np.float32), (P, 1))
    c["place"] = np.tile(np.stack([np.arange(FT) % FW, np.arange(FT)]).astype(np.float32), (P, 1, 1))
    return c


def layouts(v):
    t = lambda n: np.ascontiguousarray(v[n].T)
    col = lambda n: np.ascontiguousarray(v[n].reshape(-1, 1))
    row = lambda n: np.ascontiguousarray(v[n].reshape(1, -1))
    rep = lambda n: np.ascontiguousarray(np.broadcast_to(v[n].reshape(1, -1), (P, v[n].size)))
    a = {"x": v["x"].reshape(-1, D), "ctxT": np.ascontiguousarray(v["ctx_1024"].reshape(-1, D).T)}
    for k in ("Wq", "Wk", "Wv", "Wo"):
        a["a0_" + k] = t("L0_attn_" + k)
        a["c0_" + k] = t("L0_xattn_" + k)
    for k in ("bq", "bk", "bv"):
        a["c0_" + k] = col("L0_xattn_" + k)
    a["c0_bo"] = row("L0_xattn_bo")
    for k in ("Wq", "Wk", "Wv", "Wc", "Wo"):
        a["a1_" + k] = v["L1_attn_" + k]
    a["a1_We"] = np.ascontiguousarray(np.repeat(v["L1_attn_We"].reshape(S, 4, 1, HD), NH // 4, axis=2).reshape(S, D))
    for k in ("bq", "bk", "bv"):
        a["a1_" + k] = col("L1_attn_" + k)
    a["a1_bo"] = row("L1_attn_bo")
    a["a1_gamma"], a["a1_beta"] = rep("L1_attn_gamma"), rep("L1_attn_beta")
    qkv = v["L2_ffn_W_qkv"]
    for n, k in enumerate(("Wq", "Wk", "Wv")):
        a["f2_" + k] = np.ascontiguousarray(qkv[n * D:(n + 1) * D].T)
    a["f2_Wo"] = t("L2_ffn_W_out")
    a["f2_wr"] = rep("L2_ffn_w_router")
    a["f2_g1"], a["f2_g2"] = col("L2_ffn_g1"), col("L2_ffn_g2")
    for k, n in (("Wq", "wq"), ("Wk", "wk"), ("Wv", "wv"), ("Wo", "out")):
        a["c3_" + k] = t(f"L3_xattn_{n}_w")
        a["c3_b" + k[1]] = (row if k == "Wo" else col)(f"L3_xattn_{n}_b")
    a["f0_wi"], a["f0_wo"] = t("L0_ffn_wi_W"), t("L0_ffn_wo_W")
    lora_a = v["L0_ffn_lora_A"].reshape(-1, D)
    a["f0_ga"] = np.ascontiguousarray(np.concatenate([v["L0_ffn_gate_W"], lora_a]).T)
    a["f0_B"] = np.ascontiguousarray(v["L0_ffn_lora_B"].transpose(0, 2, 1).reshape(lora_a.shape[0], -1))
    a["f0_gb"] = rep("L0_ffn_gate_b")
    a["f0_wib"] = np.ascontiguousarray(v["L0_ffn_wi_b"].reshape(-1, P).T)
    a["f0_wob"] = row("L0_ffn_wo_b")
    a["f2_w1"], a["f2_w2"], a["f2_w3"] = t("L2_ffn_W1"), t("L2_ffn_W2"), t("L2_ffn_W3")
    a["f3_wr"], a["f3_w1"], a["f3_w2"] = v["L3_ffn_router_w"], v["L3_ffn_w1"], v["L3_ffn_w2"]
    c2 = lambda n: np.ascontiguousarray(v["L2_xattn_" + n].reshape(D, 1, NJ, 2, HW))
    a["c2_wq"], a["c2_wk"] = c2("Wq").reshape(D, NJ, P), c2("Wk").reshape(D, NJ, P)
    a["c2_wv"] = np.ascontiguousarray(c2("Wv").transpose(0, 3, 1, 2, 4)).reshape(D, 2, NJ * HW)
    a["c2_wo"] = np.ascontiguousarray(v["L2_xattn_Wo"].reshape(NJ, P, D).transpose(1, 0, 2))
    a["c2_bo"] = row("L2_xattn_bo")
    w = v["L3_attn_W_qkv"]
    nq, nk = 32, 16
    q = w[:, :nq * HW].reshape(D, 4, 2, 2, 2, HW)
    a["a3_wq"] = np.ascontiguousarray(q.transpose(0, 1, 2, 4, 3, 5)).reshape(D, 16, P)
    a["a3_wk"] = w[:, nq * HW:(nq + nk) * HW].reshape(D, 8, P)
    vv = w[:, (nq + nk) * HW:].reshape(D, 8, 2, HW)
    a["a3_wv"] = np.ascontiguousarray(vv.transpose(0, 2, 1, 3)).reshape(D, 2, 8 * HW)
    o = v["L3_attn_W_out"].reshape(4, 2, 2, 2, HW, D)
    a["a3_wo"] = np.ascontiguousarray(o.transpose(2, 4, 0, 1, 3, 5)).reshape(P, 16, D)
    wide = lambda x: np.ascontiguousarray(np.broadcast_to(x.reshape(-1, 1), (x.size, P)))
    one = lambda n: np.ascontiguousarray(np.broadcast_to(v[n].reshape(1, 1), (P, 1)))
    for n in range(3):
        a[f"f1_w{n}"], a[f"f1_b{n}"] = v[f"L1_ffn_cn_w{n + 1}"], col(f"L1_ffn_cn_b{n + 1}")
    for n in range(2):
        a[f"f1_gw{n}"], a[f"f1_gb{n}"] = v[f"L1_ffn_gc_w{n + 1}"], col(f"L1_ffn_gc_b{n + 1}")
    a["f1_w3"], a["f1_b3"] = wide(v["L1_ffn_cn_w4"]), one("L1_ffn_cn_b4")
    a["f1_gw2"], a["f1_gb2"] = wide(v["L1_ffn_gc_w3"]), one("L1_ffn_gc_b3")
    a["f1_reach"] = one("L1_ffn_adaptive_range")
    halves = lambda x: np.ascontiguousarray(x.reshape(NHF, P, -1).transpose(1, 0, 2))
    for d in ("m1", "m2"):
        m = lambda n: v[f"L2_attn_{d}_{n}"]
        a[d + "_in_w"] = np.ascontiguousarray(m("in_w").T)
        a[d + "_taps"] = np.ascontiguousarray(np.broadcast_to(m("conv_w").T[None], (P, NTAP, DI)))
        a[d + "_conv_b"], a[d + "_dt_b"], a[d + "_D"] = (halves(m(n))[:, :, 0].copy() for n in ("conv_b", "dt_b", "D"))
        a[d + "_xp"], a[d + "_out_w"] = halves(m("xproj_w").T), halves(m("out_w").T)
        a[d + "_dt_w"], a[d + "_A"] = np.ascontiguousarray(m("dt_w").T), halves(m("Alog"))
        a[d + "_g"], a[d + "_be"] = col("L2_attn_norm_g"), col("L2_attn_norm_b")
    a["m3_w1"], a["m3_w2"] = t("L2_attn_ff1_w"), t("L2_attn_ff2_w")
    a["m3_b1"], a["m3_b2"] = np.ascontiguousarray(v["L2_attn_ff1_b"].reshape(-1, P).T), row("L2_attn_ff2_b")
    a["m3_g"], a["m3_be"] = col("L2_attn_ffn_g"), col("L2_attn_ffn_b")
    a["ctx"] = v["ctx_1024"]
    wkv = v["L1_xattn_Wkv"]
    a["x1_w_q"], a["x1_w_out"] = t("L1_xattn_Wq"), t("L1_xattn_Wout")
    a["x1_w_k"], a["x1_w_v"] = np.ascontiguousarray(wkv[:D].T), np.ascontiguousarray(wkv[D:].T)
    for k in ("qh", "kh", "vh"):
        blocks_ = np.zeros((NH, HD, NH, HD), np.float32)
        for h in range(NH):
            blocks_[h, :, h, :] = v["L1_xattn_W" + k].T
        a["x1_w_" + k] = blocks_.reshape(D, D)
        a["x1_b_" + k] = np.ascontiguousarray(np.tile(v["L1_xattn_b" + k].reshape(1, HD), (P, NH)))
    a["x1_lna_g"], a["x1_lna_b"] = col("L1_xattn_lna_g"), col("L1_xattn_lna_b")
    a["x1_lnb_g"], a["x1_lnb_b"] = (np.ascontiguousarray(np.tile(v["L1_xattn_lnb_" + k].reshape(1, 1, HD), (P, 2, 1)))
                                    for k in "gb")
    for k, n in (("theta", "theta"), ("temp", "temp"), ("thr", "threshold"), ("factor", "factor")):
        a["x1_" + k] = one("L1_xattn_" + n)
    m = v["mask_1x1xSxS2_ik0"].reshape(S, S)
    a["mask"] = np.concatenate([m, m])
    return a


def pick(A, prefix, /, **names):
    return {k: A[n if n in A else prefix + n][:] for k, n in names.items()}


def blocks(C, A):
    qkvo = dict(wq="Wq", wk="Wk", wv="Wv", wo="Wo", hmask="hmask")

    def l0_attn():
        norm_scales(C, "n0a", 1e-5)
        attn16(C, "a0", "rope", pick(A, "a0_", cosT="cosT", sinT="sinT", table="table0", **qkvo))

    def l0_xattn():
        norm_scales(C, "n0c", 1e-5)
        attn16(C, "c0", "ctx", pick(A, "c0_", bq="bq", bk="bk", bv="bv", bo="bo", table="table1", **qkvo), A["ctxT"])

    def l1_attn():
        norm_scales(C, "n1a", 1e-5)
        attn16(C, "a1", "linear", pick(A, "a1_", bq="bq", bk="bk", bv="bv", bo="bo", wc="Wc", we="We", tril="tril",
                                       **qkvo))
        inner_scales(C, "n1y", 1e-5, False)
        affine_norm(C, "a1n", A["a1_gamma"], A["a1_beta"])

    def l2_ffn():
        norm_scales(C, "n2f", 1e-5, 1e-6)
        attn16(C, "f2", "rank", pick(A, "f2_", g1="g1", wr="wr", tril="tril", **qkvo))
        inner_scales(C, "n2y", 1e-6, True)
        gated_ffn(C, "g2", pick(A, "f2_", w1="w1", w2="w2", w3="w3", g="g2"))

    def l0_ffn():
        norm_scales(C, "n0f", 1e-5)
        lora_ffn(C, "f0", pick(A, "f0_", wi="wi", wo="wo", ga="ga", B="B", gb="gb", wib="wib", wob="wob", falling="falling"))

    def l3_ffn():
        norm_scales(C, "n3f", 1e-5)
        topk_ffn(C, "f3", pick(A, "f3_", wr="wr", w1="w1", w2="w2", falling="falling"))

    def l1_xattn():
        scratch = [C.nc.dram_tensor(n, (P, FT, D), F32, kind="Internal").ap() for n in ("focus_rows", "focus_out")]
        names = ["w_q", "w_k", "w_v", "w_qh", "w_kh", "w_vh", "w_out", "b_qh", "b_kh", "b_vh", "lna_g", "lna_b", "lnb_g",
                 "lnb_b", "theta", "temp", "thr", "factor", "base", "place"]
        focus_block(C, "x1", A["ctx"], *scratch, pick(A, "x1_", **{n: n for n in names}))

    def l1_ffn():
        norm_scales(C, "n1f", 1e-5)
        names = [f"{k}{n}" for k, m in (("w", 4), ("b", 4), ("gw", 3), ("gb", 3)) for n in range(m)]
        coupled_ffn(C, "f1", pick(A, "f1_", perm="perm", reach="reach", **{n: n for n in names}))

    def l2_attn():
        norm_scales(C, "n2a", 1e-5, 1e-5)
        names = ("in_w", "taps", "conv_b", "xp", "dt_w", "dt_b", "A", "D", "out_w", "sel", "flip", "g", "be")
        for d in ("m1", "m2"):
            mamba(C, d, pick(A, d + "_", **{n: n for n in names}), d == "m1")
        mamba_join(C, "mj")
        inner_scales(C, "n2m", 1e-5, False)
        gelu_ffn(C, "m3", pick(A, "m3_", w1="w1", w2="w2", b1="b1", b2="b2", g="g", be="be"))

    def l2_xattn():
        norm_scales(C, "n2c", 1e-5)
        attn64(C, "c2", pick(A, "c2_", wq="wq", wk="wk", wv="wv", wo="wo", bo="bo"), 1, 1, A["ctxT"])

    def l3_attn():
        norm_scales(C, "n3a", 1e-5)
        attn64(C, "a3", pick(A, "a3_", wq="wq", wk="wk", wv="wv", wo="wo", table="table_a3"), 4, 2)

    def l3_xattn():
        norm_scales(C, "n3c", 1e-5)
        attn16(C, "c3", "mask", pick(A, "c3_", bq="bq", bk="bk", bv="bv", bo="bo", table="table3", mask="mask",
                                     **qkvo), A["ctxT"])

    return {0: l0_attn, 1: l0_xattn, 2: l0_ffn, 3: l1_attn, 4: l1_xattn, 5: l1_ffn, 6: l2_attn, 7: l2_xattn, 8: l2_ffn, 9: l3_attn, 10: l3_xattn, 11: l3_ffn}


def program(nc, A, out, groups, which):
    with ExitStack() as ctx:
        C = Core(nc, ctx, groups)
        load_x(C, A["x"], A)
        todo = blocks(C, A)
        for n in which:
            todo[n]()
        store_x(C, out)


def kernel(**inputs):
    import concourse.bacc as bacc
    from concourse.bass_utils import run_bass_kernel_spmd

    v = {k: np.asarray(a) for k, a in inputs.items()}
    arrays = {"in_" + k: np.ascontiguousarray(a) for k, a in {**constants(), **layouts(v)}.items()}
    nc = bacc.Bacc("TRN2", target_bir_lowering=False, num_devices=1)
    A = {k[3:]: nc.dram_tensor(k, a.shape, mybir.dt.from_np(a.dtype), kind="ExternalInput").ap() for k, a in arrays.items()}
    rows_out = v["x"].shape[0] * S
    out = nc.dram_tensor("out_0_dram", (rows_out, D), F32, kind="ExternalOutput").ap()
    program(nc, A, out, rows_out // (4 * P), range(12))
    result = run_bass_kernel_spmd(nc, [arrays], core_ids=[0])
    return result.results[0]["out_0_dram"].reshape(v["x"].shape)
```

```python
import math
from contextlib import ExitStack

import numpy as np

import concourse.bass as bass
from concourse import mybir
from concourse.alu_op_type import AluOpType as ALU

F32 = mybir.dt.float32
BF16 = mybir.dt.bfloat16
I32 = mybir.dt.int32
ACT = mybir.ActivationFunctionType
AX = mybir.AxisListType.X

P = 128
D = 128
S = 64
TPG = 4
GT = TPG * P
SPG = GT // S
BIG = 1e30


class Core:

    def __init__(self, nc, ctx, groups):
        def sb(name, shape, dt=F32):
            return ctx.enter_context(nc.sbuf_tensor(name, shape, dt))
        self.nc, self.NG, self.NT = nc, groups, groups * TPG
        pad = self.NT + 2 * TPG
        self.X = sb("X", [P, pad, D])
        self.Y = sb("Y", [P, pad, D])
        self.MV = sb("MV", [P, pad, 2])
        self.RS = sb("RS", [P, pad])
        self.NM = sb("NM", [P, pad])
        self.RS2 = sb("RS2", [P, pad])
        self.NM2 = sb("NM2", [P, pad])
        self.tmp = sb("stat_tmp", [P, pad])
        self.ident = sb("ident", [P, P])
        self.ones = sb("ones", [P, P])


class Scope:

    def __init__(self, nc, ctx, name):
        self.nc, self.ctx, self.name = nc, ctx, name
        self.sems = []
        ctx.callback(self.clear)

    def clear(self):
        self.nc.clear_and_free_semaphores(self.sems)
        self.nc.all_engine_barrier()

    def sb(self, name, shape, dt=F32):
        return self.ctx.enter_context(self.nc.sbuf_tensor(f"{self.name}_{name}", shape, dt))

    def ps(self, name, shape):
        return self.ctx.enter_context(self.nc.psum_tensor(f"{self.name}_{name}", shape, F32))

    def sem(self, name):
        self.sems.append(self.nc.alloc_semaphore(name=f"{self.name}_{name}"))
        return self.sems[-1]


def bc(ap, shape):
    return ap.to_broadcast(shape)


def load_x(C, x, constants):
    nc = C.nc
    with ExitStack() as ctx:
        sc = Scope(nc, ctx, "load")
        loaded, zeroed = sc.sem("loaded"), sc.sem("zeroed")
        st = sc.sb("st", [P, TPG, 6])
        mv = sc.sb("mv", [P, TPG, 2])
        block = ctx.enter_context(nc.Block())

        @block.sync
        def _(sp):
            sp.dma_start(C.X[:, 0:C.NT, :], x.rearrange("(n p) d -> p n d", p=P)).then_inc(loaded, 16)
            sp.dma_start(C.ident[:], constants["ident"]).then_inc(loaded, 16)

        @block.gpsimd
        def _(pool):
            nc.gpsimd.memset(C.Y[:], 0.0).then_inc(zeroed, 1)
            nc.gpsimd.memset(C.ones[:], 1.0).then_inc(zeroed, 1)
            nc.gpsimd.memset(C.X[:, C.NT:, :], 0.0).then_inc(zeroed, 1)
            nc.gpsimd.memset(C.MV[:, C.NT:, :], 0.0).then_inc(zeroed, 1)

        @block.vector
        def _(dve):
            dve.wait_ge(loaded, 32)
            with dve.Fori(0, C.NG) as i:
                row_stats(nc, dve, C, C.X, st, mv, i)


def row_stats(nc, dve, C, src, st, mv, i):
    for p in range(TPG):
        nc.vector.bn_stats(st[:, p, :], src[:, i * TPG + p, :])
    dve.drain()
    for p in range(TPG):
        nc.vector.bn_aggr(mv[:, p, :], st[:, p, :])
    dve.drain()
    nc.vector.tensor_copy(C.MV[:, bass.ds(i * TPG, TPG), :], mv[:])


def norm_scales(C, name, eps, second=None):
    nc = C.nc
    with ExitStack() as ctx:
        sc = Scope(nc, ctx, name)
        shifted, rooted = sc.sem("shifted"), sc.sem("rooted")
        block = ctx.enter_context(nc.Block())
        mean, var = C.MV[:, :, 0], C.MV[:, :, 1]

        @block.vector
        def _(dve):
            nc.vector.tensor_scalar(C.tmp[:], var, eps, None, ALU.add).then_inc(shifted, 1)
            dve.wait_ge(rooted, 1)
            nc.vector.reciprocal(C.RS[:], C.tmp[:])
            dve.drain()
            nc.vector.scalar_tensor_tensor(C.NM[:], mean, -1.0, C.RS[:], ALU.mult, ALU.mult)
            if second is not None:
                nc.vector.tensor_tensor(C.tmp[:], C.RS[:], C.RS[:], ALU.mult)
                dve.drain()
                nc.vector.tensor_tensor(C.tmp[:], C.tmp[:], var, ALU.mult)
                dve.drain()
                nc.vector.tensor_scalar(C.tmp[:], C.tmp[:], second, None, ALU.add).then_inc(shifted, 1)
                dve.wait_ge(rooted, 2)
                nc.vector.reciprocal(C.tmp[:], C.tmp[:])
                dve.drain()
                nc.vector.tensor_tensor(C.RS2[:], C.tmp[:], C.RS[:], ALU.mult)
                dve.drain()
                nc.vector.scalar_tensor_tensor(C.NM2[:], mean, -1.0, C.RS2[:], ALU.mult, ALU.mult)

        @block.scalar
        def _(act):
            for n in range(1 if second is None else 2):
                act.wait_ge(shifted, n + 1)
                nc.scalar.activation(C.tmp[:], C.tmp[:], ACT.Sqrt).then_inc(rooted, 1)


def inner_scales(C, name, eps, mean_square):
    nc = C.nc
    with ExitStack() as ctx:
        sc = Scope(nc, ctx, name)
        shifted, rooted = sc.sem("shifted"), sc.sem("rooted")
        block = ctx.enter_context(nc.Block())
        mean, var = C.MV[:, :, 0], C.MV[:, :, 1]

        @block.vector
        def _(dve):
            if mean_square:
                nc.vector.tensor_tensor(C.tmp[:], mean, mean, ALU.mult)
                dve.drain()
                nc.vector.tensor_tensor(C.tmp[:], C.tmp[:], var, ALU.add)
                dve.drain()
                nc.vector.tensor_scalar(C.tmp[:], C.tmp[:], eps, None, ALU.add).then_inc(shifted, 1)
            else:
                nc.vector.tensor_scalar(C.tmp[:], var, eps, None, ALU.add).then_inc(shifted, 1)
            dve.wait_ge(rooted, 1)
            nc.vector.reciprocal(C.RS2[:], C.tmp[:])
            dve.drain()
            if not mean_square:
                nc.vector.scalar_tensor_tensor(C.NM2[:], mean, -1.0, C.RS2[:], ALU.mult, ALU.mult)

        @block.scalar
        def _(act):
            act.wait_ge(shifted, 1)
            nc.scalar.activation(C.tmp[:], C.tmp[:], ACT.Sqrt).then_inc(rooted, 1)



NH, HD = 16, 8
NB = NH // 2
RG, HR = 4, 4
UT = 2
UPG = TPG // UT
VW = HD + 1


def attn16(C, name, mode, W, kT_dram=None):
    nc = C.nc
    cross, linear, rank = mode in ("ctx", "mask"), mode == "linear", mode == "rank"
    to_y = linear or rank
    with ExitStack() as ctx:
        sc = Scope(nc, ctx, name)
        sb, ps, sem = sc.sb, sc.ps, sc.sem
        wq, wo = sb("wq", [P, D]), sb("wo", [P, D])
        bq, bv = sb("bq", [P, 1]), sb("bv", [P, 1])
        bo = sb("bo", [1, D])
        hmask = sb("hmask", [P, HR])
        bkm = sb("bkm", [P, HR])
        if linear:
            wk, wv = sb("wk", [P, 32]), sb("wv", [P, 32])
            wc, we = sb("wc", [32, S]), sb("we", [S, D])
            bk32, bv32 = sb("bk32", [32, 1]), sb("bv32", [32, 1])
            k32, c64 = sb("k32", [32, 2, GT]), sb("c64", [S, 2, GT])
        else:
            wk, wv = sb("wk", [P, D]), sb("wv", [P, D])
            bk = sb("bk", [P, 1])
        if mode == "rope":
            wqr, wkr = sb("wqr", [P, D]), sb("wkr", [P, D])
            cosT, sinT = sb("cosT", [P, S]), sb("sinT", [P, S])
        if mode in ("rope", "linear"):
            t1, t2 = sb("t1", [P, GT]), sb("t2", [P, GT])
            kf = sb("kf", [P, GT])
        if mode in ("rope", "ctx", "mask"):
            table = sb("table", [P, NH, S])
        if mode == "mask":
            keepi, keep = sb("keepi", [P, S], I32), sb("keep", [P, S])
            off = sb("off", [P, S])
        if linear or rank:
            tril = sb("tril", [P, S])
        if rank:
            g1, wr = sb("g1", [P, 1]), sb("wr", [P, D])
            s_own, s_rep = sb("s_own", [P, TPG]), sb("s_rep", [P, TPG, P])
            hidden, r1, r2 = sb("hidden", [P, TPG, S]), sb("r1", [P, TPG, S]), sb("r2", [P, TPG, S])
            prod = sb("prod", [P, D])
        xn, xnT = sb("xn", [P, TPG, D]), sb("xnT", [P, GT])
        xt = sb("xt", [P, UT, D])
        kvb = sb("kvb", [P, GT]) if cross else xnT
        qT = sb("qT", [P, GT])
        kbd = sb("kbd", [P, SPG, HR, S])
        vbd = sb("vbd", [P, SPG, NB, 2, VW])
        s1 = sb("s1", [P, UPG, UT, NH, S])
        mx = sb("mx", [P, UT, NH])
        pT = sb("pT", [P, 2, 4, P])
        rden = sb("rden", [P, UT, NH])
        on, oT = sb("on", [P, UT, D]), sb("oT", [P, UT, P])
        st, mv = sb("st", [P, UT, 6]), sb("mv", [P, TPG, 2])

        ps_s = ps("ps_s", [P, RG, UT * HR * S])
        ps_t = ps("ps_t", [P, 2, 4 * P])
        ps_j = ps("ps_j", [P, GT])
        ps_o = ps("ps_o", [P, 512])
        o_acc = ps_o[:, 0:UT * NH * VW].rearrange("p (t h e) -> p t h e", t=UT, e=VW)
        j_tr = ps_j[:, 0:UT * P].rearrange("p (t q) -> p t q", t=UT)
        j_out = ps_j[:, UT * P:2 * UT * P].rearrange("p (t q) -> p t q", t=UT)

        loaded, prepared = sem("loaded"), sem("prepared")
        kv_loaded = sem("kv_loaded")
        xn_ready, xT_done, xT_ready = sem("xn_ready"), sem("xT_done"), sem("xT_ready")
        q_done, q_ready = sem("q_done"), sem("q_ready")
        k_done, k_ready, v_done, v_ready = sem("k_done"), sem("k_ready"), sem("v_done"), sem("v_ready")
        kf_ready, e_in, e_out = sem("kf_ready"), sem("e_in"), sem("e_out")
        low_done, low_ready = sem("low_done"), sem("low_ready")
        rank_done, rank_in, rank_read = sem("rank_done"), sem("rank_in"), sem("rank_read")
        scores_done, scores_read = sem("scores_done"), sem("scores_read")
        shifted, probs = sem("shifted"), sem("probs")
        pT_done, pT_ready = sem("pT_done"), sem("pT_ready")
        pv_done, on_ready = sem("pv_done"), sem("on_ready")
        oT_done, oT_ready = sem("oT_done"), sem("oT_ready")
        out_done, out_read = sem("out_done"), sem("out_read")
        block = ctx.enter_context(nc.Block())
        loads = [(wq, W["wq"]), (wo, W["wo"]), (wk, W["wk"]), (wv, W["wv"]), (hmask, W["hmask"])]
        if "bo" in W:
            loads.append((bo, W["bo"]))
        if "bq" in W:
            loads.append((bq, W["bq"]))
        if cross:
            loads += [(bk, W["bk"]), (bv, W["bv"])]
        if mode == "rope":
            loads += [(cosT, W["cosT"]), (sinT, W["sinT"])]
        if mode in ("rope", "ctx", "mask"):
            loads.append((table, W["table"]))
        if mode == "mask":
            loads.append((keepi, W["mask"]))
        if linear:
            loads += [(wc, W["wc"]), (we, W["we"]), (bk32, W["bk"]), (bv32, W["bv"])]
        if linear or rank:
            loads.append((tril, W["tril"]))
        if rank:
            loads += [(g1, W["g1"]), (wr, W["wr"])]
        n_loaded = 16 * len(loads)

        @block.sync
        def _(sp):
            for to, of in loads:
                sp.dma_start(to[:], of).then_inc(loaded, 16)
            if cross:
                sp.dma_start(kvb[:], kT_dram[:, 0:GT]).then_inc(kv_loaded, 16)
                with sp.Fori(1, C.NG) as i:
                    sp.wait_ge(v_done, i)
                    sp.dma_start(kvb[:], kT_dram[:, bass.ds(i * GT, GT)]).then_inc(kv_loaded, 16)
                sp.wait_ge(v_done, C.NG)
                sp.dma_start(kvb[:], kT_dram[:, 0:GT]).then_inc(kv_loaded, 16)

        def front_dve(dve, j):
            rs, nm = (C.RS2, C.NM2) if rank else (C.RS, C.NM)
            for p in range(TPG):
                n = j * TPG + p
                last = nc.vector.tensor_scalar(xn[:, p, :], C.X[:, n, :], rs[:, bass.ds(n, 1)],
                                               nm[:, bass.ds(n, 1)], ALU.mult, ALU.add)
            last.then_inc(xn_ready, 1)

        def front_pe(pe, j):
            pe.wait_ge(xn_ready, j + 1)
            for p in range(TPG):
                last = nc.tensor.transpose(ps_j[:, p * P:(p + 1) * P], xn[:, p, :], C.ident[:])
            last.then_inc(xT_done, 1)

        def front_act(act, j):
            act.wait_ge(xT_done, j + 1)
            nc.scalar.activation(xnT[:], ps_j[:], ACT.Copy).then_inc(xT_ready, 1)

        @block.tensor
        def _(pe):
            pe.wait_ge(loaded, n_loaded)
            pe.wait_ge(prepared, 2)

            def queries_keys(u):
                for t in range(UT):
                    for b in range(2):
                        q = 2 * (UT * u + t) + b
                        for g in range(RG):
                            r = slice(32 * g, 32 * g + 32)
                            last = nc.tensor.matmul(ps_s[S * b:S * b + S, g, t * HR * S:(t + 1) * HR * S],
                                                    qT[r, q * S:(q + 1) * S], kbd[r, q, :, :], start=True, stop=True)
                last.then_inc(scores_done, 1)

            def turn_probs(u, m):
                for t in range(4):
                    h = (m % 2) * HR * 2 + 2 * t
                    last = nc.tensor.transpose(ps_t[:, m % 2, t * P:(t + 1) * P],
                                               s1[:, u, m // 2, h:h + 2, :].rearrange("p h k -> p (h k)"), C.ident[:])
                last.then_inc(pT_done, 1)

            def weigh_values(u, m):
                for t in range(4):
                    n = (m % 2) * 4 + t
                    for b in range(2):
                        last = nc.tensor.matmul(o_acc[S * b:S * b + S, m // 2, 2 * n:2 * n + 2, :].rearrange("p h v -> p (h v)"),
                                                pT[:, m % 2, t, S * b:S * b + S],
                                                vbd[:, 2 * (UT * u + m // 2) + b, n, :, :].rearrange("p e v -> p (e v)"),
                                                start=True, stop=True)
                return last

            def turn_output(w):
                pe.wait_ge(on_ready, w + 1)
                for t in range(UT):
                    last = nc.tensor.transpose(j_tr[:, t, :], on[:, t, :], C.ident[:])
                last.then_inc(oT_done, 1)

            def project_output(w):
                pe.wait_ge(oT_ready, w + 1)
                for t in range(UT):
                    last = nc.tensor.matmul(j_out[:, t, :], oT[:, t, :], wo[:], start=True, stop="bo" not in W)
                    if "bo" in W:
                        last = nc.tensor.matmul(j_out[:, t, :], C.ones[0:1, :], bo[0:1, :], start=False, stop=True)
                last.then_inc(out_done, 1)

            def project(j):
                pe.wait_ge(xT_ready, j + 1)
                into = lambda b, w, of: nc.tensor.matmul(ps_s[:, b, :], w[:], of[:], start=True, stop=True)
                into(0, wq, xnT).then_inc(q_done, 1)
                if mode == "rope":
                    into(1, wqr, xnT).then_inc(q_done, 1)
                    into(2, wk, xnT).then_inc(k_done, 1)
                    into(3, wkr, xnT).then_inc(k_done, 1)
                elif linear:
                    nc.tensor.matmul(ps_s[0:32, 1, :], wk[:], xnT[:], start=True, stop=True)
                    nc.tensor.matmul(ps_s[0:32, 2, :], wv[:], xnT[:], start=True, stop=True).then_inc(low_done, 1)
                else:
                    if cross:
                        pe.wait_ge(kv_loaded, j * 16 + 16)
                    into(2, wk, kvb).then_inc(k_done, 1)

            def compress(j):
                if linear:
                    pe.wait_ge(low_ready, j * 2 + 1)
                    nc.tensor.matmul(ps_s[0:S, 3, :], wc[:], k32[:, 0, :], start=True, stop=True)
                    nc.tensor.matmul(ps_s[0:S, 1, :], wc[:], k32[:, 1, :], start=True, stop=True).then_inc(low_done, 1)
                if rank:
                    pe.wait_ge(rank_in, j + 1)
                    for p in range(TPG):
                        last = nc.tensor.transpose(ps_s[:, 3, p * P:(p + 1) * P], s_rep[:, p, :], C.ident[:])
                    last.then_inc(rank_done, 1)

            def expand(j):
                if linear:
                    pe.wait_ge(low_ready, j * 2 + 2)
                    nc.tensor.matmul(ps_s[:, 2, :], we[:], c64[:, 0, :], start=True, stop=True).then_inc(k_done, 1)

            def values(j, half):
                for s in range(half * SPG // 2, (half + 1) * SPG // 2):
                    src = c64[:, 1, s * S:(s + 1) * S] if linear else kvb[:, s * S:(s + 1) * S]
                    for b in range(2):
                        last = nc.tensor.matmul(ps_t[S * b:S * b + S, s // 4, (s % 4) * D:(s % 4 + 1) * D], src,
                                                we[:] if linear else wv[:], start=True, stop=True)
                if half:
                    last.then_inc(v_done, 1)

            front_pe(pe, 0)
            for step in (project, compress, expand):
                step(0)
            values(0, 0)
            values(0, 1)
            with pe.Fori(0, C.NG) as i:
                pe.wait_ge(q_ready, i + 1)
                pe.wait_ge(k_ready, i + 1)
                if rank:
                    pe.wait_ge(rank_read, i + 1)
                queries_keys(0)
                pe.wait_ge(out_read, i * UPG + 1)
                front_pe(pe, i + 1)
                if linear:
                    pe.wait_ge(probs, i * UPG + 1)
                else:
                    pe.wait_ge(scores_read, i * UPG + 2)
                queries_keys(1)
                pe.wait_ge(v_ready, i + 1)
                for u in range(UPG):
                    w = i * UPG + u
                    pe.wait_ge(probs, w + 1)
                    turn_probs(u, 0)
                    turn_probs(u, 1)
                    if u == 1:
                        if not linear:
                            pe.wait_ge(scores_read, i * UPG + 3)
                        project(i + 1)
                        turn_output(w - 1)
                    for m in range(2 * UT):
                        pe.wait_ge(pT_ready, w * 2 * UT + m + 1)
                        last = weigh_values(u, m)
                        if m + 2 < 2 * UT:
                            turn_probs(u, m + 2)
                    last.then_inc(pv_done, 1)
                project_output(w - 1)
                compress(i + 1)
                if not linear:
                    values(i + 1, 0)
                pe.wait_ge(out_read, i * UPG + 2)
                turn_output(w)
                expand(i + 1)
                if linear:
                    values(i + 1, 0)
                values(i + 1, 1)
                project_output(w)

        @block.scalar
        def _(act):
            act.wait_ge(loaded, n_loaded)
            act.wait_ge(prepared, 2)

            def output_copy(w):
                act.wait_ge(oT_done, w + 1)
                if cross:
                    last = nc.scalar.activation(oT[:], j_tr, ACT.Identity, bias=bv[:, 0:1])
                else:
                    last = nc.scalar.activation(oT[:], j_tr, ACT.Copy)
                last.then_inc(oT_ready, 1)

            def low_rank(j):
                act.wait_ge(low_done, j * 2 + 1)
                nc.scalar.activation(k32[:, 0, :], ps_s[0:32, 1, :], ACT.Identity, bias=bk32[:, 0:1])
                nc.scalar.activation(k32[:, 1, :], ps_s[0:32, 2, :], ACT.Identity,
                                     bias=bv32[:, 0:1]).then_inc(low_ready, 1)
                act.wait_ge(e_in, j * 2 + 1)
                nc.scalar.activation(t2[:], t2[:], ACT.Exp).then_inc(e_out, 1)

            def compressed(j):
                act.wait_ge(low_done, j * 2 + 2)
                nc.scalar.activation(c64[:, 0, :], ps_s[0:S, 3, :], ACT.Copy)
                nc.scalar.activation(c64[:, 1, :], ps_s[0:S, 1, :], ACT.Copy).then_inc(low_ready, 1)
                act.wait_ge(e_in, j * 2 + 2)
                nc.scalar.activation(t2[:], t2[:], ACT.Exp).then_inc(e_out, 1)

            def diagonal_keys(j):
                if mode in ("rope", "linear"):
                    act.wait_ge(kf_ready, j + 1)
                else:
                    act.wait_ge(k_done, j + 1)
                for h in range(HR):
                    to = kbd[:, :, h, :]
                    if mode in ("rope", "linear"):
                        last = nc.scalar.activation(to, kf[:].rearrange("p (s k) -> p s k", k=S), ACT.Copy,
                                                    scale=hmask[:, h:h + 1])
                    else:
                        last = nc.scalar.activation(to, ps_s[:, 2, :].rearrange("p (s k) -> p s k", k=S),
                                                    ACT.Identity, scale=hmask[:, h:h + 1], bias=bkm[:, h:h + 1])
                last.then_inc(k_ready, 1)

            front_act(act, 0)
            if linear:
                low_rank(0)
                compressed(0)
            diagonal_keys(0)
            with act.Fori(0, C.NG) as i:
                for u in range(UPG):
                    w = i * UPG + u
                    if not linear:
                        act.wait_ge(shifted, w + 1)
                        nc.scalar.activation(s1[:, u, :, :, :], s1[:, u, :, :, :], ACT.Exp).then_inc(probs, 1)
                    if u == 0:
                        front_act(act, i + 1)
                    for m in range(2 * UT):
                        if u == 1 and m == 2:
                            output_copy(w - 1)
                            if linear:
                                low_rank(i + 1)
                        act.wait_ge(pT_done, w * 2 * UT + m + 1)
                        nc.scalar.activation(pT[:, m % 2, :, :], ps_t[:, m % 2, :].rearrange("p (t q) -> p t q", q=P),
                                             ACT.Copy).then_inc(pT_ready, 1)
                if linear:
                    output_copy(w)
                    compressed(i + 1)
                diagonal_keys(i + 1)
                if not linear:
                    output_copy(w)

        @block.gpsimd
        def _(pool):
            nc.gpsimd.memset(vbd[:], 0.0)
            pool.drain()
            for e in range(2):
                nc.gpsimd.memset(vbd[S * e:S * e + S, :, :, e, HD:VW], 1.0)
            pool.drain()
            nc.gpsimd.memset(xt[:], 0.0).then_inc(prepared, 1)
            if rank:
                pool.wait_ge(loaded, n_loaded)

        @block.vector
        def _(dve):
            dve.wait_ge(loaded, n_loaded)
            if cross:
                nc.vector.tensor_scalar(bkm[:], hmask[:], bk[:, 0:1], None, ALU.mult)
            else:
                nc.vector.memset(bkm[:], 0.0)
            if mode == "rope":
                for w, r in ((wq, wqr), (wk, wkr)):
                    pairs, turned = w[:].rearrange("p (n e) -> p n e", e=2), r[:].rearrange("p (n e) -> p n e", e=2)
                    nc.vector.tensor_scalar(turned[:, :, 0], pairs[:, :, 1], -1.0, None, ALU.mult)
                    nc.vector.tensor_copy(turned[:, :, 1], pairs[:, :, 0])
            if mode == "mask":
                nc.vector.tensor_copy(keep[:], keepi[:])
                dve.drain()
                nc.vector.tensor_scalar(keep[:], keep[:], 0.0, None, ALU.not_equal)
                dve.drain()
                nc.vector.tensor_scalar(off[:], keep[:], 1e9, -1e9, ALU.mult, ALU.add)
                nc.vector.tensor_tensor(table[:], table[:], bc(keep[:].unsqueeze(1), [P, NH, S]), ALU.mult)
                dve.drain()
                nc.vector.tensor_tensor(table[:], table[:], bc(off[:].unsqueeze(1), [P, NH, S]), ALU.add)
            if rank:
                for w in (wq, wk, wv):
                    nc.vector.tensor_scalar(w[:], w[:], g1[:, 0:1], None, ALU.mult)
            dve.drain()
            nc.vector.memset(mv[:], 0.0)
            nc.vector.memset(mx[:], 0.0).then_inc(scores_read, 1)
            nc.vector.memset(rden[:], 0.0).then_inc(out_read, 1)
            dve.wait_ge(prepared, 1)
            dve.drain()
            nc.vector.memset(st[:], 0.0).then_inc(prepared, 1)

            def rotate(to, plain, turned, at):
                cs, sn = (bc(w[:].unsqueeze(1), [P, SPG, S]) for w in (cosT, sinT))
                v = lambda a: a.rearrange("p (s k) -> p s k", k=S)
                nc.vector.tensor_tensor(v(t1[:]), v(plain), cs, ALU.mult)
                nc.vector.tensor_tensor(v(t2[:]), v(turned), sn, ALU.mult)
                dve.drain()
                return nc.vector.tensor_tensor(to, t1[:], t2[:], ALU.add)

            def feature(to, src, bias, count):
                nc.vector.tensor_scalar(t1[:], src, bias, 0.0, ALU.add, ALU.max)
                nc.vector.tensor_scalar(t2[:], src, bias, 0.0, ALU.add, ALU.min).then_inc(e_in, 1)
                dve.drain()
                dve.wait_ge(e_out, count)
                return nc.vector.tensor_tensor(to, t1[:], t2[:], ALU.add)

            def scores(u, w):
                dve.wait_ge(scores_done, w + 1)
                out = s1[:, u, :, :, :]
                if mode in ("rope", "ctx"):
                    nc.vector.tensor_tensor(out.rearrange("p t (g h) k -> p t g (h k)", g=RG),
                                            ps_s[:].rearrange("p g (t x) -> p t g x", t=UT),
                                            bc(table[:].rearrange("p (g h) k -> p g (h k)", g=RG).unsqueeze(1),
                                               [P, UT, RG, HR * S]), ALU.add).then_inc(scores_read, 1)
                else:
                    for t in range(UT):
                        with_ = tril[:] if linear else hidden[:, UT * u + t, :] if rank else keep[:]
                        last = nc.vector.tensor_tensor(
                            out[:, t, :, :].rearrange("p (g h) k -> p g h k", g=RG),
                            ps_s[:, :, t * HR * S:(t + 1) * HR * S].rearrange("p g (h k) -> p g h k", k=S),
                            bc(with_.unsqueeze(1).unsqueeze(1), [P, RG, HR, S]), ALU.add if rank else ALU.mult)
                    last.then_inc(probs if linear else scores_read, 1)
                    if linear:
                        return
                dve.drain()
                if mode == "mask":
                    nc.vector.tensor_tensor(out, out, bc(table[:].unsqueeze(1), [P, UT, NH, S]), ALU.add)
                    dve.drain()
                nc.vector.tensor_reduce(mx[:], out, AX, ALU.max)
                dve.drain()
                nc.vector.tensor_tensor(out, out, bc(mx[:].unsqueeze(3), [P, UT, NH, S]),
                                        ALU.subtract).then_inc(shifted, 1)

            def normalise(w):
                dve.wait_ge(pv_done, w + 1)
                if linear:
                    nc.vector.tensor_scalar(rden[:], o_acc[:, :, :, HD], 1e-6, None, ALU.add)
                    dve.drain()
                    nc.vector.reciprocal(rden[:], rden[:])
                else:
                    nc.vector.reciprocal(rden[:], o_acc[:, :, :, HD])
                dve.drain()
                nc.vector.tensor_tensor(on[:].rearrange("p t (h e) -> p t h e", e=HD), o_acc[:, :, :, 0:HD],
                                        bc(rden[:].unsqueeze(3), [P, UT, NH, HD]), ALU.mult).then_inc(on_ready, 1)

            def residual(u, i, w):
                rows = bass.ds(i * TPG + u * UT, UT)
                if to_y:
                    for t in range(UT):
                        n = i * TPG + u * UT + t
                        nc.vector.tensor_scalar(xt[:, t, :], C.X[:, n, :], C.RS[:, bass.ds(n, 1)],
                                                C.NM[:, bass.ds(n, 1)], ALU.mult, ALU.add)
                    dve.drain()
                dve.wait_ge(out_done, w + 1)
                to = (C.Y if to_y else C.X)[:, rows, :]
                nc.vector.tensor_tensor(to, j_out, xt[:] if to_y else to, ALU.add).then_inc(out_read, 1)
                dve.drain()
                for t in range(UT):
                    nc.vector.bn_stats(st[:, t, :], (C.Y if to_y else C.X)[:, i * TPG + u * UT + t, :])
                dve.drain()
                for t in range(UT):
                    nc.vector.bn_aggr(mv[:, u * UT + t, :], st[:, t, :])

            def router_scores(j):
                for p in range(TPG):
                    n = j * TPG + p
                    nc.vector.tensor_scalar(xt[:, 0, :], C.X[:, n, :], C.RS[:, bass.ds(n, 1)],
                                            C.NM[:, bass.ds(n, 1)], ALU.mult, ALU.add)
                    dve.drain()
                    nc.vector.tensor_tensor(prod[:], xt[:, 0, :], wr[:], ALU.mult)
                    dve.drain()
                    nc.vector.tensor_reduce(s_own[:, p:p + 1], prod[:], AX, ALU.add)
                dve.drain()
                nc.vector.tensor_copy(s_rep[:], bc(s_own[:].unsqueeze(2), [P, TPG, P])).then_inc(rank_in, 1)

            def rank_order(j):
                dve.wait_ge(rank_done, j + 1)
                row = ps_s[:, 3, :].rearrange("p (t b k) -> p t b k", t=TPG, b=2)
                for b in range(2):
                    r = slice(S * b, S * b + S)
                    own = bc(s_own[r, :].unsqueeze(2), [S, TPG, S])
                    nc.vector.tensor_tensor(r1[r, :, :], row[r, :, b, :], own, ALU.is_gt)
                    last = nc.vector.tensor_tensor(r2[r, :, :], row[r, :, b, :], own, ALU.is_equal)
                last.then_inc(rank_read, 1)
                dve.drain()
                nc.vector.tensor_tensor(r2[:], r2[:], bc(tril[:].unsqueeze(1), [P, TPG, S]), ALU.mult)
                dve.drain()
                nc.vector.tensor_tensor(r1[:], r1[:], r2[:], ALU.add)
                dve.drain()
                nc.vector.tensor_scalar(hidden[:], r1[:], BIG, -BIG, ALU.mult, ALU.add)
                dve.drain()

            def queries(j):
                if mode == "rope":
                    dve.wait_ge(q_done, j * 2 + 2)
                    rotate(qT[:], ps_s[:, 0, :], ps_s[:, 1, :], 0)
                    dve.drain()
                    nc.vector.tensor_scalar(qT[:], qT[:], HD ** -0.5, None, ALU.mult).then_inc(q_ready, 1)
                    dve.wait_ge(k_done, j * 2 + 2)
                    rotate(kf[:], ps_s[:, 2, :], ps_s[:, 3, :], 1).then_inc(kf_ready, 1)
                elif linear:
                    dve.wait_ge(q_done, j + 1)
                    feature(qT[:], ps_s[:, 0, :], bq[:, 0:1], j * 2 + 1).then_inc(q_ready, 1)
                    dve.drain()
                else:
                    dve.wait_ge(q_done, j + 1)
                    scale = 1.0 if mode == "mask" else HD ** -0.5
                    if cross:
                        nc.vector.tensor_scalar(qT[:], ps_s[:, 0, :], bq[:, 0:1], scale, ALU.add,
                                                ALU.mult).then_inc(q_ready, 1)
                    else:
                        nc.vector.tensor_scalar(qT[:], ps_s[:, 0, :], scale, None, ALU.mult).then_inc(q_ready, 1)

            def key_features(j):
                dve.wait_ge(k_done, j + 1)
                feature(kf[:], ps_s[:, 2, :], 0.0, j * 2 + 2).then_inc(kf_ready, 1)

            def diagonal_values(j):
                dve.wait_ge(v_done, j + 1)
                for t in range(2):
                    for e in range(2):
                        r = slice(S * e, S * e + S)
                        src = ps_t[r, t, :].rearrange("p (s n e d) -> p s n e d", s=4, n=NB, e=2)[:, :, :, e, :]
                        last = nc.vector.tensor_copy(vbd[r, 4 * t:4 * t + 4, :, e, 0:HD], src)
                last.then_inc(v_ready, 1)

            front_dve(dve, 0)
            if rank:
                router_scores(0)
            queries(0)
            if rank:
                rank_order(0)
            if linear:
                key_features(0)
            diagonal_values(0)
            front_dve(dve, 1)
            with dve.Fori(0, C.NG) as i:
                w = i * UPG
                scores(0, w)
                scores(1, w + 1)
                normalise(w)
                queries(i + 1)
                if rank:
                    router_scores(i + 1)
                residual(0, i, w)
                normalise(w + 1)
                if rank:
                    rank_order(i + 1)
                if linear:
                    key_features(i + 1)
                diagonal_values(i + 1)
                front_dve(dve, i + 2)
                residual(1, i, w + 1)
                dve.drain()
                nc.vector.tensor_copy(C.MV[:, bass.ds(i * TPG, TPG), :], mv[:])


class Front:

    def __init__(self, C, sc, bank, src, scale, shift):
        self.C, self.nc, self.bank, self.src, self.scale, self.shift = C, C.nc, bank, src, scale, shift
        self.xn, self.xnT = sc.sb("xn", [P, TPG, D]), sc.sb("xnT", [P, GT])
        self.xn_ready, self.xT_done, self.xT_ready = sc.sem("xn_ready"), sc.sem("xT_done"), sc.sem("xT_ready")

    def dve(self, j):
        nc = self.nc
        for p in range(TPG):
            n = j * TPG + p
            if self.shift is None:
                last = nc.vector.tensor_scalar(self.xn[:, p, :], self.src[:, n, :], self.scale[:, bass.ds(n, 1)], None,
                                               ALU.mult)
            else:
                last = nc.vector.tensor_scalar(self.xn[:, p, :], self.src[:, n, :], self.scale[:, bass.ds(n, 1)],
                                               self.shift[:, bass.ds(n, 1)], ALU.mult, ALU.add)
        last.then_inc(self.xn_ready, 1)

    def pe(self, pe, j):
        pe.wait_ge(self.xn_ready, j + 1)
        for p in range(TPG):
            last = self.nc.tensor.transpose(self.bank[:, p * P:(p + 1) * P], self.xn[:, p, :], self.C.ident[:])
        last.then_inc(self.xT_done, 1)

    def act(self, act, j):
        act.wait_ge(self.xT_done, j + 1)
        self.nc.scalar.activation(self.xnT[:], self.bank[:], ACT.Copy).then_inc(self.xT_ready, 1)


def group_stats(nc, dve, C, src, st, mv, i):
    for p in range(TPG):
        nc.vector.bn_stats(st[:, p, :], src[:, i * TPG + p, :])
    dve.drain()
    for p in range(TPG):
        nc.vector.bn_aggr(mv[:, p, :], st[:, p, :])
    dve.drain()
    nc.vector.tensor_copy(C.MV[:, bass.ds(i * TPG, TPG), :], mv[:])


def rows(t, i):
    return t[:, bass.ds(i * TPG, TPG), :]


def affine_norm(C, name, gamma_d, beta_d):
    nc = C.nc
    with ExitStack() as ctx:
        sc = Scope(nc, ctx, name)
        gamma, beta = sc.sb("gamma", [P, D]), sc.sb("beta", [P, D])
        y = sc.sb("y", [P, TPG, D])
        st, mv = sc.sb("st", [P, TPG, 6]), sc.sb("mv", [P, TPG, 2])
        loaded = sc.sem("loaded")
        block = ctx.enter_context(nc.Block())

        @block.sync
        def _(sp):
            sp.dma_start(gamma[:], gamma_d[:]).then_inc(loaded, 16)
            sp.dma_start(beta[:], beta_d[:]).then_inc(loaded, 16)

        @block.vector
        def _(dve):
            dve.wait_ge(loaded, 32)
            with dve.Fori(0, C.NG) as i:
                for p in range(TPG):
                    n = i * TPG + p
                    nc.vector.tensor_scalar(y[:, p, :], C.Y[:, n, :], C.RS2[:, bass.ds(n, 1)], C.NM2[:, bass.ds(n, 1)],
                                            ALU.mult, ALU.add)
                dve.drain()
                nc.vector.tensor_tensor(y[:], y[:], bc(gamma[:].unsqueeze(1), [P, TPG, D]), ALU.mult)
                dve.drain()
                nc.vector.tensor_tensor(y[:], y[:], bc(beta[:].unsqueeze(1), [P, TPG, D]), ALU.add)
                dve.drain()
                nc.vector.tensor_tensor(rows(C.X, i), rows(C.X, i), y[:], ALU.add)
                dve.drain()
                group_stats(nc, dve, C, C.X, st, mv, i)
                dve.drain()


def gated_ffn(C, name, W):
    nc = C.nc
    F = W["w1"].shape[1]
    chunks = [(f, min(P, F - f)) for f in range(0, F, P)]
    NF = len(chunks)
    with ExitStack() as ctx:
        sc = Scope(nc, ctx, name)
        sb, ps, sem = sc.sb, sc.ps, sc.sem
        w1, w2, w3 = sb("w1", [P, F]), sb("w2", [P, F]), sb("w3", [P, NF, D])
        g = sb("g", [P, 1])
        act_b, hid = sb("act", [P, NF, GT]), sb("hid", [P, NF, GT])
        st, mv = sb("st", [P, TPG, 6]), sb("mv", [P, TPG, 2])
        ps_j, ps_o = ps("ps_j", [P, GT]), ps("ps_o", [P, GT])
        ps_u, ps_v = ps("ps_u", [P, NF, GT]), ps("ps_v", [P, NF, GT])
        fr = Front(C, sc, ps_j, C.Y, C.RS2, None)
        loaded, folded = sem("loaded"), sem("folded")
        gate_done, up_done, gated, hidden = sem("gate_done"), sem("up_done"), sem("gated"), sem("hidden")
        out_done, out_read = sem("out_done"), sem("out_read")
        block = ctx.enter_context(nc.Block())

        @block.sync
        def _(sp):
            for to, of in ((w1[:], W["w1"]), (w2[:], W["w2"]), (g[:], W["g"])):
                sp.dma_start(to, of).then_inc(loaded, 16)
            for c, (f, n) in enumerate(chunks):
                sp.dma_start(w3[0:n, c, :], W["w3"][f:f + n, :]).then_inc(loaded, 16)

        n_loaded = 16 * (3 + NF)

        @block.tensor
        def _(pe):
            pe.wait_ge(loaded, n_loaded)
            pe.wait_ge(folded, 1)
            fr.pe(pe, 0)
            with pe.Fori(0, C.NG) as i:
                pe.wait_ge(fr.xT_ready, i + 1)
                for w, to, done in ((w1, ps_u, gate_done), (w2, ps_v, up_done)):
                    for c, (f, n) in enumerate(chunks):
                        nc.tensor.matmul(to[0:n, c, :], w[:, f:f + n], fr.xnT[:], start=True,
                                         stop=True).then_inc(done, 1)
                fr.pe(pe, i + 1)
                pe.wait_ge(out_read, i + 1)
                pe.wait_ge(hidden, i * NF + NF)
                for p in range(TPG):
                    for c, (f, n) in enumerate(chunks):
                        last = nc.tensor.matmul(ps_o[:, p * D:(p + 1) * D], hid[0:n, c, p * P:(p + 1) * P],
                                                w3[0:n, c, :], start=(c == 0), stop=(c == NF - 1))
                last.then_inc(out_done, 1)

        @block.scalar
        def _(act):
            fr.act(act, 0)
            with act.Fori(0, C.NG) as i:
                for c, (f, n) in enumerate(chunks):
                    act.wait_ge(gate_done, i * NF + c + 1)
                    nc.scalar.activation(act_b[0:n, c, :], ps_u[0:n, c, :], ACT.Silu).then_inc(gated, 1)
                fr.act(act, i + 1)

        @block.vector
        def _(dve):
            dve.wait_ge(loaded, n_loaded)
            nc.vector.tensor_scalar(w1[:], w1[:], g[:, 0:1], None, ALU.mult)
            nc.vector.tensor_scalar(w2[:], w2[:], g[:, 0:1], None, ALU.mult).then_inc(folded, 1)
            nc.vector.memset(mv[:], 0.0).then_inc(out_read, 1)
            fr.dve(0)
            with dve.Fori(0, C.NG) as i:
                dve.wait_ge(fr.xT_done, i + 1)
                fr.dve(i + 1)
                nc.vector.tensor_tensor(rows(C.X, i), rows(C.X, i), rows(C.Y, i), ALU.add)
                for c, (f, n) in enumerate(chunks):
                    dve.wait_ge(up_done, i * NF + c + 1)
                    dve.wait_ge(gated, i * NF + c + 1)
                    nc.vector.tensor_tensor(hid[0:n, c, :], act_b[0:n, c, :], ps_v[0:n, c, :],
                                            ALU.mult).then_inc(hidden, 1)
                dve.wait_ge(out_done, i + 1)
                nc.vector.tensor_tensor(rows(C.X, i), ps_o[:].rearrange("p (t d) -> p t d", d=D), rows(C.X, i),
                                        ALU.add).then_inc(out_read, 1)
                dve.drain()
                group_stats(nc, dve, C, C.X, st, mv, i)


NE = 8


def first_max(nc, dve, values, falling, onehot, best, place):
    wide = [P, TPG, NE]
    nc.vector.tensor_reduce(best[:], values, AX, ALU.max)
    dve.drain()
    nc.vector.tensor_tensor(onehot[:], values, bc(best[:].unsqueeze(2), wide), ALU.is_ge)
    dve.drain()
    nc.vector.tensor_tensor(onehot[:], onehot[:], bc(falling[:].unsqueeze(1), wide), ALU.mult)
    dve.drain()
    nc.vector.tensor_reduce(place[:], onehot[:], AX, ALU.max)
    dve.drain()
    nc.vector.tensor_tensor(onehot[:], onehot[:], bc(place[:].unsqueeze(2), wide), ALU.is_equal)
    dve.drain()


def lora_ffn(C, name, W):
    nc = C.nc
    F, R = W["wi"].shape[1], W["B"].shape[0]
    NF, RE = F // P, R // NE
    with ExitStack() as ctx:
        sc = Scope(nc, ctx, name)
        sb, ps, sem = sc.sb, sc.ps, sc.sem
        wi, wo, ga, lb = sb("wi", [P, F]), sb("wo", [P, NF, D]), sb("ga", [P, NE + R]), sb("lb", [R, F])
        gb, wib, wob, falling = sb("gb", [P, NE]), sb("wib", [P, NF]), sb("wob", [1, D]), sb("falling", [P, NE])
        logits, onehot = sb("logits", [P, TPG, NE]), sb("onehot", [P, TPG, NE])
        best, place = sb("best", [P, TPG]), sb("place", [P, TPG])
        low, lowT = sb("low", [P, TPG, R]), sb("lowT", [R, GT])
        hid = sb("hid", [P, NF, GT])
        st, mv = sb("st", [P, TPG, 6]), sb("mv", [P, TPG, 2])
        ps_j, ps_o = ps("ps_j", [P, GT]), ps("ps_o", [P, GT])
        ps_g, ps_l, ps_h = ps("ps_g", [P, TPG, NE + R]), ps("ps_l", [R, GT]), ps("ps_h", [P, NF, GT])
        fr = Front(C, sc, ps_j, C.X, C.RS, C.NM)
        loaded = sem("loaded")
        gate_done, low_ready, lowT_done, lowT_ready = (sem(n) for n in ("gate_done", "low_ready", "lowT_done", "lowT_ready"))
        hid_done, hid_ready, out_done, out_read = (sem(n) for n in ("hid_done", "hid_ready", "out_done", "out_read"))
        block = ctx.enter_context(nc.Block())
        loads = [(wi[:], W["wi"]), (wo[:], W["wo"].rearrange("(c p) d -> p c d", p=P)), (ga[:], W["ga"]), (lb[:], W["B"]),
                 (gb[:], W["gb"]), (wib[:], W["wib"]), (wob[:], W["wob"]), (falling[:], W["falling"])]
        n_loaded = 16 * len(loads)

        @block.sync
        def _(sp):
            for to, of in loads:
                sp.dma_start(to, of).then_inc(loaded, 16)

        @block.tensor
        def _(pe):
            pe.wait_ge(loaded, n_loaded)
            fr.pe(pe, 0)
            with pe.Fori(0, C.NG) as i:
                pe.wait_ge(fr.xT_ready, i + 1)
                for p in range(TPG):
                    last = nc.tensor.matmul(ps_g[:, p, :], fr.xnT[:, p * P:(p + 1) * P], ga[:], start=True, stop=True)
                last.then_inc(gate_done, 1)
                for c in range(NF):
                    nc.tensor.matmul(ps_h[:, c, :], wi[:, c * P:(c + 1) * P], fr.xnT[:], start=True, stop=False)
                pe.wait_ge(low_ready, i + 1)
                for p in range(TPG):
                    last = nc.tensor.transpose(ps_l[:, p * P:(p + 1) * P], low[:, p, :], C.ident[:])
                last.then_inc(lowT_done, 1)
                fr.pe(pe, i + 1)
                pe.wait_ge(lowT_ready, i + 1)
                for c in range(NF):
                    nc.tensor.matmul(ps_h[:, c, :], lb[:, c * P:(c + 1) * P], lowT[:], start=False,
                                     stop=True).then_inc(hid_done, 1)
                pe.wait_ge(out_read, i + 1)
                pe.wait_ge(hid_ready, i * NF + NF)
                for p in range(TPG):
                    o = ps_o[:, p * D:(p + 1) * D]
                    for c in range(NF):
                        nc.tensor.matmul(o, hid[:, c, p * P:(p + 1) * P], wo[:, c, :], start=(c == 0), stop=False)
                    last = nc.tensor.matmul(o, C.ones[0:1, :], wob[0:1, :], start=False, stop=True)
                last.then_inc(out_done, 1)

        @block.scalar
        def _(act):
            act.wait_ge(loaded, n_loaded)
            fr.act(act, 0)
            with act.Fori(0, C.NG) as i:
                act.wait_ge(lowT_done, i + 1)
                nc.scalar.activation(lowT[:], ps_l[:], ACT.Copy).then_inc(lowT_ready, 1)
                fr.act(act, i + 1)
                for c in range(NF):
                    act.wait_ge(hid_done, i * NF + c + 1)
                    nc.scalar.activation(hid[:, c, :], ps_h[:, c, :], ACT.Relu, bias=wib[:, c:c + 1]).then_inc(hid_ready, 1)

        @block.vector
        def _(dve):
            dve.wait_ge(loaded, n_loaded)
            nc.vector.memset(mv[:], 0.0).then_inc(out_read, 1)
            fr.dve(0)
            with dve.Fori(0, C.NG) as i:
                dve.wait_ge(gate_done, i + 1)
                nc.vector.tensor_tensor(logits[:], ps_g[:, :, 0:NE], bc(gb[:].unsqueeze(1), [P, TPG, NE]), ALU.add)
                dve.drain()
                first_max(nc, dve, logits[:], falling, onehot, best, place)
                for p in range(TPG):
                    last = nc.vector.tensor_tensor(low[:, p, :].rearrange("p (e r) -> p e r", r=RE),
                                                   ps_g[:, p, NE:].rearrange("p (e r) -> p e r", r=RE),
                                                   bc(onehot[:, p, :].unsqueeze(2), [P, NE, RE]), ALU.mult)
                last.then_inc(low_ready, 1)
                fr.dve(i + 1)
                dve.wait_ge(out_done, i + 1)
                nc.vector.tensor_tensor(rows(C.X, i), ps_o[:].rearrange("p (t d) -> p t d", d=D), rows(C.X, i),
                                        ALU.add).then_inc(out_read, 1)
                dve.drain()
                group_stats(nc, dve, C, C.X, st, mv, i)


def topk_ffn(C, name, W):
    nc = C.nc
    F = W["w1"].shape[2]
    NF = F // P
    with ExitStack() as ctx:
        sc = Scope(nc, ctx, name)
        sb, ps, sem = sc.sb, sc.ps, sc.sem
        w1, w2, wr = sb("w1", [P, NE, F]), sb("w2", [P, NE, NF, D]), sb("wr", [P, NE])
        falling = sb("falling", [P, NE])
        prob, rest = sb("prob", [P, TPG, NE]), sb("rest", [P, TPG, NE])
        one1, one2 = sb("one1", [P, TPG, NE]), sb("one2", [P, TPG, NE])
        best1, best2, place, total = (sb(n, [P, TPG]) for n in ("best1", "best2", "place", "total"))
        cw = sb("cw", [P, TPG, NE])
        hid = sb("hid", [P, 2, NF, GT])
        acc = sb("acc", [P, TPG, D])
        st, mv = sb("st", [P, TPG, 6]), sb("mv", [P, TPG, 2])
        ps_j = ps("ps_j", [P, GT])
        ps_g = ps("ps_g", [P, TPG, NE])
        ps_h, ps_o = ps("ps_h", [P, 2, NF, GT]), ps("ps_o", [P, 2, GT])
        fr = Front(C, sc, ps_j, C.X, C.RS, C.NM)
        loaded = sem("loaded")
        gate_done, shifted, exped = sem("gate_done"), sem("shifted"), sem("exped")
        hid_done, hid_ready, out_done, out_read = (sem(n) for n in ("hid_done", "hid_ready", "out_done", "out_read"))
        block = ctx.enter_context(nc.Block())
        loads = [(w1[:], W["w1"].rearrange("e d f -> d e f")),
                 (wr[:], W["wr"]), (falling[:], W["falling"])]
        loads += [(w2[:, e, :, :], W["w2"][e].rearrange("(c p) d -> p c d", p=P)) for e in range(NE)]
        n_loaded = 16 * len(loads)

        @block.sync
        def _(sp):
            for to, of in loads:
                sp.dma_start(to, of).then_inc(loaded, 16)

        @block.tensor
        def _(pe):
            pe.wait_ge(loaded, n_loaded)

            def expert_in(i, e):
                if e >= 2:
                    pe.wait_ge(hid_ready, i * NE + e - 1)
                for c in range(NF):
                    last = nc.tensor.matmul(ps_h[:, e % 2, c, :], w1[:, e, c * P:(c + 1) * P], fr.xnT[:],
                                            start=True, stop=True)
                last.then_inc(hid_done, 1)

            def expert_out(i, e):
                pe.wait_ge(hid_ready, i * NE + e + 1)
                pe.wait_ge(out_read, i * NE + e + 1)
                for p in range(TPG):
                    for c in range(NF):
                        last = nc.tensor.matmul(ps_o[:, e % 2, p * D:(p + 1) * D], hid[:, e % 2, c, p * P:(p + 1) * P],
                                                w2[:, e, c, :], start=(c == 0), stop=(c == NF - 1))
                last.then_inc(out_done, 1)

            fr.pe(pe, 0)
            with pe.Fori(0, C.NG) as i:
                pe.wait_ge(fr.xT_ready, i + 1)
                for p in range(TPG):
                    last = nc.tensor.matmul(ps_g[:, p, :], fr.xnT[:, p * P:(p + 1) * P], wr[:], start=True, stop=True)
                last.then_inc(gate_done, 1)
                expert_in(i, 0)
                for e in range(NE):
                    if e + 1 < NE:
                        expert_in(i, e + 1)
                    else:
                        fr.pe(pe, i + 1)
                    expert_out(i, e)

        @block.scalar
        def _(act):
            fr.act(act, 0)
            with act.Fori(0, C.NG) as i:
                act.wait_ge(shifted, i + 1)
                nc.scalar.activation(prob[:], prob[:], ACT.Exp).then_inc(exped, 1)
                for e in range(NE):
                    act.wait_ge(hid_done, i * NE + e + 1)
                    if e >= 2:
                        act.wait_ge(out_done, i * NE + e - 1)
                    nc.scalar.activation(hid[:, e % 2, :, :], ps_h[:, e % 2, :, :], ACT.Silu).then_inc(hid_ready, 1)
                fr.act(act, i + 1)

        @block.vector
        def _(dve):
            dve.wait_ge(loaded, n_loaded)
            nc.vector.memset(mv[:], 0.0).then_inc(out_read, 1)
            nc.vector.memset(st[:], 0.0).then_inc(out_read, 1)
            fr.dve(0)
            wide = [P, TPG, NE]
            over = lambda t: bc(t[:].unsqueeze(2), wide)
            with dve.Fori(0, C.NG) as i:
                dve.wait_ge(gate_done, i + 1)
                nc.vector.tensor_reduce(best1[:], ps_g[:], AX, ALU.max)
                dve.drain()
                nc.vector.tensor_tensor(prob[:], ps_g[:], over(best1), ALU.subtract).then_inc(shifted, 1)
                dve.wait_ge(fr.xT_done, i + 1)
                fr.dve(i + 1)
                dve.wait_ge(exped, i + 1)
                nc.vector.tensor_reduce(total[:], prob[:], AX, ALU.add)
                dve.drain()
                nc.vector.reciprocal(total[:], total[:])
                dve.drain()
                nc.vector.tensor_tensor(prob[:], prob[:], over(total), ALU.mult)
                dve.drain()
                first_max(nc, dve, prob[:], falling, one1, best1, place)
                nc.vector.scalar_tensor_tensor(rest[:], one1[:], -2.0, prob[:], ALU.mult, ALU.add)
                dve.drain()
                first_max(nc, dve, rest[:], falling, one2, best2, place)
                nc.vector.tensor_tensor(total[:], best1[:], best2[:], ALU.add)
                dve.drain()
                nc.vector.tensor_scalar(total[:], total[:], 1e-9, None, ALU.max)
                dve.drain()
                nc.vector.reciprocal(total[:], total[:])
                nc.vector.tensor_tensor(one1[:], one1[:], one2[:], ALU.add)
                dve.drain()
                nc.vector.tensor_tensor(cw[:], prob[:], over(total), ALU.mult)
                dve.drain()
                nc.vector.tensor_tensor(cw[:], cw[:], one1[:], ALU.mult)
                dve.drain()
                for e in range(NE):
                    dve.wait_ge(out_done, i * NE + e + 1)
                    for p in range(TPG):
                        o = ps_o[:, e % 2, p * D:(p + 1) * D]
                        before = C.X[:, i * TPG + p, :] if e == 0 else acc[:, p, :]
                        to = C.X[:, i * TPG + p, :] if e == NE - 1 else acc[:, p, :]
                        last = nc.vector.scalar_tensor_tensor(to, o, cw[:, p, e:e + 1], before, ALU.mult, ALU.add)
                    last.then_inc(out_read, 1)
                    dve.drain()



HW = 64
UH = 8
NJ = UH // 2


def attn64(C, name, W, groups_of_heads, q_per_kv, kT_dram=None):
    nc = C.nc
    HG, NK = groups_of_heads, NJ // q_per_kv
    KH = HG * NK
    chunks = [("q", c) for c in range(HG * NJ)] + [("k", c) for c in range(KH)] + [("v", s) for s in range(SPG)]
    NC_ = len(chunks)
    UPI = UPG * HG
    cross = kT_dram is not None
    with ExitStack() as ctx:
        sc = Scope(nc, ctx, name)
        sb, ps, sem = sc.sb, sc.ps, sc.sem
        wq, wk, wv = sb("wq", [P, HG * NJ, P]), sb("wk", [P, KH, P]), sb("wv", [P, 2, KH * HW])
        wo = sb("wo", [P, HG * NJ, D])
        bo = sb("bo", [1, D])
        if not cross:
            table = sb("table", [P, HG, UH, S])
        kvb = sb("kvb", [P, GT]) if cross else None
        qT, kT = sb("qT", [P, HG * NJ, GT]), sb("kT", [P, KH, GT])
        val = sb("val", [P, SPG, KH, HW])
        s1 = sb("s1", [P, 2, UT, UH, S])
        mx, den = sb("mx", [P, UT, UH]), sb("den", [P, UT, UH])
        pT, oT = sb("pT", [P, UT, NJ, P]), sb("oT", [P, UT, NJ, P])
        st, mv = sb("st", [P, TPG, 6]), sb("mv", [P, TPG, 2])
        ps_s, ps_t, ps_o = ps("ps_s", [P, 2, GT]), ps("ps_t", [P, UT, GT]), ps("ps_o", [P, UT, GT])
        ps_out, ps_j = ps("ps_out", [P, UT, D]), ps("ps_j", [P, GT])
        fr = Front(C, sc, ps_j, C.X, C.RS, C.NM)
        if not cross:
            kvb = fr.xnT
        loaded, kv_loaded = sem("loaded"), sem("kv_loaded")
        proj_done, act_taken, dve_taken = sem("proj_done"), sem("act_taken"), sem("dve_taken")
        scores_done, scores_read, shifted, exped, probs = (
            sem(n) for n in ("scores_done", "scores_read", "shifted", "exped", "probs"))
        pT_done, pT_ready, oT_done, oT_ready = (sem(n) for n in ("pT_done", "pT_ready", "oT_done", "oT_ready"))
        out_done, out_read = sem("out_done"), sem("out_read")
        begun = sem("begun")
        block = ctx.enter_context(nc.Block())
        loads = [(wq[:], W["wq"]), (wk[:], W["wk"]), (wv[:], W["wv"]), (wo[:], W["wo"])]
        loads += [(bo[:], W["bo"])] if cross else [(table[:], W["table"])]
        n_loaded = 16 * len(loads)

        def bank(c):
            return (ps_s, ps_t)[c % 4 // 2][:, c % 2, :]

        @block.sync
        def _(sp):
            for to, of in loads:
                sp.dma_start(to, of).then_inc(loaded, 16)
            if cross:
                sp.dma_start(kvb[:], kT_dram[:, 0:GT]).then_inc(kv_loaded, 16)
                with sp.Fori(1, C.NG) as i:
                    sp.wait_ge(proj_done, i * NC_)
                    sp.dma_start(kvb[:], kT_dram[:, bass.ds(i * GT, GT)]).then_inc(kv_loaded, 16)

        @block.tensor
        def _(pe):
            pe.wait_ge(loaded, n_loaded)

            def hold(pe):
                pe.sem_inc(begun, 1)

            def project(i, c):
                kind, n = chunks[c]
                if c >= 4:
                    pe.wait_ge(dve_taken if c % 2 else act_taken, i * (NC_ // 2) + (c - 4) // 2 + 1)
                if kind == "q":
                    last = nc.tensor.matmul(bank(c), wq[:, n, :], fr.xnT[:], start=True, stop=True)
                elif kind == "k":
                    last = nc.tensor.matmul(bank(c), wk[:, n, :], kvb[:], start=True, stop=True)
                else:
                    for half in range(2):
                        last = nc.tensor.matmul(bank(c)[HW * half:HW * half + HW, 0:KH * HW],
                                                kvb[:, n * S:(n + 1) * S], wv[:, half, :], start=True, stop=True)
                last.then_inc(proj_done, 1)

            def queries_keys(i, x):
                u, hg = x // HG, x % HG
                if not cross:
                    pe.wait_ge(scores_read, i * UPI + x + 1)
                elif x > 0:
                    pe.wait_ge(shifted, i * UPI + x)
                hold(pe)
                for t in range(UT):
                    for b in range(2):
                        q = 2 * (UT * u + t) + b
                        cols = slice(q * S, q * S + S)
                        for j in range(NJ):
                            for half in range(2):
                                r = slice(HW * half, HW * half + HW)
                                last = nc.tensor.matmul(
                                    ps_s[S * b:S * b + S, half, (t * NJ + j) * S:(t * NJ + j + 1) * S],
                                    qT[r, hg * NJ + j, cols], kT[r, hg * NK + j // q_per_kv, cols], start=True, stop=True)
                last.then_inc(scores_done, 1)

            def turn_probs(i, x):
                pe.wait_ge(probs, i * UPI + x + 1)
                for t in range(UT):
                    for j in range(NJ):
                        last = nc.tensor.transpose(ps_t[:, t, j * P:(j + 1) * P], 
                                               s1[:, x % 2, t, 2 * j:2 * j + 2, :].rearrange("p a k -> p (a k)"), C.ident[:])
                last.then_inc(pT_done, 1)

            def weigh_values(i, x):
                u, hg = x // HG, x % HG
                pe.wait_ge(pT_ready, i * UPI + x + 1)
                hold(pe)
                for t in range(UT):
                    for b in range(2):
                        q = 2 * (UT * u + t) + b
                        for k in range(NK):
                            for half in range(2):
                                r = slice(HW * half, HW * half + HW)
                                js = slice(k * q_per_kv, (k + 1) * q_per_kv)
                                last = nc.tensor.matmul(
                                    ps_o[r, t, :].rearrange("p (j q) -> p j q", q=P)[:, js, S * b:S * b + S],
                                    val[r, q, hg * NK + k, :], pT[r, t, js, S * b:S * b + S], start=True, stop=True)
                last.then_inc(oT_done, 1)

            def project_output(i, x):
                u, hg = x // HG, x % HG
                pe.wait_ge(oT_ready, i * UPI + x + 1)
                if hg == 0:
                    pe.wait_ge(out_read, i * UPG + u + 1)
                for t in range(UT):
                    for j in range(NJ):
                        end = hg == HG - 1 and j == NJ - 1
                        last = nc.tensor.matmul(ps_out[:, t, :], oT[:, t, j, :], wo[:, hg * NJ + j, :],
                                                start=hg == 0 and t == 0 and j == 0,
                                                stop=end and not cross, skip_group_check=True)
                    if cross and hg == HG - 1:
                        last = nc.tensor.matmul(ps_out[:, t, :], C.ones[0:1, :], bo[0:1, :], start=False, stop=True,
                                                skip_group_check=True)
                if hg == HG - 1:
                    last.then_inc(out_done, 1)

            fr.pe(pe, 0)
            with pe.Fori(0, C.NG) as i:
                pe.wait_ge(fr.xT_ready, i + 1)
                if cross:
                    pe.wait_ge(kv_loaded, i * 16 + 16)
                for c in range(NC_):
                    project(i, c)
                for taken in (act_taken, dve_taken):
                    pe.wait_ge(taken, i * (NC_ // 2) + NC_ // 2)
                queries_keys(i, 0)
                for x in range(UPI):
                    if x + 1 < UPI:
                        queries_keys(i, x + 1)
                    else:
                        fr.pe(pe, i + 1)
                    turn_probs(i, x)
                    if x > 0:
                        project_output(i, x - 1)
                    weigh_values(i, x)
                project_output(i, UPI - 1)

        def take(eng, copy, scaled, i, odd):
            for c in range(odd, NC_, 2):
                kind, n = chunks[c]
                eng.wait_ge(proj_done, i * NC_ + c + 1)
                if kind == "q":
                    last = scaled(qT[:, n, :], bank(c))
                elif kind == "k":
                    last = copy(kT[:, n, :], bank(c))
                else:
                    last = copy(val[:, n, :, :].rearrange("p k d -> p (k d)"), bank(c)[:, 0:KH * HW])
                last.then_inc(dve_taken if odd else act_taken, 1)

        @block.scalar
        def _(act):
            act_copy = lambda to, of: nc.scalar.activation(to, of, ACT.Copy)
            act_scaled = lambda to, of: nc.scalar.activation(to, of, ACT.Copy, scale=HW ** -0.5)

            def output_copy(i, x):
                act.wait_ge(oT_done, i * UPI + x + 1)
                nc.scalar.activation(oT[:].rearrange("p t j q -> p t (j q)"), ps_o[:], ACT.Copy).then_inc(oT_ready, 1)

            fr.act(act, 0)
            with act.Fori(0, C.NG) as i:
                take(act, act_copy, act_scaled, i, 0)
                for x in range(UPI):
                    act.wait_ge(shifted, i * UPI + x + 1)
                    nc.scalar.activation(s1[:, x % 2, :, :, :], s1[:, x % 2, :, :, :], ACT.Exp).then_inc(exped, 1)
                    if x > 0:
                        output_copy(i, x - 1)
                    if x == UPI - 1:
                        fr.act(act, i + 1)
                    act.wait_ge(pT_done, i * UPI + x + 1)
                    nc.scalar.activation(pT[:].rearrange("p t j q -> p t (j q)"), ps_t[:], ACT.Copy).then_inc(pT_ready, 1)
                output_copy(i, UPI - 1)

        @block.vector
        def _(dve):
            dve_copy = nc.vector.tensor_copy
            dve_scaled = lambda to, of: nc.vector.tensor_scalar(to, of, HW ** -0.5, None, ALU.mult)
            dve.wait_ge(loaded, n_loaded)
            nc.vector.memset(mx[:], 0.0).then_inc(scores_read, 1)
            nc.vector.memset(mv[:], 0.0).then_inc(out_read, 1)

            def shift(i, x):
                w, out = i * UPI + x, s1[:, x % 2, :, :, :]
                raw = ps_s[:].rearrange("p a (t j k) -> p t a j k", t=UT, k=S)
                halves = out.rearrange("p t (j a) k -> p t a j k", a=2)
                most = mx[:].rearrange("p t (j a) -> p t a j", a=2)
                dve.wait_ge(scores_done, w + 1)
                if not cross:
                    for t in range(UT):
                        last = nc.vector.tensor_tensor(halves[:, t, :, :, :], raw[:, t, :, :, :],
                                                       table[:, x % HG, :, :].rearrange("p (a j) k -> p a j k", a=2), ALU.add)
                    last.then_inc(scores_read, 1)
                    dve.drain()
                    nc.vector.tensor_reduce(mx[:], out, AX, ALU.max)
                    dve.drain()
                    nc.vector.tensor_tensor(out, out, bc(mx[:].unsqueeze(3), [P, UT, UH, S]),
                                            ALU.subtract).then_inc(shifted, 1)
                else:
                    for t in range(UT):
                        nc.vector.tensor_reduce(most[:, t, :, :], raw[:, t, :, :, :], AX, ALU.max)
                    dve.drain()
                    for t in range(UT):
                        last = nc.vector.tensor_tensor(
                            halves[:, t, :, :, :], raw[:, t, :, :, :],
                            bc(most[:, t, :, :].unsqueeze(3), [P, 2, NJ, S]), ALU.subtract)
                    last.then_inc(shifted, 1)

            def normalise(i, x):
                out = s1[:, x % 2, :, :, :]
                dve.wait_ge(exped, i * UPI + x + 1)
                nc.vector.tensor_reduce(den[:], out, AX, ALU.add)
                dve.drain()
                nc.vector.reciprocal(den[:], den[:])
                dve.drain()
                nc.vector.tensor_tensor(out, out, bc(den[:].unsqueeze(3), [P, UT, UH, S]), ALU.mult).then_inc(probs, 1)

            def residual(i, u):
                dve.wait_ge(out_done, i * UPG + u + 1)
                to = C.X[:, bass.ds(i * TPG + u * UT, UT), :]
                nc.vector.tensor_tensor(to, ps_out[:], to, ALU.add).then_inc(out_read, 1)

            fr.dve(0)
            with dve.Fori(0, C.NG) as i:
                take(dve, dve_copy, dve_scaled, i, 1)
                shift(i, 0)
                for x in range(UPI):
                    normalise(i, x)
                    if x + 1 < UPI:
                        shift(i, x + 1)
                    if x == UPI - 2:
                        fr.dve(i + 1)
                    if x % HG == 0 and x > 0:
                        residual(i, x // HG - 1)
                residual(i, UPG - 1)
                dve.drain()
                group_stats(nc, dve, C, C.X, st, mv, i)



NST = 2
CYCLES, LAYERS = 3, 4


def coupled_ffn(C, name, W):
    nc = C.nc
    widths = [D, D, D // 2, D // 4, D]
    gwidths = [D, D // 2, D // 4, D]
    with ExitStack() as ctx:
        sc = Scope(nc, ctx, name)
        sb, ps, sem = sc.sb, sc.ps, sc.sem
        w = [sb(f"w{n}", [widths[n], widths[n + 1]]) for n in range(LAYERS)]
        b = [sb(f"b{n}", [widths[n + 1], 1]) for n in range(LAYERS)]
        gw = [sb(f"gw{n}", [gwidths[n], gwidths[n + 1]]) for n in range(3)]
        gb = [sb(f"gb{n}", [gwidths[n + 1], 1]) for n in range(3)]
        perm, reach = sb("perm", [P, P]), sb("reach", [P, 1])
        reach2, offset = sb("reach2", [P, 1]), sb("offset", [P, 1])
        xn = sb("xn", [P, NST * TPG, D])
        cur, h, tf = sb("cur", [P, NST, GT]), sb("h", [P, NST, GT]), sb("tf", [P, NST, GT])
        mean, gh, gf = sb("mean", [P, NST, SPG]), sb("gh", [P, NST * SPG]), sb("gf", [P, NST, SPG])
        st, mv = sb("st", [P, TPG, 6]), sb("mv", [P, TPG, 2])
        ps_j, ps_g = ps("ps_j", [P, GT]), ps("ps_g", [P, 512])
        ps_c, ps_w, ps_b = ps("ps_c", [P, NST, GT]), ps("ps_w", [P, NST, GT]), ps("ps_b", [P, NST, GT])
        loaded, prepared = sem("loaded"), sem("prepared")
        xn_ready, xT_done, cur_ready, mean_ready = (sem(n) for n in ("xn_ready", "xT_done", "cur_ready", "mean_ready"))
        g_done, g_act = sem("g_done"), sem("g_act")
        l_done, l_act, tw_done, updated = sem("l_done"), sem("l_act"), sem("tw_done"), sem("updated")
        back_done = sem("back_done")
        begun = sem("begun")
        block = ctx.enter_context(nc.Block())
        loads = [(t[:], W[k]) for k, t in
                 [(f"w{n}", w[n]) for n in range(4)] + [(f"b{n}", b[n]) for n in range(4)]
                 + [(f"gw{n}", gw[n]) for n in range(3)] + [(f"gb{n}", gb[n]) for n in range(3)]
                 + [("perm", perm), ("reach", reach)]]
        n_loaded = 16 * len(loads)
        NL = CYCLES * LAYERS * NST

        @block.sync
        def _(sp):
            for to, of in loads:
                sp.dma_start(to, of).then_inc(loaded, 16)

        def step(c, l, k):
            return (c * LAYERS + l) * NST + k + 1

        @block.tensor
        def _(pe):
            pe.wait_ge(loaded, n_loaded)

            def hold(rows_in):
                if rows_in == S:
                    pe.sem_inc(begun, 1)

            with pe.Fori(0, C.NG // NST) as i:
                pe.wait_ge(xn_ready, i + 1)
                for k in range(NST):
                    if k:
                        pe.wait_ge(cur_ready, i * NST + k)
                    for p in range(TPG):
                        last = nc.tensor.transpose(ps_j[:, p * P:(p + 1) * P], xn[:, k * TPG + p, :], C.ident[:])
                    last.then_inc(xT_done, 1)
                for c in range(CYCLES):
                    for l in range(LAYERS):
                        for k in range(NST):
                            if l:
                                pe.wait_ge(l_act, i * NL + step(c, l - 1, k))
                            elif c:
                                pe.wait_ge(updated, i * CYCLES * NST + (c - 1) * NST + k + 1)
                            else:
                                pe.wait_ge(cur_ready, i * NST + k + 1)
                            hold(widths[l])
                            rhs = h[0:widths[l], k, :] if l else cur[:, k, :]
                            nc.tensor.matmul(ps_c[0:widths[l + 1], k, :], w[l][:], rhs, start=True,
                                             stop=True).then_inc(l_done, 1)
                            if l == 0:
                                nc.tensor.matmul(ps_w[:, k, :], perm[:], cur[:, k, :], start=True,
                                                 stop=True).then_inc(tw_done, 1)
                        if c == 0 and l < 3:
                            if l == 0:
                                pe.wait_ge(mean_ready, i + 1)
                            else:
                                pe.wait_ge(g_act, i * 3 + l)
                            hold(gwidths[l])
                            rhs = gh[0:gwidths[l], :] if l else mean[:].rearrange("p k s -> p (k s)")
                            nc.tensor.matmul(ps_g[0:gwidths[l + 1], 0:NST * SPG], gw[l][:], rhs, start=True,
                                             stop=True).then_inc(g_done, 1)
                for k in range(NST):
                    pe.wait_ge(updated, i * CYCLES * NST + (CYCLES - 1) * NST + k + 1)
                    for p in range(TPG):
                        last = nc.tensor.transpose(ps_b[:, k, p * P:(p + 1) * P], cur[:, k, p * P:(p + 1) * P], C.ident[:])
                    last.then_inc(back_done, 1)

        @block.scalar
        def _(act):
            act.wait_ge(loaded, n_loaded)
            with act.Fori(0, C.NG // NST) as i:
                for k in range(NST):
                    act.wait_ge(xT_done, i * NST + k + 1)
                    nc.scalar.activation(cur[:, k, :], ps_j[:], ACT.Copy).then_inc(cur_ready, 1)
                for c in range(CYCLES):
                    for l in range(LAYERS):
                        n = widths[l + 1]
                        if c == 0 and l:
                            act.wait_ge(g_done, i * 3 + l)
                            m = gwidths[l]
                            to = gf[:].rearrange("p k s -> p (k s)") if l == 3 else gh[0:m, :]
                            nc.scalar.activation(to, ps_g[0:m, 0:NST * SPG], ACT.Sigmoid if l == 3 else ACT.Gelu,
                                                 bias=gb[l - 1][:, 0:1]).then_inc(g_act, 1)
                        for k in range(NST):
                            act.wait_ge(l_done, i * NL + step(c, l, k))
                            to, fn = (tf[:, k, :], ACT.Sigmoid) if l == 3 else (h[0:n, k, :], ACT.Gelu)
                            nc.scalar.activation(to, ps_c[0:n, k, :], fn, bias=b[l][:, 0:1]).then_inc(l_act, 1)

        @block.vector
        def _(dve):
            dve.wait_ge(loaded, n_loaded)
            nc.vector.tensor_scalar(reach2[:], reach[:], 2.0, None, ALU.mult)
            nc.vector.tensor_scalar(offset[:], reach[:], -1.0, 0.1, ALU.mult, ALU.add)
            nc.vector.memset(mv[:], 0.0)
            dve.drain()
            seqs = lambda t: t.rearrange("p (s n) -> p s n", n=S)

            def normalise(j):
                for p in range(NST * TPG):
                    n = j * NST * TPG + p
                    last = nc.vector.tensor_scalar(xn[:, p, :], C.X[:, n, :], C.RS[:, bass.ds(n, 1)],
                                                   C.NM[:, bass.ds(n, 1)], ALU.mult, ALU.add)
                last.then_inc(xn_ready, 1)

            normalise(0)
            with dve.Fori(0, C.NG // NST) as i:
                for k in range(NST):
                    dve.wait_ge(cur_ready, i * NST + k + 1)
                    nc.vector.tensor_reduce(mean[:, k, :], seqs(cur[:, k, :]), AX, ALU.add)
                dve.drain()
                nc.vector.tensor_scalar(mean[:], mean[:], 1.0 / S, None, ALU.mult).then_inc(mean_ready, 1)
                normalise(i + 1)
                dve.wait_ge(g_act, i * 3 + 3)
                nc.vector.tensor_scalar(gf[:], gf[:], 0.7, None, ALU.mult)
                dve.drain()
                for c in range(CYCLES):
                    for k in range(NST):
                        t = tf[:, k, :]
                        dve.wait_ge(l_act, i * NL + step(c, 3, k))
                        nc.vector.scalar_tensor_tensor(seqs(t), seqs(t), 0.3, bc(gf[:, k, :].unsqueeze(2), [P, SPG, S]),
                                                       ALU.mult, ALU.add)
                        dve.drain()
                        nc.vector.tensor_scalar(t, t, reach2[:, 0:1], offset[:, 0:1], ALU.mult, ALU.add)
                        dve.drain()
                        dve.wait_ge(tw_done, i * CYCLES * NST + c * NST + k + 1)
                        nc.vector.tensor_tensor(t, t, ps_w[:, k, :], ALU.mult)
                        dve.drain()
                        nc.vector.tensor_tensor(cur[:, k, :], cur[:, k, :], t, ALU.add).then_inc(updated, 1)
                for k in range(NST):
                    g = i * NST + k
                    dve.wait_ge(back_done, i * NST + k + 1)
                    nc.vector.tensor_tensor(rows(C.X, g), ps_b[:, k, :].rearrange("p (t d) -> p t d", d=D), rows(C.X, g),
                                            ALU.add)
                    dve.drain()
                    group_stats(nc, dve, C, C.X, st, mv, g)
                    dve.drain()



DI, NS, NTAP, DTR = 256, 16, 4, 8
NHF = DI // P
PADW = S + NTAP - 1


def mamba(C, name, W, first):
    nc = C.nc
    R = 4
    AHEAD = 2
    with ExitStack() as ctx:
        sc = Scope(nc, ctx, name)
        sb, ps, sem = sc.sb, sc.ps, sc.sem
        g, be = sb("g", [P, 1]), sb("be", [P, 1])
        in_w, taps = sb("in_w", [P, 2 * DI]), sb("taps", [P, NTAP, DI])
        conv_b, xp = sb("conv_b", [P, NHF]), sb("xp", [P, NHF, P])
        dt_w, dt_b = sb("dt_w", [P, DI]), sb("dt_b", [P, NHF])
        A, Dp = sb("A", [P, NHF, NS]), sb("Dp", [P, NHF])
        diagD, out_w = sb("diagD", [P, NHF, P]), sb("out_w", [P, NHF, D])
        pick_row = sb("pick_row", [P, 2 * NS])
        sel = sb("sel", [P, 2 * NS, P], BF16)
        flip = sb("flip", [P, P])
        xn = sb("xn", [P, TPG, D])
        hT = sb("hT", [P, SPG, PADW])
        xs, sz = sb("xs", [P, 2, NHF, GT]), sb("sz", [P, 2, NHF, GT])
        low = sb("low", [P, GT])
        parts = sb("parts", [P, 2, GT], BF16)
        x, e, r, v, ln = (sb(n, [P, NHF, GT]) for n in ("x", "e", "r", "v", "ln"))
        q = e
        dt, dtx = sb("dt", [P, 2, NHF, GT]), sb("dtx", [P, 2, NHF, GT])
        dA, Bs = sb("dA", [P, R, NHF, GT]), sb("Bs", [P, R, GT])
        dBx, hs, yc = (sb(n, [P, 2, NHF, GT]) for n in ("dBx", "hs", "yc"))
        ps_B, ps_C, ps_y = ps("ps_B", [P, 2, GT]), ps("ps_C", [P, 2, GT]), ps("ps_y", [P, NHF, GT])
        ps_j, ps_k = ps("ps_j", [P, GT]), ps("ps_k", [P, GT])
        bank = (ps_j, ps_k)
        loaded, prepared, a_ready = sem("loaded"), sem("prepared"), sem("a_ready")
        xn_ready, xT_done, hT_ready = sem("xn_ready"), sem("xT_done"), sem("hT_ready")
        xs_done, z_done, xs_ready, z_ready = sem("xs_done"), sem("z_done"), sem("xs_ready"), sem("z_ready")
        dbl_done, high_ready, parts_ready = sem("dbl_done"), sem("high_ready"), sem("parts_ready")
        dt_done, x_ready, neg_ready, e_ready = sem("dt_done"), sem("x_ready"), sem("neg_ready"), sem("e_ready")
        excess, v_ready, r_ready, dt_ready = sem("excess"), sem("v_ready"), sem("r_ready"), sem("dt_ready")
        B_done, B_copied, dBx_ready, C_done = sem("B_done"), sem("B_copied"), sem("dBx_ready"), sem("C_done")
        decay, scanned, yc_ready, y_added = sem("decay"), sem("scanned"), sem("yc_ready"), sem("y_added")
        y_ready, out_done, out_read = sem("y_ready"), sem("out_done"), sem("out_read")
        begun = sem("begun")
        block = ctx.enter_context(nc.Block())
        loads = [(g, "g"), (be, "be"), (in_w, "in_w"), (taps, "taps"), (conv_b, "conv_b"), (xp, "xp"),
                 (dt_b, "dt_b"), (A, "A"), (Dp, "D"), (out_w, "out_w"), (pick_row, "pick_row")]
        if not first:
            loads.append((flip, "flip"))
        n_loaded = 16 * (len(loads) + 1)
        rank_rows = slice(32, 32 + DTR)
        both = [P, NHF, GT]

        @block.sync
        def _(sp):
            for to, k in loads:
                sp.dma_start(to[:], W[k]).then_inc(loaded, 16)
            sp.dma_start(dt_w[rank_rows, :], W["dt_w"]).then_inc(loaded, 16)

        n_prepared = 3

        @block.gpsimd
        def _(pool):
            nc.gpsimd.memset(hT[:], 0.0).then_inc(prepared, 1)
            nc.gpsimd.memset(dA[:], 0.0).then_inc(prepared, 1)
            nc.gpsimd.memset(Bs[:], 0.0).then_inc(dBx_ready, R)
            pool.drain()

            def hold():
                pool.sem_inc(begun, 1)

            def multiply(to, one, other):
                return nc.gpsimd.tensor_tensor(to, one, other, ALU.mult)

            def state(n, s, par):
                pool.wait_ge(B_copied, n + 3)
                pool.wait_ge(scanned, n - 1 + R)
                hold()
                multiply(dBx[:, s % 2, :, :], dtx[:, par, :, :], bc(Bs[:, s % R, :].unsqueeze(1), both)).then_inc(dBx_ready, 1)

            def front(j, s, par):
                if s == 11:
                    pool.wait_ge(v_ready, j + 1)
                    hold()
                    nc.gpsimd.tensor_tensor(v[:], v[:], e[:], ALU.subtract)
                    pool.drain()
                elif s == 12:
                    pool.wait_ge(r_ready, j + 1)
                    hold()
                    multiply(v[:], v[:], r[:]).then_inc(excess, 1)
                elif s == 15:
                    pool.wait_ge(dt_ready, j + 1)
                    hold()
                    multiply(dtx[:, par, :, :], dt[:, par, :, :], xs[:, par, :, :])
                    pool.drain()

            for s in range(11, 16):
                front(0, s, 0)
            for s in range(AHEAD):
                state(s, s, 0)
            with pool.Fori(0, C.NG // 2) as pair:
                for par in range(2):
                    i = pair * 2 + par
                    for s in range(AHEAD, NS):
                        state(i * NS + s, s, par)
                        front(i + 1, s, 1 - par)
                    for s in range(AHEAD):
                        state(i * NS + NS + s, s, 1 - par)

        @block.tensor
        def _(pe):
            pe.wait_ge(loaded, n_loaded)
            pe.wait_ge(prepared, n_prepared)

            def turn(j):
                pe.wait_ge(xn_ready, j + 1)
                for p in range(TPG):
                    to = ps_j[:, p * P:(p + 1) * P]
                    if first:
                        last = nc.tensor.transpose(to, xn[:, p, :], C.ident[:])
                    else:
                        last = nc.tensor.matmul(to, xn[:, p, :], flip[:], start=True, stop=True)
                last.then_inc(xT_done, 1)

            def convolve(j, m, step):
                if m == 0 and step == 0:
                    pe.wait_ge(hT_ready, j + 1)
                for k in (2 * step, 2 * step + 1):
                    last = nc.tensor.matmul(bank[m][:], taps[:, k, m * P:(m + 1) * P], hT[:, :, k:k + S],
                                            start=k == 0, stop=k == NTAP - 1)
                if step == 1:
                    last.then_inc(xs_done, 1)

            def gate(j, m):
                pe.wait_ge(xs_ready, j * NHF + m + 1)
                nc.tensor.matmul(bank[m][:], in_w[:, DI + m * P:DI + (m + 1) * P], hT[:, :, NTAP - 1:], start=True,
                                 stop=True).then_inc(z_done, 1)

            def low_products(j, par):
                pe.wait_ge(z_ready, j * NHF + 1)
                for m in range(NHF):
                    last = nc.tensor.matmul(ps_j[:], xp[:, m, :], xs[:, par, m, :], start=m == 0, stop=m == NHF - 1)
                last.then_inc(dbl_done, 1)

            def step_sizes(j):
                pe.wait_ge(parts_ready, j + 1)
                pe.wait_ge(z_ready, j * NHF + 2)
                for m in range(NHF):
                    last = nc.tensor.matmul(bank[m][:], dt_w[rank_rows, m * P:(m + 1) * P], low[rank_rows, :], start=True,
                                            stop=True)
                last.then_inc(dt_done, 1)

            def spread_B(n, s, par):
                pe.wait_ge(B_copied, n + 1)
                nc.tensor.matmul(ps_B[:, s % 2, :], sel[:, s, :], parts[:, par, :], start=True, stop=True).then_inc(B_done, 1)

            def spread_C(s, par):
                nc.tensor.matmul(ps_C[:, s % 2, :], sel[:, NS + s, :], parts[:, par, :], start=True,
                                 stop=True).then_inc(C_done, 1)

            def skip(par):
                for m in range(NHF):
                    nc.tensor.matmul(ps_y[:, m, :], diagD[:, m, :], xs[:, par, m, :], start=False, stop=False)

            def project(i):
                pe.wait_ge(y_ready, i + 2)
                pe.wait_ge(xs_ready, i * NHF + 6)
                for p in range(TPG):
                    for m in range(NHF):
                        last = nc.tensor.matmul(ps_k[:, p * D:(p + 1) * D], q[:, m, p * P:(p + 1) * P], out_w[:, m, :],
                                                start=m == 0, stop=m == NHF - 1)
                last.then_inc(out_done, 1)

            def add_state(n, s):
                pe.wait_ge(yc_ready, n + 1)
                for m in range(NHF):
                    last = nc.tensor.matmul(ps_y[:, m, :], C.ident[:], yc[:, s % 2, m, :], start=s == 0, stop=s == NS - 1)
                last.then_inc(y_added, 1)

            def front(j, s, par, in_loop):
                if s == 2:
                    gate(j, 0)
                    if in_loop:
                        pe.wait_ge(out_read, j)
                    gate(j, 1)
                elif s == 3:
                    low_products(j, par)
                elif s == 6:
                    step_sizes(j)
                elif s == 8:
                    pe.wait_ge(x_ready, j + 1)
                    turn(j + 1)
                elif 10 <= s < 14:
                    convolve(j + 1, (s - 10) // 2, s % 2)

            turn(0)
            for s in range(10, 14):
                front(-1, s, 1, False)
            for s in range(2, 14):
                front(0, s, 0, False)
            for s in range(AHEAD):
                spread_B(s, s, 0)
                spread_C(s, 0)
            for s in range(AHEAD):
                spread_B(s + 2, s + 2, 0)
                add_state(s, s)
                spread_C(s + 2, 0)
            with pe.Fori(0, C.NG // 2) as pair:
                for par in range(2):
                    i = pair * 2 + par
                    for s in range(AHEAD, NS):
                        n = i * NS + s
                        to = (s + 2) % NS
                        its = par if to == s + 2 else 1 - par
                        spread_B(n + 2, to, its)
                        front(i + 1, s, 1 - par, True)
                        if s == 9:
                            skip(par)
                        pe.wait_ge(yc_ready, n + 1)
                        spread_C(to, its)
                        add_state(n, s)
                    for s in range(AHEAD):
                        n = i * NS + NS + s
                        spread_B(n + 2, s + 2, 1 - par)
                        if s == 0:
                            project(i)
                        pe.wait_ge(yc_ready, n + 1)
                        spread_C(s + 2, 1 - par)
                        add_state(n, s)
            for m in range(NHF):
                nc.tensor.matmul(ps_y[:, m, :], C.ident[:], yc[:, 1, m, :], start=False, stop=True)

        @block.scalar
        def _(act):
            act.wait_ge(loaded, n_loaded)
            nc.scalar.activation(A[:], A[:], ACT.Exp).then_inc(a_ready, 1)
            act.wait_ge(prepared, n_prepared)
            seqs = lambda t: t.rearrange("p (s n) -> p s n", n=S)[:, :, 1:]

            def copy_rows(j):
                act.wait_ge(xT_done, j + 1)
                nc.scalar.activation(hT[:, :, NTAP - 1:], ps_j[:].rearrange("p (s n) -> p s n", n=S), ACT.Identity,
                                     scale=g[:, 0:1], bias=be[:, 0:1]).then_inc(hT_ready, 1)

            def state(n, s, par):
                act.wait_ge(B_done, n + 1)
                act.wait_ge(dBx_ready, n + 1)
                nc.scalar.activation(Bs[:, s % R, :], ps_B[:, s % 2, :], ACT.Copy).then_inc(B_copied, 1)
                act.wait_ge(scanned, n + 1)
                for m in range(NHF):
                    last = nc.scalar.activation(seqs(dA[:, s % R, m, :]), seqs(dt[:, par, m, :]), ACT.Exp, scale=A[:, m, s:s + 1])
                last.then_inc(decay, 1)

            def activate(j, par, in_loop):
                if in_loop:
                    act.wait_ge(y_added, j * NS - 2 * NS + 10)
                for m in range(NHF):
                    act.wait_ge(xs_done, j * NHF + m + 1)
                    nc.scalar.activation(xs[:, par, m, :], bank[m][:], ACT.Silu,
                                         bias=conv_b[:, m:m + 1]).then_inc(xs_ready, 1)

            def front(j, s, par, in_loop):
                if s == 4:
                    for m in range(NHF):
                        act.wait_ge(z_done, j * NHF + m + 1)
                        if m == 0 and in_loop:
                            act.wait_ge(y_ready, j)
                        nc.scalar.activation(sz[:, par, m, :], bank[m][:], ACT.Silu).then_inc(z_ready, 1)
                elif s == 6:
                    act.wait_ge(dbl_done, j + 1)
                    nc.scalar.activation(low[32:64, :], ps_j[32:64, :], ACT.Copy)
                    nc.scalar.activation(parts[:, par, :], ps_j[:], ACT.Copy).then_inc(high_ready, 1)
                elif s == 9:
                    act.wait_ge(neg_ready, j + 1)
                    nc.scalar.activation(e[:], e[:], ACT.Exp).then_inc(e_ready, 1)
                elif s == 10:
                    copy_rows(j + 1)
                elif s == 12:
                    act.drain()
                    nc.scalar.activation(ln[:], e[:], ACT.Ln, bias=1.0)
                    act.drain()
                    nc.scalar.activation(r[:], ln[:], ACT.Exp, scale=-1.0).then_inc(r_ready, 1)

            copy_rows(0)
            activate(0, 0, False)
            for s in range(4, 13):
                front(0, s, 0, False)
            act.wait_ge(dt_ready, 1)
            for s in range(AHEAD):
                state(s, s, 0)
            activate(1, 1, False)
            with act.Fori(0, C.NG // 2) as pair:
                for par in range(2):
                    i = pair * 2 + par
                    for s in range(AHEAD, NS):
                        state(i * NS + s, s, par)
                        front(i + 1, s, 1 - par, True)
                    act.wait_ge(dt_ready, i + 2)
                    state(i * NS + NS, 0, 1 - par)
                    activate(i + 2, par, True)
                    state(i * NS + NS + 1, 1, 1 - par)

        @block.vector
        def _(dve):
            dve.wait_ge(loaded, n_loaded)
            for k in range(NTAP):
                nc.vector.tensor_tensor(taps[:, k, :], taps[:, k, :], in_w[:, 0:DI], ALU.mult)
            for m in range(NHF):
                nc.vector.tensor_scalar(diagD[:, m, :], C.ident[:], Dp[:, m:m + 1], None, ALU.mult)
            nc.vector.tensor_copy(sel[:], bc(pick_row[:].unsqueeze(2), [P, 2 * NS, P]))
            nc.vector.memset(xn[:], 0.0).then_inc(out_read, 1)
            nc.vector.memset(x[:], 0.0).then_inc(y_ready, 1)
            nc.vector.memset(r[:], 0.0).then_inc(scanned, R)
            nc.vector.memset(ln[:], 0.0).then_inc(B_copied, 2)
            dve.wait_ge(a_ready, 1)
            nc.vector.tensor_scalar(A[:], A[:], -1.0, None, ALU.mult).then_inc(prepared, 1)
            dve.drain()

            def normalise(j):
                for p in range(TPG):
                    n = j * TPG + p
                    last = nc.vector.tensor_scalar(xn[:, p, :], C.X[:, n, :], C.RS2[:, bass.ds(n, 1)],
                                                   C.NM2[:, bass.ds(n, 1)], ALU.mult, ALU.add)
                last.then_inc(xn_ready, 1)

            def front(j, s, par):
                if s == 5:
                    dve.wait_ge(high_ready, j + 1)
                    nc.vector.tensor_tensor(low[64:128, :], ps_j[64:128, :], parts[64:128, par, :], ALU.subtract)
                    dve.drain()
                    nc.vector.tensor_copy(parts[64:128, par, :], low[64:128, :])
                    dve.drain()
                    nc.vector.tensor_tensor(low[96:128, :], low[96:128, :], parts[96:128, par, :], ALU.subtract)
                    dve.drain()
                    nc.vector.tensor_copy(parts[96:128, par, :], low[96:128, :]).then_inc(parts_ready, 1)
                elif s == 7:
                    dve.wait_ge(dt_done, j + 1)
                    for m in range(NHF):
                        last = nc.vector.tensor_scalar(x[:, m, :], bank[m][:], dt_b[:, m:m + 1], None, ALU.add)
                    last.then_inc(x_ready, 1)
                    dve.drain()
                    nc.vector.scalar_tensor_tensor(e[:], x[:], -1.0, x[:], ALU.mult, ALU.min).then_inc(neg_ready, 1)
                elif s == 10:
                    dve.wait_ge(e_ready, j + 1)
                    nc.vector.tensor_scalar(x[:], x[:], 0.0, None, ALU.max)
                    nc.vector.tensor_scalar(v[:], e[:], 1.0, -1.0, ALU.add, ALU.add).then_inc(v_ready, 1)
                elif s == 12:
                    dve.drain()
                    dve.wait_ge(r_ready, j + 1)
                    nc.vector.tensor_tensor(dt[:, par, :, :], x[:], ln[:], ALU.add)
                    dve.drain()
                elif s == 13:
                    dve.wait_ge(excess, j + 1)
                    nc.vector.tensor_tensor(dt[:, par, :, :], dt[:, par, :, :], v[:], ALU.subtract).then_inc(dt_ready, 1)

            flat = lambda t: t.rearrange("p m n -> p (m n)")

            def state(n, s, wait_free=True):
                h = hs[:, s % 2, :, :]
                dve.wait_ge(decay, n + 1)
                dve.wait_ge(dBx_ready, n + 1 + R)
                nc.vector.tensor_tensor_scan(flat(h), flat(dA[:, s % R, :, :]), flat(dBx[:, s % 2, :, :]), 0.0, ALU.mult,
                                             ALU.add).then_inc(scanned, 1)
                dve.drain()
                if wait_free:
                    dve.wait_ge(y_added, n - 1)
                dve.wait_ge(C_done, n + 1)
                nc.vector.tensor_tensor(yc[:, s % 2, :, :], h, bc(ps_C[:, s % 2, :].unsqueeze(1), both),
                                        ALU.mult).then_inc(yc_ready, 1)

            normalise(0)
            dve.drain()
            dve.wait_ge(xT_done, 1)
            normalise(1)
            for s in range(5, 14):
                front(0, s, 0)
            for s in range(AHEAD):
                state(s, s, False)
            with dve.Fori(0, C.NG // 2) as pair:
                for par in range(2):
                    i = pair * 2 + par
                    for s in range(AHEAD, NS):
                        state(i * NS + s, s)
                        front(i + 1, s, 1 - par)
                        if s == 4:
                            dve.wait_ge(xT_done, i + 2)
                            normalise(i + 2)
                        elif s == 14 and first:
                            for p in range(TPG):
                                n = i * TPG + p
                                nc.vector.tensor_scalar(C.Y[:, n, :], C.X[:, n, :], C.RS[:, bass.ds(n, 1)],
                                                        C.NM[:, bass.ds(n, 1)], ALU.mult, ALU.add)
                    state(i * NS + NS, 0)
                    dve.wait_ge(y_added, i * NS + NS)
                    nc.vector.tensor_tensor(q[:], sz[:, par, :, :], ps_y[:], ALU.mult).then_inc(y_ready, 1)
                    state(i * NS + NS + 1, 1)
                    dve.wait_ge(out_done, i + 1)
                    nc.vector.tensor_tensor(rows(C.Y, i), ps_k[:].rearrange("p (t d) -> p t d", d=D), rows(C.Y, i),
                                            ALU.add).then_inc(out_read, 1)
                    dve.drain()


def mamba_join(C, name):
    nc = C.nc
    with ExitStack() as ctx:
        sc = Scope(nc, ctx, name)
        xn, t = sc.sb("xn", [P, 2, TPG, D]), sc.sb("t", [P, TPG, D])
        st, mv = sc.sb("st", [P, TPG, 6]), sc.sb("mv", [P, TPG, 2])
        activated, joined = sc.sem("activated"), sc.sem("joined")
        block = ctx.enter_context(nc.Block())

        @block.scalar
        def _(act):
            with act.Fori(0, C.NG) as i:
                act.wait_ge(joined, i + 1)
                nc.scalar.activation(t[:], rows(C.Y, i), ACT.Gelu).then_inc(activated, 1)

        @block.vector
        def _(dve):
            nc.vector.memset(mv[:], 0.0).then_inc(joined, 1)
            with dve.Fori(0, C.NG) as i:
                for p in range(TPG):
                    n = i * TPG + p
                    nc.vector.tensor_scalar(xn[:, 0, p, :], C.X[:, n, :], C.RS[:, bass.ds(n, 1)],
                                            C.NM[:, bass.ds(n, 1)], ALU.mult, ALU.add)
                dve.drain()
                dve.wait_ge(activated, i + 1)
                nc.vector.tensor_tensor(rows(C.Y, i), xn[:, 0, :, :], t[:], ALU.add).then_inc(joined, 1)
                dve.drain()
                group_stats(nc, dve, C, C.Y, st, mv, i)
                dve.drain()


def gelu_ffn(C, name, W):
    nc = C.nc
    F = W["w1"].shape[1]
    NF = F // P
    with ExitStack() as ctx:
        sc = Scope(nc, ctx, name)
        sb, ps, sem = sc.sb, sc.ps, sc.sem
        w1, w2, b1, b2 = sb("w1", [P, F]), sb("w2", [P, NF, D]), sb("b1", [P, NF]), sb("b2", [1, D])
        g, be = sb("g", [P, 1]), sb("be", [P, 1])
        hid = sb("hid", [P, NF, GT])
        st, mv = sb("st", [P, TPG, 6]), sb("mv", [P, TPG, 2])
        ps_j, ps_o, ps_h = ps("ps_j", [P, GT]), ps("ps_o", [P, GT]), ps("ps_h", [P, NF, GT])
        fr = Front(C, sc, ps_j, C.Y, C.RS2, C.NM2)
        loaded, hid_done, hid_ready = sem("loaded"), sem("hid_done"), sem("hid_ready")
        out_done, out_read = sem("out_done"), sem("out_read")
        block = ctx.enter_context(nc.Block())
        loads = [(w1[:], W["w1"]), (w2[:], W["w2"].rearrange("(c p) d -> p c d", p=P)), (b1[:], W["b1"]), (b2[:], W["b2"]),
                 (g[:], W["g"]), (be[:], W["be"])]
        n_loaded = 16 * len(loads)

        @block.sync
        def _(sp):
            for to, of in loads:
                sp.dma_start(to, of).then_inc(loaded, 16)

        @block.tensor
        def _(pe):
            pe.wait_ge(loaded, n_loaded)
            fr.pe(pe, 0)
            with pe.Fori(0, C.NG) as i:
                pe.wait_ge(fr.xT_ready, i + 1)
                for c in range(NF):
                    nc.tensor.matmul(ps_h[:, c, :], w1[:, c * P:(c + 1) * P], fr.xnT[:], start=True,
                                     stop=True).then_inc(hid_done, 1)
                fr.pe(pe, i + 1)
                pe.wait_ge(out_read, i + 1)
                pe.wait_ge(hid_ready, i * NF + NF)
                for p in range(TPG):
                    o = ps_o[:, p * D:(p + 1) * D]
                    for c in range(NF):
                        nc.tensor.matmul(o, hid[:, c, p * P:(p + 1) * P], w2[:, c, :], start=c == 0, stop=False)
                    last = nc.tensor.matmul(o, C.ones[0:1, :], b2[0:1, :], start=False, stop=True)
                last.then_inc(out_done, 1)

        @block.scalar
        def _(act):
            act.wait_ge(loaded, n_loaded)

            def copy_rows(j):
                act.wait_ge(fr.xT_done, j + 1)
                nc.scalar.activation(fr.xnT[:], ps_j[:], ACT.Identity, scale=g[:, 0:1],
                                     bias=be[:, 0:1]).then_inc(fr.xT_ready, 1)

            copy_rows(0)
            with act.Fori(0, C.NG) as i:
                for c in range(NF):
                    act.wait_ge(hid_done, i * NF + c + 1)
                    nc.scalar.activation(hid[:, c, :], ps_h[:, c, :], ACT.Gelu, bias=b1[:, c:c + 1]).then_inc(hid_ready, 1)
                copy_rows(i + 1)

        @block.vector
        def _(dve):
            nc.vector.memset(mv[:], 0.0).then_inc(out_read, 1)
            fr.dve(0)
            with dve.Fori(0, C.NG) as i:
                dve.wait_ge(fr.xT_done, i + 1)
                fr.dve(i + 1)
                nc.vector.tensor_tensor(rows(C.X, i), rows(C.X, i), rows(C.Y, i), ALU.add)
                dve.drain()
                dve.wait_ge(out_done, i + 1)
                nc.vector.tensor_tensor(rows(C.X, i), ps_o[:].rearrange("p (t d) -> p t d", d=D), rows(C.X, i),
                                        ALU.add).then_inc(out_read, 1)
                dve.drain()
                group_stats(nc, dve, C, C.X, st, mv, i)



FT = 16
FW = 8
ITERS = 3
PAIRS = HD // 2
STEPS = FT // 4
TWO_PI = (6.28125, 0.0019350051879882812, 3.0199159819567553e-07)
ROUND = 1.5 * 2.0 ** 23


def focus_block(C, name, ctx_rows, scratch_in, scratch_out, W):
    nc = C.nc
    with ExitStack() as ctx:
        sc = Scope(nc, ctx, name)
        sb, ps, sem = sc.sb, sc.ps, sc.sem
        row = [P, FT, D]
        weights = {k: sb("w_" + k, [P, D]) for k in ("q", "k", "v", "qh", "kh", "vh", "out")}
        bias = {k: sb("b_" + k, [P, D]) for k in ("qh", "kh", "vh")}
        lna_g, lna_b = sb("lna_g", [P, 1]), sb("lna_b", [P, 1])
        lnb_g, lnb_b = sb("lnb_g", [P, 2, HD]), sb("lnb_b", [P, 2, HD])
        theta, temp, thr, factor = (sb(n, [P, 1]) for n in ("theta", "temp", "thr", "factor"))
        base, place = sb("base", [P, PAIRS]), sb("place", [P, 2, FT])
        xa, xb = sb("xa", row), sb("xb", row)
        hat_a, hat_b = sb("hat_a", row), sb("hat_b", row)
        cur, prev, ai = sb("cur", row), sb("prev", row), sb("ai", row)
        k0, v0 = sb("k0", row), sb("v0", row)
        qk = sb("qk", [P, 2, FT, D])
        prod = C.Y[:, 0:4 * FT, :].rearrange("p t d -> p (t d)")
        score = sb("score", [P, FT * FT * NH])
        most, den = sb("most", [P, FT, NH]), sb("den", [P, FT, NH])
        hm, hv = sb("hm", [P, 2 * FT * NH]), sb("hv", [P, 2 * FT * NH])
        st, mv, rs = sb("st", [P, FT, 6]), sb("mv", [P, FT, 2]), sb("rs", [P, FT])
        ang, turns = sb("ang", [P, 2, 2, FT, PAIRS]), sb("turns", [P, 2, 2, FT, PAIRS])
        trig = sb("trig", [P, 2, 2, FT, PAIRS])
        cond, scale = sb("cond", [P, 1]), sb("scale", [P, 1])
        diff, done, kept = sb("diff", [P, 2]), sb("done", [P, 2]), sb("kept", [P, 2])
        gst, gmv = sb("gst", [P, TPG, 6]), sb("gmv", [P, TPG, 2])
        rT = sb("rT", [P, 2, 4 * P])
        ps_t = ps("ps_t", [P, 2, 4 * P])
        ps_p = ps("ps_p", [P, 2, 3, 4 * D])
        loaded, sent, fetched, returned = sem("loaded"), sem("sent"), sem("fetched"), sem("returned")
        src_ready, turned, rT_ready, multiplied, taken = (
            sem(n) for n in ("src_ready", "turned", "rT_ready", "multiplied", "taken"))
        asked, answered = sem("asked"), sem("answered")
        sums_in, summed, out_ready = sem("sums_in"), sem("summed"), sem("out_ready")
        block = ctx.enter_context(nc.Block())
        loads = [(t, "w_" + k) for k, t in weights.items()] + [(t, "b_" + k) for k, t in bias.items()]
        loads += [(lna_g, "lna_g"), (lna_b, "lna_b"), (lnb_g, "lnb_g"), (lnb_b, "lnb_b"), (theta, "theta"), (temp, "temp"),
                  (thr, "thr"), (factor, "factor"), (base, "base"), (place, "place")]
        n_loaded = 16 * len(loads)

        FOCI = (((("a", "qkv"),), 0, 2, FT // FW), ((("a", "qkv"),), 10, 1, FT // FW), ((("a", "q"), ("b", "kv")), 20, 2, 1))
        OUT_JOB = 31
        ASKED0 = 2

        def asked_before(f):
            return ASKED0 + sum(n + 2 * ITERS for _, _, n, _ in FOCI[:f])

        @block.sync
        def _(sp):
            for to, k in loads:
                sp.dma_start(to[:], W[k]).then_inc(loaded, 16)
            by_tile = scratch_in.rearrange("(n b) t d -> b t n d", b=2)
            for b in range(2):
                sp.dma_start(by_tile[b], C.X[S * b:S * b + FT, 0:C.NT, :]).then_inc(sent, 16)
            sp.dma_start(xb[:], ctx_rows[:, 0:FT, :]).then_inc(fetched, 16)
            sp.wait_ge(sent, 32)
            sp.dma_start(xa[:], scratch_in).then_inc(fetched, 16)
            sp.wait_ge(out_ready, 1)
            sp.dma_start(scratch_out, hat_a[:]).then_inc(sent, 16)
            sp.wait_ge(sent, 48)
            by_tile = scratch_out.rearrange("(n b) t d -> b t n d", b=2)
            for b in range(2):
                sp.dma_start(C.Y[S * b:S * b + FT, 0:C.NT, :], by_tile[b]).then_inc(returned, 16)

        @block.tensor
        def _(pe):
            pe.wait_ge(loaded, n_loaded)

            def turn(src, job, t):
                n = job * STEPS + t
                for r in range(4):
                    last = nc.tensor.transpose(ps_t[:, t % 2, r * P:(r + 1) * P], src[:, 4 * t + r, :], C.ident[:])
                last.then_inc(turned, 1)

            def multiply(ws, job, t):
                n = job * STEPS + t
                pe.wait_ge(rT_ready, n + 1)
                if t >= 2:
                    pe.wait_ge(taken, n - 1)
                for o, w in enumerate(ws):
                    for r in range(4):
                        last = nc.tensor.matmul(ps_p[:, t % 2, o, r * D:(r + 1) * D], rT[:, t % 2, r * P:(r + 1) * P],
                                                weights[w][:], start=True, stop=True)
                last.then_inc(multiplied, 1)

            def run(src, ws, job):
                pe.wait_ge(src_ready, job + 1)
                pe.wait_ge(taken, job * STEPS) if not (isinstance(job, int) and job == 0) else None
                turn(src, job, 0)
                for t in range(1, STEPS):
                    turn(src, job, t)
                    multiply(ws, job, t - 1)
                multiply(ws, job, STEPS - 1)

            def iteration(job):
                for n, (src, w) in enumerate(((cur, "qh"), (k0, "kh"), (v0, "vh"))):
                    run(src, (w,), job + n)

            for f, (inputs, first, _, nw) in enumerate(FOCI):
                for n, (src, ws) in enumerate(inputs):
                    run(hat_a if src == "a" else hat_b, tuple(ws), first + n)
                with pe.Fori(0, ITERS - 1) as it:
                    iteration(it * 3 + first + len(inputs))
                iteration(first + len(inputs) + 3 * (ITERS - 1))
                pe.wait_ge(sums_in, f + 1)
                nc.tensor.matmul(ps_p[:, 0, 2, 0:nw], C.ones[:], diff[:, 0:nw], start=True, stop=True).then_inc(summed, 1)
            run(xa, ("out",), OUT_JOB)

        @block.scalar
        def _(act):
            act.wait_ge(loaded, n_loaded)

            def copies(job, affine):
                for t in range(STEPS):
                    act.wait_ge(turned, job * STEPS + t + 1)
                    if affine:
                        last = nc.scalar.activation(rT[:, t % 2, :], ps_t[:, t % 2, :], ACT.Identity, scale=lna_g[:, 0:1],
                                                    bias=lna_b[:, 0:1])
                    else:
                        last = nc.scalar.activation(rT[:, t % 2, :], ps_t[:, t % 2, :], ACT.Copy)
                    last.then_inc(rT_ready, 1)

            def answer(n, buf, fn):
                act.wait_ge(asked, n)
                nc.scalar.activation(buf, buf, fn).then_inc(answered, 1)

            def iteration(job, n, width):
                for m in range(3):
                    copies(job + m, False)
                answer(n + 1, hv[:], ACT.Sqrt)
                answer(n + 2, score[:, 0:width], ACT.Exp)

            answer(1, trig[:].rearrange("p a b t f -> p (a b t f)"), ACT.Sin)
            answer(2, scale[:], ACT.Sqrt)
            for f, (inputs, first, norms, nw) in enumerate(FOCI):
                for n in range(norms):
                    answer(asked_before(f) + n + 1, rs[:], ACT.Sqrt)
                for n in range(len(inputs)):
                    copies(first + n, True)
                width = FT * FT // nw * NH
                with act.Fori(0, ITERS - 1) as it:
                    iteration(it * 3 + first + len(inputs), it * 2 + asked_before(f) + norms, width)
                iteration(first + len(inputs) + 3 * (ITERS - 1), asked_before(f) + norms + 2 * (ITERS - 1), width)
            copies(OUT_JOB, False)

        @block.vector
        def _(dve):
            dve.wait_ge(loaded, n_loaded)
            tt, ts, stt = nc.vector.tensor_tensor, nc.vector.tensor_scalar, nc.vector.scalar_tensor_tensor

            ts(cond[:], theta[:], 1.0 / 220.0, None, ALU.mult)
            dve.drain()
            ts(base[:], base[:], cond[:, 0:1], None, ALU.mult)
            dve.drain()
            for a in range(2):
                for b in range(2):
                    tt(ang[:, a, b, :, :], bc(place[:, a, :].unsqueeze(2), [P, FT, PAIRS]),
                       bc(base[:].unsqueeze(1), [P, FT, PAIRS]), ALU.mult)
            dve.drain()
            for b in range(2):
                ts(turns[:, :, b, :, :], ang[:, :, b, :, :], 1.0 / (2.0 * math.pi), 0.25 * b, ALU.mult, ALU.add)
            dve.drain()
            ts(turns[:], turns[:], ROUND, None, ALU.add)
            dve.drain()
            ts(turns[:], turns[:], -ROUND, None, ALU.add)
            dve.drain()
            for part in TWO_PI:
                stt(ang[:].rearrange("p a b t f -> p (a b t f)"), turns[:].rearrange("p a b t f -> p (a b t f)"), -part,
                    ang[:].rearrange("p a b t f -> p (a b t f)"), ALU.mult, ALU.add)
                dve.drain()
            ts(ang[:, :, 1, :, :], ang[:, :, 1, :, :], math.pi / 2, None, ALU.add)
            dve.drain()
            edge = 3.1415925
            ts(trig[:], ang[:], edge, -edge, ALU.min, ALU.max).then_inc(asked, 1)
            dve.wait_ge(answered, 1)
            ts(cond[:], temp[:], 0.0, None, ALU.is_gt)
            ts(scale[:], temp[:], 1.0, None, ALU.not_equal)
            dve.drain()
            tt(cond[:], cond[:], scale[:], ALU.mult)
            dve.drain()
            ts(diff[:, 0:1], temp[:], 1e-38, -1.0, ALU.max, ALU.add)
            dve.drain()
            tt(diff[:, 0:1], diff[:, 0:1], cond[:], ALU.mult)
            dve.drain()
            ts(diff[:, 0:1], diff[:, 0:1], 1.0, None, ALU.add)
            dve.drain()
            nc.vector.reciprocal(scale[:], diff[:, 0:1]).then_inc(asked, 1)
            dve.wait_ge(answered, 2)
            ts(scale[:], scale[:], HD ** -0.5, None, ALU.mult)
            dve.drain()
            ts(lnb_g[:, 0, :], lnb_g[:, 0, :], scale[:, 0:1], None, ALU.mult)
            ts(lnb_b[:, 0, :], lnb_b[:, 0, :], scale[:, 0:1], None, ALU.mult)
            dve.drain()

            def norm_rows(to, src, n):
                for t in range(FT):
                    nc.vector.bn_stats(st[:, t, :], src[:, t, :])
                dve.drain()
                for t in range(FT):
                    nc.vector.bn_aggr(mv[:, t, :], st[:, t, :])
                dve.drain()
                ts(rs[:], mv[:, :, 1], 1e-5, None, ALU.add).then_inc(asked, 1)
                tt(to[:], src[:], bc(mv[:, :, 0].unsqueeze(2), row), ALU.subtract)
                dve.wait_ge(answered, n)
                nc.vector.reciprocal(rs[:], rs[:])
                dve.drain()
                last = tt(to[:], to[:], bc(rs[:].unsqueeze(2), row), ALU.mult)
                dve.drain()
                return last

            def take(job, outs):
                for t in range(STEPS):
                    dve.wait_ge(multiplied, job * STEPS + t + 1)
                    for o, (to, b) in enumerate(outs):
                        got = ps_p[:, t % 2, o, :].rearrange("p (r d) -> p r d", d=D)
                        if b is None:
                            last = nc.vector.tensor_copy(to[:, 4 * t:4 * t + 4, :], got)
                        else:
                            last = tt(to[:, 4 * t:4 * t + 4, :], got, bc(b[:].unsqueeze(1), [P, 4, D]), ALU.add)
                    last.then_inc(taken, 1)

            def rotate(buf, a):
                v = buf[:].rearrange("p t (h f e) -> p t h f e", h=NH, e=2)
                part = [prod[:, n * 1024:(n + 1) * 1024].rearrange("p (t h f) -> p t h f", t=FT, h=NH) for n in range(4)]
                sn, cs = (bc(trig[:, a, n, :, :].unsqueeze(2), [P, FT, NH, PAIRS]) for n in range(2))
                tt(part[0], v[:, :, :, :, 0], cs, ALU.mult)
                tt(part[1], v[:, :, :, :, 1], sn, ALU.mult)
                tt(part[2], v[:, :, :, :, 0], sn, ALU.mult)
                tt(part[3], v[:, :, :, :, 1], cs, ALU.mult)
                dve.drain()
                tt(v[:, :, :, :, 0], part[0], part[1], ALU.subtract)
                last = tt(v[:, :, :, :, 1], part[2], part[3], ALU.add)
                dve.drain()
                return last

            heads = lambda t: t.rearrange("p t (h e) -> p (t h) e", e=HD)
            HT = FT * NH
            wide = [P, HT, HD]

            def iteration(job, n, nw, last_one):
                ck = FT // nw
                take(job, [(qk[:, 0, :, :], bias["qh"])])
                take(job + 1, [(k0, bias["kh"])])
                take(job + 2, [(v0, bias["vh"])])
                dve.drain()
                pair = ((qk[:, 0, :, :], qk[:, 0, :, :], 0), (k0[:], qk[:, 1, :, :], 1))
                for src, to, m in pair:
                    nc.vector.tensor_reduce(hm[:, m * HT:(m + 1) * HT], heads(src), AX, ALU.add)
                dve.drain()
                ts(hm[:], hm[:], 1.0 / HD, None, ALU.mult)
                dve.drain()
                for src, to, m in pair:
                    tt(heads(to), heads(src), bc(hm[:, m * HT:(m + 1) * HT].unsqueeze(2), wide), ALU.subtract)
                dve.drain()
                both = qk[:].rearrange("p m t (h e) -> p (m t h) e", e=HD)
                square = prod[:, 0:2 * FT * D].rearrange("p (x e) -> p x e", e=HD)
                tt(square, both, both, ALU.mult)
                dve.drain()
                nc.vector.tensor_reduce(hv[:], square, AX, ALU.add)
                dve.drain()
                ts(hv[:], hv[:], 1.0 / HD, 1e-5, ALU.mult, ALU.add).then_inc(asked, 1)
                dve.wait_ge(answered, n + 1)
                nc.vector.reciprocal(hv[:], hv[:])
                dve.drain()
                tt(both, both, bc(hv[:].unsqueeze(2), [P, 2 * HT, HD]), ALU.mult)
                dve.drain()
                for m in range(2):
                    x = heads(qk[:, m, :, :])
                    tt(x, x, bc(lnb_g[:, m, :].unsqueeze(1), wide), ALU.mult)
                dve.drain()
                for m in range(2):
                    x = heads(qk[:, m, :, :])
                    tt(x, x, bc(lnb_b[:, m, :].unsqueeze(1), wide), ALU.add)
                dve.drain()
                QC = 8192 // (ck * D)
                for q in range(0, FT, QC):
                    w = q // ck * ck
                    tt(prod.rearrange("p (q k d) -> p q k d", q=QC, k=ck), bc(qk[:, 0, q:q + QC, :].unsqueeze(2), [P, QC, ck, D]),
                       bc(qk[:, 1, w:w + ck, :].unsqueeze(1), [P, QC, ck, D]), ALU.mult)
                    dve.drain()
                    nc.vector.tensor_reduce(score[:, q * ck * NH:(q + QC) * ck * NH],
                                            prod.rearrange("p (x e) -> p x e", e=HD), AX, ALU.add)
                    dve.drain()
                s = score[:, 0:FT * ck * NH].rearrange("p (q k h) -> p q k h", q=FT, k=ck)
                turned_s = s.rearrange("p q k h -> p q h k")
                nc.vector.tensor_reduce(most[:], turned_s, AX, ALU.max)
                dve.drain()
                tt(s, s, bc(most[:].unsqueeze(2), [P, FT, ck, NH]), ALU.subtract).then_inc(asked, 1)
                dve.wait_ge(answered, n + 2)
                nc.vector.tensor_reduce(den[:], turned_s, AX, ALU.add)
                dve.drain()
                nc.vector.reciprocal(den[:], den[:])
                for q in range(0, FT, QC):
                    w = q // ck * ck
                    vals = v0[:, w:w + ck, :].rearrange("p k (h e) -> p h e k", e=HD)
                    for r in range(QC):
                        to = prod[:, r * ck * D:(r + 1) * ck * D].rearrange("p (h e k) -> p h e k", h=NH, e=HD)
                        tt(to, bc(turned_s[:, q + r, :, :].unsqueeze(2), [P, NH, HD, ck]), vals, ALU.mult)
                    dve.drain()
                    nc.vector.tensor_reduce(ai[:, q:q + QC, :].rearrange("p q d -> p (q d)"),
                                            prod.rearrange("p (x k) -> p x k", k=ck), AX, ALU.add)
                    dve.drain()
                tt(heads(ai[:]), heads(ai[:]), bc(den[:].rearrange("p t h -> p (t h)").unsqueeze(2), wide), ALU.mult)
                dve.drain()
                if last_one:
                    return
                change = prod[:, 0:FT * D]
                tt(change.rearrange("p (t d) -> p t d", d=D), ai[:], prev[:], ALU.subtract)
                dve.drain()
                nc.vector.tensor_reduce(diff[:, 0:nw], change.rearrange("p (w x) -> p w x", w=nw), AX, ALU.add,
                                        apply_absolute_value=True)
                nc.vector.tensor_copy(prev[:], ai[:])
                tt(cur[:], cur[:], ai[:], ALU.add).then_inc(src_ready, 3)
                dve.drain()

            dve.wait_ge(fetched, 32)
            for f, (inputs, first, norms, nw) in enumerate(FOCI):
                n = asked_before(f)
                if f == 0:
                    norm_rows(xa, xa, n + 1)
                    norm_rows(hat_a, xa, n + 2)
                elif f == 1:
                    norm_rows(hat_a, xb, n + 1)
                else:
                    norm_rows(hat_a, xa, n + 1)
                    norm_rows(hat_b, xb, n + 2)
                nc.vector.memset(prev[:], 0.0).then_inc(src_ready, len(inputs))
                outs = [(cur, None), (k0, None), (v0, None)]
                if len(inputs) == 1:
                    take(first, outs)
                else:
                    take(first, outs[0:1])
                    take(first + 1, outs[1:3])
                dve.drain()
                rotate(cur, f // 2)
                rotate(k0, f // 2)
                nc.vector.memset(den[:], 0.0).then_inc(src_ready, 3)
                job0 = first + len(inputs)
                with dve.Fori(0, ITERS - 1) as it:
                    iteration(it * 3 + job0, it * 2 + n + norms, nw, False)
                nc.vector.tensor_copy(done[:, 0:nw], diff[:, 0:nw]).then_inc(sums_in, 1)
                iteration(job0 + 3 * (ITERS - 1), n + norms + 2 * (ITERS - 1), nw, True)
                dve.wait_ge(summed, f + 1)
                count = P * NH * (FW if nw > 1 else S) * HD
                ts(kept[:, 0:nw], ps_p[:, 0, 2, 0:nw], 1.0 / count, None, ALU.mult)
                dve.drain()
                ts(done[:, 0:nw], kept[:, 0:nw], factor[:, 0:1], thr[:, 0:1], ALU.mult, ALU.add)
                dve.drain()
                tt(done[:, 0:nw], kept[:, 0:nw], done[:, 0:nw], ALU.is_lt)
                dve.drain()
                ts(kept[:, 0:nw], done[:, 0:nw], -1.0, 1.0, ALU.mult, ALU.add)
                dve.drain()
                to = xb if f == 1 else xa
                flat = lambda t, w: t[:, w * FT // nw:(w + 1) * FT // nw, :].rearrange("p t d -> p (t d)")
                for w in range(nw):
                    ts(flat(ai, w), flat(ai, w), kept[:, w:w + 1], None, ALU.mult)
                dve.drain()
                for w in range(nw):
                    last = stt(flat(to, w), flat(prev, w), done[:, w:w + 1], flat(ai, w), ALU.mult, ALU.add)
                if f == 2:
                    last.then_inc(src_ready, 1)
                dve.drain()
            take(OUT_JOB, [(hat_a, None)])
            dve.drain()
            nc.vector.memset(den[:], 0.0).then_inc(out_ready, 1)
            dve.wait_ge(returned, 32)
            for b in range(2):
                r = slice(S * b, S * b + FT)
                tt(C.X[r, 0:C.NT, :], C.X[r, 0:C.NT, :], C.Y[r, 0:C.NT, :], ALU.add)
            dve.drain()
            with dve.Fori(0, C.NG) as i:
                row_stats(nc, dve, C, C.X, gst, gmv, i)
                dve.drain()


def store_x(C, out):
    nc = C.nc
    with ExitStack() as ctx:
        sc = Scope(nc, ctx, "store")
        stored = sc.sem("stored")
        block = ctx.enter_context(nc.Block())

        @block.sync
        def _(sp):
            sp.dma_start(out.rearrange("(n p) d -> p n d", p=P), C.X[:, 0:C.NT, :]).then_inc(stored, 16)
            sp.wait_ge(stored, 16)



def constants():
    c = {"ident": np.eye(P, dtype=np.float32)}
    pos = np.arange(S, dtype=np.float32)
    lower = np.tril(np.ones((S, S), np.float32))
    c["tril"] = np.concatenate([lower, lower])
    row = np.arange(P)
    c["hmask"] = (row[:, None] // HD % HR == np.arange(HR)[None, :]).astype(np.float32)
    inv = (1.0 / 10000.0 ** (np.arange(0, HD, 2, dtype=np.float32) / HD)).astype(np.float32)
    ang = (pos[:, None] * inv[None, :]).astype(np.float32)
    c["cosT"] = np.tile(np.repeat(np.cos(ang), 2, axis=1).T, (NH, 1)).astype(np.float32)
    c["sinT"] = np.tile(np.repeat(np.sin(ang), 2, axis=1).T, (NH, 1)).astype(np.float32)
    c["falling"] = np.tile(np.arange(NE, 0, -1, dtype=np.float32), (P, 1))
    dist = np.abs(pos[:, None] - pos[None, :])

    def twice(t):
        t = t.astype(np.float32).transpose(1, 0, 2)
        return np.concatenate([t, t])
    slopes = 2.0 ** (-8.0 * np.arange(NH) / NH)
    c["table0"] = twice(-slopes[:, None, None].astype(np.float32) * dist)
    m = np.exp(-np.power(5000.0, (np.arange(1, NH + 1) - 1.0) / (NH - 1.0) * 0.8))
    c["table1"] = twice(m[:, None, None].astype(np.float32) * (1000.0 + dist))
    slopes = 0.5 ** np.arange(1, NH + 1)
    c["table3"] = twice(-np.maximum(pos[:, None] - pos[None, :], 0) * slopes[:, None, None].astype(np.float32))
    slopes = (2.0 ** (-2.0 ** -(math.log2(32) - 3))) ** np.arange(1, 33, dtype=np.float32)
    rel = pos[None, :] - pos[:, None]
    bias = np.where(rel <= 0, slopes.astype(np.float32)[:, None, None] * rel, np.float32(-BIG))
    bias = bias.reshape(4, 2, 2, 2, S, S).transpose(0, 2, 1, 3, 4, 5).reshape(32, S, S)
    c["table_a3"] = twice(bias).reshape(P, 4, UH, S)
    perm = np.zeros((P, P), np.float32)
    quarter = np.arange(D // 4)
    for to, of, sign in ((0, 2, 1), (1, 3, -1), (2, 0, -1), (3, 1, 1)):
        perm[of * 32 + quarter, to * 32 + quarter] = sign
    c["perm"] = perm
    pick_row = np.zeros((P, 2 * NS), np.float32)
    for part in (0, 64, 96):
        pick_row[part + np.arange(2 * NS), np.arange(2 * NS)] = 1
    c["pick_row"] = pick_row
    c["flip"] = np.kron(np.eye(2, dtype=np.float32), np.eye(S, dtype=np.float32)[::-1]).astype(np.float32)
    mel = np.linspace(0.0, 2595.0 * np.log10(1.0 + 4000.0 / 200.0), PAIRS)
    c["base"] = np.tile((200.0 * (10.0 ** (mel / 2595.0) - 1.0) / 1000.0).astype(np.float32), (P, 1))
    c["place"] = np.tile(np.stack([np.arange(FT) % FW, np.arange(FT)]).astype(np.float32), (P, 1, 1))
    return c


def layouts(v):
    t = lambda n: np.ascontiguousarray(v[n].T)
    col = lambda n: np.ascontiguousarray(v[n].reshape(-1, 1))
    row = lambda n: np.ascontiguousarray(v[n].reshape(1, -1))
    rep = lambda n: np.ascontiguousarray(np.broadcast_to(v[n].reshape(1, -1), (P, v[n].size)))
    a = {"x": v["x"].reshape(-1, D), "ctxT": np.ascontiguousarray(v["ctx_1024"].reshape(-1, D).T)}
    for k in ("Wq", "Wk", "Wv", "Wo"):
        a["a0_" + k] = t("L0_attn_" + k)
        a["c0_" + k] = t("L0_xattn_" + k)
    for k in ("bq", "bk", "bv"):
        a["c0_" + k] = col("L0_xattn_" + k)
    a["c0_bo"] = row("L0_xattn_bo")
    for k in ("Wq", "Wk", "Wv", "Wc", "Wo"):
        a["a1_" + k] = v["L1_attn_" + k]
    a["a1_We"] = np.ascontiguousarray(np.repeat(v["L1_attn_We"].reshape(S, 4, 1, HD), NH // 4, axis=2).reshape(S, D))
    for k in ("bq", "bk", "bv"):
        a["a1_" + k] = col("L1_attn_" + k)
    a["a1_bo"] = row("L1_attn_bo")
    a["a1_gamma"], a["a1_beta"] = rep("L1_attn_gamma"), rep("L1_attn_beta")
    qkv = v["L2_ffn_W_qkv"]
    for n, k in enumerate(("Wq", "Wk", "Wv")):
        a["f2_" + k] = np.ascontiguousarray(qkv[n * D:(n + 1) * D].T)
    a["f2_Wo"] = t("L2_ffn_W_out")
    a["f2_wr"] = rep("L2_ffn_w_router")
    a["f2_g1"], a["f2_g2"] = col("L2_ffn_g1"), col("L2_ffn_g2")
    for k, n in (("Wq", "wq"), ("Wk", "wk"), ("Wv", "wv"), ("Wo", "out")):
        a["c3_" + k] = t(f"L3_xattn_{n}_w")
        a["c3_b" + k[1]] = (row if k == "Wo" else col)(f"L3_xattn_{n}_b")
    a["f0_wi"], a["f0_wo"] = t("L0_ffn_wi_W"), t("L0_ffn_wo_W")
    lora_a = v["L0_ffn_lora_A"].reshape(-1, D)
    a["f0_ga"] = np.ascontiguousarray(np.concatenate([v["L0_ffn_gate_W"], lora_a]).T)
    a["f0_B"] = np.ascontiguousarray(v["L0_ffn_lora_B"].transpose(0, 2, 1).reshape(lora_a.shape[0], -1))
    a["f0_gb"] = rep("L0_ffn_gate_b")
    a["f0_wib"] = np.ascontiguousarray(v["L0_ffn_wi_b"].reshape(-1, P).T)
    a["f0_wob"] = row("L0_ffn_wo_b")
    a["f2_w1"], a["f2_w2"], a["f2_w3"] = t("L2_ffn_W1"), t("L2_ffn_W2"), t("L2_ffn_W3")
    a["f3_wr"], a["f3_w1"], a["f3_w2"] = v["L3_ffn_router_w"], v["L3_ffn_w1"], v["L3_ffn_w2"]
    c2 = lambda n: np.ascontiguousarray(v["L2_xattn_" + n].reshape(D, 1, NJ, 2, HW))
    a["c2_wq"], a["c2_wk"] = c2("Wq").reshape(D, NJ, P), c2("Wk").reshape(D, NJ, P)
    a["c2_wv"] = np.ascontiguousarray(c2("Wv").transpose(0, 3, 1, 2, 4)).reshape(D, 2, NJ * HW)
    a["c2_wo"] = np.ascontiguousarray(v["L2_xattn_Wo"].reshape(NJ, P, D).transpose(1, 0, 2))
    a["c2_bo"] = row("L2_xattn_bo")
    w = v["L3_attn_W_qkv"]
    nq, nk = 32, 16
    q = w[:, :nq * HW].reshape(D, 4, 2, 2, 2, HW)
    a["a3_wq"] = np.ascontiguousarray(q.transpose(0, 1, 2, 4, 3, 5)).reshape(D, 16, P)
    a["a3_wk"] = w[:, nq * HW:(nq + nk) * HW].reshape(D, 8, P)
    vv = w[:, (nq + nk) * HW:].reshape(D, 8, 2, HW)
    a["a3_wv"] = np.ascontiguousarray(vv.transpose(0, 2, 1, 3)).reshape(D, 2, 8 * HW)
    o = v["L3_attn_W_out"].reshape(4, 2, 2, 2, HW, D)
    a["a3_wo"] = np.ascontiguousarray(o.transpose(2, 4, 0, 1, 3, 5)).reshape(P, 16, D)
    wide = lambda x: np.ascontiguousarray(np.broadcast_to(x.reshape(-1, 1), (x.size, P)))
    one = lambda n: np.ascontiguousarray(np.broadcast_to(v[n].reshape(1, 1), (P, 1)))
    for n in range(3):
        a[f"f1_w{n}"], a[f"f1_b{n}"] = v[f"L1_ffn_cn_w{n + 1}"], col(f"L1_ffn_cn_b{n + 1}")
    for n in range(2):
        a[f"f1_gw{n}"], a[f"f1_gb{n}"] = v[f"L1_ffn_gc_w{n + 1}"], col(f"L1_ffn_gc_b{n + 1}")
    a["f1_w3"], a["f1_b3"] = wide(v["L1_ffn_cn_w4"]), one("L1_ffn_cn_b4")
    a["f1_gw2"], a["f1_gb2"] = wide(v["L1_ffn_gc_w3"]), one("L1_ffn_gc_b3")
    a["f1_reach"] = one("L1_ffn_adaptive_range")
    halves = lambda x: np.ascontiguousarray(x.reshape(NHF, P, -1).transpose(1, 0, 2))
    for d in ("m1", "m2"):
        m = lambda n: v[f"L2_attn_{d}_{n}"]
        a[d + "_in_w"] = np.ascontiguousarray(m("in_w").T)
        a[d + "_taps"] = np.ascontiguousarray(np.broadcast_to(m("conv_w").T[None], (P, NTAP, DI)))
        a[d + "_conv_b"], a[d + "_dt_b"], a[d + "_D"] = (halves(m(n))[:, :, 0].copy() for n in ("conv_b", "dt_b", "D"))
        low = np.zeros((DI, P), np.float32)
        low[:, 32:32 + DTR] = m("xproj_w")[:DTR].T
        for at in (0, 64, 96):
            low[:, at:at + 2 * NS] = m("xproj_w")[DTR:].T
        a[d + "_xp"], a[d + "_out_w"] = halves(low), halves(m("out_w").T)
        a[d + "_dt_w"], a[d + "_A"] = np.ascontiguousarray(m("dt_w").T), halves(m("Alog"))
        a[d + "_g"], a[d + "_be"] = col("L2_attn_norm_g"), col("L2_attn_norm_b")
    a["m3_w1"], a["m3_w2"] = t("L2_attn_ff1_w"), t("L2_attn_ff2_w")
    a["m3_b1"], a["m3_b2"] = np.ascontiguousarray(v["L2_attn_ff1_b"].reshape(-1, P).T), row("L2_attn_ff2_b")
    a["m3_g"], a["m3_be"] = col("L2_attn_ffn_g"), col("L2_attn_ffn_b")
    a["ctx"] = v["ctx_1024"]
    wkv = v["L1_xattn_Wkv"]
    a["x1_w_q"], a["x1_w_out"] = t("L1_xattn_Wq"), t("L1_xattn_Wout")
    a["x1_w_k"], a["x1_w_v"] = np.ascontiguousarray(wkv[:D].T), np.ascontiguousarray(wkv[D:].T)
    for k in ("qh", "kh", "vh"):
        blocks_ = np.zeros((NH, HD, NH, HD), np.float32)
        for h in range(NH):
            blocks_[h, :, h, :] = v["L1_xattn_W" + k].T
        a["x1_w_" + k] = blocks_.reshape(D, D)
        a["x1_b_" + k] = np.ascontiguousarray(np.tile(v["L1_xattn_b" + k].reshape(1, HD), (P, NH)))
    a["x1_lna_g"], a["x1_lna_b"] = col("L1_xattn_lna_g"), col("L1_xattn_lna_b")
    a["x1_lnb_g"], a["x1_lnb_b"] = (np.ascontiguousarray(np.tile(v["L1_xattn_lnb_" + k].reshape(1, 1, HD), (P, 2, 1)))
                                    for k in "gb")
    for k, n in (("theta", "theta"), ("temp", "temp"), ("thr", "threshold"), ("factor", "factor")):
        a["x1_" + k] = one("L1_xattn_" + n)
    m = v["mask_1x1xSxS2_ik0"].reshape(S, S)
    a["mask"] = np.concatenate([m, m])
    return a


def pick(A, prefix, /, **names):
    return {k: A[n if n in A else prefix + n][:] for k, n in names.items()}


def blocks(C, A):
    qkvo = dict(wq="Wq", wk="Wk", wv="Wv", wo="Wo", hmask="hmask")

    def l0_attn():
        norm_scales(C, "n0a", 1e-5)
        attn16(C, "a0", "rope", pick(A, "a0_", cosT="cosT", sinT="sinT", table="table0", **qkvo))

    def l0_xattn():
        norm_scales(C, "n0c", 1e-5)
        attn16(C, "c0", "ctx", pick(A, "c0_", bq="bq", bk="bk", bv="bv", bo="bo", table="table1", **qkvo), A["ctxT"])

    def l1_attn():
        norm_scales(C, "n1a", 1e-5)
        attn16(C, "a1", "linear", pick(A, "a1_", bq="bq", bk="bk", bv="bv", bo="bo", wc="Wc", we="We", tril="tril",
                                       **qkvo))
        inner_scales(C, "n1y", 1e-5, False)
        affine_norm(C, "a1n", A["a1_gamma"], A["a1_beta"])

    def l2_ffn():
        norm_scales(C, "n2f", 1e-5, 1e-6)
        attn16(C, "f2", "rank", pick(A, "f2_", g1="g1", wr="wr", tril="tril", **qkvo))
        inner_scales(C, "n2y", 1e-6, True)
        gated_ffn(C, "g2", pick(A, "f2_", w1="w1", w2="w2", w3="w3", g="g2"))

    def l0_ffn():
        norm_scales(C, "n0f", 1e-5)
        lora_ffn(C, "f0", pick(A, "f0_", wi="wi", wo="wo", ga="ga", B="B", gb="gb", wib="wib", wob="wob", falling="falling"))

    def l3_ffn():
        norm_scales(C, "n3f", 1e-5)
        topk_ffn(C, "f3", pick(A, "f3_", wr="wr", w1="w1", w2="w2", falling="falling"))

    def l1_xattn():
        scratch = [C.nc.dram_tensor(n, (P, FT, D), F32, kind="Internal").ap() for n in ("focus_rows", "focus_out")]
        names = ["w_q", "w_k", "w_v", "w_qh", "w_kh", "w_vh", "w_out", "b_qh", "b_kh", "b_vh", "lna_g", "lna_b", "lnb_g",
                 "lnb_b", "theta", "temp", "thr", "factor", "base", "place"]
        focus_block(C, "x1", A["ctx"], *scratch, pick(A, "x1_", **{n: n for n in names}))

    def l1_ffn():
        norm_scales(C, "n1f", 1e-5)
        names = [f"{k}{n}" for k, m in (("w", 4), ("b", 4), ("gw", 3), ("gb", 3)) for n in range(m)]
        coupled_ffn(C, "f1", pick(A, "f1_", perm="perm", reach="reach", **{n: n for n in names}))

    def l2_attn():
        norm_scales(C, "n2a", 1e-5, 1e-5)
        names = ("in_w", "taps", "conv_b", "xp", "dt_w", "dt_b", "A", "D", "out_w", "pick_row", "flip", "g", "be")
        for d in ("m1", "m2"):
            mamba(C, d, pick(A, d + "_", **{n: n for n in names}), d == "m1")
        mamba_join(C, "mj")
        inner_scales(C, "n2m", 1e-5, False)
        gelu_ffn(C, "m3", pick(A, "m3_", w1="w1", w2="w2", b1="b1", b2="b2", g="g", be="be"))

    def l2_xattn():
        norm_scales(C, "n2c", 1e-5)
        attn64(C, "c2", pick(A, "c2_", wq="wq", wk="wk", wv="wv", wo="wo", bo="bo"), 1, 1, A["ctxT"])

    def l3_attn():
        norm_scales(C, "n3a", 1e-5)
        attn64(C, "a3", pick(A, "a3_", wq="wq", wk="wk", wv="wv", wo="wo", table="table_a3"), 4, 2)

    def l3_xattn():
        norm_scales(C, "n3c", 1e-5)
        attn16(C, "c3", "mask", pick(A, "c3_", bq="bq", bk="bk", bv="bv", bo="bo", table="table3", mask="mask",
                                     **qkvo), A["ctxT"])

    return {0: l0_attn, 1: l0_xattn, 2: l0_ffn, 3: l1_attn, 4: l1_xattn, 5: l1_ffn, 6: l2_attn, 7: l2_xattn, 8: l2_ffn, 9: l3_attn, 10: l3_xattn, 11: l3_ffn}


def program(nc, A, out, groups, which):
    with ExitStack() as ctx:
        C = Core(nc, ctx, groups)
        load_x(C, A["x"], A)
        todo = blocks(C, A)
        for n in which:
            todo[n]()
        store_x(C, out)


def kernel(**inputs):
    import concourse.bacc as bacc
    from concourse.bass_utils import run_bass_kernel_spmd

    v = {k: np.asarray(a) for k, a in inputs.items()}
    arrays = {"in_" + k: np.ascontiguousarray(a) for k, a in {**constants(), **layouts(v)}.items()}
    nc = bacc.Bacc("TRN2", target_bir_lowering=False, num_devices=1)
    A = {k[3:]: nc.dram_tensor(k, a.shape, mybir.dt.from_np(a.dtype), kind="ExternalInput").ap() for k, a in arrays.items()}
    rows_out = v["x"].shape[0] * S
    out = nc.dram_tensor("out_0_dram", (rows_out, D), F32, kind="ExternalOutput").ap()
    program(nc, A, out, rows_out // (4 * P), range(12))
    result = run_bass_kernel_spmd(nc, [arrays], core_ids=[0])
    return result.results[0]["out_0_dram"].reshape(v["x"].shape)
```

```python
import math
from contextlib import ExitStack

import numpy as np

import concourse.bass as bass
from concourse import mybir
from concourse.alu_op_type import AluOpType as ALU

F32 = mybir.dt.float32
BF16 = mybir.dt.bfloat16
I32 = mybir.dt.int32
ACT = mybir.ActivationFunctionType
AX = mybir.AxisListType.X

P = 128
D = 128
S = 64
TPG = 4
GT = TPG * P
SPG = GT // S
BIG = 1e30


class Core:

    def __init__(self, nc, ctx, groups):
        def sb(name, shape, dt=F32):
            return ctx.enter_context(nc.sbuf_tensor(name, shape, dt))
        self.nc, self.NG, self.NT = nc, groups, groups * TPG
        pad = self.NT + 2 * TPG
        self.X = sb("X", [P, pad, D])
        self.Y = sb("Y", [P, pad, D])
        self.MV = sb("MV", [P, pad, 2])
        self.RS = sb("RS", [P, pad])
        self.NM = sb("NM", [P, pad])
        self.RS2 = sb("RS2", [P, pad])
        self.NM2 = sb("NM2", [P, pad])
        self.tmp = sb("stat_tmp", [P, pad])
        self.ident = sb("ident", [P, P])
        self.ones = sb("ones", [P, P])


class Scope:

    def __init__(self, nc, ctx, name):
        self.nc, self.ctx, self.name = nc, ctx, name
        self.sems = []
        ctx.callback(self.clear)

    def clear(self):
        self.nc.clear_and_free_semaphores(self.sems)
        self.nc.all_engine_barrier()

    def sb(self, name, shape, dt=F32):
        return self.ctx.enter_context(self.nc.sbuf_tensor(f"{self.name}_{name}", shape, dt))

    def ps(self, name, shape):
        return self.ctx.enter_context(self.nc.psum_tensor(f"{self.name}_{name}", shape, F32))

    def sem(self, name):
        self.sems.append(self.nc.alloc_semaphore(name=f"{self.name}_{name}"))
        return self.sems[-1]


def bc(ap, shape):
    return ap.to_broadcast(shape)


def load_x(C, x, constants):
    nc = C.nc
    with ExitStack() as ctx:
        sc = Scope(nc, ctx, "load")
        steps = C.NT // ROW_TILES
        loaded, zeroed = sc.sem("loaded"), sc.sem("zeroed")
        x_loaded = [sc.sem(f"x_loaded{n}") for n in range(steps)]
        st = sc.sb("st", [P, ROW_TILES, 6])
        mv = sc.sb("mv", [P, ROW_TILES, 2])
        block = ctx.enter_context(nc.Block())

        @block.sync
        def _(sp):
            for n in range(steps):
                tiles = slice(n * ROW_TILES, (n + 1) * ROW_TILES)
                sp.dma_start(C.X[:, tiles, :], x.rearrange("(n p) d -> p n d", p=P)[:, tiles, :]).then_inc(x_loaded[n], 16)
            sp.dma_start(C.ident[:], constants["ident"]).then_inc(loaded, 16)

        @block.gpsimd
        def _(pool):
            nc.gpsimd.memset(C.Y[:], 0.0).then_inc(zeroed, 1)
            nc.gpsimd.memset(C.ones[:], 1.0).then_inc(zeroed, 1)
            nc.gpsimd.memset(C.X[:, C.NT:, :], 0.0).then_inc(zeroed, 1)
            nc.gpsimd.memset(C.MV[:, C.NT:, :], 0.0).then_inc(zeroed, 1)

        @block.vector
        def _(dve):
            for n in range(steps):
                dve.wait_ge(x_loaded[n], 16)
                row_stats(nc, dve, C, C.X, st, mv, n, ROW_TILES)
                dve.drain()
            dve.wait_ge(loaded, 16)


ROW_TILES = 16


def row_stats(nc, dve, C, src, st, mv, i, tiles):
    for p in range(tiles):
        nc.vector.bn_stats(st[:, p, :], src[:, i * tiles + p, :])
    dve.drain()
    for p in range(tiles):
        nc.vector.bn_aggr(mv[:, p, :], st[:, p, :])
    dve.drain()
    nc.vector.tensor_copy(C.MV[:, bass.ds(i * tiles, tiles), :], mv[:])


class NormScales:

    def __init__(self, C, sc, eps, second=None):
        self.C, self.eps, self.second = C, eps, second
        self.shifted, self.rooted = sc.sem("shifted_var"), sc.sem("rooted_var")

    def dve(self, dve):
        C, nc = self.C, self.C.nc
        mean, var = C.MV[:, :, 0], C.MV[:, :, 1]
        nc.vector.tensor_scalar(C.tmp[:], var, self.eps, None, ALU.add).then_inc(self.shifted, 1)
        dve.wait_ge(self.rooted, 1)
        nc.vector.reciprocal(C.RS[:], C.tmp[:])
        dve.drain()
        nc.vector.scalar_tensor_tensor(C.NM[:], mean, -1.0, C.RS[:], ALU.mult, ALU.mult)
        if self.second is not None:
            nc.vector.tensor_tensor(C.tmp[:], C.RS[:], C.RS[:], ALU.mult)
            dve.drain()
            nc.vector.tensor_tensor(C.tmp[:], C.tmp[:], var, ALU.mult)
            dve.drain()
            nc.vector.tensor_scalar(C.tmp[:], C.tmp[:], self.second, None, ALU.add).then_inc(self.shifted, 1)
            dve.wait_ge(self.rooted, 2)
            nc.vector.reciprocal(C.tmp[:], C.tmp[:])
            dve.drain()
            nc.vector.tensor_tensor(C.RS2[:], C.tmp[:], C.RS[:], ALU.mult)
            dve.drain()
            nc.vector.scalar_tensor_tensor(C.NM2[:], mean, -1.0, C.RS2[:], ALU.mult, ALU.mult)
        dve.drain()

    def act(self, act):
        for n in range(1 if self.second is None else 2):
            act.wait_ge(self.shifted, n + 1)
            self.C.nc.scalar.activation(self.C.tmp[:], self.C.tmp[:], ACT.Sqrt).then_inc(self.rooted, 1)


class InnerScales:

    def __init__(self, C, sc, eps, mean_square):
        self.C, self.eps, self.mean_square = C, eps, mean_square
        self.shifted, self.rooted = sc.sem("shifted_var"), sc.sem("rooted_var")

    def dve(self, dve):
        C, nc = self.C, self.C.nc
        mean, var = C.MV[:, :, 0], C.MV[:, :, 1]
        if self.mean_square:
            nc.vector.tensor_tensor(C.tmp[:], mean, mean, ALU.mult)
            dve.drain()
            nc.vector.tensor_tensor(C.tmp[:], C.tmp[:], var, ALU.add)
            dve.drain()
            nc.vector.tensor_scalar(C.tmp[:], C.tmp[:], self.eps, None, ALU.add).then_inc(self.shifted, 1)
        else:
            nc.vector.tensor_scalar(C.tmp[:], var, self.eps, None, ALU.add).then_inc(self.shifted, 1)
        dve.wait_ge(self.rooted, 1)
        nc.vector.reciprocal(C.RS2[:], C.tmp[:])
        dve.drain()
        if not self.mean_square:
            nc.vector.scalar_tensor_tensor(C.NM2[:], mean, -1.0, C.RS2[:], ALU.mult, ALU.mult)
            dve.drain()

    def act(self, act):
        act.wait_ge(self.shifted, 1)
        self.C.nc.scalar.activation(self.C.tmp[:], self.C.tmp[:], ACT.Sqrt).then_inc(self.rooted, 1)



NH, HD = 16, 8
NB = NH // 2
RG, HR = 4, 4
UT = 2
UPG = TPG // UT
VW = HD + 1


def attn16(C, name, mode, W, kT_dram=None):
    nc = C.nc
    cross, linear, rank = mode in ("ctx", "mask"), mode == "linear", mode == "rank"
    to_y = linear or rank
    with ExitStack() as ctx:
        sc = Scope(nc, ctx, name)
        sb, ps, sem = sc.sb, sc.ps, sc.sem
        wq, wo = sb("wq", [P, D]), sb("wo", [P, D])
        bq, bv = sb("bq", [P, 1]), sb("bv", [P, 1])
        bo = sb("bo", [1, D])
        hmask = sb("hmask", [P, HR])
        bkm = sb("bkm", [P, HR])
        if linear:
            wk, wv = sb("wk", [P, 32]), sb("wv", [P, 32])
            wc, we = sb("wc", [32, S]), sb("we", [S, D])
            bk32, bv32 = sb("bk32", [32, 1]), sb("bv32", [32, 1])
            k32, c64 = sb("k32", [32, 2, GT]), sb("c64", [S, 2, GT])
        else:
            wk, wv = sb("wk", [P, D]), sb("wv", [P, D])
            bk = sb("bk", [P, 1])
        if mode == "rope":
            wqr, wkr = sb("wqr", [P, D]), sb("wkr", [P, D])
            cosT, sinT = sb("cosT", [P, S]), sb("sinT", [P, S])
        if mode in ("rope", "linear"):
            t1, t2 = sb("t1", [P, GT]), sb("t2", [P, GT])
            kf = sb("kf", [P, GT])
        if mode in ("rope", "ctx", "mask"):
            table = sb("table", [P, NH, S])
        if mode == "mask":
            keepi, keep = sb("keepi", [P, S], I32), sb("keep", [P, S])
            off = sb("off", [P, S])
        if linear or rank:
            tril = sb("tril", [P, S])
        if rank:
            g1, wr = sb("g1", [P, 1]), sb("wr", [P, D])
            s_own, s_rep = sb("s_own", [P, TPG]), sb("s_rep", [P, TPG, P])
            hidden, r1, r2 = sb("hidden", [P, TPG, S]), sb("r1", [P, TPG, S]), sb("r2", [P, TPG, S])
            prod = sb("prod", [P, D])
        xn, xnT = sb("xn", [P, TPG, D]), sb("xnT", [P, GT])
        xt = sb("xt", [P, UT, D])
        kvb = sb("kvb", [P, GT]) if cross else xnT
        qT = sb("qT", [P, GT])
        kbd = sb("kbd", [P, SPG, HR, S])
        vbd = sb("vbd", [P, SPG, NB, 2, VW])
        s1 = sb("s1", [P, UPG, UT, NH, S])
        mx = sb("mx", [P, UT, NH])
        pT = sb("pT", [P, 2, 4, P])
        rden = sb("rden", [P, UT, NH])
        on, oT = sb("on", [P, UT, D]), sb("oT", [P, UT, P])
        st, mv = sb("st", [P, UT, 6]), sb("mv", [P, TPG, 2])

        ps_s = ps("ps_s", [P, RG, UT * HR * S])
        ps_t = ps("ps_t", [P, 2, 4 * P])
        ps_j = ps("ps_j", [P, GT])
        ps_o = ps("ps_o", [P, 512])
        o_acc = ps_o[:, 0:UT * NH * VW].rearrange("p (t h e) -> p t h e", t=UT, e=VW)
        j_tr = ps_j[:, 0:UT * P].rearrange("p (t q) -> p t q", t=UT)
        j_out = ps_j[:, UT * P:2 * UT * P].rearrange("p (t q) -> p t q", t=UT)

        loaded, prepared = sem("loaded"), sem("prepared")
        kv_loaded = sem("kv_loaded")
        xn_ready, xT_done, xT_ready = sem("xn_ready"), sem("xT_done"), sem("xT_ready")
        q_done, q_ready = sem("q_done"), sem("q_ready")
        k_done, k_ready, v_done, v_ready = sem("k_done"), sem("k_ready"), sem("v_done"), sem("v_ready")
        kf_ready, e_in, e_out = sem("kf_ready"), sem("e_in"), sem("e_out")
        low_done, low_ready = sem("low_done"), sem("low_ready")
        rank_done, rank_in, rank_read = sem("rank_done"), sem("rank_in"), sem("rank_read")
        scores_done, scores_read = sem("scores_done"), sem("scores_read")
        shifted, probs = sem("shifted"), sem("probs")
        pT_done, pT_ready = sem("pT_done"), sem("pT_ready")
        pv_done, on_ready = sem("pv_done"), sem("on_ready")
        oT_done, oT_ready = sem("oT_done"), sem("oT_ready")
        out_done, out_read = sem("out_done"), sem("out_read")
        scales = NormScales(C, sc, 1e-5, 1e-6 if rank else None)
        block = ctx.enter_context(nc.Block())
        loads = [(wq, W["wq"]), (wo, W["wo"]), (wk, W["wk"]), (wv, W["wv"]), (hmask, W["hmask"])]
        if "bo" in W:
            loads.append((bo, W["bo"]))
        if "bq" in W:
            loads.append((bq, W["bq"]))
        if cross:
            loads += [(bk, W["bk"]), (bv, W["bv"])]
        if mode == "rope":
            loads += [(cosT, W["cosT"]), (sinT, W["sinT"])]
        if mode in ("rope", "ctx", "mask"):
            loads.append((table, W["table"]))
        if mode == "mask":
            loads.append((keepi, W["mask"]))
        if linear:
            loads += [(wc, W["wc"]), (we, W["we"]), (bk32, W["bk"]), (bv32, W["bv"])]
        if linear or rank:
            loads.append((tril, W["tril"]))
        if rank:
            loads += [(g1, W["g1"]), (wr, W["wr"])]
        n_loaded = 16 * len(loads)

        @block.sync
        def _(sp):
            for to, of in loads:
                sp.dma_start(to[:], of).then_inc(loaded, 16)
            if cross:
                sp.dma_start(kvb[:], kT_dram[:, 0:GT]).then_inc(kv_loaded, 16)
                with sp.Fori(1, C.NG) as i:
                    sp.wait_ge(v_done, i)
                    sp.dma_start(kvb[:], kT_dram[:, bass.ds(i * GT, GT)]).then_inc(kv_loaded, 16)
                sp.wait_ge(v_done, C.NG)
                sp.dma_start(kvb[:], kT_dram[:, 0:GT]).then_inc(kv_loaded, 16)

        def front_dve(dve, j):
            rs, nm = (C.RS2, C.NM2) if rank else (C.RS, C.NM)
            for p in range(TPG):
                n = j * TPG + p
                last = nc.vector.tensor_scalar(xn[:, p, :], C.X[:, n, :], rs[:, bass.ds(n, 1)],
                                               nm[:, bass.ds(n, 1)], ALU.mult, ALU.add)
            last.then_inc(xn_ready, 1)

        def front_pe(pe, j):
            pe.wait_ge(xn_ready, j + 1)
            for p in range(TPG):
                last = nc.tensor.transpose(ps_j[:, p * P:(p + 1) * P], xn[:, p, :], C.ident[:])
            last.then_inc(xT_done, 1)

        def front_act(act, j):
            act.wait_ge(xT_done, j + 1)
            nc.scalar.activation(xnT[:], ps_j[:], ACT.Copy).then_inc(xT_ready, 1)

        @block.tensor
        def _(pe):
            pe.wait_ge(loaded, n_loaded)
            pe.wait_ge(prepared, 2)

            def queries_keys(u):
                for t in range(UT):
                    for b in range(2):
                        q = 2 * (UT * u + t) + b
                        for g in range(RG):
                            r = slice(32 * g, 32 * g + 32)
                            last = nc.tensor.matmul(ps_s[S * b:S * b + S, g, t * HR * S:(t + 1) * HR * S],
                                                    qT[r, q * S:(q + 1) * S], kbd[r, q, :, :], start=True, stop=True)
                last.then_inc(scores_done, 1)

            def turn_probs(u, m):
                for t in range(4):
                    h = (m % 2) * HR * 2 + 2 * t
                    last = nc.tensor.transpose(ps_t[:, m % 2, t * P:(t + 1) * P],
                                               s1[:, u, m // 2, h:h + 2, :].rearrange("p h k -> p (h k)"), C.ident[:])
                last.then_inc(pT_done, 1)

            def weigh_values(u, m):
                for t in range(4):
                    n = (m % 2) * 4 + t
                    for b in range(2):
                        last = nc.tensor.matmul(o_acc[S * b:S * b + S, m // 2, 2 * n:2 * n + 2, :].rearrange("p h v -> p (h v)"),
                                                pT[:, m % 2, t, S * b:S * b + S],
                                                vbd[:, 2 * (UT * u + m // 2) + b, n, :, :].rearrange("p e v -> p (e v)"),
                                                start=True, stop=True)
                return last

            def turn_output(w):
                pe.wait_ge(on_ready, w + 1)
                for t in range(UT):
                    last = nc.tensor.transpose(j_tr[:, t, :], on[:, t, :], C.ident[:])
                last.then_inc(oT_done, 1)

            def project_output(w):
                pe.wait_ge(oT_ready, w + 1)
                for t in range(UT):
                    last = nc.tensor.matmul(j_out[:, t, :], oT[:, t, :], wo[:], start=True, stop="bo" not in W)
                    if "bo" in W:
                        last = nc.tensor.matmul(j_out[:, t, :], C.ones[0:1, :], bo[0:1, :], start=False, stop=True)
                last.then_inc(out_done, 1)

            def project(j):
                pe.wait_ge(xT_ready, j + 1)
                into = lambda b, w, of: nc.tensor.matmul(ps_s[:, b, :], w[:], of[:], start=True, stop=True)
                into(0, wq, xnT).then_inc(q_done, 1)
                if mode == "rope":
                    into(1, wqr, xnT).then_inc(q_done, 1)
                    into(2, wk, xnT).then_inc(k_done, 1)
                    into(3, wkr, xnT).then_inc(k_done, 1)
                elif linear:
                    nc.tensor.matmul(ps_s[0:32, 1, :], wk[:], xnT[:], start=True, stop=True)
                    nc.tensor.matmul(ps_s[0:32, 2, :], wv[:], xnT[:], start=True, stop=True).then_inc(low_done, 1)
                else:
                    if cross:
                        pe.wait_ge(kv_loaded, j * 16 + 16)
                    into(2, wk, kvb).then_inc(k_done, 1)

            def compress(j):
                if linear:
                    pe.wait_ge(low_ready, j * 2 + 1)
                    nc.tensor.matmul(ps_s[0:S, 3, :], wc[:], k32[:, 0, :], start=True, stop=True)
                    nc.tensor.matmul(ps_s[0:S, 1, :], wc[:], k32[:, 1, :], start=True, stop=True).then_inc(low_done, 1)
                if rank:
                    pe.wait_ge(rank_in, j + 1)
                    for p in range(TPG):
                        last = nc.tensor.transpose(ps_s[:, 3, p * P:(p + 1) * P], s_rep[:, p, :], C.ident[:])
                    last.then_inc(rank_done, 1)

            def expand(j):
                if linear:
                    pe.wait_ge(low_ready, j * 2 + 2)
                    nc.tensor.matmul(ps_s[:, 2, :], we[:], c64[:, 0, :], start=True, stop=True).then_inc(k_done, 1)

            def values(j, half):
                for s in range(half * SPG // 2, (half + 1) * SPG // 2):
                    src = c64[:, 1, s * S:(s + 1) * S] if linear else kvb[:, s * S:(s + 1) * S]
                    for b in range(2):
                        last = nc.tensor.matmul(ps_t[S * b:S * b + S, s // 4, (s % 4) * D:(s % 4 + 1) * D], src,
                                                we[:] if linear else wv[:], start=True, stop=True)
                if half:
                    last.then_inc(v_done, 1)

            front_pe(pe, 0)
            for step in (project, compress, expand):
                step(0)
            values(0, 0)
            values(0, 1)
            with pe.Fori(0, C.NG) as i:
                pe.wait_ge(q_ready, i + 1)
                pe.wait_ge(k_ready, i + 1)
                if rank:
                    pe.wait_ge(rank_read, i + 1)
                queries_keys(0)
                pe.wait_ge(out_read, i * UPG + 1)
                front_pe(pe, i + 1)
                if linear:
                    pe.wait_ge(probs, i * UPG + 1)
                else:
                    pe.wait_ge(scores_read, i * UPG + 2)
                queries_keys(1)
                pe.wait_ge(v_ready, i + 1)
                for u in range(UPG):
                    w = i * UPG + u
                    pe.wait_ge(probs, w + 1)
                    turn_probs(u, 0)
                    turn_probs(u, 1)
                    if u == 1:
                        if not linear:
                            pe.wait_ge(scores_read, i * UPG + 3)
                        project(i + 1)
                        turn_output(w - 1)
                    for m in range(2 * UT):
                        pe.wait_ge(pT_ready, w * 2 * UT + m + 1)
                        last = weigh_values(u, m)
                        if m + 2 < 2 * UT:
                            turn_probs(u, m + 2)
                    last.then_inc(pv_done, 1)
                project_output(w - 1)
                compress(i + 1)
                if not linear:
                    values(i + 1, 0)
                pe.wait_ge(out_read, i * UPG + 2)
                turn_output(w)
                expand(i + 1)
                if linear:
                    values(i + 1, 0)
                values(i + 1, 1)
                project_output(w)

        @block.scalar
        def _(act):
            scales.act(act)
            act.wait_ge(loaded, n_loaded)
            act.wait_ge(prepared, 2)

            def output_copy(w):
                act.wait_ge(oT_done, w + 1)
                if cross:
                    last = nc.scalar.activation(oT[:], j_tr, ACT.Identity, bias=bv[:, 0:1])
                else:
                    last = nc.scalar.activation(oT[:], j_tr, ACT.Copy)
                last.then_inc(oT_ready, 1)

            def low_rank(j):
                act.wait_ge(low_done, j * 2 + 1)
                nc.scalar.activation(k32[:, 0, :], ps_s[0:32, 1, :], ACT.Identity, bias=bk32[:, 0:1])
                nc.scalar.activation(k32[:, 1, :], ps_s[0:32, 2, :], ACT.Identity,
                                     bias=bv32[:, 0:1]).then_inc(low_ready, 1)
                act.wait_ge(e_in, j * 2 + 1)
                nc.scalar.activation(t2[:], t2[:], ACT.Exp).then_inc(e_out, 1)

            def compressed(j):
                act.wait_ge(low_done, j * 2 + 2)
                nc.scalar.activation(c64[:, 0, :], ps_s[0:S, 3, :], ACT.Copy)
                nc.scalar.activation(c64[:, 1, :], ps_s[0:S, 1, :], ACT.Copy).then_inc(low_ready, 1)
                act.wait_ge(e_in, j * 2 + 2)
                nc.scalar.activation(t2[:], t2[:], ACT.Exp).then_inc(e_out, 1)

            def diagonal_keys(j):
                if mode in ("rope", "linear"):
                    act.wait_ge(kf_ready, j + 1)
                else:
                    act.wait_ge(k_done, j + 1)
                for h in range(HR):
                    to = kbd[:, :, h, :]
                    if mode in ("rope", "linear"):
                        last = nc.scalar.activation(to, kf[:].rearrange("p (s k) -> p s k", k=S), ACT.Copy,
                                                    scale=hmask[:, h:h + 1])
                    else:
                        last = nc.scalar.activation(to, ps_s[:, 2, :].rearrange("p (s k) -> p s k", k=S),
                                                    ACT.Identity, scale=hmask[:, h:h + 1], bias=bkm[:, h:h + 1])
                last.then_inc(k_ready, 1)

            front_act(act, 0)
            if linear:
                low_rank(0)
                compressed(0)
            diagonal_keys(0)
            with act.Fori(0, C.NG) as i:
                for u in range(UPG):
                    w = i * UPG + u
                    if not linear:
                        act.wait_ge(shifted, w + 1)
                        nc.scalar.activation(s1[:, u, :, :, :], s1[:, u, :, :, :], ACT.Exp).then_inc(probs, 1)
                    if u == 0:
                        front_act(act, i + 1)
                    for m in range(2 * UT):
                        if u == 1 and m == 2:
                            output_copy(w - 1)
                            if linear:
                                low_rank(i + 1)
                        act.wait_ge(pT_done, w * 2 * UT + m + 1)
                        nc.scalar.activation(pT[:, m % 2, :, :], ps_t[:, m % 2, :].rearrange("p (t q) -> p t q", q=P),
                                             ACT.Copy).then_inc(pT_ready, 1)
                if linear:
                    output_copy(w)
                    compressed(i + 1)
                diagonal_keys(i + 1)
                if not linear:
                    output_copy(w)

        @block.gpsimd
        def _(pool):
            nc.gpsimd.memset(vbd[:], 0.0)
            pool.drain()
            for e in range(2):
                nc.gpsimd.memset(vbd[S * e:S * e + S, :, :, e, HD:VW], 1.0)
            pool.drain()
            nc.gpsimd.memset(xt[:], 0.0).then_inc(prepared, 1)
            if rank:
                pool.wait_ge(loaded, n_loaded)

        @block.vector
        def _(dve):
            scales.dve(dve)
            dve.wait_ge(loaded, n_loaded)
            if cross:
                nc.vector.tensor_scalar(bkm[:], hmask[:], bk[:, 0:1], None, ALU.mult)
            else:
                nc.vector.memset(bkm[:], 0.0)
            if mode == "rope":
                for w, r in ((wq, wqr), (wk, wkr)):
                    pairs, turned = w[:].rearrange("p (n e) -> p n e", e=2), r[:].rearrange("p (n e) -> p n e", e=2)
                    nc.vector.tensor_scalar(turned[:, :, 0], pairs[:, :, 1], -1.0, None, ALU.mult)
                    nc.vector.tensor_copy(turned[:, :, 1], pairs[:, :, 0])
            if mode == "mask":
                nc.vector.tensor_copy(keep[:], keepi[:])
                dve.drain()
                nc.vector.tensor_scalar(keep[:], keep[:], 0.0, None, ALU.not_equal)
                dve.drain()
                nc.vector.tensor_scalar(off[:], keep[:], 1e9, -1e9, ALU.mult, ALU.add)
                nc.vector.tensor_tensor(table[:], table[:], bc(keep[:].unsqueeze(1), [P, NH, S]), ALU.mult)
                dve.drain()
                nc.vector.tensor_tensor(table[:], table[:], bc(off[:].unsqueeze(1), [P, NH, S]), ALU.add)
            if rank:
                for w in (wq, wk, wv):
                    nc.vector.tensor_scalar(w[:], w[:], g1[:, 0:1], None, ALU.mult)
            dve.drain()
            nc.vector.memset(mv[:], 0.0)
            nc.vector.memset(mx[:], 0.0).then_inc(scores_read, 1)
            nc.vector.memset(rden[:], 0.0).then_inc(out_read, 1)
            dve.wait_ge(prepared, 1)
            dve.drain()
            nc.vector.memset(st[:], 0.0).then_inc(prepared, 1)

            def rotate(to, plain, turned, at):
                cs, sn = (bc(w[:].unsqueeze(1), [P, SPG, S]) for w in (cosT, sinT))
                v = lambda a: a.rearrange("p (s k) -> p s k", k=S)
                nc.vector.tensor_tensor(v(t1[:]), v(plain), cs, ALU.mult)
                nc.vector.tensor_tensor(v(t2[:]), v(turned), sn, ALU.mult)
                dve.drain()
                return nc.vector.tensor_tensor(to, t1[:], t2[:], ALU.add)

            def feature(to, src, bias, count):
                nc.vector.tensor_scalar(t1[:], src, bias, 0.0, ALU.add, ALU.max)
                nc.vector.tensor_scalar(t2[:], src, bias, 0.0, ALU.add, ALU.min).then_inc(e_in, 1)
                dve.drain()
                dve.wait_ge(e_out, count)
                return nc.vector.tensor_tensor(to, t1[:], t2[:], ALU.add)

            def scores(u, w):
                dve.wait_ge(scores_done, w + 1)
                out = s1[:, u, :, :, :]
                if mode in ("rope", "ctx"):
                    nc.vector.tensor_tensor(out.rearrange("p t (g h) k -> p t g (h k)", g=RG),
                                            ps_s[:].rearrange("p g (t x) -> p t g x", t=UT),
                                            bc(table[:].rearrange("p (g h) k -> p g (h k)", g=RG).unsqueeze(1),
                                               [P, UT, RG, HR * S]), ALU.add).then_inc(scores_read, 1)
                else:
                    for t in range(UT):
                        with_ = tril[:] if linear else hidden[:, UT * u + t, :] if rank else keep[:]
                        last = nc.vector.tensor_tensor(
                            out[:, t, :, :].rearrange("p (g h) k -> p g h k", g=RG),
                            ps_s[:, :, t * HR * S:(t + 1) * HR * S].rearrange("p g (h k) -> p g h k", k=S),
                            bc(with_.unsqueeze(1).unsqueeze(1), [P, RG, HR, S]), ALU.add if rank else ALU.mult)
                    last.then_inc(probs if linear else scores_read, 1)
                    if linear:
                        return
                dve.drain()
                if mode == "mask":
                    nc.vector.tensor_tensor(out, out, bc(table[:].unsqueeze(1), [P, UT, NH, S]), ALU.add)
                    dve.drain()
                nc.vector.tensor_reduce(mx[:], out, AX, ALU.max)
                dve.drain()
                nc.vector.tensor_tensor(out, out, bc(mx[:].unsqueeze(3), [P, UT, NH, S]),
                                        ALU.subtract).then_inc(shifted, 1)

            def normalise(w):
                dve.wait_ge(pv_done, w + 1)
                if linear:
                    nc.vector.tensor_scalar(rden[:], o_acc[:, :, :, HD], 1e-6, None, ALU.add)
                    dve.drain()
                    nc.vector.reciprocal(rden[:], rden[:])
                else:
                    nc.vector.reciprocal(rden[:], o_acc[:, :, :, HD])
                dve.drain()
                nc.vector.tensor_tensor(on[:].rearrange("p t (h e) -> p t h e", e=HD), o_acc[:, :, :, 0:HD],
                                        bc(rden[:].unsqueeze(3), [P, UT, NH, HD]), ALU.mult).then_inc(on_ready, 1)

            def residual(u, i, w):
                rows = bass.ds(i * TPG + u * UT, UT)
                if to_y:
                    for t in range(UT):
                        n = i * TPG + u * UT + t
                        nc.vector.tensor_scalar(xt[:, t, :], C.X[:, n, :], C.RS[:, bass.ds(n, 1)],
                                                C.NM[:, bass.ds(n, 1)], ALU.mult, ALU.add)
                    dve.drain()
                dve.wait_ge(out_done, w + 1)
                to = (C.Y if to_y else C.X)[:, rows, :]
                nc.vector.tensor_tensor(to, j_out, xt[:] if to_y else to, ALU.add).then_inc(out_read, 1)
                dve.drain()
                for t in range(UT):
                    nc.vector.bn_stats(st[:, t, :], (C.Y if to_y else C.X)[:, i * TPG + u * UT + t, :])
                dve.drain()
                for t in range(UT):
                    nc.vector.bn_aggr(mv[:, u * UT + t, :], st[:, t, :])

            def router_scores(j):
                for p in range(TPG):
                    n = j * TPG + p
                    nc.vector.tensor_scalar(xt[:, 0, :], C.X[:, n, :], C.RS[:, bass.ds(n, 1)],
                                            C.NM[:, bass.ds(n, 1)], ALU.mult, ALU.add)
                    dve.drain()
                    nc.vector.tensor_tensor(prod[:], xt[:, 0, :], wr[:], ALU.mult)
                    dve.drain()
                    nc.vector.tensor_reduce(s_own[:, p:p + 1], prod[:], AX, ALU.add)
                dve.drain()
                nc.vector.tensor_copy(s_rep[:], bc(s_own[:].unsqueeze(2), [P, TPG, P])).then_inc(rank_in, 1)

            def rank_order(j):
                dve.wait_ge(rank_done, j + 1)
                row = ps_s[:, 3, :].rearrange("p (t b k) -> p t b k", t=TPG, b=2)
                for b in range(2):
                    r = slice(S * b, S * b + S)
                    own = bc(s_own[r, :].unsqueeze(2), [S, TPG, S])
                    nc.vector.tensor_tensor(r1[r, :, :], row[r, :, b, :], own, ALU.is_gt)
                    last = nc.vector.tensor_tensor(r2[r, :, :], row[r, :, b, :], own, ALU.is_equal)
                last.then_inc(rank_read, 1)
                dve.drain()
                nc.vector.tensor_tensor(r2[:], r2[:], bc(tril[:].unsqueeze(1), [P, TPG, S]), ALU.mult)
                dve.drain()
                nc.vector.tensor_tensor(r1[:], r1[:], r2[:], ALU.add)
                dve.drain()
                nc.vector.tensor_scalar(hidden[:], r1[:], BIG, -BIG, ALU.mult, ALU.add)
                dve.drain()

            def queries(j):
                if mode == "rope":
                    dve.wait_ge(q_done, j * 2 + 2)
                    rotate(qT[:], ps_s[:, 0, :], ps_s[:, 1, :], 0)
                    dve.drain()
                    nc.vector.tensor_scalar(qT[:], qT[:], HD ** -0.5, None, ALU.mult).then_inc(q_ready, 1)
                    dve.wait_ge(k_done, j * 2 + 2)
                    rotate(kf[:], ps_s[:, 2, :], ps_s[:, 3, :], 1).then_inc(kf_ready, 1)
                elif linear:
                    dve.wait_ge(q_done, j + 1)
                    feature(qT[:], ps_s[:, 0, :], bq[:, 0:1], j * 2 + 1).then_inc(q_ready, 1)
                    dve.drain()
                else:
                    dve.wait_ge(q_done, j + 1)
                    scale = 1.0 if mode == "mask" else HD ** -0.5
                    if cross:
                        nc.vector.tensor_scalar(qT[:], ps_s[:, 0, :], bq[:, 0:1], scale, ALU.add,
                                                ALU.mult).then_inc(q_ready, 1)
                    else:
                        nc.vector.tensor_scalar(qT[:], ps_s[:, 0, :], scale, None, ALU.mult).then_inc(q_ready, 1)

            def key_features(j):
                dve.wait_ge(k_done, j + 1)
                feature(kf[:], ps_s[:, 2, :], 0.0, j * 2 + 2).then_inc(kf_ready, 1)

            def diagonal_values(j):
                dve.wait_ge(v_done, j + 1)
                for t in range(2):
                    for e in range(2):
                        r = slice(S * e, S * e + S)
                        src = ps_t[r, t, :].rearrange("p (s n e d) -> p s n e d", s=4, n=NB, e=2)[:, :, :, e, :]
                        last = nc.vector.tensor_copy(vbd[r, 4 * t:4 * t + 4, :, e, 0:HD], src)
                last.then_inc(v_ready, 1)

            front_dve(dve, 0)
            if rank:
                router_scores(0)
            queries(0)
            if rank:
                rank_order(0)
            if linear:
                key_features(0)
            diagonal_values(0)
            front_dve(dve, 1)
            with dve.Fori(0, C.NG) as i:
                w = i * UPG
                scores(0, w)
                scores(1, w + 1)
                normalise(w)
                queries(i + 1)
                if rank:
                    router_scores(i + 1)
                residual(0, i, w)
                normalise(w + 1)
                if rank:
                    rank_order(i + 1)
                if linear:
                    key_features(i + 1)
                diagonal_values(i + 1)
                front_dve(dve, i + 2)
                residual(1, i, w + 1)
                dve.drain()
                nc.vector.tensor_copy(C.MV[:, bass.ds(i * TPG, TPG), :], mv[:])


class Front:

    def __init__(self, C, sc, bank, src, scale, shift):
        self.C, self.nc, self.bank, self.src, self.scale, self.shift = C, C.nc, bank, src, scale, shift
        self.xn, self.xnT = sc.sb("xn", [P, TPG, D]), sc.sb("xnT", [P, GT])
        self.xn_ready, self.xT_done, self.xT_ready = sc.sem("xn_ready"), sc.sem("xT_done"), sc.sem("xT_ready")

    def dve(self, j):
        nc = self.nc
        for p in range(TPG):
            n = j * TPG + p
            if self.shift is None:
                last = nc.vector.tensor_scalar(self.xn[:, p, :], self.src[:, n, :], self.scale[:, bass.ds(n, 1)], None,
                                               ALU.mult)
            else:
                last = nc.vector.tensor_scalar(self.xn[:, p, :], self.src[:, n, :], self.scale[:, bass.ds(n, 1)],
                                               self.shift[:, bass.ds(n, 1)], ALU.mult, ALU.add)
        last.then_inc(self.xn_ready, 1)

    def pe(self, pe, j):
        pe.wait_ge(self.xn_ready, j + 1)
        for p in range(TPG):
            last = self.nc.tensor.transpose(self.bank[:, p * P:(p + 1) * P], self.xn[:, p, :], self.C.ident[:])
        last.then_inc(self.xT_done, 1)

    def act(self, act, j):
        act.wait_ge(self.xT_done, j + 1)
        self.nc.scalar.activation(self.xnT[:], self.bank[:], ACT.Copy).then_inc(self.xT_ready, 1)


def group_stats(nc, dve, C, src, st, mv, i):
    for p in range(TPG):
        nc.vector.bn_stats(st[:, p, :], src[:, i * TPG + p, :])
    dve.drain()
    for p in range(TPG):
        nc.vector.bn_aggr(mv[:, p, :], st[:, p, :])
    dve.drain()
    nc.vector.tensor_copy(C.MV[:, bass.ds(i * TPG, TPG), :], mv[:])


def rows(t, i):
    return t[:, bass.ds(i * TPG, TPG), :]


PAIR = 2 * TPG


def affine_norm(C, name, gamma_d, beta_d):
    nc = C.nc
    with ExitStack() as ctx:
        sc = Scope(nc, ctx, name)
        gamma, beta = sc.sb("gamma", [P, D]), sc.sb("beta", [P, D])
        y = sc.sb("y", [P, 2, PAIR, D])
        st, mv = sc.sb("st", [P, PAIR, 6]), sc.sb("mv", [P, PAIR, 2])
        loaded, begun = sc.sem("loaded"), sc.sem("begun")
        normed, shifted, used = sc.sem("normed"), sc.sem("shifted"), sc.sem("used")
        scales = InnerScales(C, sc, 1e-5, False)
        block = ctx.enter_context(nc.Block())
        steps = C.NT // PAIR

        @block.sync
        def _(sp):
            sp.dma_start(gamma[:], gamma_d[:]).then_inc(loaded, 16)
            sp.dma_start(beta[:], beta_d[:]).then_inc(loaded, 16)

        @block.gpsimd
        def _(pool):
            pool.wait_ge(loaded, 32)
            pool.sem_inc(begun, 1)
            with pool.Fori(0, steps) as i:
                x = C.X[:, bass.ds(i * PAIR, PAIR), :]
                nc.gpsimd.tensor_tensor(x, x, bc(beta[:].unsqueeze(1), [P, PAIR, D]), ALU.add).then_inc(shifted, 1)

        @block.scalar
        def _(act):
            scales.act(act)
            with act.Fori(0, steps // 2) as i:
                for h in range(2):
                    act.wait_ge(used, i * 2 + h + 1)
                    for p in range(PAIR):
                        n = i * (2 * PAIR) + h * PAIR + p
                        last = nc.scalar.activation(y[:, h, p, :], C.Y[:, n, :], ACT.Identity, scale=C.RS2[:, bass.ds(n, 1)],
                                                    bias=C.NM2[:, bass.ds(n, 1)])
                    last.then_inc(normed, 1)

        @block.vector
        def _(dve):
            scales.dve(dve)
            nc.vector.memset(st[:], 0.0).then_inc(used, 1)
            nc.vector.memset(mv[:], 0.0).then_inc(used, 1)
            dve.wait_ge(loaded, 32)
            dve.drain()
            with dve.Fori(0, steps // 2) as i:
                for h in range(2):
                    x = C.X[:, bass.ds(i * (2 * PAIR) + h * PAIR, PAIR), :]
                    dve.wait_ge(normed, i * 2 + h + 1)
                    nc.vector.tensor_tensor(y[:, h, :, :], y[:, h, :, :], bc(gamma[:].unsqueeze(1), [P, PAIR, D]), ALU.mult)
                    dve.drain()
                    dve.wait_ge(shifted, i * 2 + h + 1)
                    nc.vector.tensor_tensor(x, x, y[:, h, :, :], ALU.add).then_inc(used, 1)
                    dve.drain()
                    row_stats(nc, dve, C, C.X, st, mv, i * 2 + h, PAIR)
                    dve.drain()


def gated_ffn(C, name, W):
    nc = C.nc
    F = W["w1"].shape[1]
    chunks = [(f, min(P, F - f)) for f in range(0, F, P)]
    NF = len(chunks)
    with ExitStack() as ctx:
        sc = Scope(nc, ctx, name)
        sb, ps, sem = sc.sb, sc.ps, sc.sem
        w1, w2, w3 = sb("w1", [P, F]), sb("w2", [P, F]), sb("w3", [P, NF, D])
        g = sb("g", [P, 1])
        act_b, hid = sb("act", [P, NF, GT]), sb("hid", [P, NF, GT])
        st, mv = sb("st", [P, TPG, 6]), sb("mv", [P, TPG, 2])
        ps_j, ps_o = ps("ps_j", [P, GT]), ps("ps_o", [P, GT])
        ps_u, ps_v = ps("ps_u", [P, NF, GT]), ps("ps_v", [P, NF, GT])
        fr = Front(C, sc, ps_j, C.Y, C.RS2, None)
        loaded, folded = sem("loaded"), sem("folded")
        gate_done, up_done, gated, hidden = sem("gate_done"), sem("up_done"), sem("gated"), sem("hidden")
        out_done, out_read = sem("out_done"), sem("out_read")
        scales = InnerScales(C, sc, 1e-6, True)
        block = ctx.enter_context(nc.Block())

        @block.sync
        def _(sp):
            for to, of in ((w1[:], W["w1"]), (w2[:], W["w2"]), (g[:], W["g"])):
                sp.dma_start(to, of).then_inc(loaded, 16)
            for c, (f, n) in enumerate(chunks):
                sp.dma_start(w3[0:n, c, :], W["w3"][f:f + n, :]).then_inc(loaded, 16)

        n_loaded = 16 * (3 + NF)

        @block.tensor
        def _(pe):
            pe.wait_ge(loaded, n_loaded)
            pe.wait_ge(folded, 1)
            fr.pe(pe, 0)
            with pe.Fori(0, C.NG) as i:
                pe.wait_ge(fr.xT_ready, i + 1)
                for w, to, done in ((w1, ps_u, gate_done), (w2, ps_v, up_done)):
                    for c, (f, n) in enumerate(chunks):
                        nc.tensor.matmul(to[0:n, c, :], w[:, f:f + n], fr.xnT[:], start=True,
                                         stop=True).then_inc(done, 1)
                fr.pe(pe, i + 1)
                pe.wait_ge(out_read, i + 1)
                pe.wait_ge(hidden, i * NF + NF)
                for p in range(TPG):
                    for c, (f, n) in enumerate(chunks):
                        last = nc.tensor.matmul(ps_o[:, p * D:(p + 1) * D], hid[0:n, c, p * P:(p + 1) * P],
                                                w3[0:n, c, :], start=(c == 0), stop=(c == NF - 1))
                last.then_inc(out_done, 1)

        @block.scalar
        def _(act):
            scales.act(act)
            fr.act(act, 0)
            with act.Fori(0, C.NG) as i:
                for c, (f, n) in enumerate(chunks):
                    act.wait_ge(gate_done, i * NF + c + 1)
                    nc.scalar.activation(act_b[0:n, c, :], ps_u[0:n, c, :], ACT.Silu).then_inc(gated, 1)
                fr.act(act, i + 1)

        @block.vector
        def _(dve):
            scales.dve(dve)
            dve.wait_ge(loaded, n_loaded)
            nc.vector.tensor_scalar(w1[:], w1[:], g[:, 0:1], None, ALU.mult)
            nc.vector.tensor_scalar(w2[:], w2[:], g[:, 0:1], None, ALU.mult).then_inc(folded, 1)
            nc.vector.memset(mv[:], 0.0).then_inc(out_read, 1)
            fr.dve(0)
            with dve.Fori(0, C.NG) as i:
                dve.wait_ge(fr.xT_done, i + 1)
                fr.dve(i + 1)
                nc.vector.tensor_tensor(rows(C.X, i), rows(C.X, i), rows(C.Y, i), ALU.add)
                for c, (f, n) in enumerate(chunks):
                    dve.wait_ge(up_done, i * NF + c + 1)
                    dve.wait_ge(gated, i * NF + c + 1)
                    nc.vector.tensor_tensor(hid[0:n, c, :], act_b[0:n, c, :], ps_v[0:n, c, :],
                                            ALU.mult).then_inc(hidden, 1)
                dve.wait_ge(out_done, i + 1)
                nc.vector.tensor_tensor(rows(C.X, i), ps_o[:].rearrange("p (t d) -> p t d", d=D), rows(C.X, i),
                                        ALU.add).then_inc(out_read, 1)
                dve.drain()
                group_stats(nc, dve, C, C.X, st, mv, i)


NE = 8


def first_max(nc, dve, values, falling, onehot, best, place):
    wide = [P, TPG, NE]
    nc.vector.tensor_reduce(best[:], values, AX, ALU.max)
    dve.drain()
    nc.vector.tensor_tensor(onehot[:], values, bc(best[:].unsqueeze(2), wide), ALU.is_ge)
    dve.drain()
    nc.vector.tensor_tensor(onehot[:], onehot[:], bc(falling[:].unsqueeze(1), wide), ALU.mult)
    dve.drain()
    nc.vector.tensor_reduce(place[:], onehot[:], AX, ALU.max)
    dve.drain()
    nc.vector.tensor_tensor(onehot[:], onehot[:], bc(place[:].unsqueeze(2), wide), ALU.is_equal)
    dve.drain()


def lora_ffn(C, name, W):
    nc = C.nc
    F, R = W["wi"].shape[1], W["B"].shape[0]
    NF, RE = F // P, R // NE
    with ExitStack() as ctx:
        sc = Scope(nc, ctx, name)
        sb, ps, sem = sc.sb, sc.ps, sc.sem
        wi, wo, ga, lb = sb("wi", [P, F]), sb("wo", [P, NF, D]), sb("ga", [P, NE + R]), sb("lb", [R, F])
        gb, wib, wob, falling = sb("gb", [P, NE]), sb("wib", [P, NF]), sb("wob", [1, D]), sb("falling", [P, NE])
        logits, onehot = sb("logits", [P, TPG, NE]), sb("onehot", [P, TPG, NE])
        best, place = sb("best", [P, TPG]), sb("place", [P, TPG])
        low, lowT = sb("low", [P, TPG, R]), sb("lowT", [R, GT])
        hid = sb("hid", [P, NF, GT])
        st, mv = sb("st", [P, TPG, 6]), sb("mv", [P, TPG, 2])
        ps_j, ps_o = ps("ps_j", [P, GT]), ps("ps_o", [P, GT])
        ps_g, ps_l, ps_h = ps("ps_g", [P, TPG, NE + R]), ps("ps_l", [R, GT]), ps("ps_h", [P, NF, GT])
        fr = Front(C, sc, ps_j, C.X, C.RS, C.NM)
        loaded = sem("loaded")
        gate_done, low_ready, lowT_done, lowT_ready = (sem(n) for n in ("gate_done", "low_ready", "lowT_done", "lowT_ready"))
        hid_done, hid_ready, out_done, out_read = (sem(n) for n in ("hid_done", "hid_ready", "out_done", "out_read"))
        scales = NormScales(C, sc, 1e-5)
        block = ctx.enter_context(nc.Block())
        loads = [(wi[:], W["wi"]), (wo[:], W["wo"].rearrange("(c p) d -> p c d", p=P)), (ga[:], W["ga"]), (lb[:], W["B"]),
                 (gb[:], W["gb"]), (wib[:], W["wib"]), (wob[:], W["wob"]), (falling[:], W["falling"])]
        n_loaded = 16 * len(loads)

        @block.sync
        def _(sp):
            for to, of in loads:
                sp.dma_start(to, of).then_inc(loaded, 16)

        @block.tensor
        def _(pe):
            pe.wait_ge(loaded, n_loaded)
            fr.pe(pe, 0)
            with pe.Fori(0, C.NG) as i:
                pe.wait_ge(fr.xT_ready, i + 1)
                for p in range(TPG):
                    last = nc.tensor.matmul(ps_g[:, p, :], fr.xnT[:, p * P:(p + 1) * P], ga[:], start=True, stop=True)
                last.then_inc(gate_done, 1)
                for c in range(NF):
                    nc.tensor.matmul(ps_h[:, c, :], wi[:, c * P:(c + 1) * P], fr.xnT[:], start=True, stop=False)
                pe.wait_ge(low_ready, i + 1)
                for p in range(TPG):
                    last = nc.tensor.transpose(ps_l[:, p * P:(p + 1) * P], low[:, p, :], C.ident[:])
                last.then_inc(lowT_done, 1)
                fr.pe(pe, i + 1)
                pe.wait_ge(lowT_ready, i + 1)
                for c in range(NF):
                    nc.tensor.matmul(ps_h[:, c, :], lb[:, c * P:(c + 1) * P], lowT[:], start=False,
                                     stop=True).then_inc(hid_done, 1)
                pe.wait_ge(out_read, i + 1)
                pe.wait_ge(hid_ready, i * NF + NF)
                for p in range(TPG):
                    o = ps_o[:, p * D:(p + 1) * D]
                    for c in range(NF):
                        nc.tensor.matmul(o, hid[:, c, p * P:(p + 1) * P], wo[:, c, :], start=(c == 0), stop=False)
                    last = nc.tensor.matmul(o, C.ones[0:1, :], wob[0:1, :], start=False, stop=True)
                last.then_inc(out_done, 1)

        @block.scalar
        def _(act):
            scales.act(act)
            act.wait_ge(loaded, n_loaded)
            fr.act(act, 0)
            with act.Fori(0, C.NG) as i:
                act.wait_ge(lowT_done, i + 1)
                nc.scalar.activation(lowT[:], ps_l[:], ACT.Copy).then_inc(lowT_ready, 1)
                fr.act(act, i + 1)
                for c in range(NF):
                    act.wait_ge(hid_done, i * NF + c + 1)
                    nc.scalar.activation(hid[:, c, :], ps_h[:, c, :], ACT.Relu, bias=wib[:, c:c + 1]).then_inc(hid_ready, 1)

        @block.vector
        def _(dve):
            scales.dve(dve)
            dve.wait_ge(loaded, n_loaded)
            nc.vector.memset(mv[:], 0.0).then_inc(out_read, 1)
            fr.dve(0)
            with dve.Fori(0, C.NG) as i:
                dve.wait_ge(gate_done, i + 1)
                nc.vector.tensor_tensor(logits[:], ps_g[:, :, 0:NE], bc(gb[:].unsqueeze(1), [P, TPG, NE]), ALU.add)
                dve.drain()
                first_max(nc, dve, logits[:], falling, onehot, best, place)
                for p in range(TPG):
                    last = nc.vector.tensor_tensor(low[:, p, :].rearrange("p (e r) -> p e r", r=RE),
                                                   ps_g[:, p, NE:].rearrange("p (e r) -> p e r", r=RE),
                                                   bc(onehot[:, p, :].unsqueeze(2), [P, NE, RE]), ALU.mult)
                last.then_inc(low_ready, 1)
                fr.dve(i + 1)
                dve.wait_ge(out_done, i + 1)
                nc.vector.tensor_tensor(rows(C.X, i), ps_o[:].rearrange("p (t d) -> p t d", d=D), rows(C.X, i),
                                        ALU.add).then_inc(out_read, 1)
                dve.drain()
                group_stats(nc, dve, C, C.X, st, mv, i)


def topk_ffn(C, name, W):
    nc = C.nc
    F = W["w1"].shape[2]
    NF = F // P
    with ExitStack() as ctx:
        sc = Scope(nc, ctx, name)
        sb, ps, sem = sc.sb, sc.ps, sc.sem
        w1, w2, wr = sb("w1", [P, NE, F]), sb("w2", [P, NE, NF, D]), sb("wr", [P, NE])
        falling = sb("falling", [P, NE])
        prob, rest = sb("prob", [P, TPG, NE]), sb("rest", [P, TPG, NE])
        one1, one2 = sb("one1", [P, TPG, NE]), sb("one2", [P, TPG, NE])
        best1, best2, place, total = (sb(n, [P, TPG]) for n in ("best1", "best2", "place", "total"))
        cw = sb("cw", [P, TPG, NE])
        hid = sb("hid", [P, 2, NF, GT])
        acc = sb("acc", [P, TPG, D])
        st, mv = sb("st", [P, TPG, 6]), sb("mv", [P, TPG, 2])
        ps_j = ps("ps_j", [P, GT])
        ps_g = ps("ps_g", [P, TPG, NE])
        ps_h, ps_o = ps("ps_h", [P, 2, NF, GT]), ps("ps_o", [P, 2, GT])
        fr = Front(C, sc, ps_j, C.X, C.RS, C.NM)
        loaded = sem("loaded")
        gate_done, shifted, exped = sem("gate_done"), sem("shifted"), sem("exped")
        hid_done, hid_ready, out_done, out_read = (sem(n) for n in ("hid_done", "hid_ready", "out_done", "out_read"))
        scales = NormScales(C, sc, 1e-5)
        block = ctx.enter_context(nc.Block())
        loads = [(w1[:], W["w1"].rearrange("e d f -> d e f")),
                 (wr[:], W["wr"]), (falling[:], W["falling"])]
        loads += [(w2[:, e, :, :], W["w2"][e].rearrange("(c p) d -> p c d", p=P)) for e in range(NE)]
        n_loaded = 16 * len(loads)

        @block.sync
        def _(sp):
            for to, of in loads:
                sp.dma_start(to, of).then_inc(loaded, 16)

        @block.tensor
        def _(pe):
            pe.wait_ge(loaded, n_loaded)

            def expert_in(i, e):
                if e >= 2:
                    pe.wait_ge(hid_ready, i * NE + e - 1)
                for c in range(NF):
                    last = nc.tensor.matmul(ps_h[:, e % 2, c, :], w1[:, e, c * P:(c + 1) * P], fr.xnT[:],
                                            start=True, stop=True)
                last.then_inc(hid_done, 1)

            def expert_out(i, e):
                pe.wait_ge(hid_ready, i * NE + e + 1)
                pe.wait_ge(out_read, i * NE + e + 1)
                for p in range(TPG):
                    for c in range(NF):
                        last = nc.tensor.matmul(ps_o[:, e % 2, p * D:(p + 1) * D], hid[:, e % 2, c, p * P:(p + 1) * P],
                                                w2[:, e, c, :], start=(c == 0), stop=(c == NF - 1))
                last.then_inc(out_done, 1)

            fr.pe(pe, 0)
            with pe.Fori(0, C.NG) as i:
                pe.wait_ge(fr.xT_ready, i + 1)
                for p in range(TPG):
                    last = nc.tensor.matmul(ps_g[:, p, :], fr.xnT[:, p * P:(p + 1) * P], wr[:], start=True, stop=True)
                last.then_inc(gate_done, 1)
                expert_in(i, 0)
                for e in range(NE):
                    if e + 1 < NE:
                        expert_in(i, e + 1)
                    else:
                        fr.pe(pe, i + 1)
                    expert_out(i, e)

        @block.scalar
        def _(act):
            scales.act(act)
            fr.act(act, 0)
            with act.Fori(0, C.NG) as i:
                act.wait_ge(shifted, i + 1)
                nc.scalar.activation(prob[:], prob[:], ACT.Exp).then_inc(exped, 1)
                for e in range(NE):
                    act.wait_ge(hid_done, i * NE + e + 1)
                    if e >= 2:
                        act.wait_ge(out_done, i * NE + e - 1)
                    nc.scalar.activation(hid[:, e % 2, :, :], ps_h[:, e % 2, :, :], ACT.Silu).then_inc(hid_ready, 1)
                fr.act(act, i + 1)

        @block.vector
        def _(dve):
            scales.dve(dve)
            dve.wait_ge(loaded, n_loaded)
            nc.vector.memset(mv[:], 0.0).then_inc(out_read, 1)
            nc.vector.memset(st[:], 0.0).then_inc(out_read, 1)
            fr.dve(0)
            wide = [P, TPG, NE]
            over = lambda t: bc(t[:].unsqueeze(2), wide)
            with dve.Fori(0, C.NG) as i:
                dve.wait_ge(gate_done, i + 1)
                nc.vector.tensor_reduce(best1[:], ps_g[:], AX, ALU.max)
                dve.drain()
                nc.vector.tensor_tensor(prob[:], ps_g[:], over(best1), ALU.subtract).then_inc(shifted, 1)
                dve.wait_ge(fr.xT_done, i + 1)
                fr.dve(i + 1)
                dve.wait_ge(exped, i + 1)
                nc.vector.tensor_reduce(total[:], prob[:], AX, ALU.add)
                dve.drain()
                nc.vector.reciprocal(total[:], total[:])
                dve.drain()
                nc.vector.tensor_tensor(prob[:], prob[:], over(total), ALU.mult)
                dve.drain()
                first_max(nc, dve, prob[:], falling, one1, best1, place)
                nc.vector.scalar_tensor_tensor(rest[:], one1[:], -2.0, prob[:], ALU.mult, ALU.add)
                dve.drain()
                first_max(nc, dve, rest[:], falling, one2, best2, place)
                nc.vector.tensor_tensor(total[:], best1[:], best2[:], ALU.add)
                dve.drain()
                nc.vector.tensor_scalar(total[:], total[:], 1e-9, None, ALU.max)
                dve.drain()
                nc.vector.reciprocal(total[:], total[:])
                nc.vector.tensor_tensor(one1[:], one1[:], one2[:], ALU.add)
                dve.drain()
                nc.vector.tensor_tensor(cw[:], prob[:], over(total), ALU.mult)
                dve.drain()
                nc.vector.tensor_tensor(cw[:], cw[:], one1[:], ALU.mult)
                dve.drain()
                for e in range(NE):
                    dve.wait_ge(out_done, i * NE + e + 1)
                    for p in range(TPG):
                        o = ps_o[:, e % 2, p * D:(p + 1) * D]
                        before = C.X[:, i * TPG + p, :] if e == 0 else acc[:, p, :]
                        to = C.X[:, i * TPG + p, :] if e == NE - 1 else acc[:, p, :]
                        last = nc.vector.scalar_tensor_tensor(to, o, cw[:, p, e:e + 1], before, ALU.mult, ALU.add)
                    last.then_inc(out_read, 1)
                    dve.drain()



HW = 64
UH = 8
NJ = UH // 2


def attn64(C, name, W, groups_of_heads, q_per_kv, kT_dram=None):
    nc = C.nc
    HG, NK = groups_of_heads, NJ // q_per_kv
    KH = HG * NK
    chunks = [("q", c) for c in range(HG * NJ)] + [("k", c) for c in range(KH)] + [("v", s) for s in range(SPG)]
    NC_ = len(chunks)
    NQK, EARLY = NC_ - SPG, 4
    UPI = UPG * HG
    cross = kT_dram is not None
    with ExitStack() as ctx:
        sc = Scope(nc, ctx, name)
        sb, ps, sem = sc.sb, sc.ps, sc.sem
        wq, wk, wv = sb("wq", [P, HG * NJ, P]), sb("wk", [P, KH, P]), sb("wv", [P, 2, KH * HW])
        wo = sb("wo", [P, HG * NJ, D])
        bo = sb("bo", [1, D])
        if not cross:
            table = sb("table", [P, HG, UH, S])
        kvb = sb("kvb", [P, GT]) if cross else None
        qT, kT = sb("qT", [P, HG * NJ, GT]), sb("kT", [P, KH, GT])
        val = sb("val", [P, SPG, KH, HW])
        s1 = sb("s1", [P, 2, UT, UH, S])
        mx, den = sb("mx", [P, UT, UH]), sb("den", [P, UT, UH])
        pT, oT = sb("pT", [P, UT, NJ, P]), sb("oT", [P, UT, NJ, P])
        st, mv = sb("st", [P, TPG, 6]), sb("mv", [P, TPG, 2])
        ps_s, ps_t, ps_o = ps("ps_s", [P, 2, GT]), ps("ps_t", [P, UT, GT]), ps("ps_o", [P, UT, GT])
        ps_out, ps_j = ps("ps_out", [P, UT, D]), ps("ps_j", [P, GT])
        fr = Front(C, sc, ps_j, C.X, C.RS, C.NM)
        if not cross:
            kvb = fr.xnT
        loaded, kv_loaded = sem("loaded"), sem("kv_loaded")
        proj_done, act_taken, dve_taken = sem("proj_done"), sem("act_taken"), sem("dve_taken")
        scores_done, scores_read, shifted, exped, probs = (
            sem(n) for n in ("scores_done", "scores_read", "shifted", "exped", "probs"))
        pT_done, pT_ready, oT_done, oT_ready = (sem(n) for n in ("pT_done", "pT_ready", "oT_done", "oT_ready"))
        out_done, out_read = sem("out_done"), sem("out_read")
        begun = sem("begun")
        scales = NormScales(C, sc, 1e-5)
        block = ctx.enter_context(nc.Block())
        loads = [(wq[:], W["wq"]), (wk[:], W["wk"]), (wv[:], W["wv"]), (wo[:], W["wo"])]
        loads += [(bo[:], W["bo"])] if cross else [(table[:], W["table"])]
        n_loaded = 16 * len(loads)

        def bank(c):
            return ((ps_s, ps_t) if c < NQK else (ps_t, ps_o))[c % 4 // 2][:, c % 2, :]

        @block.sync
        def _(sp):
            for to, of in loads:
                sp.dma_start(to, of).then_inc(loaded, 16)
            if cross:
                sp.dma_start(kvb[:], kT_dram[:, 0:GT]).then_inc(kv_loaded, 16)
                with sp.Fori(1, C.NG) as i:
                    sp.wait_ge(proj_done, i * NC_)
                    sp.dma_start(kvb[:], kT_dram[:, bass.ds(i * GT, GT)]).then_inc(kv_loaded, 16)

        @block.tensor
        def _(pe):
            pe.wait_ge(loaded, n_loaded)

            def hold(pe):
                pe.sem_inc(begun, 1)

            def project(i, c):
                kind, n = chunks[c]
                before = c - 2 if NQK <= c < NQK + 2 else c - 4
                if before >= 0 and not NQK + 2 <= c < NQK + 4:
                    pe.wait_ge(dve_taken if c % 2 else act_taken, i * (NC_ // 2) + before // 2 + 1)
                if kind == "q":
                    last = nc.tensor.matmul(bank(c), wq[:, n, :], fr.xnT[:], start=True, stop=True)
                elif kind == "k":
                    last = nc.tensor.matmul(bank(c), wk[:, n, :], kvb[:], start=True, stop=True)
                else:
                    for half in range(2):
                        last = nc.tensor.matmul(bank(c)[HW * half:HW * half + HW, 0:KH * HW],
                                                kvb[:, n * S:(n + 1) * S], wv[:, half, :], start=True, stop=True)
                last.then_inc(proj_done, 1)

            def queries_keys(i, x):
                u, hg = x // HG, x % HG
                if not cross:
                    pe.wait_ge(scores_read, i * UPI + x + 1)
                elif x > 0:
                    pe.wait_ge(shifted, i * UPI + x)
                hold(pe)
                for t in range(UT):
                    for b in range(2):
                        q = 2 * (UT * u + t) + b
                        cols = slice(q * S, q * S + S)
                        for j in range(NJ):
                            for half in range(2):
                                r = slice(HW * half, HW * half + HW)
                                last = nc.tensor.matmul(
                                    ps_s[S * b:S * b + S, half, (t * NJ + j) * S:(t * NJ + j + 1) * S],
                                    qT[r, hg * NJ + j, cols], kT[r, hg * NK + j // q_per_kv, cols], start=True, stop=True)
                last.then_inc(scores_done, 1)

            def turn_probs(i, x):
                pe.wait_ge(probs, i * UPI + x + 1)
                for t in range(UT):
                    for j in range(NJ):
                        last = nc.tensor.transpose(ps_t[:, t, j * P:(j + 1) * P], 
                                               s1[:, x % 2, t, 2 * j:2 * j + 2, :].rearrange("p a k -> p (a k)"), C.ident[:])
                last.then_inc(pT_done, 1)

            def weigh_values(i, x):
                u, hg = x // HG, x % HG
                pe.wait_ge(pT_ready, i * UPI + x + 1)
                hold(pe)
                for t in range(UT):
                    for b in range(2):
                        q = 2 * (UT * u + t) + b
                        for k in range(NK):
                            for half in range(2):
                                r = slice(HW * half, HW * half + HW)
                                js = slice(k * q_per_kv, (k + 1) * q_per_kv)
                                last = nc.tensor.matmul(
                                    ps_o[r, t, :].rearrange("p (j q) -> p j q", q=P)[:, js, S * b:S * b + S],
                                    val[r, q, hg * NK + k, :], pT[r, t, js, S * b:S * b + S], start=True, stop=True)
                last.then_inc(oT_done, 1)

            def project_output(i, x):
                u, hg = x // HG, x % HG
                pe.wait_ge(oT_ready, i * UPI + x + 1)
                if hg == 0:
                    pe.wait_ge(out_read, i * UPG + u + 1)
                for t in range(UT):
                    for j in range(NJ):
                        end = hg == HG - 1 and j == NJ - 1
                        last = nc.tensor.matmul(ps_out[:, t, :], oT[:, t, j, :], wo[:, hg * NJ + j, :],
                                                start=hg == 0 and t == 0 and j == 0,
                                                stop=end and not cross, skip_group_check=True)
                    if cross and hg == HG - 1:
                        last = nc.tensor.matmul(ps_out[:, t, :], C.ones[0:1, :], bo[0:1, :], start=False, stop=True,
                                                skip_group_check=True)
                if hg == HG - 1:
                    last.then_inc(out_done, 1)

            fr.pe(pe, 0)
            pe.wait_ge(fr.xT_ready, 1)
            for c in range(EARLY):
                project(0, c)
            with pe.Fori(0, C.NG) as i:
                if cross:
                    pe.wait_ge(kv_loaded, i * 16 + 16)
                for c in range(EARLY, NQK):
                    project(i, c)
                for taken in (act_taken, dve_taken):
                    pe.wait_ge(taken, i * (NC_ // 2) + NQK // 2)
                queries_keys(i, 0)
                for c in range(NQK, NQK + 4):
                    project(i, c)
                for x in range(UPI):
                    if x + 1 < UPI:
                        queries_keys(i, x + 1)
                    else:
                        fr.pe(pe, i + 1)
                        pe.wait_ge(fr.xT_ready, i + 2)
                        if cross:
                            pe.wait_ge(shifted, i * UPI + UPI)
                        else:
                            pe.wait_ge(scores_read, i * UPI + UPI + 1)
                        project(i + 1, 0)
                        project(i + 1, 1)
                    if x == 0:
                        for c in range(NQK + 4, NC_):
                            project(i, c)
                        for taken in (act_taken, dve_taken):
                            pe.wait_ge(taken, i * (NC_ // 2) + NC_ // 2)
                    turn_probs(i, x)
                    if x > 0:
                        project_output(i, x - 1)
                    weigh_values(i, x)
                project(i + 1, 2)
                project(i + 1, 3)
                project_output(i, UPI - 1)

        def take(eng, copy, scaled, i, odd, start, end):
            for c in range(start + odd, end, 2):
                kind, n = chunks[c]
                eng.wait_ge(proj_done, i * NC_ + c + 1)
                if kind == "q":
                    last = scaled(qT[:, n, :], bank(c))
                elif kind == "k":
                    last = copy(kT[:, n, :], bank(c))
                else:
                    last = copy(val[:, n, :, :].rearrange("p k d -> p (k d)"), bank(c)[:, 0:KH * HW])
                last.then_inc(dve_taken if odd else act_taken, 1)

        @block.scalar
        def _(act):
            scales.act(act)
            act_copy = lambda to, of: nc.scalar.activation(to, of, ACT.Copy)
            act_scaled = lambda to, of: nc.scalar.activation(to, of, ACT.Copy, scale=HW ** -0.5)

            def output_copy(i, x):
                act.wait_ge(oT_done, i * UPI + x + 1)
                nc.scalar.activation(oT[:].rearrange("p t j q -> p t (j q)"), ps_o[:], ACT.Copy).then_inc(oT_ready, 1)

            fr.act(act, 0)
            with act.Fori(0, C.NG) as i:
                take(act, act_copy, act_scaled, i, 0, 0, NQK + 4)
                for x in range(UPI):
                    act.wait_ge(shifted, i * UPI + x + 1)
                    nc.scalar.activation(s1[:, x % 2, :, :, :], s1[:, x % 2, :, :, :], ACT.Exp).then_inc(exped, 1)
                    if x == 0:
                        take(act, act_copy, act_scaled, i, 0, NQK + 4, NC_)
                    if x > 0:
                        output_copy(i, x - 1)
                    if x == UPI - 1:
                        fr.act(act, i + 1)
                    act.wait_ge(pT_done, i * UPI + x + 1)
                    nc.scalar.activation(pT[:].rearrange("p t j q -> p t (j q)"), ps_t[:], ACT.Copy).then_inc(pT_ready, 1)
                output_copy(i, UPI - 1)

        @block.vector
        def _(dve):
            scales.dve(dve)
            dve_copy = nc.vector.tensor_copy
            dve_scaled = lambda to, of: nc.vector.tensor_scalar(to, of, HW ** -0.5, None, ALU.mult)
            dve.wait_ge(loaded, n_loaded)
            nc.vector.memset(mx[:], 0.0).then_inc(scores_read, 1)
            nc.vector.memset(mv[:], 0.0).then_inc(out_read, 1)

            def shift(i, x):
                w, out = i * UPI + x, s1[:, x % 2, :, :, :]
                raw = ps_s[:].rearrange("p a (t j k) -> p t a j k", t=UT, k=S)
                halves = out.rearrange("p t (j a) k -> p t a j k", a=2)
                most = mx[:].rearrange("p t (j a) -> p t a j", a=2)
                dve.wait_ge(scores_done, w + 1)
                if not cross:
                    for t in range(UT):
                        last = nc.vector.tensor_tensor(halves[:, t, :, :, :], raw[:, t, :, :, :],
                                                       table[:, x % HG, :, :].rearrange("p (a j) k -> p a j k", a=2), ALU.add)
                    last.then_inc(scores_read, 1)
                    dve.drain()
                    nc.vector.tensor_reduce(mx[:], out, AX, ALU.max)
                    dve.drain()
                    nc.vector.tensor_tensor(out, out, bc(mx[:].unsqueeze(3), [P, UT, UH, S]),
                                            ALU.subtract).then_inc(shifted, 1)
                else:
                    for t in range(UT):
                        nc.vector.tensor_reduce(most[:, t, :, :], raw[:, t, :, :, :], AX, ALU.max)
                    dve.drain()
                    for t in range(UT):
                        last = nc.vector.tensor_tensor(
                            halves[:, t, :, :, :], raw[:, t, :, :, :],
                            bc(most[:, t, :, :].unsqueeze(3), [P, 2, NJ, S]), ALU.subtract)
                    last.then_inc(shifted, 1)

            def normalise(i, x):
                out = s1[:, x % 2, :, :, :]
                dve.wait_ge(exped, i * UPI + x + 1)
                nc.vector.tensor_reduce(den[:], out, AX, ALU.add)
                dve.drain()
                nc.vector.reciprocal(den[:], den[:])
                dve.drain()
                nc.vector.tensor_tensor(out, out, bc(den[:].unsqueeze(3), [P, UT, UH, S]), ALU.mult).then_inc(probs, 1)

            def residual(i, u):
                dve.wait_ge(out_done, i * UPG + u + 1)
                to = C.X[:, bass.ds(i * TPG + u * UT, UT), :]
                nc.vector.tensor_tensor(to, ps_out[:], to, ALU.add).then_inc(out_read, 1)

            fr.dve(0)
            take(dve, dve_copy, dve_scaled, 0, 1, 0, EARLY)
            with dve.Fori(0, C.NG) as i:
                take(dve, dve_copy, dve_scaled, i, 1, EARLY, NQK)
                shift(i, 0)
                take(dve, dve_copy, dve_scaled, i, 1, NQK, NQK + 4)
                for x in range(UPI):
                    normalise(i, x)
                    if x == 0:
                        take(dve, dve_copy, dve_scaled, i, 1, NQK + 4, NC_)
                    if x + 1 < UPI:
                        shift(i, x + 1)
                    if x == UPI - 2:
                        fr.dve(i + 1)
                    if x % HG == 0 and x > 0:
                        residual(i, x // HG - 1)
                take(dve, dve_copy, dve_scaled, i + 1, 1, 0, EARLY)
                residual(i, UPG - 1)
                dve.drain()
                group_stats(nc, dve, C, C.X, st, mv, i)



NST = 2
CYCLES, LAYERS = 3, 4


def coupled_ffn(C, name, W):
    nc = C.nc
    widths = [D, D, D // 2, D // 4, D]
    gwidths = [D, D // 2, D // 4, D]
    with ExitStack() as ctx:
        sc = Scope(nc, ctx, name)
        sb, ps, sem = sc.sb, sc.ps, sc.sem
        w = [sb(f"w{n}", [widths[n], widths[n + 1]]) for n in range(LAYERS)]
        b = [sb(f"b{n}", [widths[n + 1], 1]) for n in range(LAYERS)]
        gw = [sb(f"gw{n}", [gwidths[n], gwidths[n + 1]]) for n in range(3)]
        gb = [sb(f"gb{n}", [gwidths[n + 1], 1]) for n in range(3)]
        perm, reach = sb("perm", [P, P]), sb("reach", [P, 1])
        reach2, offset = sb("reach2", [P, 1]), sb("offset", [P, 1])
        xn = sb("xn", [P, NST * TPG, D])
        cur, h, tf = sb("cur", [P, NST, GT]), sb("h", [P, NST, GT]), sb("tf", [P, NST, GT])
        mean, gh, gf = sb("mean", [P, NST, SPG]), sb("gh", [P, NST * SPG]), sb("gf", [P, NST, SPG])
        st, mv = sb("st", [P, TPG, 6]), sb("mv", [P, TPG, 2])
        ps_j, ps_g = ps("ps_j", [P, GT]), ps("ps_g", [P, 512])
        ps_c, ps_w, ps_b = ps("ps_c", [P, NST, GT]), ps("ps_w", [P, NST, GT]), ps("ps_b", [P, NST, GT])
        loaded, prepared = sem("loaded"), sem("prepared")
        xn_ready, xT_done, cur_ready, mean_ready = (sem(n) for n in ("xn_ready", "xT_done", "cur_ready", "mean_ready"))
        g_done, g_act = sem("g_done"), sem("g_act")
        l_done, l_act, tw_done, updated = sem("l_done"), sem("l_act"), sem("tw_done"), sem("updated")
        back_done = sem("back_done")
        begun = sem("begun")
        scales = NormScales(C, sc, 1e-5)
        block = ctx.enter_context(nc.Block())
        loads = [(t[:], W[k]) for k, t in
                 [(f"w{n}", w[n]) for n in range(4)] + [(f"b{n}", b[n]) for n in range(4)]
                 + [(f"gw{n}", gw[n]) for n in range(3)] + [(f"gb{n}", gb[n]) for n in range(3)]
                 + [("perm", perm), ("reach", reach)]]
        n_loaded = 16 * len(loads)
        NL = CYCLES * LAYERS * NST

        @block.sync
        def _(sp):
            for to, of in loads:
                sp.dma_start(to, of).then_inc(loaded, 16)

        def step(c, l, k):
            return (c * LAYERS + l) * NST + k + 1

        @block.tensor
        def _(pe):
            pe.wait_ge(loaded, n_loaded)

            def hold(rows_in):
                if rows_in == S:
                    pe.sem_inc(begun, 1)

            with pe.Fori(0, C.NG // NST) as i:
                pe.wait_ge(xn_ready, i + 1)
                for k in range(NST):
                    if k:
                        pe.wait_ge(cur_ready, i * NST + k)
                    for p in range(TPG):
                        last = nc.tensor.transpose(ps_j[:, p * P:(p + 1) * P], xn[:, k * TPG + p, :], C.ident[:])
                    last.then_inc(xT_done, 1)
                for c in range(CYCLES):
                    for l in range(LAYERS):
                        for k in range(NST):
                            if l:
                                pe.wait_ge(l_act, i * NL + step(c, l - 1, k))
                            elif c:
                                pe.wait_ge(updated, i * CYCLES * NST + (c - 1) * NST + k + 1)
                            else:
                                pe.wait_ge(cur_ready, i * NST + k + 1)
                            hold(widths[l])
                            rhs = h[0:widths[l], k, :] if l else cur[:, k, :]
                            nc.tensor.matmul(ps_c[0:widths[l + 1], k, :], w[l][:], rhs, start=True,
                                             stop=True).then_inc(l_done, 1)
                            if l == 0:
                                nc.tensor.matmul(ps_w[:, k, :], perm[:], cur[:, k, :], start=True,
                                                 stop=True).then_inc(tw_done, 1)
                        if c == 0 and l < 3:
                            if l == 0:
                                pe.wait_ge(mean_ready, i + 1)
                            else:
                                pe.wait_ge(g_act, i * 3 + l)
                            hold(gwidths[l])
                            rhs = gh[0:gwidths[l], :] if l else mean[:].rearrange("p k s -> p (k s)")
                            nc.tensor.matmul(ps_g[0:gwidths[l + 1], 0:NST * SPG], gw[l][:], rhs, start=True,
                                             stop=True).then_inc(g_done, 1)
                for k in range(NST):
                    pe.wait_ge(updated, i * CYCLES * NST + (CYCLES - 1) * NST + k + 1)
                    for p in range(TPG):
                        last = nc.tensor.transpose(ps_b[:, k, p * P:(p + 1) * P], cur[:, k, p * P:(p + 1) * P], C.ident[:])
                    last.then_inc(back_done, 1)

        @block.scalar
        def _(act):
            scales.act(act)
            act.wait_ge(loaded, n_loaded)
            with act.Fori(0, C.NG // NST) as i:
                for k in range(NST):
                    act.wait_ge(xT_done, i * NST + k + 1)
                    nc.scalar.activation(cur[:, k, :], ps_j[:], ACT.Copy).then_inc(cur_ready, 1)
                for c in range(CYCLES):
                    for l in range(LAYERS):
                        n = widths[l + 1]
                        if c == 0 and l:
                            act.wait_ge(g_done, i * 3 + l)
                            m = gwidths[l]
                            to = gf[:].rearrange("p k s -> p (k s)") if l == 3 else gh[0:m, :]
                            nc.scalar.activation(to, ps_g[0:m, 0:NST * SPG], ACT.Sigmoid if l == 3 else ACT.Gelu,
                                                 bias=gb[l - 1][:, 0:1]).then_inc(g_act, 1)
                        for k in range(NST):
                            act.wait_ge(l_done, i * NL + step(c, l, k))
                            to, fn = (tf[:, k, :], ACT.Sigmoid) if l == 3 else (h[0:n, k, :], ACT.Gelu)
                            nc.scalar.activation(to, ps_c[0:n, k, :], fn, bias=b[l][:, 0:1]).then_inc(l_act, 1)

        @block.vector
        def _(dve):
            scales.dve(dve)
            dve.wait_ge(loaded, n_loaded)
            nc.vector.tensor_scalar(reach2[:], reach[:], 2.0, None, ALU.mult)
            nc.vector.tensor_scalar(offset[:], reach[:], -1.0, 0.1, ALU.mult, ALU.add)
            nc.vector.memset(mv[:], 0.0)
            dve.drain()
            seqs = lambda t: t.rearrange("p (s n) -> p s n", n=S)

            def normalise(j):
                for p in range(NST * TPG):
                    n = j * NST * TPG + p
                    last = nc.vector.tensor_scalar(xn[:, p, :], C.X[:, n, :], C.RS[:, bass.ds(n, 1)],
                                                   C.NM[:, bass.ds(n, 1)], ALU.mult, ALU.add)
                last.then_inc(xn_ready, 1)

            normalise(0)
            with dve.Fori(0, C.NG // NST) as i:
                for k in range(NST):
                    dve.wait_ge(cur_ready, i * NST + k + 1)
                    nc.vector.tensor_reduce(mean[:, k, :], seqs(cur[:, k, :]), AX, ALU.add)
                dve.drain()
                nc.vector.tensor_scalar(mean[:], mean[:], 1.0 / S, None, ALU.mult).then_inc(mean_ready, 1)
                normalise(i + 1)
                dve.wait_ge(g_act, i * 3 + 3)
                nc.vector.tensor_scalar(gf[:], gf[:], 0.7, None, ALU.mult)
                dve.drain()
                for c in range(CYCLES):
                    for k in range(NST):
                        t = tf[:, k, :]
                        dve.wait_ge(l_act, i * NL + step(c, 3, k))
                        nc.vector.scalar_tensor_tensor(seqs(t), seqs(t), 0.3, bc(gf[:, k, :].unsqueeze(2), [P, SPG, S]),
                                                       ALU.mult, ALU.add)
                        dve.drain()
                        nc.vector.tensor_scalar(t, t, reach2[:, 0:1], offset[:, 0:1], ALU.mult, ALU.add)
                        dve.drain()
                        dve.wait_ge(tw_done, i * CYCLES * NST + c * NST + k + 1)
                        nc.vector.tensor_tensor(t, t, ps_w[:, k, :], ALU.mult)
                        dve.drain()
                        nc.vector.tensor_tensor(cur[:, k, :], cur[:, k, :], t, ALU.add).then_inc(updated, 1)
                for k in range(NST):
                    g = i * NST + k
                    dve.wait_ge(back_done, i * NST + k + 1)
                    nc.vector.tensor_tensor(rows(C.X, g), ps_b[:, k, :].rearrange("p (t d) -> p t d", d=D), rows(C.X, g),
                                            ALU.add)
                    dve.drain()
                    group_stats(nc, dve, C, C.X, st, mv, g)
                    dve.drain()



DI, NS, NTAP, DTR = 256, 16, 4, 8
NHF = DI // P
PADW = S + NTAP - 1


def mamba(C, name, W, first):
    nc = C.nc
    R = 4
    AHEAD = 2
    with ExitStack() as ctx:
        sc = Scope(nc, ctx, name)
        sb, ps, sem = sc.sb, sc.ps, sc.sem
        g, be = sb("g", [P, 1]), sb("be", [P, 1])
        in_w, taps = sb("in_w", [P, 2 * DI]), sb("taps", [P, NTAP, DI])
        conv_b, xp = sb("conv_b", [P, NHF]), sb("xp", [P, NHF, P])
        dt_w, dt_b = sb("dt_w", [P, DI]), sb("dt_b", [P, NHF])
        A, Dp = sb("A", [P, NHF, NS]), sb("Dp", [P, NHF])
        diagD, out_w = sb("diagD", [P, NHF, P]), sb("out_w", [P, NHF, D])
        pick_row = sb("pick_row", [P, 2 * NS])
        sel = sb("sel", [P, 2 * NS, P], BF16)
        flip = sb("flip", [P, P])
        xn = sb("xn", [P, TPG, D])
        hT = sb("hT", [P, SPG, PADW])
        xs, sz = sb("xs", [P, 2, NHF, GT]), sb("sz", [P, 2, NHF, GT])
        low = sb("low", [P, GT])
        parts = sb("parts", [P, 2, GT], BF16)
        x, e, r, v, ln = (sb(n, [P, NHF, GT]) for n in ("x", "e", "r", "v", "ln"))
        q = e
        dt, dtx = sb("dt", [P, 2, NHF, GT]), sb("dtx", [P, 2, NHF, GT])
        dA, Bs = sb("dA", [P, R, NHF, GT]), sb("Bs", [P, R, GT])
        dBx, hs, yc = (sb(n, [P, 2, NHF, GT]) for n in ("dBx", "hs", "yc"))
        ps_B, ps_C, ps_y = ps("ps_B", [P, 2, GT]), ps("ps_C", [P, 2, GT]), ps("ps_y", [P, NHF, GT])
        ps_j, ps_k = ps("ps_j", [P, GT]), ps("ps_k", [P, GT])
        bank = (ps_j, ps_k)
        loaded, prepared, a_ready = sem("loaded"), sem("prepared"), sem("a_ready")
        xn_ready, xT_done, hT_ready = sem("xn_ready"), sem("xT_done"), sem("hT_ready")
        xs_done, z_done, xs_ready, z_ready = sem("xs_done"), sem("z_done"), sem("xs_ready"), sem("z_ready")
        dbl_done, high_ready, parts_ready = sem("dbl_done"), sem("high_ready"), sem("parts_ready")
        dt_done, x_ready, neg_ready, e_ready = sem("dt_done"), sem("x_ready"), sem("neg_ready"), sem("e_ready")
        excess, v_ready, r_ready, dt_ready = sem("excess"), sem("v_ready"), sem("r_ready"), sem("dt_ready")
        B_done, B_copied, dBx_ready, C_done = sem("B_done"), sem("B_copied"), sem("dBx_ready"), sem("C_done")
        decay, scanned, yc_ready, y_added = sem("decay"), sem("scanned"), sem("yc_ready"), sem("y_added")
        y_ready, out_done, out_read = sem("y_ready"), sem("out_done"), sem("out_read")
        begun = sem("begun")
        scales = NormScales(C, sc, 1e-5, 1e-5) if first else None
        block = ctx.enter_context(nc.Block())
        loads = [(g, "g"), (be, "be"), (in_w, "in_w"), (taps, "taps"), (conv_b, "conv_b"), (xp, "xp"),
                 (dt_b, "dt_b"), (A, "A"), (Dp, "D"), (out_w, "out_w"), (pick_row, "pick_row")]
        if not first:
            loads.append((flip, "flip"))
        n_loaded = 16 * (len(loads) + 1)
        rank_rows = slice(32, 32 + DTR)
        both = [P, NHF, GT]

        @block.sync
        def _(sp):
            for to, k in loads:
                sp.dma_start(to[:], W[k]).then_inc(loaded, 16)
            sp.dma_start(dt_w[rank_rows, :], W["dt_w"]).then_inc(loaded, 16)

        n_prepared = 3

        @block.gpsimd
        def _(pool):
            nc.gpsimd.memset(hT[:], 0.0).then_inc(prepared, 1)
            nc.gpsimd.memset(dA[:], 0.0).then_inc(prepared, 1)
            nc.gpsimd.memset(Bs[:], 0.0).then_inc(dBx_ready, R)
            pool.drain()

            def hold():
                pool.sem_inc(begun, 1)

            def multiply(to, one, other):
                return nc.gpsimd.tensor_tensor(to, one, other, ALU.mult)

            def state(n, s, par):
                pool.wait_ge(B_copied, n + 3)
                pool.wait_ge(scanned, n - 1 + R)
                hold()
                multiply(dBx[:, s % 2, :, :], dtx[:, par, :, :], bc(Bs[:, s % R, :].unsqueeze(1), both)).then_inc(dBx_ready, 1)

            def front(j, s, par):
                if s == 11:
                    pool.wait_ge(v_ready, j + 1)
                    hold()
                    nc.gpsimd.tensor_tensor(v[:], v[:], e[:], ALU.subtract)
                    pool.drain()
                elif s == 12:
                    pool.wait_ge(r_ready, j + 1)
                    hold()
                    multiply(v[:], v[:], r[:]).then_inc(excess, 1)
                elif s == 15:
                    pool.wait_ge(dt_ready, j + 1)
                    hold()
                    multiply(dtx[:, par, :, :], dt[:, par, :, :], xs[:, par, :, :])
                    pool.drain()

            for s in range(11, 16):
                front(0, s, 0)
            for s in range(AHEAD):
                state(s, s, 0)
            with pool.Fori(0, C.NG // 2) as pair:
                for par in range(2):
                    i = pair * 2 + par
                    for s in range(AHEAD, NS):
                        state(i * NS + s, s, par)
                        front(i + 1, s, 1 - par)
                    for s in range(AHEAD):
                        state(i * NS + NS + s, s, 1 - par)

        @block.tensor
        def _(pe):
            pe.wait_ge(loaded, n_loaded)
            pe.wait_ge(prepared, n_prepared)

            def turn(j):
                pe.wait_ge(xn_ready, j + 1)
                for p in range(TPG):
                    to = ps_j[:, p * P:(p + 1) * P]
                    if first:
                        last = nc.tensor.transpose(to, xn[:, p, :], C.ident[:])
                    else:
                        last = nc.tensor.matmul(to, xn[:, p, :], flip[:], start=True, stop=True)
                last.then_inc(xT_done, 1)

            def convolve(j, m, step):
                if m == 0 and step == 0:
                    pe.wait_ge(hT_ready, j + 1)
                for k in (2 * step, 2 * step + 1):
                    last = nc.tensor.matmul(bank[m][:], taps[:, k, m * P:(m + 1) * P], hT[:, :, k:k + S],
                                            start=k == 0, stop=k == NTAP - 1)
                if step == 1:
                    last.then_inc(xs_done, 1)

            def gate(j, m):
                pe.wait_ge(xs_ready, j * NHF + m + 1)
                nc.tensor.matmul(bank[m][:], in_w[:, DI + m * P:DI + (m + 1) * P], hT[:, :, NTAP - 1:], start=True,
                                 stop=True).then_inc(z_done, 1)

            def low_products(j, par):
                pe.wait_ge(z_ready, j * NHF + 1)
                for m in range(NHF):
                    last = nc.tensor.matmul(ps_j[:], xp[:, m, :], xs[:, par, m, :], start=m == 0, stop=m == NHF - 1)
                last.then_inc(dbl_done, 1)

            def step_sizes(j):
                pe.wait_ge(parts_ready, j + 1)
                pe.wait_ge(z_ready, j * NHF + 2)
                for m in range(NHF):
                    last = nc.tensor.matmul(bank[m][:], dt_w[rank_rows, m * P:(m + 1) * P], low[rank_rows, :], start=True,
                                            stop=True)
                last.then_inc(dt_done, 1)

            def spread_B(n, s, par):
                pe.wait_ge(B_copied, n + 1)
                nc.tensor.matmul(ps_B[:, s % 2, :], sel[:, s, :], parts[:, par, :], start=True, stop=True).then_inc(B_done, 1)

            def spread_C(s, par):
                nc.tensor.matmul(ps_C[:, s % 2, :], sel[:, NS + s, :], parts[:, par, :], start=True,
                                 stop=True).then_inc(C_done, 1)

            def skip(par):
                for m in range(NHF):
                    nc.tensor.matmul(ps_y[:, m, :], diagD[:, m, :], xs[:, par, m, :], start=False, stop=False)

            def project(i):
                pe.wait_ge(y_ready, i + 2)
                pe.wait_ge(xs_ready, i * NHF + 6)
                for p in range(TPG):
                    for m in range(NHF):
                        last = nc.tensor.matmul(ps_k[:, p * D:(p + 1) * D], q[:, m, p * P:(p + 1) * P], out_w[:, m, :],
                                                start=m == 0, stop=m == NHF - 1)
                last.then_inc(out_done, 1)

            def add_state(n, s):
                pe.wait_ge(yc_ready, n + 1)
                for m in range(NHF):
                    last = nc.tensor.matmul(ps_y[:, m, :], C.ident[:], yc[:, s % 2, m, :], start=s == 0, stop=s == NS - 1)
                last.then_inc(y_added, 1)

            def front(j, s, par, in_loop):
                if s == 2:
                    gate(j, 0)
                    if in_loop:
                        pe.wait_ge(out_read, j)
                    gate(j, 1)
                elif s == 3:
                    low_products(j, par)
                elif s == 6:
                    step_sizes(j)
                elif s == 8:
                    pe.wait_ge(x_ready, j + 1)
                    turn(j + 1)
                elif 10 <= s < 14:
                    convolve(j + 1, (s - 10) // 2, s % 2)

            turn(0)
            for s in range(10, 14):
                front(-1, s, 1, False)
            for s in range(2, 14):
                front(0, s, 0, False)
            for s in range(AHEAD):
                spread_B(s, s, 0)
                spread_C(s, 0)
            for s in range(AHEAD):
                spread_B(s + 2, s + 2, 0)
                add_state(s, s)
                spread_C(s + 2, 0)
            with pe.Fori(0, C.NG // 2) as pair:
                for par in range(2):
                    i = pair * 2 + par
                    for s in range(AHEAD, NS):
                        n = i * NS + s
                        to = (s + 2) % NS
                        its = par if to == s + 2 else 1 - par
                        spread_B(n + 2, to, its)
                        front(i + 1, s, 1 - par, True)
                        if s == 9:
                            skip(par)
                        pe.wait_ge(yc_ready, n + 1)
                        spread_C(to, its)
                        add_state(n, s)
                    for s in range(AHEAD):
                        n = i * NS + NS + s
                        spread_B(n + 2, s + 2, 1 - par)
                        if s == 0:
                            project(i)
                        pe.wait_ge(yc_ready, n + 1)
                        spread_C(s + 2, 1 - par)
                        add_state(n, s)
            for m in range(NHF):
                nc.tensor.matmul(ps_y[:, m, :], C.ident[:], yc[:, 1, m, :], start=False, stop=True)

        @block.scalar
        def _(act):
            if first:
                scales.act(act)
            act.wait_ge(loaded, n_loaded)
            nc.scalar.activation(A[:], A[:], ACT.Exp).then_inc(a_ready, 1)
            act.wait_ge(prepared, n_prepared)
            seqs = lambda t: t.rearrange("p (s n) -> p s n", n=S)[:, :, 1:]

            def copy_rows(j):
                act.wait_ge(xT_done, j + 1)
                nc.scalar.activation(hT[:, :, NTAP - 1:], ps_j[:].rearrange("p (s n) -> p s n", n=S), ACT.Identity,
                                     scale=g[:, 0:1], bias=be[:, 0:1]).then_inc(hT_ready, 1)

            def state(n, s, par):
                act.wait_ge(B_done, n + 1)
                act.wait_ge(dBx_ready, n + 1)
                nc.scalar.activation(Bs[:, s % R, :], ps_B[:, s % 2, :], ACT.Copy).then_inc(B_copied, 1)
                act.wait_ge(scanned, n + 1)
                for m in range(NHF):
                    last = nc.scalar.activation(seqs(dA[:, s % R, m, :]), seqs(dt[:, par, m, :]), ACT.Exp, scale=A[:, m, s:s + 1])
                last.then_inc(decay, 1)

            def activate(j, par, in_loop):
                if in_loop:
                    act.wait_ge(y_added, j * NS - 2 * NS + 10)
                for m in range(NHF):
                    act.wait_ge(xs_done, j * NHF + m + 1)
                    nc.scalar.activation(xs[:, par, m, :], bank[m][:], ACT.Silu,
                                         bias=conv_b[:, m:m + 1]).then_inc(xs_ready, 1)

            def front(j, s, par, in_loop):
                if s == 4:
                    for m in range(NHF):
                        act.wait_ge(z_done, j * NHF + m + 1)
                        if m == 0 and in_loop:
                            act.wait_ge(y_ready, j)
                        nc.scalar.activation(sz[:, par, m, :], bank[m][:], ACT.Silu).then_inc(z_ready, 1)
                elif s == 6:
                    act.wait_ge(dbl_done, j + 1)
                    nc.scalar.activation(low[32:64, :], ps_j[32:64, :], ACT.Copy)
                    nc.scalar.activation(parts[:, par, :], ps_j[:], ACT.Copy).then_inc(high_ready, 1)
                elif s == 9:
                    act.wait_ge(neg_ready, j + 1)
                    nc.scalar.activation(e[:], e[:], ACT.Exp).then_inc(e_ready, 1)
                elif s == 10:
                    copy_rows(j + 1)
                elif s == 12:
                    act.drain()
                    nc.scalar.activation(ln[:], e[:], ACT.Ln, bias=1.0)
                    act.drain()
                    nc.scalar.activation(r[:], ln[:], ACT.Exp, scale=-1.0).then_inc(r_ready, 1)

            copy_rows(0)
            activate(0, 0, False)
            for s in range(4, 13):
                front(0, s, 0, False)
            act.wait_ge(dt_ready, 1)
            for s in range(AHEAD):
                state(s, s, 0)
            activate(1, 1, False)
            with act.Fori(0, C.NG // 2) as pair:
                for par in range(2):
                    i = pair * 2 + par
                    for s in range(AHEAD, NS):
                        state(i * NS + s, s, par)
                        front(i + 1, s, 1 - par, True)
                    act.wait_ge(dt_ready, i + 2)
                    state(i * NS + NS, 0, 1 - par)
                    activate(i + 2, par, True)
                    state(i * NS + NS + 1, 1, 1 - par)

        @block.vector
        def _(dve):
            if first:
                scales.dve(dve)
            dve.wait_ge(loaded, n_loaded)
            for k in range(NTAP):
                nc.vector.tensor_tensor(taps[:, k, :], taps[:, k, :], in_w[:, 0:DI], ALU.mult)
            for m in range(NHF):
                nc.vector.tensor_scalar(diagD[:, m, :], C.ident[:], Dp[:, m:m + 1], None, ALU.mult)
            nc.vector.tensor_copy(sel[:], bc(pick_row[:].unsqueeze(2), [P, 2 * NS, P]))
            nc.vector.memset(xn[:], 0.0).then_inc(out_read, 1)
            nc.vector.memset(x[:], 0.0).then_inc(y_ready, 1)
            nc.vector.memset(r[:], 0.0).then_inc(scanned, R)
            nc.vector.memset(ln[:], 0.0).then_inc(B_copied, 2)
            dve.wait_ge(a_ready, 1)
            nc.vector.tensor_scalar(A[:], A[:], -1.0, None, ALU.mult).then_inc(prepared, 1)
            dve.drain()

            def normalise(j):
                for p in range(TPG):
                    n = j * TPG + p
                    last = nc.vector.tensor_scalar(xn[:, p, :], C.X[:, n, :], C.RS2[:, bass.ds(n, 1)],
                                                   C.NM2[:, bass.ds(n, 1)], ALU.mult, ALU.add)
                last.then_inc(xn_ready, 1)

            def front(j, s, par):
                if s == 5:
                    dve.wait_ge(high_ready, j + 1)
                    nc.vector.tensor_tensor(low[64:128, :], ps_j[64:128, :], parts[64:128, par, :], ALU.subtract)
                    dve.drain()
                    nc.vector.tensor_copy(parts[64:128, par, :], low[64:128, :])
                    dve.drain()
                    nc.vector.tensor_tensor(low[96:128, :], low[96:128, :], parts[96:128, par, :], ALU.subtract)
                    dve.drain()
                    nc.vector.tensor_copy(parts[96:128, par, :], low[96:128, :]).then_inc(parts_ready, 1)
                elif s == 7:
                    dve.wait_ge(dt_done, j + 1)
                    for m in range(NHF):
                        last = nc.vector.tensor_scalar(x[:, m, :], bank[m][:], dt_b[:, m:m + 1], None, ALU.add)
                    last.then_inc(x_ready, 1)
                    dve.drain()
                    nc.vector.scalar_tensor_tensor(e[:], x[:], -1.0, x[:], ALU.mult, ALU.min).then_inc(neg_ready, 1)
                elif s == 10:
                    dve.wait_ge(e_ready, j + 1)
                    nc.vector.tensor_scalar(x[:], x[:], 0.0, None, ALU.max)
                    nc.vector.tensor_scalar(v[:], e[:], 1.0, -1.0, ALU.add, ALU.add).then_inc(v_ready, 1)
                elif s == 12:
                    dve.drain()
                    dve.wait_ge(r_ready, j + 1)
                    nc.vector.tensor_tensor(dt[:, par, :, :], x[:], ln[:], ALU.add)
                    dve.drain()
                elif s == 13:
                    dve.wait_ge(excess, j + 1)
                    nc.vector.tensor_tensor(dt[:, par, :, :], dt[:, par, :, :], v[:], ALU.subtract).then_inc(dt_ready, 1)

            flat = lambda t: t.rearrange("p m n -> p (m n)")

            def state(n, s, wait_free=True):
                h = hs[:, s % 2, :, :]
                dve.wait_ge(decay, n + 1)
                dve.wait_ge(dBx_ready, n + 1 + R)
                nc.vector.tensor_tensor_scan(flat(h), flat(dA[:, s % R, :, :]), flat(dBx[:, s % 2, :, :]), 0.0, ALU.mult,
                                             ALU.add).then_inc(scanned, 1)
                dve.drain()
                if wait_free:
                    dve.wait_ge(y_added, n - 1)
                dve.wait_ge(C_done, n + 1)
                nc.vector.tensor_tensor(yc[:, s % 2, :, :], h, bc(ps_C[:, s % 2, :].unsqueeze(1), both),
                                        ALU.mult).then_inc(yc_ready, 1)

            normalise(0)
            dve.drain()
            dve.wait_ge(xT_done, 1)
            normalise(1)
            for s in range(5, 14):
                front(0, s, 0)
            for s in range(AHEAD):
                state(s, s, False)
            with dve.Fori(0, C.NG // 2) as pair:
                for par in range(2):
                    i = pair * 2 + par
                    for s in range(AHEAD, NS):
                        state(i * NS + s, s)
                        front(i + 1, s, 1 - par)
                        if s == 4:
                            dve.wait_ge(xT_done, i + 2)
                            normalise(i + 2)
                        elif s == 14 and first:
                            for p in range(TPG):
                                n = i * TPG + p
                                nc.vector.tensor_scalar(C.Y[:, n, :], C.X[:, n, :], C.RS[:, bass.ds(n, 1)],
                                                        C.NM[:, bass.ds(n, 1)], ALU.mult, ALU.add)
                    state(i * NS + NS, 0)
                    dve.wait_ge(y_added, i * NS + NS)
                    nc.vector.tensor_tensor(q[:], sz[:, par, :, :], ps_y[:], ALU.mult).then_inc(y_ready, 1)
                    state(i * NS + NS + 1, 1)
                    dve.wait_ge(out_done, i + 1)
                    nc.vector.tensor_tensor(rows(C.Y, i), ps_k[:].rearrange("p (t d) -> p t d", d=D), rows(C.Y, i),
                                            ALU.add).then_inc(out_read, 1)
                    dve.drain()


def mamba_join(C, name):
    nc = C.nc
    with ExitStack() as ctx:
        sc = Scope(nc, ctx, name)
        xn, t = sc.sb("xn", [P, 2, PAIR, D]), sc.sb("t", [P, 2, PAIR, D])
        st, mv = sc.sb("st", [P, PAIR, 6]), sc.sb("mv", [P, PAIR, 2])
        activated, joined = sc.sem("activated"), sc.sem("joined")
        block = ctx.enter_context(nc.Block())
        steps = C.NT // PAIR

        @block.scalar
        def _(act):
            with act.Fori(0, steps // 2) as i:
                for h in range(2):
                    act.wait_ge(joined, i * 2 + h + 1)
                    for p in range(PAIR):
                        n = i * (2 * PAIR) + h * PAIR + p
                        nc.scalar.activation(xn[:, h, p, :], C.X[:, n, :], ACT.Identity, scale=C.RS[:, bass.ds(n, 1)],
                                             bias=C.NM[:, bass.ds(n, 1)])
                    nc.scalar.activation(t[:, h, :, :], C.Y[:, bass.ds(i * (2 * PAIR) + h * PAIR, PAIR), :],
                                         ACT.Gelu).then_inc(activated, 1)

        @block.vector
        def _(dve):
            nc.vector.memset(st[:], 0.0).then_inc(joined, 1)
            nc.vector.memset(mv[:], 0.0).then_inc(joined, 1)
            dve.drain()
            with dve.Fori(0, steps // 2) as i:
                for h in range(2):
                    dve.wait_ge(activated, i * 2 + h + 1)
                    nc.vector.tensor_tensor(C.Y[:, bass.ds(i * (2 * PAIR) + h * PAIR, PAIR), :], xn[:, h, :, :],
                                            t[:, h, :, :], ALU.add).then_inc(joined, 1)
                    dve.drain()
                    row_stats(nc, dve, C, C.Y, st, mv, i * 2 + h, PAIR)
                    dve.drain()


def gelu_ffn(C, name, W):
    nc = C.nc
    F = W["w1"].shape[1]
    NF = F // P
    with ExitStack() as ctx:
        sc = Scope(nc, ctx, name)
        sb, ps, sem = sc.sb, sc.ps, sc.sem
        w1, w2, b1, b2 = sb("w1", [P, F]), sb("w2", [P, NF, D]), sb("b1", [P, NF]), sb("b2", [1, D])
        g, be = sb("g", [P, 1]), sb("be", [P, 1])
        hid = sb("hid", [P, NF, GT])
        st, mv = sb("st", [P, TPG, 6]), sb("mv", [P, TPG, 2])
        ps_j, ps_o, ps_h = ps("ps_j", [P, GT]), ps("ps_o", [P, GT]), ps("ps_h", [P, NF, GT])
        fr = Front(C, sc, ps_j, C.Y, C.RS2, C.NM2)
        loaded, hid_done, hid_ready = sem("loaded"), sem("hid_done"), sem("hid_ready")
        out_done, out_read = sem("out_done"), sem("out_read")
        scales = InnerScales(C, sc, 1e-5, False)
        block = ctx.enter_context(nc.Block())
        loads = [(w1[:], W["w1"]), (w2[:], W["w2"].rearrange("(c p) d -> p c d", p=P)), (b1[:], W["b1"]), (b2[:], W["b2"]),
                 (g[:], W["g"]), (be[:], W["be"])]
        n_loaded = 16 * len(loads)

        @block.sync
        def _(sp):
            for to, of in loads:
                sp.dma_start(to, of).then_inc(loaded, 16)

        @block.tensor
        def _(pe):
            pe.wait_ge(loaded, n_loaded)
            fr.pe(pe, 0)
            with pe.Fori(0, C.NG) as i:
                pe.wait_ge(fr.xT_ready, i + 1)
                for c in range(NF):
                    nc.tensor.matmul(ps_h[:, c, :], w1[:, c * P:(c + 1) * P], fr.xnT[:], start=True,
                                     stop=True).then_inc(hid_done, 1)
                fr.pe(pe, i + 1)
                pe.wait_ge(out_read, i + 1)
                pe.wait_ge(hid_ready, i * NF + NF)
                for p in range(TPG):
                    o = ps_o[:, p * D:(p + 1) * D]
                    for c in range(NF):
                        nc.tensor.matmul(o, hid[:, c, p * P:(p + 1) * P], w2[:, c, :], start=c == 0, stop=False)
                    last = nc.tensor.matmul(o, C.ones[0:1, :], b2[0:1, :], start=False, stop=True)
                last.then_inc(out_done, 1)

        @block.scalar
        def _(act):
            scales.act(act)
            act.wait_ge(loaded, n_loaded)

            def copy_rows(j):
                act.wait_ge(fr.xT_done, j + 1)
                nc.scalar.activation(fr.xnT[:], ps_j[:], ACT.Identity, scale=g[:, 0:1],
                                     bias=be[:, 0:1]).then_inc(fr.xT_ready, 1)

            copy_rows(0)
            with act.Fori(0, C.NG) as i:
                for c in range(NF):
                    act.wait_ge(hid_done, i * NF + c + 1)
                    nc.scalar.activation(hid[:, c, :], ps_h[:, c, :], ACT.Gelu, bias=b1[:, c:c + 1]).then_inc(hid_ready, 1)
                copy_rows(i + 1)

        @block.vector
        def _(dve):
            scales.dve(dve)
            nc.vector.memset(mv[:], 0.0).then_inc(out_read, 1)
            fr.dve(0)
            with dve.Fori(0, C.NG) as i:
                dve.wait_ge(fr.xT_done, i + 1)
                fr.dve(i + 1)
                nc.vector.tensor_tensor(rows(C.X, i), rows(C.X, i), rows(C.Y, i), ALU.add)
                dve.drain()
                dve.wait_ge(out_done, i + 1)
                nc.vector.tensor_tensor(rows(C.X, i), ps_o[:].rearrange("p (t d) -> p t d", d=D), rows(C.X, i),
                                        ALU.add).then_inc(out_read, 1)
                dve.drain()
                group_stats(nc, dve, C, C.X, st, mv, i)



FT = 16
FW = 8
ITERS = 3
PAIRS = HD // 2
STEPS = FT // 4
TWO_PI = (6.28125, 0.0019350051879882812, 3.0199159819567553e-07)
ROUND = 1.5 * 2.0 ** 23


def focus_block(C, name, ctx_rows, scratch_in, scratch_out, W):
    nc = C.nc
    with ExitStack() as ctx:
        sc = Scope(nc, ctx, name)
        sb, ps, sem = sc.sb, sc.ps, sc.sem
        row = [P, FT, D]
        weights = {k: sb("w_" + k, [P, D]) for k in ("q", "k", "v", "qh", "kh", "vh", "out")}
        bias = {k: sb("b_" + k, [P, D]) for k in ("qh", "kh", "vh")}
        lna_g, lna_b = sb("lna_g", [P, 1]), sb("lna_b", [P, 1])
        lnb_g, lnb_b = sb("lnb_g", [P, 2, HD]), sb("lnb_b", [P, 2, HD])
        theta, temp, thr, factor = (sb(n, [P, 1]) for n in ("theta", "temp", "thr", "factor"))
        base, place = sb("base", [P, PAIRS]), sb("place", [P, 2, FT])
        xa, xb = sb("xa", row), sb("xb", row)
        hat_a, hat_b = sb("hat_a", row), sb("hat_b", row)
        cur, prev, ai = sb("cur", row), sb("prev", row), sb("ai", row)
        k0, v0 = sb("k0", row), sb("v0", row)
        qk = sb("qk", [P, 2, FT, D])
        prod = C.Y[:, 0:4 * FT, :].rearrange("p t d -> p (t d)")
        score = sb("score", [P, FT * FT * NH])
        most, den = sb("most", [P, FT, NH]), sb("den", [P, FT, NH])
        hm, hv = sb("hm", [P, 2 * FT * NH]), sb("hv", [P, 2 * FT * NH])
        st, mv, rs = sb("st", [P, FT, 6]), sb("mv", [P, FT, 2]), sb("rs", [P, FT])
        ang, turns = sb("ang", [P, 2, 2, FT, PAIRS]), sb("turns", [P, 2, 2, FT, PAIRS])
        trig = sb("trig", [P, 2, 2, FT, PAIRS])
        cond, scale = sb("cond", [P, 1]), sb("scale", [P, 1])
        diff, done, kept = sb("diff", [P, 2]), sb("done", [P, 2]), sb("kept", [P, 2])
        gst, gmv = sb("gst", [P, ROW_TILES, 6]), sb("gmv", [P, ROW_TILES, 2])
        rT = sb("rT", [P, 2, 4 * P])
        ps_t = ps("ps_t", [P, 2, 4 * P])
        ps_p = ps("ps_p", [P, 2, 3, 4 * D])
        loaded, sent, fetched, returned = sem("loaded"), sem("sent"), sem("fetched"), sem("returned")
        src_ready, turned, rT_ready, multiplied, dve_taken, act_taken = (
            sem(n) for n in ("src_ready", "turned", "rT_ready", "multiplied", "dve_taken", "act_taken"))
        k_mean, k_square, spread_ready, k_scaled = (
            sem(n) for n in ("k_mean", "k_square", "spread_ready", "k_scaled"))
        asked, answered = sem("asked"), sem("answered")
        sums_in, summed, out_ready = sem("sums_in"), sem("summed"), sem("out_ready")
        stage_ready, own_ready, own_summed, own_copied = (
            sem(n) for n in ("stage_ready", "own_ready", "own_summed", "own_copied"))
        pool_ready, pool_used, begun = sem("pool_ready"), sem("pool_used"), sem("begun")
        block = ctx.enter_context(nc.Block())
        loads = [(t, "w_" + k) for k, t in weights.items()] + [(t, "b_" + k) for k, t in bias.items()]
        loads += [(lna_g, "lna_g"), (lna_b, "lna_b"), (lnb_g, "lnb_g"), (lnb_b, "lnb_b"), (theta, "theta"), (temp, "temp"),
                  (thr, "thr"), (factor, "factor"), (base, "base"), (place, "place")]
        n_loaded = 16 * len(loads)

        FOCI = (((("a", "qkv"),), 0, 2, FT // FW), ((("a", "qkv"),), 10, 1, FT // FW), ((("a", "q"), ("b", "kv")), 20, 2, 1))
        OUT_JOB = 31
        CHUNK = 2048
        chunk_buf = lambda n: prod[:, n * CHUNK:(n + 1) * CHUNK]
        sum_bank = lambda n: ps_p[:, n % 4 // 2, 1 + n % 2, :]
        ASKED0 = 2

        def vector_steps(f):
            return STEPS * sum(len(inputs) + ITERS for inputs, _, _, _ in FOCI[:f])

        def scalar_steps(f):
            return STEPS * 2 * ITERS * f

        def half_chunks(nw):
            queries = CHUNK // (FT // nw * D)
            return FT // 2 // queries, queries

        def chunks_before(f):
            return sum(2 * ITERS * half_chunks(nw)[0] for _, _, _, nw in FOCI[:f])

        def products(eng, kind, q, nw, to):
            ck, (_, queries) = FT // nw, half_chunks(nw)
            w = q // ck * ck
            if kind == "scores":
                return eng.tensor_tensor(to.rearrange("p (q k d) -> p q k d", q=queries, k=ck),
                                         bc(qk[:, 0, q:q + queries, :].unsqueeze(2), [P, queries, ck, D]),
                                         bc(qk[:, 1, w:w + ck, :].unsqueeze(1), [P, queries, ck, D]), ALU.mult)
            vals = v0[:, w:w + ck, :].rearrange("p k (h e) -> p h e k", e=HD)
            s = score[:, 0:FT * ck * NH].rearrange("p (q k h) -> p q h k", q=FT, k=ck)
            for r in range(queries):
                last = eng.tensor_tensor(to[:, r * ck * D:(r + 1) * ck * D].rearrange("p (h e k) -> p h e k", h=NH, e=HD),
                                         bc(s[:, q + r, :, :].unsqueeze(2), [P, NH, HD, ck]), vals, ALU.mult)
            return last

        def sums_of(kind, q, nw):
            ck, (_, queries) = FT // nw, half_chunks(nw)
            if kind == "scores":
                return score[:, q * ck * NH:(q + queries) * ck * NH], HD
            return ai[:, q:q + queries, :].rearrange("p q d -> p (q d)"), ck

        def asked_before(f):
            return ASKED0 + sum(n + 2 * ITERS for _, _, n, _ in FOCI[:f])

        @block.sync
        def _(sp):
            for to, k in loads:
                sp.dma_start(to[:], W[k]).then_inc(loaded, 16)
            by_tile = scratch_in.rearrange("(n b) t d -> b t n d", b=2)
            for b in range(2):
                sp.dma_start(by_tile[b], C.X[S * b:S * b + FT, 0:C.NT, :]).then_inc(sent, 16)
            sp.dma_start(xb[:], ctx_rows[:, 0:FT, :]).then_inc(fetched, 16)
            sp.wait_ge(sent, 32)
            sp.dma_start(xa[:], scratch_in).then_inc(fetched, 16)
            sp.wait_ge(out_ready, 1)
            sp.dma_start(scratch_out, hat_a[:]).then_inc(sent, 16)
            sp.wait_ge(sent, 48)
            by_tile = scratch_out.rearrange("(n b) t d -> b t n d", b=2)
            for b in range(2):
                sp.dma_start(C.Y[S * b:S * b + FT, 0:C.NT, :], by_tile[b]).then_inc(returned, 16)

        @block.tensor
        def _(pe):
            pe.wait_ge(loaded, n_loaded)

            def turn(src, job, t):
                n = job * STEPS + t
                for r in range(4):
                    last = nc.tensor.transpose(ps_t[:, t % 2, r * P:(r + 1) * P], src[:, 4 * t + r, :], C.ident[:])
                last.then_inc(turned, 1)

            def multiply(ws, job, t, own, by_scalar):
                n = job * STEPS + t
                pe.wait_ge(rT_ready, n + 1)
                if t >= 2:
                    pe.wait_ge(act_taken if by_scalar else dve_taken, own + t - 1)
                for o, w in enumerate(ws):
                    for r in range(4):
                        to = ps_p[:, t % 2, o, r * D:(r + 1) * D]
                        last = nc.tensor.matmul(to, rT[:, t % 2, r * P:(r + 1) * P], weights[w][:], start=True,
                                                stop=not by_scalar)
                        if by_scalar:
                            last = nc.tensor.matmul(to, C.ones[0:1, :], bias[w][0:1, :], start=False, stop=True)
                last.then_inc(multiplied, 1)

            def run(src, ws, job, own, by_scalar, before):
                pe.wait_ge(src_ready, job + 1)
                if before is not None:
                    pe.wait_ge(*before)
                turn(src, job, 0)
                for t in range(1, STEPS):
                    turn(src, job, t)
                    multiply(ws, job, t - 1, own, by_scalar)
                multiply(ws, job, STEPS - 1, own, by_scalar)

            def sums(kind, nw, at):
                for c in range(half_chunks(nw)[0]):
                    to, n = sums_of(kind, c * half_chunks(nw)[1], nw)
                    width = CHUNK // n
                    parts = chunk_buf(c % 2).rearrange("p (x n) -> p x n", n=n)
                    pe.wait_ge(own_ready, at + c + 1)
                    pe.wait_ge(own_copied, at + c + 1)
                    for e in range(n):
                        last = nc.tensor.matmul(sum_bank(c)[:, 0:width], C.ident[:], parts[:, :, e], start=e == 0, stop=e == n - 1)
                    last.then_inc(own_summed, 1)

            def iteration(job, nw, at, ours, theirs, last_one):
                run(cur, ("qh",), job, ours, False, (act_taken, theirs))
                run(v0, ("vh",), job + 1, theirs, True, (dve_taken, ours + STEPS))
                sums("scores", nw, at)
                if not last_one:
                    run(k0, ("kh",), job + 2, theirs + STEPS, True, (act_taken, theirs + STEPS))
                sums("values", nw, at + half_chunks(nw)[0])

            for f, (inputs, first, _, nw) in enumerate(FOCI):
                chunks, n_in = 2 * half_chunks(nw)[0], len(inputs)
                before = (act_taken, scalar_steps(f)) if f else None
                for n, (src, ws) in enumerate(inputs):
                    run(hat_a if src == "a" else hat_b, tuple(ws), first + n, vector_steps(f) + n * STEPS, False, before)
                    before = (dve_taken, vector_steps(f) + (n + 1) * STEPS)
                run(k0, ("kh",), first + n_in, scalar_steps(f), True, before)
                ours, theirs = vector_steps(f) + n_in * STEPS, scalar_steps(f) + STEPS
                with pe.Fori(0, ITERS - 1) as it:
                    iteration(it * 3 + (first + n_in + 1), nw, it * chunks + chunks_before(f), it * STEPS + ours,
                              it * (2 * STEPS) + theirs, False)
                it = ITERS - 1
                iteration(it * 3 + (first + n_in + 1), nw, it * chunks + chunks_before(f), it * STEPS + ours,
                          it * (2 * STEPS) + theirs, True)
                pe.wait_ge(own_copied, chunks_before(f + 1) + 4)
                pe.wait_ge(sums_in, f + 1)
                nc.tensor.matmul(ps_p[:, 0, 2, 0:nw], C.ones[:], diff[:, 0:nw], start=True, stop=True).then_inc(summed, 1)
            run(xa, ("out",), OUT_JOB, vector_steps(len(FOCI)), False, (act_taken, scalar_steps(len(FOCI))))

        @block.scalar
        def _(act):
            act.wait_ge(loaded, n_loaded)

            def copies(job, affine):
                for t in range(STEPS):
                    act.wait_ge(turned, job * STEPS + t + 1)
                    if affine:
                        last = nc.scalar.activation(rT[:, t % 2, :], ps_t[:, t % 2, :], ACT.Identity, scale=lna_g[:, 0:1],
                                                    bias=lna_b[:, 0:1])
                    else:
                        last = nc.scalar.activation(rT[:, t % 2, :], ps_t[:, t % 2, :], ACT.Copy)
                    last.then_inc(rT_ready, 1)

            def copies_takes(job, to, asked_midway=None):
                def take(t):
                    act.wait_ge(multiplied, job * STEPS + t + 1)
                    nc.scalar.activation(to[:, 4 * t:4 * t + 4, :], ps_p[:, t % 2, 0, :].rearrange("p (r d) -> p r d", d=D),
                                         ACT.Copy).then_inc(act_taken, 1)

                for t in range(STEPS):
                    act.wait_ge(turned, job * STEPS + t + 1)
                    nc.scalar.activation(rT[:, t % 2, :], ps_t[:, t % 2, :], ACT.Copy).then_inc(rT_ready, 1)
                    if t:
                        take(t - 1)
                    if asked_midway and t == 1:
                        answer(*asked_midway)
                take(STEPS - 1)

            def answer(n, buf, fn):
                act.wait_ge(asked, n)
                nc.scalar.activation(buf, buf, fn).then_inc(answered, 1)

            def copy_sums(kind, nw, at):
                for c in range(half_chunks(nw)[0]):
                    to, n = sums_of(kind, c * half_chunks(nw)[1], nw)
                    act.wait_ge(own_summed, at + c + 1)
                    nc.scalar.activation(to, sum_bank(c)[:, 0:CHUNK // n], ACT.Copy).then_inc(own_copied, 1)

            def iteration(job, n, nw, at, last_one):
                copies(job, False)
                copies_takes(job + 1, v0)
                answer(n + 1, hv[:], ACT.Sqrt)
                copy_sums("scores", nw, at)
                if last_one:
                    answer(n + 2, score[:, 0:FT * FT // nw * NH], ACT.Exp)
                else:
                    copies_takes(job + 2, k0, (n + 2, score[:, 0:FT * FT // nw * NH], ACT.Exp))
                copy_sums("values", nw, at + half_chunks(nw)[0])

            answer(1, trig[:].rearrange("p a b t f -> p (a b t f)"), ACT.Sin)
            answer(2, scale[:], ACT.Sqrt)
            for f, (inputs, first, norms, nw) in enumerate(FOCI):
                for n in range(norms):
                    answer(asked_before(f) + n + 1, rs[:], ACT.Sqrt)
                for n in range(len(inputs)):
                    copies(first + n, True)
                copies_takes(first + len(inputs), k0)
                job0, n0, chunks = first + len(inputs) + 1, asked_before(f) + norms, 2 * half_chunks(nw)[0]
                with act.Fori(0, ITERS - 1) as it:
                    iteration(it * 3 + job0, it * 2 + n0, nw, it * chunks + chunks_before(f), False)
                it = ITERS - 1
                iteration(it * 3 + job0, it * 2 + n0, nw, it * chunks + chunks_before(f), True)
            copies(OUT_JOB, False)

        @block.gpsimd
        def _(pool):
            def multiply(kind, nw, at, stage):
                chunks, queries = half_chunks(nw)
                pool.wait_ge(stage_ready, stage + 1)
                pool.sem_inc(begun, 1)
                for c in range(chunks):
                    if c >= 2:
                        pool.wait_ge(pool_used, at + c - 1)
                        pool.sem_inc(begun, 1)
                    products(nc.gpsimd, kind, FT // 2 + c * queries, nw, chunk_buf(2 + c % 2)).then_inc(pool_ready, 1)

            def iteration(nw, at, stage, turn):
                wide = [P, FT * NH, HD]
                heads = lambda t: t.rearrange("p t (h e) -> p (t h) e", e=HD)
                k_hat = heads(qk[:, 1, :, :])
                pool.wait_ge(k_mean, turn + 1)
                pool.sem_inc(begun, 1)
                nc.gpsimd.tensor_tensor(k_hat, heads(k0[:]), bc(hm[:, FT * NH:].unsqueeze(2), wide), ALU.subtract)
                pool.drain()
                nc.gpsimd.tensor_tensor(prod[:, FT * D:2 * FT * D].rearrange("p (x e) -> p x e", e=HD), k_hat, k_hat,
                                        ALU.mult).then_inc(k_square, 1)
                pool.wait_ge(spread_ready, turn + 1)
                pool.sem_inc(begun, 1)
                nc.gpsimd.tensor_tensor(k_hat, k_hat, bc(hv[:, FT * NH:].unsqueeze(2), wide), ALU.mult).then_inc(k_scaled, 1)
                multiply("scores", nw, at, stage)
                multiply("values", nw, at + half_chunks(nw)[0], stage + 1)

            for f, (_, _, _, nw) in enumerate(FOCI):
                chunks = 2 * half_chunks(nw)[0]
                with pool.Fori(0, ITERS - 1) as it:
                    iteration(nw, it * chunks + chunks_before(f), it * 2 + 2 * ITERS * f, it + ITERS * f)
                iteration(nw, (ITERS - 1) * chunks + chunks_before(f), 2 * (ITERS - 1) + 2 * ITERS * f, ITERS * f + ITERS - 1)

        @block.vector
        def _(dve):
            dve.wait_ge(loaded, n_loaded)
            tt, ts, stt = nc.vector.tensor_tensor, nc.vector.tensor_scalar, nc.vector.scalar_tensor_tensor

            ts(cond[:], theta[:], 1.0 / 220.0, None, ALU.mult)
            dve.drain()
            ts(base[:], base[:], cond[:, 0:1], None, ALU.mult)
            dve.drain()
            for a in range(2):
                for b in range(2):
                    tt(ang[:, a, b, :, :], bc(place[:, a, :].unsqueeze(2), [P, FT, PAIRS]),
                       bc(base[:].unsqueeze(1), [P, FT, PAIRS]), ALU.mult)
            dve.drain()
            for b in range(2):
                ts(turns[:, :, b, :, :], ang[:, :, b, :, :], 1.0 / (2.0 * math.pi), 0.25 * b, ALU.mult, ALU.add)
            dve.drain()
            ts(turns[:], turns[:], ROUND, None, ALU.add)
            dve.drain()
            ts(turns[:], turns[:], -ROUND, None, ALU.add)
            dve.drain()
            for part in TWO_PI:
                stt(ang[:].rearrange("p a b t f -> p (a b t f)"), turns[:].rearrange("p a b t f -> p (a b t f)"), -part,
                    ang[:].rearrange("p a b t f -> p (a b t f)"), ALU.mult, ALU.add)
                dve.drain()
            ts(ang[:, :, 1, :, :], ang[:, :, 1, :, :], math.pi / 2, None, ALU.add)
            dve.drain()
            edge = 3.1415925
            ts(trig[:], ang[:], edge, -edge, ALU.min, ALU.max).then_inc(asked, 1)
            dve.wait_ge(answered, 1)
            ts(cond[:], temp[:], 0.0, None, ALU.is_gt)
            ts(scale[:], temp[:], 1.0, None, ALU.not_equal)
            dve.drain()
            tt(cond[:], cond[:], scale[:], ALU.mult)
            dve.drain()
            ts(diff[:, 0:1], temp[:], 1e-38, -1.0, ALU.max, ALU.add)
            dve.drain()
            tt(diff[:, 0:1], diff[:, 0:1], cond[:], ALU.mult)
            dve.drain()
            ts(diff[:, 0:1], diff[:, 0:1], 1.0, None, ALU.add)
            dve.drain()
            nc.vector.reciprocal(scale[:], diff[:, 0:1]).then_inc(asked, 1)
            dve.wait_ge(answered, 2)
            ts(scale[:], scale[:], HD ** -0.5, None, ALU.mult)
            dve.drain()
            ts(lnb_g[:, 0, :], lnb_g[:, 0, :], scale[:, 0:1], None, ALU.mult)
            ts(lnb_b[:, 0, :], lnb_b[:, 0, :], scale[:, 0:1], None, ALU.mult)
            dve.drain()

            def norm_rows(to, src, n):
                for t in range(FT):
                    nc.vector.bn_stats(st[:, t, :], src[:, t, :])
                dve.drain()
                for t in range(FT):
                    nc.vector.bn_aggr(mv[:, t, :], st[:, t, :])
                dve.drain()
                ts(rs[:], mv[:, :, 1], 1e-5, None, ALU.add).then_inc(asked, 1)
                tt(to[:], src[:], bc(mv[:, :, 0].unsqueeze(2), row), ALU.subtract)
                dve.wait_ge(answered, n)
                nc.vector.reciprocal(rs[:], rs[:])
                dve.drain()
                last = tt(to[:], to[:], bc(rs[:].unsqueeze(2), row), ALU.mult)
                dve.drain()
                return last

            def take(job, outs):
                for t in range(STEPS):
                    dve.wait_ge(multiplied, job * STEPS + t + 1)
                    for o, (to, b) in enumerate(outs):
                        got = ps_p[:, t % 2, o, :].rearrange("p (r d) -> p r d", d=D)
                        if b is None:
                            last = nc.vector.tensor_copy(to[:, 4 * t:4 * t + 4, :], got)
                        else:
                            last = tt(to[:, 4 * t:4 * t + 4, :], got, bc(b[:].unsqueeze(1), [P, 4, D]), ALU.add)
                    last.then_inc(dve_taken, 1)

            def rotate(buf, a):
                v = buf[:].rearrange("p t (h f e) -> p t h f e", h=NH, e=2)
                part = [prod[:, n * 1024:(n + 1) * 1024].rearrange("p (t h f) -> p t h f", t=FT, h=NH) for n in range(4)]
                sn, cs = (bc(trig[:, a, n, :, :].unsqueeze(2), [P, FT, NH, PAIRS]) for n in range(2))
                tt(part[0], v[:, :, :, :, 0], cs, ALU.mult)
                tt(part[1], v[:, :, :, :, 1], sn, ALU.mult)
                tt(part[2], v[:, :, :, :, 0], sn, ALU.mult)
                tt(part[3], v[:, :, :, :, 1], cs, ALU.mult)
                dve.drain()
                tt(v[:, :, :, :, 0], part[0], part[1], ALU.subtract)
                last = tt(v[:, :, :, :, 1], part[2], part[3], ALU.add)
                dve.drain()
                return last

            heads = lambda t: t.rearrange("p t (h e) -> p (t h) e", e=HD)
            HT = FT * NH
            wide = [P, HT, HD]

            def stage(kind, nw, at):
                chunks, queries = half_chunks(nw)

                def reduce(c):
                    dve.wait_ge(pool_ready, at + c + 1)
                    to, n = sums_of(kind, FT // 2 + c * queries, nw)
                    nc.vector.tensor_reduce(to, chunk_buf(2 + c % 2).rearrange("p (x n) -> p x n", n=n), AX,
                                            ALU.add).then_inc(pool_used, 1)

                for c in range(chunks):
                    if c >= 2:
                        dve.wait_ge(own_summed, at + c - 1)
                    products(nc.vector, kind, c * queries, nw, chunk_buf(c % 2)).then_inc(own_ready, 1)
                    if c:
                        reduce(c - 1)
                reduce(chunks - 1)
                dve.drain()
                dve.wait_ge(own_copied, at + chunks + 4)

            def iteration(job, n, nw, at, theirs, turn, last_one):
                ck = FT // nw
                mean, spread = hm[:, 0:HT], hv[:, 0:HT]
                dve.wait_ge(act_taken, theirs)
                nc.vector.tensor_reduce(hm[:, HT:], heads(k0[:]), AX, ALU.add)
                dve.drain()
                ts(hm[:, HT:], hm[:, HT:], 1.0 / HD, None, ALU.mult).then_inc(k_mean, 1)
                take(job, [(qk[:, 0, :, :], bias["qh"])])
                dve.drain()
                query, key = heads(qk[:, 0, :, :]), heads(qk[:, 1, :, :])
                square = [prod[:, m * FT * D:(m + 1) * FT * D].rearrange("p (x e) -> p x e", e=HD) for m in range(2)]
                nc.vector.tensor_reduce(mean, query, AX, ALU.add)
                dve.drain()
                ts(mean, mean, 1.0 / HD, None, ALU.mult)
                dve.drain()
                tt(query, query, bc(mean.unsqueeze(2), wide), ALU.subtract)
                dve.drain()
                tt(square[0], query, query, ALU.mult)
                dve.drain()
                nc.vector.tensor_reduce(spread, square[0], AX, ALU.add)
                dve.wait_ge(k_square, turn + 1)
                last = nc.vector.tensor_reduce(hv[:, HT:], square[1], AX, ALU.add)
                if not last_one:
                    last.then_inc(src_ready, 1)
                dve.drain()
                ts(hv[:], hv[:], 1.0 / HD, 1e-5, ALU.mult, ALU.add).then_inc(asked, 1)
                dve.wait_ge(answered, n + 1)
                nc.vector.reciprocal(hv[:], hv[:]).then_inc(spread_ready, 1)
                dve.drain()
                tt(query, query, bc(spread.unsqueeze(2), wide), ALU.mult)
                for m, x in ((0, query), (1, key)):
                    dve.drain()
                    if m:
                        dve.wait_ge(k_scaled, turn + 1)
                    tt(x, x, bc(lnb_g[:, m, :].unsqueeze(1), wide), ALU.mult)
                    dve.drain()
                    tt(x, x, bc(lnb_b[:, m, :].unsqueeze(1), wide), ALU.add)
                dve.drain()
                nc.vector.memset(most[:], 0.0).then_inc(stage_ready, 1)
                stage("scores", nw, at)
                s = score[:, 0:FT * ck * NH].rearrange("p (q k h) -> p q k h", q=FT, k=ck)
                turned_s = s.rearrange("p q k h -> p q h k")
                nc.vector.tensor_reduce(most[:], turned_s, AX, ALU.max)
                dve.drain()
                tt(s, s, bc(most[:].unsqueeze(2), [P, FT, ck, NH]), ALU.subtract).then_inc(asked, 1)
                dve.drain()
                dve.wait_ge(answered, n + 2)
                dve.wait_ge(act_taken, theirs + STEPS)
                nc.vector.memset(most[:], 0.0).then_inc(stage_ready, 1)
                nc.vector.tensor_reduce(den[:], turned_s, AX, ALU.add)
                dve.drain()
                nc.vector.reciprocal(den[:], den[:])
                stage("values", nw, at + half_chunks(nw)[0])
                tt(heads(ai[:]), heads(ai[:]), bc(den[:].rearrange("p t h -> p (t h)").unsqueeze(2), wide), ALU.mult)
                dve.drain()
                if last_one:
                    return
                change = prod[:, 0:FT * D]
                tt(change.rearrange("p (t d) -> p t d", d=D), ai[:], prev[:], ALU.subtract)
                dve.drain()
                nc.vector.tensor_reduce(diff[:, 0:nw], change.rearrange("p (w x) -> p w x", w=nw), AX, ALU.add,
                                        apply_absolute_value=True)
                nc.vector.tensor_copy(prev[:], ai[:])
                tt(cur[:], cur[:], ai[:], ALU.add).then_inc(src_ready, 2)
                dve.drain()

            nc.vector.memset(most[:], 0.0).then_inc(own_copied, 4)
            dve.wait_ge(fetched, 32)
            for f, (inputs, first, norms, nw) in enumerate(FOCI):
                n = asked_before(f)
                if f == 0:
                    norm_rows(xa, xa, n + 1)
                    norm_rows(hat_a, xa, n + 2)
                elif f == 1:
                    norm_rows(hat_a, xb, n + 1)
                else:
                    norm_rows(hat_a, xa, n + 1)
                    norm_rows(hat_b, xb, n + 2)
                nc.vector.memset(prev[:], 0.0).then_inc(src_ready, len(inputs))
                outs = [(cur, None), (k0, None), (v0, None)]
                if len(inputs) == 1:
                    take(first, outs)
                else:
                    take(first, outs[0:1])
                    take(first + 1, outs[1:3])
                dve.drain()
                rotate(k0, f // 2)
                nc.vector.memset(den[:], 0.0).then_inc(src_ready, 1)
                rotate(cur, f // 2)
                nc.vector.memset(den[:], 0.0).then_inc(src_ready, 2)
                job0, theirs = first + len(inputs) + 1, scalar_steps(f) + STEPS
                chunks = 2 * half_chunks(nw)[0]
                with dve.Fori(0, ITERS - 1) as it:
                    iteration(it * 3 + job0, it * 2 + n + norms, nw, it * chunks + chunks_before(f),
                              it * (2 * STEPS) + theirs, it + ITERS * f, False)
                nc.vector.tensor_copy(done[:, 0:nw], diff[:, 0:nw]).then_inc(sums_in, 1)
                it = ITERS - 1
                iteration(it * 3 + job0, it * 2 + n + norms, nw, it * chunks + chunks_before(f), it * (2 * STEPS) + theirs,
                          it + ITERS * f, True)
                dve.wait_ge(summed, f + 1)
                count = P * NH * (FW if nw > 1 else S) * HD
                ts(kept[:, 0:nw], ps_p[:, 0, 2, 0:nw], 1.0 / count, None, ALU.mult)
                dve.drain()
                ts(done[:, 0:nw], kept[:, 0:nw], factor[:, 0:1], thr[:, 0:1], ALU.mult, ALU.add)
                dve.drain()
                tt(done[:, 0:nw], kept[:, 0:nw], done[:, 0:nw], ALU.is_lt)
                dve.drain()
                ts(kept[:, 0:nw], done[:, 0:nw], -1.0, 1.0, ALU.mult, ALU.add)
                dve.drain()
                to = xb if f == 1 else xa
                flat = lambda t, w: t[:, w * FT // nw:(w + 1) * FT // nw, :].rearrange("p t d -> p (t d)")
                for w in range(nw):
                    ts(flat(ai, w), flat(ai, w), kept[:, w:w + 1], None, ALU.mult)
                dve.drain()
                for w in range(nw):
                    last = stt(flat(to, w), flat(prev, w), done[:, w:w + 1], flat(ai, w), ALU.mult, ALU.add)
                if f == 2:
                    last.then_inc(src_ready, 1)
                dve.drain()
            take(OUT_JOB, [(hat_a, None)])
            dve.drain()
            nc.vector.memset(den[:], 0.0).then_inc(out_ready, 1)
            dve.wait_ge(returned, 32)
            for b in range(2):
                r = slice(S * b, S * b + FT)
                tt(C.X[r, 0:C.NT, :], C.X[r, 0:C.NT, :], C.Y[r, 0:C.NT, :], ALU.add)
            dve.drain()
            with dve.Fori(0, C.NT // ROW_TILES) as i:
                row_stats(nc, dve, C, C.X, gst, gmv, i, ROW_TILES)
                dve.drain()


def store_x(C, out):
    nc = C.nc
    with ExitStack() as ctx:
        sc = Scope(nc, ctx, "store")
        stored = sc.sem("stored")
        block = ctx.enter_context(nc.Block())

        @block.sync
        def _(sp):
            sp.dma_start(out.rearrange("(n p) d -> p n d", p=P), C.X[:, 0:C.NT, :]).then_inc(stored, 16)
            sp.wait_ge(stored, 16)



def constants():
    c = {"ident": np.eye(P, dtype=np.float32)}
    pos = np.arange(S, dtype=np.float32)
    lower = np.tril(np.ones((S, S), np.float32))
    c["tril"] = np.concatenate([lower, lower])
    row = np.arange(P)
    c["hmask"] = (row[:, None] // HD % HR == np.arange(HR)[None, :]).astype(np.float32)
    inv = (1.0 / 10000.0 ** (np.arange(0, HD, 2, dtype=np.float32) / HD)).astype(np.float32)
    ang = (pos[:, None] * inv[None, :]).astype(np.float32)
    c["cosT"] = np.tile(np.repeat(np.cos(ang), 2, axis=1).T, (NH, 1)).astype(np.float32)
    c["sinT"] = np.tile(np.repeat(np.sin(ang), 2, axis=1).T, (NH, 1)).astype(np.float32)
    c["falling"] = np.tile(np.arange(NE, 0, -1, dtype=np.float32), (P, 1))
    dist = np.abs(pos[:, None] - pos[None, :])

    def twice(t):
        t = t.astype(np.float32).transpose(1, 0, 2)
        return np.concatenate([t, t])
    slopes = 2.0 ** (-8.0 * np.arange(NH) / NH)
    c["table0"] = twice(-slopes[:, None, None].astype(np.float32) * dist)
    m = np.exp(-np.power(5000.0, (np.arange(1, NH + 1) - 1.0) / (NH - 1.0) * 0.8))
    c["table1"] = twice(m[:, None, None].astype(np.float32) * (1000.0 + dist))
    slopes = 0.5 ** np.arange(1, NH + 1)
    c["table3"] = twice(-np.maximum(pos[:, None] - pos[None, :], 0) * slopes[:, None, None].astype(np.float32))
    slopes = (2.0 ** (-2.0 ** -(math.log2(32) - 3))) ** np.arange(1, 33, dtype=np.float32)
    rel = pos[None, :] - pos[:, None]
    bias = np.where(rel <= 0, slopes.astype(np.float32)[:, None, None] * rel, np.float32(-BIG))
    bias = bias.reshape(4, 2, 2, 2, S, S).transpose(0, 2, 1, 3, 4, 5).reshape(32, S, S)
    c["table_a3"] = twice(bias).reshape(P, 4, UH, S)
    perm = np.zeros((P, P), np.float32)
    quarter = np.arange(D // 4)
    for to, of, sign in ((0, 2, 1), (1, 3, -1), (2, 0, -1), (3, 1, 1)):
        perm[of * 32 + quarter, to * 32 + quarter] = sign
    c["perm"] = perm
    pick_row = np.zeros((P, 2 * NS), np.float32)
    for part in (0, 64, 96):
        pick_row[part + np.arange(2 * NS), np.arange(2 * NS)] = 1
    c["pick_row"] = pick_row
    c["flip"] = np.kron(np.eye(2, dtype=np.float32), np.eye(S, dtype=np.float32)[::-1]).astype(np.float32)
    mel = np.linspace(0.0, 2595.0 * np.log10(1.0 + 4000.0 / 200.0), PAIRS)
    c["base"] = np.tile((200.0 * (10.0 ** (mel / 2595.0) - 1.0) / 1000.0).astype(np.float32), (P, 1))
    c["place"] = np.tile(np.stack([np.arange(FT) % FW, np.arange(FT)]).astype(np.float32), (P, 1, 1))
    return c


def layouts(v):
    t = lambda n: np.ascontiguousarray(v[n].T)
    col = lambda n: np.ascontiguousarray(v[n].reshape(-1, 1))
    row = lambda n: np.ascontiguousarray(v[n].reshape(1, -1))
    rep = lambda n: np.ascontiguousarray(np.broadcast_to(v[n].reshape(1, -1), (P, v[n].size)))
    a = {"x": v["x"].reshape(-1, D), "ctxT": np.ascontiguousarray(v["ctx_1024"].reshape(-1, D).T)}
    for k in ("Wq", "Wk", "Wv", "Wo"):
        a["a0_" + k] = t("L0_attn_" + k)
        a["c0_" + k] = t("L0_xattn_" + k)
    for k in ("bq", "bk", "bv"):
        a["c0_" + k] = col("L0_xattn_" + k)
    a["c0_bo"] = row("L0_xattn_bo")
    for k in ("Wq", "Wk", "Wv", "Wc", "Wo"):
        a["a1_" + k] = v["L1_attn_" + k]
    a["a1_We"] = np.ascontiguousarray(np.repeat(v["L1_attn_We"].reshape(S, 4, 1, HD), NH // 4, axis=2).reshape(S, D))
    for k in ("bq", "bk", "bv"):
        a["a1_" + k] = col("L1_attn_" + k)
    a["a1_bo"] = row("L1_attn_bo")
    a["a1_gamma"], a["a1_beta"] = rep("L1_attn_gamma"), rep("L1_attn_beta")
    qkv = v["L2_ffn_W_qkv"]
    for n, k in enumerate(("Wq", "Wk", "Wv")):
        a["f2_" + k] = np.ascontiguousarray(qkv[n * D:(n + 1) * D].T)
    a["f2_Wo"] = t("L2_ffn_W_out")
    a["f2_wr"] = rep("L2_ffn_w_router")
    a["f2_g1"], a["f2_g2"] = col("L2_ffn_g1"), col("L2_ffn_g2")
    for k, n in (("Wq", "wq"), ("Wk", "wk"), ("Wv", "wv"), ("Wo", "out")):
        a["c3_" + k] = t(f"L3_xattn_{n}_w")
        a["c3_b" + k[1]] = (row if k == "Wo" else col)(f"L3_xattn_{n}_b")
    a["f0_wi"], a["f0_wo"] = t("L0_ffn_wi_W"), t("L0_ffn_wo_W")
    lora_a = v["L0_ffn_lora_A"].reshape(-1, D)
    a["f0_ga"] = np.ascontiguousarray(np.concatenate([v["L0_ffn_gate_W"], lora_a]).T)
    a["f0_B"] = np.ascontiguousarray(v["L0_ffn_lora_B"].transpose(0, 2, 1).reshape(lora_a.shape[0], -1))
    a["f0_gb"] = rep("L0_ffn_gate_b")
    a["f0_wib"] = np.ascontiguousarray(v["L0_ffn_wi_b"].reshape(-1, P).T)
    a["f0_wob"] = row("L0_ffn_wo_b")
    a["f2_w1"], a["f2_w2"], a["f2_w3"] = t("L2_ffn_W1"), t("L2_ffn_W2"), t("L2_ffn_W3")
    a["f3_wr"], a["f3_w1"], a["f3_w2"] = v["L3_ffn_router_w"], v["L3_ffn_w1"], v["L3_ffn_w2"]
    c2 = lambda n: np.ascontiguousarray(v["L2_xattn_" + n].reshape(D, 1, NJ, 2, HW))
    a["c2_wq"], a["c2_wk"] = c2("Wq").reshape(D, NJ, P), c2("Wk").reshape(D, NJ, P)
    a["c2_wv"] = np.ascontiguousarray(c2("Wv").transpose(0, 3, 1, 2, 4)).reshape(D, 2, NJ * HW)
    a["c2_wo"] = np.ascontiguousarray(v["L2_xattn_Wo"].reshape(NJ, P, D).transpose(1, 0, 2))
    a["c2_bo"] = row("L2_xattn_bo")
    w = v["L3_attn_W_qkv"]
    nq, nk = 32, 16
    q = w[:, :nq * HW].reshape(D, 4, 2, 2, 2, HW)
    a["a3_wq"] = np.ascontiguousarray(q.transpose(0, 1, 2, 4, 3, 5)).reshape(D, 16, P)
    a["a3_wk"] = w[:, nq * HW:(nq + nk) * HW].reshape(D, 8, P)
    vv = w[:, (nq + nk) * HW:].reshape(D, 8, 2, HW)
    a["a3_wv"] = np.ascontiguousarray(vv.transpose(0, 2, 1, 3)).reshape(D, 2, 8 * HW)
    o = v["L3_attn_W_out"].reshape(4, 2, 2, 2, HW, D)
    a["a3_wo"] = np.ascontiguousarray(o.transpose(2, 4, 0, 1, 3, 5)).reshape(P, 16, D)
    wide = lambda x: np.ascontiguousarray(np.broadcast_to(x.reshape(-1, 1), (x.size, P)))
    one = lambda n: np.ascontiguousarray(np.broadcast_to(v[n].reshape(1, 1), (P, 1)))
    for n in range(3):
        a[f"f1_w{n}"], a[f"f1_b{n}"] = v[f"L1_ffn_cn_w{n + 1}"], col(f"L1_ffn_cn_b{n + 1}")
    for n in range(2):
        a[f"f1_gw{n}"], a[f"f1_gb{n}"] = v[f"L1_ffn_gc_w{n + 1}"], col(f"L1_ffn_gc_b{n + 1}")
    a["f1_w3"], a["f1_b3"] = wide(v["L1_ffn_cn_w4"]), one("L1_ffn_cn_b4")
    a["f1_gw2"], a["f1_gb2"] = wide(v["L1_ffn_gc_w3"]), one("L1_ffn_gc_b3")
    a["f1_reach"] = one("L1_ffn_adaptive_range")
    halves = lambda x: np.ascontiguousarray(x.reshape(NHF, P, -1).transpose(1, 0, 2))
    for d in ("m1", "m2"):
        m = lambda n: v[f"L2_attn_{d}_{n}"]
        a[d + "_in_w"] = np.ascontiguousarray(m("in_w").T)
        a[d + "_taps"] = np.ascontiguousarray(np.broadcast_to(m("conv_w").T[None], (P, NTAP, DI)))
        a[d + "_conv_b"], a[d + "_dt_b"], a[d + "_D"] = (halves(m(n))[:, :, 0].copy() for n in ("conv_b", "dt_b", "D"))
        low = np.zeros((DI, P), np.float32)
        low[:, 32:32 + DTR] = m("xproj_w")[:DTR].T
        for at in (0, 64, 96):
            low[:, at:at + 2 * NS] = m("xproj_w")[DTR:].T
        a[d + "_xp"], a[d + "_out_w"] = halves(low), halves(m("out_w").T)
        a[d + "_dt_w"], a[d + "_A"] = np.ascontiguousarray(m("dt_w").T), halves(m("Alog"))
        a[d + "_g"], a[d + "_be"] = col("L2_attn_norm_g"), col("L2_attn_norm_b")
    a["m3_w1"], a["m3_w2"] = t("L2_attn_ff1_w"), t("L2_attn_ff2_w")
    a["m3_b1"], a["m3_b2"] = np.ascontiguousarray(v["L2_attn_ff1_b"].reshape(-1, P).T), row("L2_attn_ff2_b")
    a["m3_g"], a["m3_be"] = col("L2_attn_ffn_g"), col("L2_attn_ffn_b")
    a["ctx"] = v["ctx_1024"]
    wkv = v["L1_xattn_Wkv"]
    a["x1_w_q"], a["x1_w_out"] = t("L1_xattn_Wq"), t("L1_xattn_Wout")
    a["x1_w_k"], a["x1_w_v"] = np.ascontiguousarray(wkv[:D].T), np.ascontiguousarray(wkv[D:].T)
    for k in ("qh", "kh", "vh"):
        blocks_ = np.zeros((NH, HD, NH, HD), np.float32)
        for h in range(NH):
            blocks_[h, :, h, :] = v["L1_xattn_W" + k].T
        a["x1_w_" + k] = blocks_.reshape(D, D)
        a["x1_b_" + k] = np.ascontiguousarray(np.tile(v["L1_xattn_b" + k].reshape(1, HD), (P, NH)))
    a["x1_lna_g"], a["x1_lna_b"] = col("L1_xattn_lna_g"), col("L1_xattn_lna_b")
    a["x1_lnb_g"], a["x1_lnb_b"] = (np.ascontiguousarray(np.tile(v["L1_xattn_lnb_" + k].reshape(1, 1, HD), (P, 2, 1)))
                                    for k in "gb")
    for k, n in (("theta", "theta"), ("temp", "temp"), ("thr", "threshold"), ("factor", "factor")):
        a["x1_" + k] = one("L1_xattn_" + n)
    m = v["mask_1x1xSxS2_ik0"].reshape(S, S)
    a["mask"] = np.concatenate([m, m])
    return a


def pick(A, prefix, /, **names):
    return {k: A[n if n in A else prefix + n][:] for k, n in names.items()}


def blocks(C, A):
    qkvo = dict(wq="Wq", wk="Wk", wv="Wv", wo="Wo", hmask="hmask")

    def l0_attn():
        attn16(C, "a0", "rope", pick(A, "a0_", cosT="cosT", sinT="sinT", table="table0", **qkvo))

    def l0_xattn():
        attn16(C, "c0", "ctx", pick(A, "c0_", bq="bq", bk="bk", bv="bv", bo="bo", table="table1", **qkvo), A["ctxT"])

    def l1_attn():
        attn16(C, "a1", "linear", pick(A, "a1_", bq="bq", bk="bk", bv="bv", bo="bo", wc="Wc", we="We", tril="tril",
                                       **qkvo))
        affine_norm(C, "a1n", A["a1_gamma"], A["a1_beta"])

    def l2_ffn():
        attn16(C, "f2", "rank", pick(A, "f2_", g1="g1", wr="wr", tril="tril", **qkvo))
        gated_ffn(C, "g2", pick(A, "f2_", w1="w1", w2="w2", w3="w3", g="g2"))

    def l0_ffn():
        lora_ffn(C, "f0", pick(A, "f0_", wi="wi", wo="wo", ga="ga", B="B", gb="gb", wib="wib", wob="wob", falling="falling"))

    def l3_ffn():
        topk_ffn(C, "f3", pick(A, "f3_", wr="wr", w1="w1", w2="w2", falling="falling"))

    def l1_xattn():
        scratch = [C.nc.dram_tensor(n, (P, FT, D), F32, kind="Internal").ap() for n in ("focus_rows", "focus_out")]
        names = ["w_q", "w_k", "w_v", "w_qh", "w_kh", "w_vh", "w_out", "b_qh", "b_kh", "b_vh", "lna_g", "lna_b", "lnb_g",
                 "lnb_b", "theta", "temp", "thr", "factor", "base", "place"]
        focus_block(C, "x1", A["ctx"], *scratch, pick(A, "x1_", **{n: n for n in names}))

    def l1_ffn():
        names = [f"{k}{n}" for k, m in (("w", 4), ("b", 4), ("gw", 3), ("gb", 3)) for n in range(m)]
        coupled_ffn(C, "f1", pick(A, "f1_", perm="perm", reach="reach", **{n: n for n in names}))

    def l2_attn():
        names = ("in_w", "taps", "conv_b", "xp", "dt_w", "dt_b", "A", "D", "out_w", "pick_row", "flip", "g", "be")
        for d in ("m1", "m2"):
            mamba(C, d, pick(A, d + "_", **{n: n for n in names}), d == "m1")
        mamba_join(C, "mj")
        gelu_ffn(C, "m3", pick(A, "m3_", w1="w1", w2="w2", b1="b1", b2="b2", g="g", be="be"))

    def l2_xattn():
        attn64(C, "c2", pick(A, "c2_", wq="wq", wk="wk", wv="wv", wo="wo", bo="bo"), 1, 1, A["ctxT"])

    def l3_attn():
        attn64(C, "a3", pick(A, "a3_", wq="wq", wk="wk", wv="wv", wo="wo", table="table_a3"), 4, 2)

    def l3_xattn():
        attn16(C, "c3", "mask", pick(A, "c3_", bq="bq", bk="bk", bv="bv", bo="bo", table="table3", mask="mask",
                                     **qkvo), A["ctxT"])

    return {0: l0_attn, 1: l0_xattn, 2: l0_ffn, 3: l1_attn, 4: l1_xattn, 5: l1_ffn, 6: l2_attn, 7: l2_xattn, 8: l2_ffn, 9: l3_attn, 10: l3_xattn, 11: l3_ffn}


def program(nc, A, out, groups, which):
    with ExitStack() as ctx:
        C = Core(nc, ctx, groups)
        load_x(C, A["x"], A)
        todo = blocks(C, A)
        for n in which:
            todo[n]()
        store_x(C, out)


def kernel(**inputs):
    import concourse.bacc as bacc
    from concourse.bass_utils import run_bass_kernel_spmd

    v = {k: np.asarray(a) for k, a in inputs.items()}
    arrays = {"in_" + k: np.ascontiguousarray(a) for k, a in {**constants(), **layouts(v)}.items()}
    nc = bacc.Bacc("TRN2", target_bir_lowering=False, num_devices=1)
    A = {k[3:]: nc.dram_tensor(k, a.shape, mybir.dt.from_np(a.dtype), kind="ExternalInput").ap() for k, a in arrays.items()}
    rows_out = v["x"].shape[0] * S
    out = nc.dram_tensor("out_0_dram", (rows_out, D), F32, kind="ExternalOutput").ap()
    program(nc, A, out, rows_out // (4 * P), range(12))
    result = run_bass_kernel_spmd(nc, [arrays], core_ids=[0])
    return result.results[0]["out_0_dram"].reshape(v["x"].shape)
```
